# Optimizing a Trainium2 kernel written in Bass

```python
import numpy as np
import jax
import jax.numpy as jnp

def _softmax(x, axis=-1):
    return jax.nn.softmax(x, axis=axis)

def _gelu(x):
    return jax.nn.gelu(x, approximate=True)

def _silu(x):
    return jax.nn.silu(x)

def _sigmoid(x):
    return jax.nn.sigmoid(x)

def _layernorm(x, axis=-1, eps=1e-05):
    m = jnp.mean(x, axis=axis, keepdims=True)
    v = jnp.var(x, axis=axis, keepdims=True)
    return (x - m) / jnp.sqrt(v + eps)

def _scatter_add(tgt, idx, src, axis=0):
    return tgt.at[idx].add(src)

def _segment_sum(src, seg, n):
    return jax.ops.segment_sum(src, seg, n)
kernel_name = 'mk_perceiver_d4_seqx_r8_edff40'

def setup_inputs(seed: int=0):
    np.random.seed(seed)
    _w = jnp.asarray

    def _rec_inputs():
        import jax
        import jax.numpy as jnp
        _rk = jax.random.key(seed)
        x = -0.0003929 + 0.9999 * jax.random.normal(jax.random.fold_in(_rk, 1), (32, 64, 128), jnp.float32)
        _lenS = 64 - jax.random.randint(jax.random.fold_in(_rk, 7), (32,), 0, max(1, 64 // 4) + 1, jnp.int32)
        _lenS2 = 1601 - jax.random.randint(jax.random.fold_in(_rk, 8), (32,), 0, max(1, 1601 // 4) + 1, jnp.int32)
        _ctx_1024P = jax.random.normal(jax.random.fold_in(_rk, 11), (32, 16, 128), jnp.float32)
        _ctx_1024c = jax.random.dirichlet(jax.random.fold_in(_rk, 511), 0.3 * jnp.ones((16,), jnp.float32), (32, 1601))
        _ctx_1024t = jnp.einsum('bsk,bkd->bsd', _ctx_1024c, _ctx_1024P)
        _ctx_1024t = _ctx_1024t * jax.lax.rsqrt(jnp.mean(jnp.square(_ctx_1024t)) + 1e-12) * 0.953939
        ctx_1024 = 2.81802e-05 + 1.00001 * (_ctx_1024t + 0.3 * jax.random.normal(jax.random.fold_in(_rk, 611), (32, 1601, 128), jnp.float32))
        _validS = jnp.arange(64)[None, :] < _lenS[:, None]
        _validS2 = jnp.arange(1601)[None, :] < _lenS2[:, None]
        _causal = jnp.tril(jnp.ones((64, 64), dtype=bool))
        mask_BxS2_ik0 = jnp.where(jnp.broadcast_to(_validS2[:, :], (32, 1601)), 0, 1).astype(jnp.int32)
        mask_1x1xSxS2_bk1 = jnp.broadcast_to(_validS2[0:1, None, None, :], (1, 1, 64, 1601))
        mask_BxSxS2_bk1 = jnp.broadcast_to(_validS2[:, None, :], (32, 64, 1601))
        return (x, ctx_1024, mask_BxS2_ik0, mask_1x1xSxS2_bk1, mask_BxSxS2_bk1)
    x, ctx_1024, mask_BxS2_ik0, mask_1x1xSxS2_bk1, mask_BxSxS2_bk1 = _rec_inputs()

    def _L0_xattn_setup():
        import jax, jax.numpy as jnp
        import numpy as np
        D = 128
        NEG = -1000000000.0
        key = jax.random.key(seed)
        ks = jax.random.split(key, 9)
        B, Lq, Lk, d = (8, 256, 256, D)
        s = 1.0 / np.sqrt(d)
        return {'hm_tokens': jax.random.normal(ks[0], (B, Lq, d), jnp.float32), 'text_tokens': jax.random.normal(ks[1], (B, Lk, d), jnp.float32), 'text_mask': jax.random.randint(ks[2], (B, Lk), 0, 2, jnp.int32), 'Wq': jax.random.normal(ks[3], (d, d), jnp.float32) * s, 'bq': jnp.zeros((d,), jnp.float32), 'Wk': jax.random.normal(ks[4], (d, d), jnp.float32) * s, 'bk': jnp.zeros((d,), jnp.float32), 'Wv': jax.random.normal(ks[5], (d, d), jnp.float32) * s, 'bv': jnp.zeros((d,), jnp.float32)}
    _L0_xattn_all = _L0_xattn_setup()
    _L0_xattn_in = {k: v for k, v in _L0_xattn_all.items() if k in ('Wq', 'bq', 'Wk', 'bk', 'Wv', 'bv')}
    del _L0_xattn_all

    def _L0_attn_setup():
        import jax, jax.numpy as jnp
        import numpy as np
        B, S, D, F = (4, 512, 128, 32)

        def _ln(x, g, b, eps=1e-05):
            m = x.mean(-1, keepdims=True)
            v = ((x - m) ** 2).mean(-1, keepdims=True)
            return (x - m) / jnp.sqrt(v + eps) * g + b
        key = jax.random.key(seed)
        ks = jax.random.split(key, 8)
        return {'x': jax.random.normal(ks[0], (B, S, D), jnp.float32), 'W_to': jax.random.normal(ks[1], (2 * F, D), jnp.float32) * 0.02, 'log_decay': jnp.zeros((F,), jnp.float32), 'frequencies': jax.random.normal(ks[2], (F,), jnp.float32) * 0.01, 'W_from': jax.random.normal(ks[3], (D, 2 * F), jnp.float32) * 0.02, 'ln1_g': jnp.ones((D,), jnp.float32), 'ln1_b': jnp.zeros((D,), jnp.float32), 'ln3_g': jnp.ones((D,), jnp.float32), 'ln3_b': jnp.zeros((D,), jnp.float32), 'W_ffn1': jax.random.normal(ks[4], (4 * D, D), jnp.float32) * 0.02, 'b_ffn1': jnp.zeros((4 * D,), jnp.float32), 'W_ffn2': jax.random.normal(ks[5], (D, 4 * D), jnp.float32) * 0.02, 'b_ffn2': jnp.zeros((D,), jnp.float32)}
    _L0_attn_all = _L0_attn_setup()
    _L0_attn_in = {k: v for k, v in _L0_attn_all.items() if k in ('W_to', 'log_decay', 'frequencies', 'W_from', 'ln1_g', 'ln1_b', 'ln3_g', 'ln3_b', 'W_ffn1', 'b_ffn1', 'W_ffn2', 'b_ffn2')}
    del _L0_attn_all

    def _L0_ffn_setup():
        import jax, jax.numpy as jnp
        import numpy as np
        key = jax.random.key(seed)
        k1, k2, k3, k4 = jax.random.split(key, 4)
        B, T, M = (4, 256, 128)
        E, F = (16, 512)
        x = jax.random.normal(k1, (B, T, M), dtype=jnp.float32) * 0.02
        Wg = jax.random.normal(k2, (M, E), dtype=jnp.float32) * 0.02
        w1 = jax.random.normal(k3, (E, M, F), dtype=jnp.float32) * 0.02
        w2 = jax.random.normal(k4, (E, F, M), dtype=jnp.float32) * 0.02
        return {'x': x, 'Wg': Wg, 'w1': w1, 'w2': w2}
    _L0_ffn_all = _L0_ffn_setup()
    _L0_ffn_in = {k: v for k, v in _L0_ffn_all.items() if k in ('Wg', 'w1', 'w2')}
    del _L0_ffn_all

    def _L1_xattn_setup():
        import jax, jax.numpy as jnp
        import numpy as np
        B, L, D = (8, 256, 128)
        key = jax.random.key(seed)
        k1, k2, k3 = jax.random.split(key, 3)
        enc_outputs = jax.random.normal(k1, (B, L, D), dtype=jnp.float32)
        x = jax.random.normal(k2, (B, L, D), dtype=jnp.float32)
        Wq = jax.random.normal(k3, (D, D), dtype=jnp.float32) * (1.0 / np.sqrt(D))
        return {'enc_outputs': enc_outputs, 'x': x, 'Wq': Wq}
    _L1_xattn_all = _L1_xattn_setup()
    _L1_xattn_in = {k: v for k, v in _L1_xattn_all.items() if k in ('Wq',)}
    del _L1_xattn_all

    def _L1_attn_setup():
        import jax, jax.numpy as jnp
        import numpy as np
        import math
        N_HEAD = 16

        def _causal_attn(q, k, v):
            d_k = q.shape[-1]
            s = jnp.einsum('bhqd,bhkd->bhqk', q, k) / math.sqrt(d_k)
            L, S = (q.shape[-2], k.shape[-2])
            mask = jnp.tril(jnp.ones((L, S), dtype=bool))
            s = jnp.where(mask, s, -jnp.inf)
            a = jax.nn.softmax(s, axis=-1)
            return jnp.einsum('bhqk,bhkd->bhqd', a, v)
        key = jax.random.key(seed)
        ks = jax.random.split(key, 8)
        B, T, C = (2, 256, 128)
        scale = 0.02
        return {'x': jax.random.normal(ks[0], (B, T, C), dtype=jnp.float32), 'W_attn': jax.random.normal(ks[1], (C, 2 * C), dtype=jnp.float32) * scale, 'b_attn': jnp.zeros((2 * C,), dtype=jnp.float32), 'W_k2': jax.random.normal(ks[2], (C, C), dtype=jnp.float32) * scale, 'b_k2': jnp.zeros((C,), dtype=jnp.float32), 'W_proj': jax.random.normal(ks[3], (C, C), dtype=jnp.float32) * scale, 'b_proj': jnp.zeros((C,), dtype=jnp.float32)}
    _L1_attn_all = _L1_attn_setup()
    _L1_attn_in = {k: v for k, v in _L1_attn_all.items() if k in ('W_attn', 'b_attn', 'W_k2', 'b_k2', 'W_proj', 'b_proj')}
    del _L1_attn_all

    def _L1_ffn_setup():
        import jax, jax.numpy as jnp
        import numpy as np
        from jax import lax
        LOKAL_GRUP = 7
        TOP_K = 2
        EPS = 1e-08
        CACHE_BONUS = 0.1

        def _route(tokens, uzman_embeddings, onbellek_durumu):
            sim = tokens @ uzman_embeddings.T
            _, local_idx = lax.top_k(sim, LOKAL_GRUP)
            t_norm = tokens / (jnp.linalg.norm(tokens, axis=-1, keepdims=True) + EPS)
            e_norm = uzman_embeddings / (jnp.linalg.norm(uzman_embeddings, axis=-1, keepdims=True) + EPS)
            local_embs = e_norm[local_idx]
            scores = jnp.einsum('nld,nd->nl', local_embs, t_norm)
            scores = scores + CACHE_BONUS * onbellek_durumu[local_idx]
            top_scores, top_local = lax.top_k(scores, TOP_K)
            global_idx = jnp.take_along_axis(local_idx, top_local, axis=1)
            weights = jax.nn.softmax(top_scores, axis=-1)
            return (global_idx, lax.stop_gradient(weights))
        key = jax.random.key(seed)
        ks = jax.random.split(key, 6)
        B, S, D, E, H = (2, 256, 128, 8, 512)
        return {'x': jax.random.normal(ks[0], (B, S, D), jnp.float32), 'uzman_embeddings': jax.random.normal(ks[1], (E, D), jnp.float32) * 0.01, 'W1': jax.random.normal(ks[2], (E, D, H), jnp.float32) * 0.02, 'b1': jax.random.normal(ks[3], (E, H), jnp.float32) * 0.02, 'W2': jax.random.normal(ks[4], (E, H, D), jnp.float32) * 0.02, 'b2': jax.random.normal(ks[5], (E, D), jnp.float32) * 0.02, 'onbellek_durumu': jnp.ones((E,), jnp.float32)}
    _L1_ffn_all = _L1_ffn_setup()
    _L1_ffn_in = {k: v for k, v in _L1_ffn_all.items() if k in ('uzman_embeddings', 'W1', 'b1', 'W2', 'b2', 'onbellek_durumu')}
    del _L1_ffn_all

    def _L2_xattn_setup():
        import jax, jax.numpy as jnp
        import numpy as np
        D_MODEL = 128
        NUM_HEADS = 16
        D_K = D_MODEL // NUM_HEADS

        def _split(x):
            B, S, _ = x.shape
            return x.reshape(B, S, NUM_HEADS, D_K).transpose(0, 2, 1, 3)
        key = jax.random.key(seed)
        ks = jax.random.split(key, 8)
        B, S = (2, 256)
        query = jax.random.normal(ks[0], (B, S, D_MODEL), dtype=jnp.float32)
        k_in = jax.random.normal(ks[1], (B, S, D_MODEL), dtype=jnp.float32)
        value = jax.random.normal(ks[2], (B, S, D_MODEL), dtype=jnp.float32)
        mask = jnp.triu(jnp.ones((S, S), dtype=bool), k=1)[None, None, :, :]
        scale = 1.0 / np.sqrt(D_MODEL)
        W_q = jax.random.normal(ks[3], (D_MODEL, D_MODEL), dtype=jnp.float32) * scale
        W_k = jax.random.normal(ks[4], (D_MODEL, D_MODEL), dtype=jnp.float32) * scale
        W_v = jax.random.normal(ks[5], (D_MODEL, D_MODEL), dtype=jnp.float32) * scale
        W_o = jax.random.normal(ks[6], (D_MODEL, D_MODEL), dtype=jnp.float32) * scale
        return {'query': query, 'key': k_in, 'value': value, 'mask': mask, 'W_q': W_q, 'W_k': W_k, 'W_v': W_v, 'W_o': W_o}
    _L2_xattn_all = _L2_xattn_setup()
    _L2_xattn_in = {k: v for k, v in _L2_xattn_all.items() if k in ('W_q', 'W_k', 'W_v', 'W_o')}
    del _L2_xattn_all

    def _L2_attn_setup():
        import jax, jax.numpy as jnp
        import numpy as np
        DT_MIN, DT_MAX = (0.001, 0.1)
        DT_RANK, D_STATE, D_CONV = (64, 16, 4)
        key = jax.random.key(seed)
        ks = jax.random.split(key, 8)
        B, T, Dm = (4, 512, 128)
        Dn = 2 * Dm
        s = lambda k, shape, scale=0.02: jax.random.normal(k, shape, jnp.float32) * scale
        return {'x': jax.random.normal(ks[0], (B, T, Dm), jnp.float32), 'W_in': s(ks[1], (2 * Dn, Dm)), 'conv_w': s(ks[2], (Dn, 1, D_CONV), 0.1), 'conv_b': jnp.zeros((Dn,), jnp.float32), 'W_x': s(ks[3], (DT_RANK + 2 * D_STATE, Dn)), 'W_dt': s(ks[4], (Dn, DT_RANK)), 'b_dt': jnp.zeros((Dn,), jnp.float32), 'log_A': jax.random.uniform(ks[5], (Dn, D_STATE), jnp.float32), 'D_param': jnp.ones((Dn,), jnp.float32), 'W_out': s(ks[6], (Dm, Dn)), 'ln_w': jnp.ones((Dm,), jnp.float32), 'ln_b': jnp.zeros((Dm,), jnp.float32)}
    _L2_attn_all = _L2_attn_setup()
    _L2_attn_in = {k: v for k, v in _L2_attn_all.items() if k in ('W_in', 'conv_w', 'conv_b', 'W_x', 'W_dt', 'b_dt', 'log_A', 'D_param', 'W_out', 'ln_w', 'ln_b')}
    del _L2_attn_all

    def _L2_ffn_setup():
        import jax, jax.numpy as jnp
        import numpy as np
        E = 8
        D = 128
        DO = 128
        R = 64
        H = 32
        B, T = (8, 256)
        key = jax.random.key(seed)
        ks = jax.random.split(key, 12)
        s = lambda k, shape, fan: jax.random.normal(k, shape, jnp.float32) / np.sqrt(fan)
        return {'x': jax.random.normal(ks[0], (B, T, D), jnp.float32), 'W_base': s(ks[1], (D, DO), D), 'b_base': jnp.zeros((DO,), jnp.float32), 'Wd1': s(ks[2], (E, D, H), D), 'bd1': jnp.zeros((E, H), jnp.float32), 'Wd2': s(ks[3], (E, H, D), H), 'bd2': jnp.zeros((E, D), jnp.float32), 'Wa_down': s(ks[4], (E, D, R), D), 'ba_down': jnp.zeros((E, R), jnp.float32), 'Wa_up': s(ks[5], (E, R, DO), R), 'ba_up': jnp.zeros((E, DO), jnp.float32)}
    _L2_ffn_all = _L2_ffn_setup()
    _L2_ffn_in = {k: v for k, v in _L2_ffn_all.items() if k in ('W_base', 'b_base', 'Wd1', 'bd1', 'Wd2', 'bd2', 'Wa_down', 'ba_down', 'Wa_up', 'ba_up')}
    del _L2_ffn_all

    def _L3_xattn_setup():
        import jax, jax.numpy as jnp
        import numpy as np
        import math
        B, S, DIN, DQ, DV = (8, 256, 128, 128, 128)
        key = jax.random.key(seed)
        ks = jax.random.split(key, 9)
        c_q = math.sqrt(6.0 / (DIN + DQ))
        c_v = math.sqrt(6.0 / (DIN + DV))
        query = jax.random.normal(ks[0], (B, S, DIN), dtype=jnp.float32)
        key_t = jax.random.normal(ks[1], (B, S, DIN), dtype=jnp.float32)
        value = jax.random.normal(ks[2], (B, S, DIN), dtype=jnp.float32)
        Wq = jax.random.uniform(ks[3], (DIN, DQ), jnp.float32, -c_q, c_q)
        Wk = jax.random.uniform(ks[4], (DIN, DQ), jnp.float32, -c_q, c_q)
        Wv = jax.random.uniform(ks[5], (DIN, DV), jnp.float32, -c_v, c_v)
        bq = jax.random.uniform(ks[6], (DQ,), jnp.float32, -c_q, c_q)
        bk = jax.random.uniform(ks[7], (DQ,), jnp.float32, -c_q, c_q)
        bv = jax.random.uniform(ks[8], (DV,), jnp.float32, -c_v, c_v)
        mask = jnp.broadcast_to(jnp.triu(jnp.ones((S, S), dtype=bool), k=1), (B, S, S))
        return {'query': query, 'key': key_t, 'value': value, 'Wq': Wq, 'bq': bq, 'Wk': Wk, 'bk': bk, 'Wv': Wv, 'bv': bv, 'mask': mask}
    _L3_xattn_all = _L3_xattn_setup()
    _L3_xattn_in = {k: v for k, v in _L3_xattn_all.items() if k in ('Wq', 'bq', 'Wk', 'bk', 'Wv', 'bv')}
    del _L3_xattn_all

    def _L3_attn_setup():
        import jax, jax.numpy as jnp
        import numpy as np
        N_HEADS = 16
        ROPE_BASE = 10000.0

        def _rope(x):
            B, L, H, Dh = x.shape
            half = Dh // 2
            inv_freq = 1.0 / ROPE_BASE ** (jnp.arange(0, half, dtype=jnp.float32) / half)
            ang = jnp.arange(L, dtype=jnp.float32)[:, None] * inv_freq[None, :]
            cos = jnp.concatenate([jnp.cos(ang), jnp.cos(ang)], axis=-1).astype(x.dtype)
            sin = jnp.concatenate([jnp.sin(ang), jnp.sin(ang)], axis=-1).astype(x.dtype)
            cos = cos[None, :, None, :]
            sin = sin[None, :, None, :]
            x1, x2 = (x[..., :half], x[..., half:])
            rot = jnp.concatenate([-x2, x1], axis=-1)
            return x * cos + rot * sin
        key = jax.random.key(seed)
        k1, k2, k3 = jax.random.split(key, 3)
        B, L, D = (2, 256, 128)
        x = jax.random.normal(k1, (B, L, D), dtype=jnp.float32)
        w_qkv = jax.random.normal(k2, (3 * D, D), dtype=jnp.float32) * D ** (-0.5)
        w_out = jax.random.normal(k3, (D, D), dtype=jnp.float32) * D ** (-0.5)
        return {'x': x, 'w_qkv': w_qkv, 'w_out': w_out}
    _L3_attn_all = _L3_attn_setup()
    _L3_attn_in = {k: v for k, v in _L3_attn_all.items() if k in ('w_qkv', 'w_out')}
    del _L3_attn_all

    def _L3_ffn_setup():
        import jax, jax.numpy as jnp
        import numpy as np
        BLOCK = 16
        _GRID = jnp.array([0.0, 0.5, 1.0, 1.5, 2.0, 3.0, 4.0, 6.0], dtype=jnp.float32)
        _MID = jnp.array([0.25, 0.75, 1.25, 1.75, 2.5, 3.5, 5.0], dtype=jnp.float32)

        def fp4_quant_dequant(x):
            shape = x.shape
            xb = x.reshape(shape[:-1] + (shape[-1] // BLOCK, BLOCK))
            scale = jnp.max(jnp.abs(xb), axis=-1, keepdims=True) / 6.0
            scale = jnp.maximum(scale, jnp.float32(1e-12))
            xn = xb / scale
            idx = jnp.searchsorted(_MID, jnp.abs(xn))
            q = _GRID[idx] * jnp.sign(xn) * scale
            return q.reshape(shape)

        def fp4_linear(x, w):
            xq = fp4_quant_dequant(x)
            wq = fp4_quant_dequant(w)
            return jnp.einsum('bsk,nk->bsn', xq, wq)
        key = jax.random.key(seed)
        k1, k2, k3, k4 = jax.random.split(key, 4)
        H, I = (128, 352)
        x = jax.random.normal(k1, (4, 512, H), dtype=jnp.float32)
        w_gate = jax.random.normal(k2, (I, H), dtype=jnp.float32) * 0.02
        w_up = jax.random.normal(k3, (I, H), dtype=jnp.float32) * 0.02
        w_down = jax.random.normal(k4, (H, I), dtype=jnp.float32) * 0.02
        return {'x': x, 'w_gate': w_gate, 'w_up': w_up, 'w_down': w_down}
    _L3_ffn_all = _L3_ffn_setup()
    _L3_ffn_in = {k: v for k, v in _L3_ffn_all.items() if k in ('w_gate', 'w_up', 'w_down')}
    del _L3_ffn_all
    return {'x': x, 'ctx_1024': ctx_1024, 'mask_BxS2_ik0': mask_BxS2_ik0, 'mask_1x1xSxS2_bk1': mask_1x1xSxS2_bk1, 'mask_BxSxS2_bk1': mask_BxSxS2_bk1, 'L0_xattn_Wq': _L0_xattn_in['Wq'], 'L0_xattn_bq': _L0_xattn_in['bq'], 'L0_xattn_Wk': _L0_xattn_in['Wk'], 'L0_xattn_bk': _L0_xattn_in['bk'], 'L0_xattn_Wv': _L0_xattn_in['Wv'], 'L0_xattn_bv': _L0_xattn_in['bv'], 'L0_attn_W_to': _L0_attn_in['W_to'], 'L0_attn_log_decay': _L0_attn_in['log_decay'], 'L0_attn_frequencies': _L0_attn_in['frequencies'], 'L0_attn_W_from': _L0_attn_in['W_from'], 'L0_attn_ln1_g': _L0_attn_in['ln1_g'], 'L0_attn_ln1_b': _L0_attn_in['ln1_b'], 'L0_attn_ln3_g': _L0_attn_in['ln3_g'], 'L0_attn_ln3_b': _L0_attn_in['ln3_b'], 'L0_attn_W_ffn1': _L0_attn_in['W_ffn1'], 'L0_attn_b_ffn1': _L0_attn_in['b_ffn1'], 'L0_attn_W_ffn2': _L0_attn_in['W_ffn2'], 'L0_attn_b_ffn2': _L0_attn_in['b_ffn2'], 'L0_ffn_Wg': _L0_ffn_in['Wg'], 'L0_ffn_w1': _L0_ffn_in['w1'], 'L0_ffn_w2': _L0_ffn_in['w2'], 'L1_xattn_Wq': _L1_xattn_in['Wq'], 'L1_attn_W_attn': _L1_attn_in['W_attn'], 'L1_attn_b_attn': _L1_attn_in['b_attn'], 'L1_attn_W_k2': _L1_attn_in['W_k2'], 'L1_attn_b_k2': _L1_attn_in['b_k2'], 'L1_attn_W_proj': _L1_attn_in['W_proj'], 'L1_attn_b_proj': _L1_attn_in['b_proj'], 'L1_ffn_uzman_embeddings': _L1_ffn_in['uzman_embeddings'], 'L1_ffn_W1': _L1_ffn_in['W1'], 'L1_ffn_b1': _L1_ffn_in['b1'], 'L1_ffn_W2': _L1_ffn_in['W2'], 'L1_ffn_b2': _L1_ffn_in['b2'], 'L1_ffn_onbellek_durumu': _L1_ffn_in['onbellek_durumu'], 'L2_xattn_W_q': _L2_xattn_in['W_q'], 'L2_xattn_W_k': _L2_xattn_in['W_k'], 'L2_xattn_W_v': _L2_xattn_in['W_v'], 'L2_xattn_W_o': _L2_xattn_in['W_o'], 'L2_attn_W_in': _L2_attn_in['W_in'], 'L2_attn_conv_w': _L2_attn_in['conv_w'], 'L2_attn_conv_b': _L2_attn_in['conv_b'], 'L2_attn_W_x': _L2_attn_in['W_x'], 'L2_attn_W_dt': _L2_attn_in['W_dt'], 'L2_attn_b_dt': _L2_attn_in['b_dt'], 'L2_attn_log_A': _L2_attn_in['log_A'], 'L2_attn_D_param': _L2_attn_in['D_param'], 'L2_attn_W_out': _L2_attn_in['W_out'], 'L2_attn_ln_w': _L2_attn_in['ln_w'], 'L2_attn_ln_b': _L2_attn_in['ln_b'], 'L2_ffn_W_base': _L2_ffn_in['W_base'], 'L2_ffn_b_base': _L2_ffn_in['b_base'], 'L2_ffn_Wd1': _L2_ffn_in['Wd1'], 'L2_ffn_bd1': _L2_ffn_in['bd1'], 'L2_ffn_Wd2': _L2_ffn_in['Wd2'], 'L2_ffn_bd2': _L2_ffn_in['bd2'], 'L2_ffn_Wa_down': _L2_ffn_in['Wa_down'], 'L2_ffn_ba_down': _L2_ffn_in['ba_down'], 'L2_ffn_Wa_up': _L2_ffn_in['Wa_up'], 'L2_ffn_ba_up': _L2_ffn_in['ba_up'], 'L3_xattn_Wq': _L3_xattn_in['Wq'], 'L3_xattn_bq': _L3_xattn_in['bq'], 'L3_xattn_Wk': _L3_xattn_in['Wk'], 'L3_xattn_bk': _L3_xattn_in['bk'], 'L3_xattn_Wv': _L3_xattn_in['Wv'], 'L3_xattn_bv': _L3_xattn_in['bv'], 'L3_attn_w_qkv': _L3_attn_in['w_qkv'], 'L3_attn_w_out': _L3_attn_in['w_out'], 'L3_ffn_w_gate': _L3_ffn_in['w_gate'], 'L3_ffn_w_up': _L3_ffn_in['w_up'], 'L3_ffn_w_down': _L3_ffn_in['w_down']}

def reference(x, ctx_1024, mask_BxS2_ik0, mask_1x1xSxS2_bk1, mask_BxSxS2_bk1, L0_xattn_Wq, L0_xattn_bq, L0_xattn_Wk, L0_xattn_bk, L0_xattn_Wv, L0_xattn_bv, L0_attn_W_to, L0_attn_log_decay, L0_attn_frequencies, L0_attn_W_from, L0_attn_ln1_g, L0_attn_ln1_b, L0_attn_ln3_g, L0_attn_ln3_b, L0_attn_W_ffn1, L0_attn_b_ffn1, L0_attn_W_ffn2, L0_attn_b_ffn2, L0_ffn_Wg, L0_ffn_w1, L0_ffn_w2, L1_xattn_Wq, L1_attn_W_attn, L1_attn_b_attn, L1_attn_W_k2, L1_attn_b_k2, L1_attn_W_proj, L1_attn_b_proj, L1_ffn_uzman_embeddings, L1_ffn_W1, L1_ffn_b1, L1_ffn_W2, L1_ffn_b2, L1_ffn_onbellek_durumu, L2_xattn_W_q, L2_xattn_W_k, L2_xattn_W_v, L2_xattn_W_o, L2_attn_W_in, L2_attn_conv_w, L2_attn_conv_b, L2_attn_W_x, L2_attn_W_dt, L2_attn_b_dt, L2_attn_log_A, L2_attn_D_param, L2_attn_W_out, L2_attn_ln_w, L2_attn_ln_b, L2_ffn_W_base, L2_ffn_b_base, L2_ffn_Wd1, L2_ffn_bd1, L2_ffn_Wd2, L2_ffn_bd2, L2_ffn_Wa_down, L2_ffn_ba_down, L2_ffn_Wa_up, L2_ffn_ba_up, L3_xattn_Wq, L3_xattn_bq, L3_xattn_Wk, L3_xattn_bk, L3_xattn_Wv, L3_xattn_bv, L3_attn_w_qkv, L3_attn_w_out, L3_ffn_w_gate, L3_ffn_w_up, L3_ffn_w_down):
    import jax
    import jax.numpy as jnp

    def _L0_xattn_ref(hm_tokens, text_tokens, text_mask, Wq, bq, Wk, bk, Wv, bv):
        import jax, jax.numpy as jnp
        import numpy as np
        D = 128
        NEG = -1000000000.0
        d = hm_tokens.shape[-1]
        Q = hm_tokens @ Wq + bq
        K = text_tokens @ Wk + bk
        V = text_tokens @ Wv + bv
        scores = jnp.einsum('bqd,bkd->bqk', Q, K) / jnp.sqrt(jnp.float32(d))
        scores = jnp.where(text_mask[:, None, :] == 0, jnp.float32(NEG), scores)
        attn = jax.nn.softmax(scores, axis=-1)
        return jnp.einsum('bqk,bkd->bqd', attn, V)

    def _L0_attn_ref(x, W_to, log_decay, frequencies, W_from, ln1_g, ln1_b, ln3_g, ln3_b, W_ffn1, b_ffn1, W_ffn2, b_ffn2):
        import jax, jax.numpy as jnp
        import numpy as np
        B, S, D, F = (4, 512, 128, 32)

        def _ln(x, g, b, eps=1e-05):
            m = x.mean(-1, keepdims=True)
            v = ((x - m) ** 2).mean(-1, keepdims=True)
            return (x - m) / jnp.sqrt(v + eps) * g + b
        Bc, Sc, Dc = x.shape
        Fc = log_decay.shape[0]
        dt = 1.0
        residual = x
        h = _ln(x, ln1_g, ln1_b)
        spec = jnp.einsum('bsd,fd->bsf', h, W_to)
        real, imag = (spec[..., :Fc], spec[..., Fc:])
        decay = jax.nn.sigmoid(log_decay)
        omega = jnp.tanh(frequencies) * 0.1
        c, s = (jnp.cos(omega * dt), jnp.sin(omega * dt))

        def step(carry, u):
            sr, si = carry
            r, i = u
            sr = sr * decay + r * 0.1
            si = si * decay + i * 0.1
            nr = jnp.clip(sr * c - si * s, -10.0, 10.0)
            ni = jnp.clip(sr * s + si * c, -10.0, 10.0)
            return ((nr, ni), (nr, ni))
        init = (jnp.zeros((Bc, Fc), x.dtype), jnp.zeros((Bc, Fc), x.dtype))
        _, (out_r, out_i) = jax.lax.scan(step, init, (real.transpose(1, 0, 2), imag.transpose(1, 0, 2)))
        spectral_out = jnp.concatenate([out_r.transpose(1, 0, 2), out_i.transpose(1, 0, 2)], axis=-1)
        h = jnp.einsum('bsf,df->bsd', spectral_out, W_from)
        x2 = residual + h * 0.1
        r3 = x2
        h = _ln(x2, ln3_g, ln3_b)
        h = jnp.einsum('bsd,ed->bse', h, W_ffn1) + b_ffn1
        h = jax.nn.gelu(h, approximate=False)
        h = jnp.einsum('bse,de->bsd', h, W_ffn2) + b_ffn2
        return r3 + h * 0.1

    def _L0_ffn_ref(x, Wg, w1, w2):
        import jax, jax.numpy as jnp
        import numpy as np
        d = x.shape[-1]
        xr = x.reshape(-1, d)
        S = xr.shape[0]
        E = Wg.shape[1]
        C = (S + E - 1) // E
        gate = jax.nn.softmax(xr @ Wg, axis=-1)
        idx = jnp.argmax(gate, axis=1)
        gates_s = jnp.take_along_axis(gate, idx[:, None], axis=1)[:, 0]
        onehot = jax.nn.one_hot(idx, E, dtype=jnp.int32)
        loc = jnp.sum((jnp.cumsum(onehot, axis=0) - 1) * onehot, axis=1)
        valid = loc < C
        loc_pad = jnp.minimum(loc, C)
        dispatched = jnp.zeros((E, C + 1, d), dtype=x.dtype).at[idx, loc_pad].set(xr)
        dispatched = dispatched[:, :C]
        h = jax.nn.relu(jnp.einsum('ecm,emf->ecf', dispatched, w1))
        expert_out = jnp.einsum('ecf,efm->ecm', h, w2)
        gathered = expert_out[idx, jnp.minimum(loc, C - 1)]
        combined = gathered * (gates_s * valid.astype(x.dtype))[:, None]
        return combined.reshape(x.shape)

    def _L1_xattn_ref(enc_outputs, x, Wq):
        import jax, jax.numpy as jnp
        import numpy as np
        B, L, D = (8, 256, 128)
        d_k = x.shape[-1]
        q = jnp.einsum('bld,hd->blh', x, Wq)
        k = jnp.einsum('bld,hd->blh', enc_outputs, Wq)
        v = k
        scores = jnp.einsum('bqh,bkh->bqk', q, k) / jnp.sqrt(jnp.float32(d_k))
        Lq, Lk = (scores.shape[1], scores.shape[2])
        causal = jnp.tril(jnp.ones((Lq, Lk), dtype=bool))
        scores = jnp.where(causal, scores, -jnp.inf)
        attn = jax.nn.softmax(scores, axis=-1)
        return jnp.einsum('bqk,bkh->bqh', attn, v)

    def _L1_attn_ref(x, W_attn, b_attn, W_k2, b_k2, W_proj, b_proj):
        import jax, jax.numpy as jnp
        import numpy as np
        import math
        N_HEAD = 16

        def _causal_attn(q, k, v):
            d_k = q.shape[-1]
            s = jnp.einsum('bhqd,bhkd->bhqk', q, k) / math.sqrt(d_k)
            L, S = (q.shape[-2], k.shape[-2])
            mask = jnp.tril(jnp.ones((L, S), dtype=bool))
            s = jnp.where(mask, s, -jnp.inf)
            a = jax.nn.softmax(s, axis=-1)
            return jnp.einsum('bhqk,bhkd->bhqd', a, v)
        B, T, C = x.shape
        H = N_HEAD
        d = C // H
        qk = x @ W_attn + b_attn
        q, k = (qk[..., :C], qk[..., C:])
        q = q.reshape(B, T, H, d).transpose(0, 2, 1, 3)
        k = k.reshape(B, T, H, d).transpose(0, 2, 1, 3)
        v = x.reshape(B, T, H, d).transpose(0, 2, 1, 3)
        y = _causal_attn(q, k, v)
        e = v[:, :, 1:, :] - y[:, :, :-1, :]
        k2 = (x[:, :-1] @ W_k2 + b_k2).reshape(B, T - 1, H, d).transpose(0, 2, 1, 3)
        q2 = q[:, :, 1:, :]
        y2 = _causal_attn(q2, k2, e)
        y2 = jnp.concatenate([jnp.zeros_like(y2[:, :, :1, :]), y2], axis=2)

        def proj(t):
            return t.transpose(0, 2, 1, 3).reshape(B, T, C) @ W_proj + b_proj
        return proj(y) + proj(y2)

    def _L1_ffn_ref(x, uzman_embeddings, W1, b1, W2, b2, onbellek_durumu):
        import jax, jax.numpy as jnp
        import numpy as np
        from jax import lax
        LOKAL_GRUP = 7
        TOP_K = 2
        EPS = 1e-08
        CACHE_BONUS = 0.1

        def _route(tokens, uzman_embeddings, onbellek_durumu):
            sim = tokens @ uzman_embeddings.T
            _, local_idx = lax.top_k(sim, LOKAL_GRUP)
            t_norm = tokens / (jnp.linalg.norm(tokens, axis=-1, keepdims=True) + EPS)
            e_norm = uzman_embeddings / (jnp.linalg.norm(uzman_embeddings, axis=-1, keepdims=True) + EPS)
            local_embs = e_norm[local_idx]
            scores = jnp.einsum('nld,nd->nl', local_embs, t_norm)
            scores = scores + CACHE_BONUS * onbellek_durumu[local_idx]
            top_scores, top_local = lax.top_k(scores, TOP_K)
            global_idx = jnp.take_along_axis(local_idx, top_local, axis=1)
            weights = jax.nn.softmax(top_scores, axis=-1)
            return (global_idx, lax.stop_gradient(weights))
        B, S, D = x.shape
        tokens = x.reshape(-1, D)
        global_idx, weights = _route(tokens, uzman_embeddings, onbellek_durumu)
        h = jnp.einsum('nd,edh->enh', tokens, W1) + b1[:, None, :]
        h = jax.nn.gelu(h, approximate=False)
        out_all = jnp.einsum('enh,ehd->end', h, W2) + b2[:, None, :]
        N = tokens.shape[0]
        out_sel = out_all[global_idx, jnp.arange(N)[:, None]]
        out = jnp.sum(weights[..., None] * out_sel, axis=1)
        return out.reshape(B, S, D)

    def _L2_xattn_ref(query, key, value, mask, W_q, W_k, W_v, W_o):
        import jax, jax.numpy as jnp
        import numpy as np
        D_MODEL = 128
        NUM_HEADS = 16
        D_K = D_MODEL // NUM_HEADS

        def _split(x):
            B, S, _ = x.shape
            return x.reshape(B, S, NUM_HEADS, D_K).transpose(0, 2, 1, 3)
        Q = _split(query @ W_q.T)
        K = _split(key @ W_k.T)
        V = _split(value @ W_v.T)
        scores = jnp.einsum('bhqd,bhkd->bhqk', Q, K) / jnp.sqrt(jnp.float32(D_K))
        scores = jnp.where(mask, -jnp.inf, scores)
        attn_w = jax.nn.softmax(scores, axis=-1)
        attn_w = jnp.nan_to_num(attn_w, nan=0.0)
        out = jnp.einsum('bhqk,bhkd->bhqd', attn_w, V)
        B, _, Sq, _ = out.shape
        merged = out.transpose(0, 2, 1, 3).reshape(B, Sq, D_MODEL)
        return merged @ W_o.T

    def _L2_attn_ref(x, W_in, conv_w, conv_b, W_x, W_dt, b_dt, log_A, D_param, W_out, ln_w, ln_b):
        import jax, jax.numpy as jnp
        import numpy as np
        DT_MIN, DT_MAX = (0.001, 0.1)
        DT_RANK, D_STATE, D_CONV = (64, 16, 4)
        B, T, Dm = x.shape
        Dn = W_dt.shape[0]
        residual = x
        mu = x.mean(-1, keepdims=True)
        var = x.var(-1, keepdims=True)
        xn = (x - mu) / jnp.sqrt(var + 1e-05) * ln_w + ln_b
        xz = xn @ W_in.T
        x_inner, z = jnp.split(xz, 2, axis=-1)
        xc = jnp.transpose(x_inner, (0, 2, 1))
        xc = jax.lax.conv_general_dilated(xc, conv_w, window_strides=(1,), padding=[(D_CONV - 1, 0)], dimension_numbers=('NCH', 'OIH', 'NCH'), feature_group_count=Dn)
        xc = xc + conv_b[None, :, None]
        u = jax.nn.silu(jnp.transpose(xc, (0, 2, 1)))
        xbc = u @ W_x.T
        dt_low, B_ssm, C_ssm = jnp.split(xbc, [DT_RANK, DT_RANK + D_STATE], axis=-1)
        dt = jax.nn.softplus(dt_low @ W_dt.T + b_dt) + DT_MIN
        dt = jnp.clip(dt, DT_MIN, DT_MAX)
        A = -jnp.exp(log_A)

        def step(h, inp):
            dt_t, u_t, B_t, C_t = inp
            dA = jnp.exp(dt_t[:, :, None] * A)
            h = dA * h + (dt_t * u_t)[:, :, None] * B_t[:, None, :]
            y = jnp.einsum('bdn,bn->bd', h, C_t)
            return (h, y)
        h0 = jnp.zeros((B, Dn, D_STATE), x.dtype)
        _, ys = jax.lax.scan(step, h0, (jnp.moveaxis(dt, 1, 0), jnp.moveaxis(u, 1, 0), jnp.moveaxis(B_ssm, 1, 0), jnp.moveaxis(C_ssm, 1, 0)))
        y = jnp.moveaxis(ys, 0, 1)
        y = y + u * D_param
        y = y * jax.nn.silu(z)
        return y @ W_out.T + residual

    def _L2_ffn_ref(x, W_base, b_base, Wd1, bd1, Wd2, bd2, Wa_down, ba_down, Wa_up, ba_up):
        import jax, jax.numpy as jnp
        import numpy as np
        E = 8
        D = 128
        DO = 128
        R = 64
        H = 32
        B, T = (8, 256)
        base = jnp.einsum('btd,do->bto', x, W_base) + b_base
        h = jax.nn.relu(jnp.einsum('btd,edh->ebth', x, Wd1) + bd1[:, None, None, :])
        recon = jnp.einsum('ebth,ehd->ebtd', h, Wd2) + bd2[:, None, None, :]
        losses = jnp.mean((recon - x[None]) ** 2, axis=(2, 3))
        idx = jnp.argmin(losses, axis=0)
        a = jax.nn.relu(jnp.einsum('btd,bdr->btr', x, Wa_down[idx]) + ba_down[idx][:, None, :])
        adapter_out = jnp.einsum('btr,bro->bto', a, Wa_up[idx]) + ba_up[idx][:, None, :]
        return base + adapter_out

    def _L3_xattn_ref(query, key, value, Wq, bq, Wk, bk, Wv, bv, mask):
        import jax, jax.numpy as jnp
        import numpy as np
        import math
        B, S, DIN, DQ, DV = (8, 256, 128, 128, 128)
        q = query @ Wq + bq
        k = key @ Wk + bk
        v = value @ Wv + bv
        scores = jnp.einsum('bsd,btd->bst', q, k) / math.sqrt(DQ)
        scores = jnp.where(mask, jnp.float32(-1000000000.0), scores)
        weights = jax.nn.softmax(scores, axis=2)
        y = jnp.einsum('bst,btd->bsd', weights, v)
        return y

    def _L3_attn_ref(x, w_qkv, w_out):
        import jax, jax.numpy as jnp
        import numpy as np
        N_HEADS = 16
        ROPE_BASE = 10000.0

        def _rope(x):
            B, L, H, Dh = x.shape
            half = Dh // 2
            inv_freq = 1.0 / ROPE_BASE ** (jnp.arange(0, half, dtype=jnp.float32) / half)
            ang = jnp.arange(L, dtype=jnp.float32)[:, None] * inv_freq[None, :]
            cos = jnp.concatenate([jnp.cos(ang), jnp.cos(ang)], axis=-1).astype(x.dtype)
            sin = jnp.concatenate([jnp.sin(ang), jnp.sin(ang)], axis=-1).astype(x.dtype)
            cos = cos[None, :, None, :]
            sin = sin[None, :, None, :]
            x1, x2 = (x[..., :half], x[..., half:])
            rot = jnp.concatenate([-x2, x1], axis=-1)
            return x * cos + rot * sin
        B, L, D = x.shape
        H = N_HEADS
        Dh = D // H
        qkv = jnp.einsum('bld,ed->ble', x, w_qkv)
        q, k, v = jnp.split(qkv, 3, axis=-1)
        q = q.reshape(B, L, H, Dh)
        k = k.reshape(B, L, H, Dh)
        v = v.reshape(B, L, H, Dh)
        q = _rope(q)
        k = _rope(k)
        scale = 1.0 / jnp.sqrt(jnp.asarray(Dh, dtype=x.dtype))
        scores = jnp.einsum('blhd,bmhd->bhlm', q, k) * scale
        attn = jax.nn.softmax(scores, axis=-1)
        out = jnp.einsum('bhlm,bmhd->blhd', attn, v).reshape(B, L, D)
        return jnp.einsum('bld,ed->ble', out, w_out)

    def _L3_ffn_ref(x, w_gate, w_up, w_down):
        import jax, jax.numpy as jnp
        import numpy as np
        BLOCK = 16
        _GRID = jnp.array([0.0, 0.5, 1.0, 1.5, 2.0, 3.0, 4.0, 6.0], dtype=jnp.float32)
        _MID = jnp.array([0.25, 0.75, 1.25, 1.75, 2.5, 3.5, 5.0], dtype=jnp.float32)

        def fp4_quant_dequant(x):
            shape = x.shape
            xb = x.reshape(shape[:-1] + (shape[-1] // BLOCK, BLOCK))
            scale = jnp.max(jnp.abs(xb), axis=-1, keepdims=True) / 6.0
            scale = jnp.maximum(scale, jnp.float32(1e-12))
            xn = xb / scale
            idx = jnp.searchsorted(_MID, jnp.abs(xn))
            q = _GRID[idx] * jnp.sign(xn) * scale
            return q.reshape(shape)

        def fp4_linear(x, w):
            xq = fp4_quant_dequant(x)
            wq = fp4_quant_dequant(w)
            return jnp.einsum('bsk,nk->bsn', xq, wq)
        gate = fp4_linear(x, w_gate)
        y = fp4_linear(x, w_up)
        h = jax.nn.silu(gate) * y
        return fp4_linear(h, w_down)
    x = x + _L0_xattn_ref(_layernorm(x, axis=-1), ctx_1024, mask_BxS2_ik0, L0_xattn_Wq, L0_xattn_bq, L0_xattn_Wk, L0_xattn_bk, L0_xattn_Wv, L0_xattn_bv)
    x = x + _L0_attn_ref(_layernorm(x, axis=-1), L0_attn_W_to, L0_attn_log_decay, L0_attn_frequencies, L0_attn_W_from, L0_attn_ln1_g, L0_attn_ln1_b, L0_attn_ln3_g, L0_attn_ln3_b, L0_attn_W_ffn1, L0_attn_b_ffn1, L0_attn_W_ffn2, L0_attn_b_ffn2)
    x = x + _L0_ffn_ref(_layernorm(x, axis=-1), L0_ffn_Wg, L0_ffn_w1, L0_ffn_w2)
    x = x + _L1_xattn_ref(ctx_1024, _layernorm(x, axis=-1), L1_xattn_Wq)
    x = x + _L1_attn_ref(_layernorm(x, axis=-1), L1_attn_W_attn, L1_attn_b_attn, L1_attn_W_k2, L1_attn_b_k2, L1_attn_W_proj, L1_attn_b_proj)
    x = x + _L1_ffn_ref(_layernorm(x, axis=-1), L1_ffn_uzman_embeddings, L1_ffn_W1, L1_ffn_b1, L1_ffn_W2, L1_ffn_b2, L1_ffn_onbellek_durumu)
    x = x + _L2_xattn_ref(_layernorm(x, axis=-1), ctx_1024, ctx_1024, mask_1x1xSxS2_bk1, L2_xattn_W_q, L2_xattn_W_k, L2_xattn_W_v, L2_xattn_W_o)
    x = x + _L2_attn_ref(_layernorm(x, axis=-1), L2_attn_W_in, L2_attn_conv_w, L2_attn_conv_b, L2_attn_W_x, L2_attn_W_dt, L2_attn_b_dt, L2_attn_log_A, L2_attn_D_param, L2_attn_W_out, L2_attn_ln_w, L2_attn_ln_b)
    x = x + _L2_ffn_ref(_layernorm(x, axis=-1), L2_ffn_W_base, L2_ffn_b_base, L2_ffn_Wd1, L2_ffn_bd1, L2_ffn_Wd2, L2_ffn_bd2, L2_ffn_Wa_down, L2_ffn_ba_down, L2_ffn_Wa_up, L2_ffn_ba_up)
    x = x + _L3_xattn_ref(_layernorm(x, axis=-1), ctx_1024, ctx_1024, L3_xattn_Wq, L3_xattn_bq, L3_xattn_Wk, L3_xattn_bk, L3_xattn_Wv, L3_xattn_bv, mask_BxSxS2_bk1)
    x = x + _L3_attn_ref(_layernorm(x, axis=-1), L3_attn_w_qkv, L3_attn_w_out)
    x = x + _L3_ffn_ref(_layernorm(x, axis=-1), L3_ffn_w_gate, L3_ffn_w_up, L3_ffn_w_down)
    return x

_drawn_inputs = setup_inputs


def setup_inputs(seed=0):
    import zlib

    import numpy as np

    out = dict(_drawn_inputs(seed))
    spreads = {'L0_xattn_bq': (0.0, 0.413),
     'L0_xattn_bk': (0.0, 2.0),
     'L0_xattn_bv': (0.0, 0.1),
     'L0_attn_log_decay': (0.0, 0.8),
     'L0_attn_ln1_g': (1.0, 0.6),
     'L0_attn_ln1_b': (0.0, 0.8),
     'L0_attn_ln3_g': (1.0, 0.6),
     'L0_attn_ln3_b': (0.0, 0.8),
     'L0_attn_b_ffn1': (0.0, 0.8),
     'L0_attn_b_ffn2': (0.0, 0.8),
     'L1_attn_b_attn': (0.0, 0.8),
     'L1_attn_b_k2': (0.0, 2.0),
     'L1_attn_b_proj': (0.0, 0.1),
     'L1_ffn_onbellek_durumu': (1.0, 0.6),
     'L2_attn_conv_b': (0.0, 0.8),
     'L2_attn_b_dt': (0.0, 0.767),
     'L2_attn_D_param': (1.0, 0.6),
     'L2_attn_ln_w': (1.0, 0.6),
     'L2_attn_ln_b': (0.0, 0.8),
     'L2_ffn_b_base': (0.0, 2.0),
     'L2_ffn_bd1': (0.0, 0.8),
     'L2_ffn_bd2': (0.0, 0.8),
     'L2_ffn_ba_down': (0.0, 2.0),
     'L2_ffn_ba_up': (0.0, 2.0)}
    factors = {'L0_attn_W_to': 8.0,
     'L0_attn_frequencies': 58.674,
     'L0_attn_W_from': 8.0,
     'L0_attn_W_ffn1': 8.0,
     'L0_attn_W_ffn2': 8.0,
     'L0_ffn_Wg': 8.0,
     'L0_ffn_w1': 8.0,
     'L0_ffn_w2': 8.0,
     'L1_attn_W_attn': 8.0,
     'L1_attn_W_k2': 8.0,
     'L1_ffn_uzman_embeddings': 4.087,
     'L1_ffn_W1': 3.797,
     'L1_ffn_b1': 8.0,
     'L1_ffn_W2': 3.728,
     'L1_ffn_b2': 8.0,
     'L2_attn_W_in': 8.0,
     'L2_attn_conv_w': 8.0,
     'L2_attn_W_x': 8.0,
     'L2_attn_log_A': 8.0,
     'L2_attn_W_out': 8.0,
     'L3_xattn_bq': 64.0,
     'L3_xattn_bk': 64.0,
     'L3_ffn_w_gate': 64.0,
     'L3_ffn_w_up': 64.0,
     'L3_ffn_w_down': 64.0,
     'L2_ffn_W_base': 8.0,
     'L2_ffn_Wd1': 8.0,
     'L2_ffn_Wd2': 8.0,
     'L2_ffn_Wa_down': 8.0,
     'L2_ffn_Wa_up': 8.0,
     'L3_xattn_Wq': 8.0,
     'L3_xattn_Wk': 8.0,
     'L3_xattn_Wv': 8.0,
     'L3_xattn_bv': 8.0,
     'L3_attn_w_qkv': 8.0,
     'L3_attn_w_out': 8.0}
    for name, (base, spread) in spreads.items():
        noise = np.random.default_rng([zlib.crc32(name.encode()), seed]).standard_normal(out[name].shape)
        drawn = base * np.exp(spread * noise) if base else spread * noise
        out[name] = jnp.asarray(drawn.astype(out[name].dtype))
    for name, factor in factors.items():
        out[name] = (out[name] * factor).astype(out[name].dtype)
    return out
```

```python
from contextlib import ExitStack

import numpy as np

import concourse.bass as bass
from concourse import mybir

STAGES = tuple(range(12))

F32 = mybir.dt.float32
I32 = mybir.dt.int32
U32 = mybir.dt.uint32
U8 = mybir.dt.uint8
ALU = mybir.AluOpType
ACT = mybir.ActivationFunctionType
AX = mybir.AxisListType

P = 128
B, S, D = 32, 64, 128
TOK = B * S
NT = TOK // P
KEYS = 1601
KC = -(-KEYS // P)
KREST = KEYS - (KC - 1) * P
SPANS = [(k, min(512, KEYS - k)) for k in range(0, KEYS, 512)]
H, DH = 16, 8
EPS = 1e-5
OUT = -2.0 ** 100


class Steps:

    def __init__(self, sem, *parts):
        self.sem, self.where, self.order, self.next = sem, {}, [], 0
        base = 0
        for times, names, *copies in parts:
            for i, n in enumerate(names):
                assert n not in self.where, n
                self.where[n] = (base + i + 1, len(names))
            self.order += names * (copies[0] if copies else 1)
            base += times * len(names)

    def at(self, name, t=0):
        first, per = self.where[name]
        return self.sem, t * per + first

    def before(self, name, t, rounds=1):
        first, per = self.where[name]
        assert first - rounds * per >= 1, name
        return self.sem, t * per + (first - rounds * per)

    def did(self, name):
        assert self.order[self.next] == name, (self.order[self.next], name)
        self.next += 1
        return self.sem


class Core:

    def __init__(self, nc, ctx, a):
        self.nc, self.a = nc, a
        self.sb = lambda name, shape, dt=F32: ctx.enter_context(nc.sbuf_tensor(name, shape, dt))
        self.x = self.sb("x", [P, NT, D])
        self.xn = self.sb("xn", [P, NT, D])
        self.xnT = self.sb("xnT", [P, TOK])
        self.ident = self.sb("ident", [P, P])
        self.eps = self.sb("eps", [P, 1])
        self.pause = self.sb("pause", [P, 1])
        self.sum = self.sb("ln_sum", [P, NT])
        self.mean = self.sb("ln_mean", [P, NT])
        self.sq = self.sb("ln_sq", [P, NT, D])
        self.var = self.sb("ln_var", [P, NT])
        self.std = self.sb("ln_std", [P, NT])
        self.rstd = self.sb("ln_rstd", [P, NT])


class Stage:

    def __init__(self, core, name):
        self.core, self.nc, self.name, self.ctx = core, core.nc, name, ExitStack()

    def __enter__(self):
        return self

    def __exit__(self, *exc):
        return self.ctx.__exit__(*exc)

    def sb(self, name, shape, dt=F32):
        return self.ctx.enter_context(self.nc.sbuf_tensor(f"{self.name}_{name}", shape, dt))

    def ps(self, name, shape):
        return self.ctx.enter_context(self.nc.psum_tensor(f"{self.name}_ps_{name}", shape, F32))

    def sem(self, name):
        return self.ctx.enter_context(self.nc.semaphore(f"{self.name}_{name}"))

    def block(self):
        return self.ctx.enter_context(self.nc.Block())


class Norm:

    def __init__(self, c, tag="ln", x=None, xn=None, xnT=None, gain=None, bias=None, turned=True):
        self.x, self.xn = (c.x, c.xn) if x is None else (x, xn)
        self.xnT = c.xnT if xnT is None else xnT
        self.tag, self.gain, self.bias, self.turned = tag, gain, bias, turned
        turns = [0, 1, 2, 3] if turned else []
        name = lambda n: f"{tag}_{n}"
        self.V = [name(n) for n in ["sum", "mean", "centred", "var", "rstd", "xn"] + [f"T{i}" for i in turns[::2]]]
        self.A = [name(n) for n in ["sq", "std"] + [f"T{i}" for i in turns[1::2]]]
        self.P = [name(f"PT{i}") for i in turns]


LN_V = ["ln_sum", "ln_mean", "ln_centred", "ln_var", "ln_rstd", "ln_xn", "ln_T0", "ln_T2"]
LN_A = ["ln_sq", "ln_std", "ln_T1", "ln_T3"]
LN_P = ["ln_PT0", "ln_PT1", "ln_PT2", "ln_PT3"]


def ln_vector(c, dve, V, A, PE, tp, n=None):
    nc, n = c.nc, n or Norm(c)
    g = n.tag

    def wide(m):
        return m[:, :].unsqueeze(2).broadcast_to([P, NT, D])

    nc.vector.tensor_reduce(c.sum[:, :], n.x[:, :, :], AX.X, ALU.add).then_inc(V.did(f"{g}_sum"), 1)
    dve.wait_ge(*V.at(f"{g}_sum"))
    nc.vector.tensor_scalar(c.mean[:, :], c.sum[:, :], 1.0 / D, None, ALU.mult).then_inc(V.did(f"{g}_mean"), 1)
    dve.wait_ge(*V.at(f"{g}_mean"))
    nc.vector.tensor_tensor(n.xn[:, :, :], n.x[:, :, :], wide(c.mean), ALU.subtract).then_inc(V.did(f"{g}_centred"), 1)
    dve.wait_ge(*A.at(f"{g}_sq"))
    nc.vector.tensor_reduce(c.var[:, :], c.sq[:, :, :], AX.X, ALU.add).then_inc(V.did(f"{g}_var"), 1)
    dve.wait_ge(*A.at(f"{g}_std"))
    nc.vector.reciprocal(c.rstd[:, :], c.std[:, :]).then_inc(V.did(f"{g}_rstd"), 1)
    dve.wait_ge(*V.at(f"{g}_rstd"))
    nc.vector.tensor_tensor(n.xn[:, :, :], n.xn[:, :, :], wide(c.rstd), ALU.mult).then_inc(V.did(f"{g}_xn"), 1)
    for i in (0, 2) if n.turned else ():
        dve.wait_ge(*PE.at(f"{g}_PT{i}"))
        dst = n.xnT[:, 512 * i:512 * i + 512]
        if n.gain is None:
            nc.vector.tensor_copy(dst, tp[0]).then_inc(V.did(f"{g}_T{i}"), 1)
        else:
            nc.vector.tensor_scalar(dst, tp[0], n.gain, n.bias, ALU.mult, ALU.add).then_inc(V.did(f"{g}_T{i}"), 1)


def ln_scalar(c, act, V, A, PE, tp, n=None):
    nc, n = c.nc, n or Norm(c)
    g = n.tag
    act.wait_ge(*V.at(f"{g}_centred"))
    nc.scalar.activation(c.sq[:, :, :], n.xn[:, :, :], ACT.Square).then_inc(A.did(f"{g}_sq"), 1)
    act.wait_ge(*V.at(f"{g}_var"))
    nc.scalar.activation(c.std[:, :], c.var[:, :], ACT.Sqrt, bias=c.eps[:, 0:1], scale=1.0 / D)\
        .then_inc(A.did(f"{g}_std"), 1)
    for i in (1, 3) if n.turned else ():
        act.wait_ge(*PE.at(f"{g}_PT{i}"))
        dst = n.xnT[:, 512 * i:512 * i + 512]
        if n.gain is None:
            nc.scalar.copy(dst, tp[1]).then_inc(A.did(f"{g}_T{i}"), 1)
        else:
            nc.scalar.activation(dst, tp[1], ACT.Identity, bias=n.bias, scale=n.gain).then_inc(A.did(f"{g}_T{i}"), 1)


def ln_tensor(c, pe, V, A, PE, tp, n=None):
    nc, n = c.nc, n or Norm(c)
    g = n.tag
    pe.wait_ge(*V.at(f"{g}_xn"))
    for i in range(4):
        if i == 2:
            pe.wait_ge(*V.at(f"{g}_T0"))
        if i == 3:
            pe.wait_ge(*A.at(f"{g}_T1"))
        for j in range(4):
            last = nc.tensor.transpose(tp[i % 2][:, P * j:P * j + P], n.xn[:, 4 * i + j, :], c.ident[:, :])
        last.then_inc(PE.did(f"{g}_PT{i}"), 1)


def start(c):
    with Stage(c, "start") as s:
        nc, a = c.nc, c.a
        loaded, eps_set = s.sem("loaded"), s.sem("eps_set")
        block = s.block()

        @block.sync
        def _(sp):
            sp.dma_start(c.x[:, :, :], a["x"].rearrange("(t p) d -> p t d", p=P)).then_inc(loaded, 16)
            sp.dma_start(c.ident[:, :], a["c_ident"]).then_inc(loaded, 16)
            sp.wait_ge(loaded, 32)

        @block.vector
        def _(dve):
            nc.vector.memset(c.eps[:, :], EPS).then_inc(eps_set, 1)
            dve.wait_ge(eps_set, 1)


def finish(c):
    with Stage(c, "finish") as s:
        stored = s.sem("stored")
        block = s.block()

        @block.sync
        def _(sp):
            sp.dma_start(c.a["out"].rearrange("(t p) d -> p t d", p=P), c.x[:, :, :]).then_inc(stored, 16)
            sp.wait_ge(stored, 16)


def cross_attention(c, name, mask_name, mask_rows):
    NG = -(-KC // 4)
    TILE = [(b, g) for b in (0, 1) for g in range(NG)]
    with Stage(c, name) as s:
        nc, a = c.nc, c.a
        wq, wkT, wv = s.sb("wq", [P, D]), s.sb("wkT", [P, D]), s.sb("wv", [P, D])
        bq, bk, bv = s.sb("bq", [P, 1]), s.sb("bk", [P, 1]), s.sb("bv", [P, D])
        qT = s.sb("qT", [P, TOK])
        qkT = s.sb("qkT", [P, TOK])
        q1 = s.sb("q1", [P, P])
        qk1 = s.sb("qk1", [P, P])
        qbk = s.sb("qbk", [P, 1])
        mask = s.sb("mask", [P, 2, KEYS], I32 if mask_rows == 1 else U8)
        out_ = s.sb("out_keys", [P, KEYS])
        shift = s.sb("shift", [P, KEYS])
        ctx = s.sb("ctx", [P, 2, 2, KC, D])
        ctxT = s.sb("ctxT", [P, 2, KEYS])
        sc = s.sb("sc", [P, KEYS])
        probs = s.sb("probs", [P, KEYS])
        probsT = s.sb("probsT", [P, KC, P])
        mx, nmx = s.sb("mx", [P, 1]), s.sb("nmx", [P, 1])
        rows, rinv = s.sb("rows", [P, 1]), s.sb("rinv", [P, 1])
        oT, o = s.sb("oT", [P, P]), s.sb("o", [P, D])
        turn = s.ps("turn", [P, 2, 512])
        scores = s.ps("scores", [P, 4, 512])
        mixed = s.ps("mixed", [P, 512])
        small = s.ps("small", [P, 512])
        weights, first = s.sem("weights"), s.sem("first")
        ctx_in = [s.sem("ctx_in0"), s.sem("ctx_in1")]
        mask_in = [s.sem("mask_in0"), s.sem("mask_in1")]
        V = Steps(s.sem("vector_steps"), (1, LN_V + [f"q{i}" for i in range(4)]),
                  (NT, ["tile_q", "qbk", "ind"] + [f"ctxT{b}{g}" for b, g in TILE if g % 2 == 0] +
                   ["masked", "nmax"] + [f"pT{g}" for g in range(0, NG, 2)] + ["oT", "rinv", "out", "x"], 2))
        A = Steps(s.sem("scalar_steps"), (1, LN_A + [f"qk{i}" for i in range(4)]),
                  (NT, ["tile_qk", "shift"] + [f"ctxT{b}{g}" for b, g in TILE if g % 2] + ["exp"] +
                   [f"pT{g}" for g in range(1, NG, 2)], 2))
        PE = Steps(s.sem("tensor_steps"), (1, LN_P + [x for i in range(4) for x in (f"q{i}", f"qk{i}")]),
                   (NT, ["qbk"] + [f"ctxT{b}{g}" for b, g in TILE] + ["scores"] +
                    [f"pT{g}" for g in range(NG)] + ["oT", "out"], 2))
        tp = [turn[:, i, :] for i in (0, 1)]
        flat = scores[:, :, :].rearrange("p a n -> p (a n)")[:, 0:KEYS]
        wide = [min(512, KEYS - 512 * g) for g in range(NG)]
        block = s.block()

        @block.sync
        def _(sp):
            for dst, src in ((wq, "Wq"), (wkT, "WkT"), (wv, "Wv"), (bq, "bq"), (bk, "bk")):
                sp.dma_start(dst[:, :], a[f"{name}_{src}"]).then_inc(weights, 16)
            sp.dma_start(bv[:, :], a[f"{name}_bv"].broadcast_to([P, D])).then_inc(weights, 16)

            def load(t, u):
                for b in (0, 1):
                    keys = a["ctx"][bass.ds(2 * t + b, 1), :, :].rearrange("a k d -> (a k) d")
                    sp.dma_start(ctx[:, u, b, 0:KC - 1, :], keys[0:(KC - 1) * P, :].rearrange("(j p) d -> p j d", p=P))\
                        .then_inc(ctx_in[u], 16)
                    sp.dma_start(ctx[0:KREST, u, b, KC - 1, :], keys[(KC - 1) * P:KEYS, :]).then_inc(ctx_in[u], 16)
                    m = a[mask_name][bass.ds(2 * t + b, 1), :, :].rearrange("a q k -> (a q) k")
                    if mask_rows == 1:
                        m = m.broadcast_to([S, KEYS])
                    sp.dma_start(mask[S * b:S * b + S, u, :], m).then_inc(mask_in[u], 16)

            load(0, 0)
            load(1, 1)
            with sp.Fori(1, NT // 2) as t2:
                for u in (0, 1):
                    sp.wait_ge(*PE.at("oT", 2 * t2 + u - 2))
                    load(2 * t2 + u, u)

        @block.tensor
        def _(pe):
            ln_tensor(c, pe, V, A, PE, tp)
            pe.wait_ge(weights, 96)
            pe.wait_ge(*V.at("ln_T2"))
            pe.wait_ge(*A.at("ln_T3"))
            for i in range(4):
                nc.tensor.matmul(scores[:, i, :], wq[:, :], c.xnT[:, 512 * i:512 * i + 512], start=True, stop=True)\
                    .then_inc(PE.did(f"q{i}"), 1)
                pe.wait_ge(*V.at(f"q{i}"))
                if i >= 2:
                    pe.wait_ge(*A.at(f"qk{i - 2}"))
                nc.tensor.matmul(tp[i % 2], wkT[:, :], qT[:, 512 * i:512 * i + 512], start=True, stop=True)\
                    .then_inc(PE.did(f"qk{i}"), 1)
            with pe.Fori(0, NT // 2) as t2:
                for u in (0, 1):
                    t = 2 * t2 + u
                    pe.wait_ge(*V.at("tile_q", t))
                    nc.tensor.matmul(small[:, 0:1], q1[:, :], bk[:, :], start=True, stop=True).then_inc(PE.did("qbk"), 1)
                    pe.wait_ge(*A.at("tile_qk", t))
                    pe.wait_ge(ctx_in[u], 64 * t2 + 64)
                    for n, (b, g) in enumerate(TILE):
                        if n >= 2:
                            pe.wait_ge(*(A if g % 2 else V).at("ctxT%d%d" % TILE[n - 2], t))
                        for j in range(4 * g, min(4 * g + 4, KC)):
                            k = min(P, KEYS - P * j)
                            last = nc.tensor.transpose(tp[g % 2][:, P * (j % 4):P * (j % 4) + k], ctx[0:k, u, b, j, :],
                                                       c.ident[0:k, 0:k])
                        last.then_inc(PE.did(f"ctxT{b}{g}"), 1)
                    pe.wait_ge(*V.at(f"ctxT1{NG - 2}", t))
                    pe.wait_ge(*A.at(f"ctxT1{NG - 1}", t))
                    for b in (0, 1):
                        for g in range(NG):
                            last = nc.tensor.matmul(scores[S * b:S * b + S, g, 0:wide[g]], qk1[:, S * b:S * b + S],
                                                    ctxT[:, b, 512 * g:512 * g + wide[g]], start=True, stop=True)
                    last.then_inc(PE.did("scores"), 1)
                    pe.wait_ge(*A.at("exp", t))
                    for g in range(NG):
                        if g >= 2:
                            pe.wait_ge(*(A if g % 2 else V).at(f"pT{g - 2}", t))
                        for j in range(4 * g, min(4 * g + 4, KC)):
                            k = min(P, KEYS - P * j)
                            last = nc.tensor.transpose(tp[g % 2][0:k, P * (j % 4):P * (j % 4) + P], probs[:, P * j:P * j + k],
                                                       c.ident[:, :])
                        last.then_inc(PE.did(f"pT{g}"), 1)
                    pe.wait_ge(*V.at(f"pT{NG - 2}", t))
                    pe.wait_ge(*A.at(f"pT{NG - 1}", t))
                    for b in (0, 1):
                        for j in range(KC):
                            k = min(P, KEYS - P * j)
                            last = nc.tensor.matmul(mixed[:, S * b:S * b + S], ctx[0:k, u, b, j, :],
                                                    probsT[0:k, j, S * b:S * b + S], start=(j == 0), stop=(j == KC - 1))
                    last.then_inc(PE.did("oT"), 1)
                    pe.wait_ge(*V.at("oT", t))
                    nc.tensor.matmul(small[:, P:2 * P], oT[:, :], wv[:, :], start=True, stop=True).then_inc(PE.did("out"), 1)

        @block.vector
        def _(dve):
            ln_vector(c, dve, V, A, PE, tp)
            dve.wait_ge(weights, 96)
            for i in range(4):
                dve.wait_ge(*PE.at(f"q{i}"))
                nc.vector.tensor_scalar(qT[:, 512 * i:512 * i + 512], scores[:, i, :], bq[:, 0:1], D ** -0.5,
                                        ALU.add, ALU.mult).then_inc(V.did(f"q{i}"), 1)
            with dve.Fori(0, NT // 2) as t2:
                for u in (0, 1):
                    t = 2 * t2 + u
                    nc.vector.tensor_copy(q1[:, :], qT[:, bass.ds(P * t, P)]).then_inc(V.did("tile_q"), 1)
                    dve.wait_ge(*PE.at("qbk", t))
                    nc.vector.tensor_copy(qbk[:, :], small[:, 0:1]).then_inc(V.did("qbk"), 1)
                    dve.wait_ge(mask_in[u], 32 * t2 + 32)
                    if mask_rows == 1:
                        nc.vector.tensor_scalar(out_[:, :], mask[:, u, :], 0.0, None, ALU.is_equal).then_inc(V.did("ind"), 1)
                    else:
                        nc.vector.tensor_copy(out_[:, :], mask[:, u, :]).then_inc(V.did("ind"), 1)
                    for b, g in TILE:
                        if g % 2 == 0:
                            dve.wait_ge(*PE.at(f"ctxT{b}{g}", t))
                            nc.vector.tensor_copy(ctxT[:, b, 512 * g:512 * g + wide[g]], tp[0][:, 0:wide[g]])\
                                .then_inc(V.did(f"ctxT{b}{g}"), 1)
                    dve.wait_ge(*A.at("shift", t))
                    dve.wait_ge(*PE.at("scores", t))
                    nc.vector.memset(c.pause[:, :], 0.0)
                    nc.vector.tensor_tensor_reduce(out=sc[:, :], in0=flat, in1=shift[:, :], scale=1.0, scalar=3 * OUT,
                                                   op0=ALU.add, op1=ALU.max, accum_out=mx[:, :]).then_inc(V.did("masked"), 1)
                    dve.wait_ge(*V.at("masked", t))
                    nc.vector.tensor_scalar(nmx[:, :], mx[:, :], -1.0, None, ALU.mult).then_inc(V.did("nmax"), 1)
                    for g in range(0, NG, 2):
                        dve.wait_ge(*PE.at(f"pT{g}", t))
                        nc.vector.tensor_copy(probsT[:, 4 * g:4 * g + 4, :].rearrange("p j q -> p (j q)"), tp[0])\
                            .then_inc(V.did(f"pT{g}"), 1)
                    dve.wait_ge(*PE.at("oT", t))
                    nc.vector.tensor_copy(oT[:, :], mixed[:, 0:P]).then_inc(V.did("oT"), 1)
                    nc.vector.reciprocal(rinv[:, :], rows[:, :]).then_inc(V.did("rinv"), 1)
                    dve.wait_ge(*V.at("rinv", t))
                    dve.wait_ge(*PE.at("out", t))
                    nc.vector.scalar_tensor_tensor(out=o[:, :], in0=small[:, P:2 * P], scalar=rinv[:, 0:1], in1=bv[:, :],
                                                   op0=ALU.mult, op1=ALU.add).then_inc(V.did("out"), 1)
                    dve.wait_ge(*V.at("out", t))
                    xt = c.x[:, bass.ds(t, 1), :].rearrange("p a d -> p (a d)")
                    nc.vector.tensor_tensor(xt, xt, o[:, :], ALU.add).then_inc(V.did("x"), 1)

        @block.scalar
        def _(act):
            ln_scalar(c, act, V, A, PE, tp)
            for i in range(4):
                act.wait_ge(*PE.at(f"qk{i}"))
                nc.scalar.copy(qkT[:, 512 * i:512 * i + 512], tp[i % 2]).then_inc(A.did(f"qk{i}"), 1)
            with act.Fori(0, NT // 2) as t2:
                for u in (0, 1):
                    t = 2 * t2 + u
                    act.wait_ge(*V.at("tile_q", t))
                    nc.scalar.copy(qk1[:, :], qkT[:, bass.ds(P * t, P)]).then_inc(A.did("tile_qk"), 1)
                    act.wait_ge(*V.at("ind", t))
                    nc.scalar.activation(shift[:, :], out_[:, :], ACT.Identity, bias=qbk[:, 0:1], scale=OUT)\
                        .then_inc(A.did("shift"), 1)
                    for b, g in TILE:
                        if g % 2:
                            act.wait_ge(*PE.at(f"ctxT{b}{g}", t))
                            nc.scalar.copy(ctxT[:, b, 512 * g:512 * g + wide[g]], tp[1][:, 0:wide[g]])\
                                .then_inc(A.did(f"ctxT{b}{g}"), 1)
                    act.wait_ge(*V.at("nmax", t))
                    nc.scalar.activation(probs[:, :], sc[:, :], ACT.Exp, bias=nmx[:, 0:1], scale=1.0, accum_out=rows[:, :])\
                        .then_inc(A.did("exp"), 1)
                    for g in range(1, NG, 2):
                        act.wait_ge(*PE.at(f"pT{g}", t))
                        k = P if g < NG - 1 else KREST
                        j = min(4 * g + 4, KC)
                        nc.scalar.copy(probsT[0:k, 4 * g:j, :].rearrange("p j q -> p (j q)"), tp[1][0:k, 0:P * (j - 4 * g)])\
                            .then_inc(A.did(f"pT{g}"), 1)


def causal_cross_attention(c, name):
    with Stage(c, name) as s:
        nc, a = c.nc, c.a
        G = NT // 4
        w, wT = s.sb("w", [P, D]), s.sb("wT", [P, D])
        mask = s.sb("mask", [P, P])
        keys_all = s.sb("keys_all", [P, NT, D])
        keys = s.sb("keys", [P, 4, D])
        keysT = s.sb("keysT", [P, 512])
        q, qk = s.sb("q", [P, 512]), s.sb("qk", [P, 512])
        sc, probsT = s.sb("sc", [P, 4, P]), s.sb("probsT", [P, 4, P])
        mx, rows, rinv = s.sb("mx", [P, 4]), s.sb("rows", [P, 4]), s.sb("rinv", [P, 4])
        oT, o = s.sb("oT", [P, 4, P]), s.sb("o", [P, 4, D])
        turn = s.ps("turn", [P, 2, 512])
        pq, pqk, psc = s.ps("q", [P, 512]), s.ps("qk", [P, 512]), s.ps("sc", [P, 512])
        po, pout = s.ps("oT", [P, 512]), s.ps("out", [P, 512])
        loaded = s.sem("loaded")
        V = Steps(s.sem("vector_steps"), (1, LN_V), (G, ["keysT", "q", "masked", "max", "less", "rows", "rinv", "probs",
                                                        "oT", "x"]))
        A = Steps(s.sem("scalar_steps"), (1, LN_A), (G, ["keys", "qk", "exp", "probsT"]))
        PE = Steps(s.sem("tensor_steps"), (1, LN_P), (G, ["keysT", "q", "qk", "scores", "probsT", "oT", "out"]))
        tp = [turn[:, i, :] for i in (0, 1)]
        four = lambda m: m.rearrange("p (i k) -> p i k", i=4)
        wide = lambda m: m[:, :].unsqueeze(2).broadcast_to([P, 4, P])
        block = s.block()

        @block.sync
        def _(sp):
            sp.dma_start(w[:, :], a[f"{name}_Wq"]).then_inc(loaded, 16)
            sp.dma_start(wT[:, :], a[f"{name}_WqT"]).then_inc(loaded, 16)
            sp.dma_start(mask[:, :], a["c_pair_causal"]).then_inc(loaded, 16)
            for b in (0, 1):
                src = a["ctx"].rearrange("(t b) k d -> b k t d", b=2)[b, 0:S, :, :]
                sp.dma_start(keys_all[S * b:S * b + S, :, :], src).then_inc(loaded, 16)

        @block.tensor
        def _(pe):
            ln_tensor(c, pe, V, A, PE, tp)
            pe.wait_ge(*V.at("ln_T2"))
            pe.wait_ge(*A.at("ln_T3"))
            with pe.Fori(0, G) as g:
                pe.wait_ge(*A.at("keys", g))
                for i in range(4):
                    last = nc.tensor.transpose(tp[0][:, P * i:P * i + P], keys[:, i, :], c.ident[:, :])
                last.then_inc(PE.did("keysT"), 1)
                nc.tensor.matmul(pq[:, :], wT[:, :], c.xnT[:, bass.ds(512 * g, 512)], start=True, stop=True)\
                    .then_inc(PE.did("q"), 1)
                pe.wait_ge(*V.at("q", g))
                nc.tensor.matmul(pqk[:, :], w[:, :], q[:, :], start=True, stop=True).then_inc(PE.did("qk"), 1)
                pe.wait_ge(*A.at("qk", g))
                for i in range(4):
                    last = nc.tensor.matmul(psc[:, P * i:P * i + P], qk[:, P * i:P * i + P], keysT[:, P * i:P * i + P],
                                            start=True, stop=True)
                last.then_inc(PE.did("scores"), 1)
                pe.wait_ge(*V.at("probs", g))
                for i in range(4):
                    last = nc.tensor.transpose(tp[1][:, P * i:P * i + P], sc[:, i, :], c.ident[:, :])
                last.then_inc(PE.did("probsT"), 1)
                pe.wait_ge(*A.at("probsT", g))
                for i in range(4):
                    last = nc.tensor.matmul(po[:, P * i:P * i + P], keys[:, i, :], probsT[:, i, :], start=True, stop=True)
                last.then_inc(PE.did("oT"), 1)
                pe.wait_ge(*V.at("oT", g))
                for i in range(4):
                    last = nc.tensor.matmul(pout[:, P * i:P * i + P], oT[:, i, :], wT[:, :], start=True, stop=True)
                last.then_inc(PE.did("out"), 1)

        @block.vector
        def _(dve):
            ln_vector(c, dve, V, A, PE, tp)
            with dve.Fori(0, G) as g:
                dve.wait_ge(*PE.at("keysT", g))
                nc.vector.tensor_copy(keysT[:, :], tp[0]).then_inc(V.did("keysT"), 1)
                dve.wait_ge(*PE.at("q", g))
                nc.vector.tensor_scalar(q[:, :], pq[:, :], D ** -0.5, None, ALU.mult).then_inc(V.did("q"), 1)
                dve.wait_ge(*PE.at("scores", g))
                nc.vector.tensor_tensor(sc[:, :, :], four(psc[:, :]), mask[:, :].unsqueeze(1).broadcast_to([P, 4, P]),
                                        ALU.add).then_inc(V.did("masked"), 1)
                dve.wait_ge(*V.at("masked", g))
                nc.vector.tensor_reduce(mx[:, :], sc[:, :, :], AX.X, ALU.max).then_inc(V.did("max"), 1)
                dve.wait_ge(*V.at("max", g))
                nc.vector.tensor_tensor(sc[:, :, :], sc[:, :, :], wide(mx), ALU.subtract).then_inc(V.did("less"), 1)
                dve.wait_ge(*A.at("exp", g))
                nc.vector.tensor_reduce(rows[:, :], sc[:, :, :], AX.X, ALU.add).then_inc(V.did("rows"), 1)
                dve.wait_ge(*V.at("rows", g))
                nc.vector.reciprocal(rinv[:, :], rows[:, :]).then_inc(V.did("rinv"), 1)
                dve.wait_ge(*V.at("rinv", g))
                nc.vector.tensor_tensor(sc[:, :, :], sc[:, :, :], wide(rinv), ALU.mult).then_inc(V.did("probs"), 1)
                dve.wait_ge(*PE.at("oT", g))
                nc.vector.tensor_copy(oT[:, :, :], four(po[:, :])).then_inc(V.did("oT"), 1)
                dve.wait_ge(*PE.at("out", g))
                xg = c.x[:, bass.ds(4 * g, 4), :]
                nc.vector.tensor_tensor(xg, four(pout[:, :]), xg, ALU.add).then_inc(V.did("x"), 1)

        @block.scalar
        def _(act):
            ln_scalar(c, act, V, A, PE, tp)
            act.wait_ge(loaded, 80)
            with act.Fori(0, G) as g:
                act.wait_ge(*PE.before("oT", g))
                nc.scalar.copy(keys[:, :, :], keys_all[:, bass.ds(4 * g, 4), :]).then_inc(A.did("keys"), 1)
                act.wait_ge(*PE.at("qk", g))
                nc.scalar.copy(qk[:, :], pqk[:, :]).then_inc(A.did("qk"), 1)
                act.wait_ge(*V.at("less", g))
                nc.scalar.activation(sc[:, :, :], sc[:, :, :], ACT.Exp).then_inc(A.did("exp"), 1)
                act.wait_ge(*PE.at("probsT", g))
                nc.scalar.copy(probsT[:, :, :], four(tp[1])).then_inc(A.did("probsT"), 1)


MH_V = ["spread", "masked", "max", "less", "rows", "rinv", "diag", "own", "sum", "scale"]
MH_A = ["exp", "pT0", "pT1"]
MH_P = ["scores", "pT0", "pT1", "norm", "pv"]


def named(tag, names):
    return [f"{tag}_{n}" for n in names]


class Heads:

    def __init__(self, s):
        self.hb = s.sb("hb", [P, 4])
        self.which = s.sb("which", [P, 8, P])
        self.delta = s.sb("delta", [P, S])
        self.qd = s.sb("qd", [P, 2, 4, S])
        self.sc = s.sb("sc", [P, 16, S])
        self.mx, self.rows, self.rinv = s.sb("mx", [P, 16]), s.sb("rows", [P, 16]), s.sb("rinv", [P, 16])
        self.diag = s.sb("diag", [P, 16, S])
        self.pT = s.sb("pT", [P, 8, P])
        self.own = s.sb("own", [P, 2, 4, S])
        self.sum = s.sb("sum", [P, 2, S])
        self.ps = s.ps("scores", [P, 4, 512])
        self.turn = s.ps("turn", [P, 2, 512])

    def load(self, eng, a, sem):
        eng.dma_start(self.hb[:, :], a["c_heads"]).then_inc(sem, 16)
        eng.dma_start(self.which[:, :, :], a["c_which"]).then_inc(sem, 16)
        eng.dma_start(self.delta[:, :], a["c_delta"]).then_inc(sem, 16)


def heads_vector(c, dve, h, V, A, PE, tag, t, q, mask, delta, out, before):
    nc = c.nc
    for w in before:
        dve.wait_ge(*w)
    nc.vector.tensor_tensor(h.qd[:, :, :, :], q.rearrange("p (b q) -> p b q", b=2).unsqueeze(2).broadcast_to([P, 2, 4, S]),
                            h.hb[:, :].unsqueeze(1).unsqueeze(3).broadcast_to([P, 2, 4, S]), ALU.mult)\
        .then_inc(V.did(f"{tag}_spread"), 1)
    dve.wait_ge(*PE.at(f"{tag}_scores", t))
    four = h.ps[:, :, 0:256].rearrange("p g (r k) -> p g r k", k=S)
    sc4 = h.sc[:, :, :].rearrange("p (g r) k -> p g r k", g=4)
    if mask is not None:
        nc.vector.tensor_tensor(sc4, four, mask[:, :].unsqueeze(1).unsqueeze(1).broadcast_to([P, 4, 4, S]), ALU.add)\
            .then_inc(V.did(f"{tag}_masked"), 1)
    else:
        nc.vector.tensor_copy(sc4, four).then_inc(V.did(f"{tag}_masked"), 1)
    dve.wait_ge(*V.at(f"{tag}_masked", t))
    nc.vector.tensor_reduce(h.mx[:, :], h.sc[:, :, :], AX.X, ALU.max).then_inc(V.did(f"{tag}_max"), 1)
    dve.wait_ge(*V.at(f"{tag}_max", t))
    nc.vector.tensor_tensor(h.sc[:, :, :], h.sc[:, :, :], h.mx[:, :].unsqueeze(2).broadcast_to([P, 16, S]), ALU.subtract)\
        .then_inc(V.did(f"{tag}_less"), 1)
    dve.wait_ge(*A.at(f"{tag}_exp", t))
    nc.vector.tensor_reduce(h.rows[:, :], h.sc[:, :, :], AX.X, ALU.add).then_inc(V.did(f"{tag}_rows"), 1)
    dve.wait_ge(*V.at(f"{tag}_rows", t))
    nc.vector.reciprocal(h.rinv[:, :], h.rows[:, :]).then_inc(V.did(f"{tag}_rinv"), 1)
    dve.wait_ge(*V.at(f"{tag}_rinv", t))
    nc.vector.tensor_tensor(h.diag[:, :, :], h.rinv[:, :].unsqueeze(2).broadcast_to([P, 16, S]),
                            delta[:, :].unsqueeze(1).broadcast_to([P, 16, S]), ALU.mult).then_inc(V.did(f"{tag}_diag"), 1)
    dve.wait_ge(*PE.at(f"{tag}_pv", t))
    nc.vector.tensor_tensor(h.own[:, :, :, :], h.ps[:, 0:2, 0:256].rearrange("p b (h q) -> p b h q", h=4),
                            h.hb[:, :].unsqueeze(1).unsqueeze(3).broadcast_to([P, 2, 4, S]), ALU.mult)\
        .then_inc(V.did(f"{tag}_own"), 1)
    dve.wait_ge(*V.at(f"{tag}_own", t))
    nc.vector.tensor_reduce(h.sum[:, :, :], h.own[:, :, :, :].rearrange("p b h q -> p b q h"), AX.X, ALU.add)\
        .then_inc(V.did(f"{tag}_sum"), 1)
    dve.wait_ge(*V.at(f"{tag}_sum", t))
    nc.vector.tensor_tensor(out, h.sum[:, :, :].rearrange("p b q -> p (b q)"), h.ps[:, 2, 0:P], ALU.mult)\
        .then_inc(V.did(f"{tag}_scale"), 1)


def heads_scalar(c, act, h, V, A, PE, tag, t):
    nc = c.nc
    act.wait_ge(*V.at(f"{tag}_less", t))
    nc.scalar.activation(h.sc[:, :, :], h.sc[:, :, :], ACT.Exp).then_inc(A.did(f"{tag}_exp"), 1)
    for i in (0, 1):
        act.wait_ge(*PE.at(f"{tag}_pT{i}", t))
        nc.scalar.copy(h.pT[:, 4 * i:4 * i + 4, :].rearrange("p r q -> p (r q)"), h.turn[:, i, :])\
            .then_inc(A.did(f"{tag}_pT{i}"), 1)


def heads_tensor(c, pe, h, V, A, PE, tag, t, k, v, before):
    nc = c.nc
    pe.wait_ge(*V.at(f"{tag}_spread", t))
    for w in before:
        pe.wait_ge(*w)
    for j in (0, 1):
        for b in (0, 1):
            for g in range(4):
                last = nc.tensor.matmul(h.ps[:, g, P * j + S * b:P * j + S * b + S],
                                        h.qd[32 * g:32 * g + 32, b, 2 * j:2 * j + 2, :].rearrange("p h q -> p (h q)"),
                                        k[32 * g:32 * g + 32, S * b:S * b + S], start=True, stop=True)
    last.then_inc(PE.did(f"{tag}_scores"), 1)
    pe.wait_ge(*A.at(f"{tag}_exp", t))
    for i in (0, 1):
        for r in range(4):
            last = nc.tensor.transpose(h.turn[:, i, P * r:P * r + P],
                                       h.sc[:, 8 * i + 2 * r:8 * i + 2 * r + 2, :].rearrange("p b k -> p (b k)"), c.ident[:, :])
        last.then_inc(PE.did(f"{tag}_pT{i}"), 1)
    pe.wait_ge(*A.at(f"{tag}_pT1", t))
    pe.wait_ge(*V.at(f"{tag}_diag", t))
    for r in range(8):
        last = nc.tensor.matmul(h.ps[:, 2, 0:P], h.which[:, r, :],
                                h.diag[:, 2 * r:2 * r + 2, :].rearrange("p b q -> p (b q)"), start=(r == 0), stop=(r == 7))
    last.then_inc(PE.did(f"{tag}_norm"), 1)
    for b in (0, 1):
        for g in range(4):
            last = nc.tensor.matmul(h.ps[32 * g:32 * g + 32, b, 0:256], v[S * b:S * b + S, 32 * g:32 * g + 32],
                                    h.pT[S * b:S * b + S, 2 * g:2 * g + 2, :].rearrange("p r q -> p (r q)"),
                                    start=True, stop=True, tile_position=(S * b, 32 * g))
    last.then_inc(PE.did(f"{tag}_pv"), 1)


def self_attention(c, name):
    with Stage(c, name) as s:
        nc, a = c.nc, c.a
        h = Heads(s)
        w = s.sb("w", [P, 5, D])
        wo = s.sb("wo", [P, D])
        cos, sin = s.sb("cos", [P, S]), s.sb("sin", [P, S])
        xg = s.sb("xg", [P, 512])
        straight, turned = s.sb("straight", [P, 2, 512]), s.sb("turned", [P, 2, 512])
        qT, kT, v, yT = s.sb("qT", [P, 512]), s.sb("kT", [P, 512]), s.sb("v", [P, 4, D]), s.sb("yT", [P, 4, P])
        pa, pb = s.ps("a", [P, 512]), s.ps("b", [P, 512])
        loaded = s.sem("loaded")
        tags = [f"t{i}" for i in range(4)]
        G = NT // 4
        V = Steps(s.sem("vector_steps"), (1, LN_V),
                  (G, ["q_cos", "q_sin", "q", "k_cos", "k_sin", "k"] + sum([named(n, MH_V) for n in tags], []) + ["x"]))
        A = Steps(s.sem("scalar_steps"), (1, LN_A), (G, ["xg", "v"] + sum([named(n, MH_A) for n in tags], [])))
        PE = Steps(s.sem("tensor_steps"), (1, LN_P), (G, ["q", "k", "v"] + sum([named(n, MH_P) for n in tags], []) + ["out"]))
        tp = [h.turn[:, i, :] for i in (0, 1)]
        eight = lambda m: m.rearrange("p (b q) -> p b q", q=S)
        wide = lambda m: m[:, :].unsqueeze(1).broadcast_to([P, 8, S])
        block = s.block()

        @block.sync
        def _(sp):
            h.load(sp, a, loaded)
            sp.dma_start(w[:, :, :], a[f"{name}_w"].rearrange("n p d -> p n d")).then_inc(loaded, 16)
            sp.dma_start(wo[:, :], a[f"{name}_wo"]).then_inc(loaded, 16)
            sp.dma_start(cos[:, :], a["c_cos"]).then_inc(loaded, 16)
            sp.dma_start(sin[:, :], a["c_sin"]).then_inc(loaded, 16)

        @block.tensor
        def _(pe):
            ln_tensor(c, pe, V, A, PE, tp)
            pe.wait_ge(loaded, 112)
            with pe.Fori(0, G) as g:
                pe.wait_ge(*A.at("xg", g))
                nc.tensor.matmul(pa[:, :], w[:, 0, :], xg[:, :], start=True, stop=True)
                nc.tensor.matmul(pb[:, :], w[:, 1, :], xg[:, :], start=True, stop=True).then_inc(PE.did("q"), 1)
                pe.wait_ge(*V.at("q_sin", g))
                nc.tensor.matmul(pa[:, :], w[:, 2, :], xg[:, :], start=True, stop=True)
                nc.tensor.matmul(pb[:, :], w[:, 3, :], xg[:, :], start=True, stop=True).then_inc(PE.did("k"), 1)
                pe.wait_ge(*V.at("k_sin", g))
                for i in range(4):
                    last = nc.tensor.matmul(pa[:, P * i:P * i + P], xg[:, P * i:P * i + P], w[:, 4, :], start=True, stop=True)
                last.then_inc(PE.did("v"), 1)
                for i, tag in enumerate(tags):
                    heads_tensor(c, pe, h, V, A, PE, tag, g, kT[:, P * i:P * i + P], v[:, i, :], [V.at("k", g), A.at("v", g)])
                pe.wait_ge(*V.at("t3_scale", g))
                for i in range(4):
                    last = nc.tensor.matmul(pb[:, P * i:P * i + P], yT[:, i, :], wo[:, :], start=True, stop=True)
                last.then_inc(PE.did("out"), 1)

        @block.vector
        def _(dve):
            ln_vector(c, dve, V, A, PE, tp)
            with dve.Fori(0, G) as g:
                for m, (n, dst, scale) in enumerate((("q", qT, DH ** -0.5), ("k", kT, 1.0))):
                    dve.wait_ge(*PE.at(n, g))
                    nc.vector.scalar_tensor_tensor(out=eight(straight[:, m, :]), in0=eight(pa[:, :]), scalar=scale,
                                                   in1=wide(cos), op0=ALU.mult, op1=ALU.mult).then_inc(V.did(f"{n}_cos"), 1)
                    nc.vector.scalar_tensor_tensor(out=eight(turned[:, m, :]), in0=eight(pb[:, :]), scalar=scale,
                                                   in1=wide(sin), op0=ALU.mult, op1=ALU.mult).then_inc(V.did(f"{n}_sin"), 1)
                    dve.wait_ge(*V.at(f"{n}_sin", g))
                    nc.vector.tensor_tensor(dst[:, :], straight[:, m, :], turned[:, m, :], ALU.add).then_inc(V.did(n), 1)
                for i, tag in enumerate(tags):
                    heads_vector(c, dve, h, V, A, PE, tag, g, qT[:, P * i:P * i + P], None, h.delta, yT[:, i, :], [V.at("q", g)])
                dve.wait_ge(*PE.at("out", g))
                xs = c.x[:, bass.ds(4 * g, 4), :]
                nc.vector.tensor_tensor(xs, pb[:, :].rearrange("p (i d) -> p i d", i=4), xs, ALU.add).then_inc(V.did("x"), 1)

        @block.scalar
        def _(act):
            ln_scalar(c, act, V, A, PE, tp)
            with act.Fori(0, G) as g:
                act.wait_ge(*V.at("ln_T2"))
                act.wait_ge(*V.before("x", g))
                nc.scalar.copy(xg[:, :], c.xnT[:, bass.ds(512 * g, 512)]).then_inc(A.did("xg"), 1)
                act.wait_ge(*PE.at("v", g))
                nc.scalar.copy(v[:, :, :], pa[:, :].rearrange("p (i d) -> p i d", i=4)).then_inc(A.did("v"), 1)
                for i, tag in enumerate(tags):
                    heads_scalar(c, act, h, V, A, PE, tag, g)


def two_step_attention(c, name):
    with Stage(c, name) as s:
        nc, a = c.nc, c.a
        h = Heads(s)
        w, wp = s.sb("w", [P, 3, D]), s.sb("wp", [P, D])
        bias = s.sb("bias", [P, 3])
        bp, bp2 = s.sb("bp", [P, D]), s.sb("bp2", [P, D])
        causal, strict = s.sb("causal", [P, S]), s.sb("strict", [P, S])
        later = s.sb("later", [P, S])
        vg = s.sb("vg", [P, 4, D])
        qT, kT, k2T = s.sb("qT", [P, 512]), s.sb("kT", [P, 512]), s.sb("k2T", [P, 512])
        xg = s.sb("xg", [P, 512])
        yT, y2T, sumT = s.sb("yT", [P, P]), s.sb("y2T", [P, P]), s.sb("sumT", [P, 4, P])
        eT, e = s.sb("eT", [P, 2, S]), s.sb("e", [P, D])
        pa, pb = s.ps("a", [P, 512]), s.ps("b", [P, 512])
        loaded = s.sem("loaded")
        G = NT // 4
        tags = [f"t{i}" for i in range(4)]
        V = Steps(s.sem("vector_steps"), (1, LN_V + ["bp2", "eT"]),
                  (G, ["q", "k2"] + sum([named(n, MH_V) + [f"{n}_err"] + named(n + "b", MH_V) + [f"{n}_total"] for n in
                                         ("u0", "u1", "u2", "u3")], []) + ["bias", "x"]))
        A = Steps(s.sem("scalar_steps"), (1, LN_A),
                  (G, ["xg", "vg", "k"] + sum([named(n, MH_A) + [f"{n}_e"] + named(n + "b", MH_A) for n in
                                               ("u0", "u1", "u2", "u3")], [])))
        PE = Steps(s.sem("tensor_steps"), (1, LN_P),
                   (G, ["q", "k", "k2"] + sum([named(n, MH_P) + [f"{n}_e"] + named(n + "b", MH_P) for n in
                                               ("u0", "u1", "u2", "u3")], []) + ["out"]))
        tags = ["u0", "u1", "u2", "u3"]
        tp = [h.turn[:, i, :] for i in (0, 1)]
        four = lambda m: m.rearrange("p (i d) -> p i d", i=4)
        block = s.block()

        @block.sync
        def _(sp):
            h.load(sp, a, loaded)
            sp.dma_start(w[:, :, :], a[f"{name}_w"].rearrange("n p d -> p n d")).then_inc(loaded, 16)
            sp.dma_start(bias[:, :], a[f"{name}_bias"]).then_inc(loaded, 16)
            sp.dma_start(wp[:, :], a[f"{name}_W_proj"]).then_inc(loaded, 16)
            sp.dma_start(bp[:, :], a[f"{name}_b_proj"].broadcast_to([P, D])).then_inc(loaded, 16)
            sp.dma_start(causal[:, :], a["c_causal"]).then_inc(loaded, 16)
            sp.dma_start(strict[:, :], a["c_strict"]).then_inc(loaded, 16)
            sp.dma_start(later[:, :], a["c_later"]).then_inc(loaded, 16)

        @block.tensor
        def _(pe):
            ln_tensor(c, pe, V, A, PE, tp)
            pe.wait_ge(loaded, 160)
            with pe.Fori(0, G) as g:
                pe.wait_ge(*A.at("xg", g))
                nc.tensor.matmul(pa[:, :], w[:, 0, :], xg[:, :], start=True, stop=True).then_inc(PE.did("q"), 1)
                pe.wait_ge(*V.before("x", g))
                nc.tensor.matmul(pb[:, :], w[:, 1, :], xg[:, :], start=True, stop=True).then_inc(PE.did("k"), 1)
                pe.wait_ge(*V.at("q", g))
                nc.tensor.matmul(pa[:, :], w[:, 2, :], xg[:, :], start=True, stop=True).then_inc(PE.did("k2"), 1)
                for i, tag in enumerate(tags):
                    part = slice(P * i, P * i + P)
                    heads_tensor(c, pe, h, V, A, PE, tag, g, kT[:, part], vg[:, i, :], [A.at("k", g)])
                    pe.wait_ge(*V.at(f"{tag}_err", g))
                    nc.tensor.transpose(pa[:, 0:P], eT[:, :, :].rearrange("p b q -> p (b q)"), c.ident[:, :])\
                        .then_inc(PE.did(f"{tag}_e"), 1)
                    heads_tensor(c, pe, h, V, A, PE, tag + "b", g, k2T[:, part], e[:, :], [A.at(f"{tag}_e", g)])
                pe.wait_ge(*V.at("u3_total", g))
                for i in range(4):
                    last = nc.tensor.matmul(pb[:, P * i:P * i + P], sumT[:, i, :], wp[:, :], start=True, stop=True)
                last.then_inc(PE.did("out"), 1)

        @block.vector
        def _(dve):
            ln_vector(c, dve, V, A, PE, tp)
            dve.wait_ge(loaded, 160)
            nc.vector.tensor_tensor(bp2[:, :], bp[:, :], bp[:, :], ALU.add).then_inc(V.did("bp2"), 1)
            nc.vector.memset(eT[:, :, S - 1:S], 0.0).then_inc(V.did("eT"), 1)
            with dve.Fori(0, G) as g:
                dve.wait_ge(*PE.at("q", g))
                nc.vector.tensor_scalar(qT[:, :], pa[:, :], bias[:, 0:1], DH ** -0.5, ALU.add, ALU.mult)\
                    .then_inc(V.did("q"), 1)
                dve.wait_ge(*PE.at("k2", g))
                nc.vector.tensor_scalar(k2T[:, :], pa[:, :], bias[:, 2:3], None, ALU.add).then_inc(V.did("k2"), 1)
                for i, tag in enumerate(tags):
                    part = slice(P * i, P * i + P)
                    heads_vector(c, dve, h, V, A, PE, tag, g, qT[:, part], causal, h.delta, yT[:, :], [V.at("q", g)])
                    dve.wait_ge(*V.at(f"{tag}_scale", g))
                    v2, y2 = (m.rearrange("p (b q) -> p b q", b=2) for m in (xg[:, part], yT[:, :]))
                    nc.vector.tensor_tensor(eT[:, :, 0:S - 1], v2[:, :, 1:S], y2[:, :, 0:S - 1], ALU.subtract)\
                        .then_inc(V.did(f"{tag}_err"), 1)
                    heads_vector(c, dve, h, V, A, PE, tag + "b", g, qT[:, part], strict, later, y2T[:, :], [])
                    dve.wait_ge(*V.at(f"{tag}b_scale", g))
                    nc.vector.tensor_tensor(sumT[:, i, :], yT[:, :], y2T[:, :], ALU.add).then_inc(V.did(f"{tag}_total"), 1)
                xs = c.x[:, bass.ds(4 * g, 4), :]
                nc.vector.tensor_tensor(xs, xs, bp2[:, :].unsqueeze(1).broadcast_to([P, 4, D]), ALU.add)\
                    .then_inc(V.did("bias"), 1)
                dve.wait_ge(*V.at("bias", g))
                dve.wait_ge(*PE.at("out", g))
                nc.vector.tensor_tensor(xs, four(pb[:, :]), xs, ALU.add).then_inc(V.did("x"), 1)

        @block.scalar
        def _(act):
            ln_scalar(c, act, V, A, PE, tp)
            with act.Fori(0, G) as g:
                act.wait_ge(*V.before("x", g))
                nc.scalar.copy(xg[:, :], c.xnT[:, bass.ds(512 * g, 512)]).then_inc(A.did("xg"), 1)
                nc.scalar.copy(vg[:, :, :], c.xn[:, bass.ds(4 * g, 4), :]).then_inc(A.did("vg"), 1)
                act.wait_ge(*PE.at("k", g))
                nc.scalar.activation(kT[:, :], pb[:, :], ACT.Identity, bias=bias[:, 1:2]).then_inc(A.did("k"), 1)
                for i, tag in enumerate(tags):
                    heads_scalar(c, act, h, V, A, PE, tag, g)
                    act.wait_ge(*PE.at(f"{tag}_e", g))
                    nc.scalar.copy(e[:, :], pa[:, 0:P]).then_inc(A.did(f"{tag}_e"), 1)
                    heads_scalar(c, act, h, V, A, PE, tag + "b", g)


def spectral_layer(c, name):
    F2 = P
    with Stage(c, name) as s:
        nc, a = c.nc, c.a
        cols = s.sb("cols", [P, 4])
        wto, wfrom = s.sb("wto", [P, F2]), s.sb("wfrom", [F2, D])
        w1, b1 = s.sb("w1", [P, 4 * D]), s.sb("b1", [P, 4])
        w2, b2 = s.sb("w2", [P, 4, D]), s.sb("b2", [P, D])
        b2s = s.sb("b2s", [P, D])
        halves, freq = s.sb("halves", [F2, 2]), s.sb("freq", [F2, 32])
        raw = s.sb("raw", [F2, 2])
        decay, omega = s.sb("decay", [F2, 1]), s.sb("omega", [F2, 1])
        sine, half = s.sb("sine", [F2, 1]), s.sb("half", [F2, 1])
        half2, cosine = s.sb("half2", [F2, 1]), s.sb("cosine", [F2, 1])
        part = s.sb("part", [F2, 2])
        factor = s.sb("factor", [F2, 2])
        rot = s.sb("rot", [F2, F2])
        rot_u, rot_z = s.sb("rot_u", [F2, F2]), s.sb("rot_z", [F2, F2])
        h, hT = s.sb("h", [P, NT, D]), s.sb("hT", [P, TOK])
        uT = s.sb("uT", [F2, TOK])
        z = s.sb("z", [F2, B, S + 1])
        x2, x2b = s.sb("x2", [P, NT, D]), s.sb("x2b", [P, NT, D])
        g = s.sb("gelu", [P, 4, 512])
        turn = s.ps("turn", [P, 2, 512])
        step = s.ps("step", [P, 2, 512])
        big = s.ps("big", [P, 2, 512])
        loaded = s.sem("loaded")
        n1 = Norm(c, turned=False)
        n2 = Norm(c, "in", c.xn, h, hT, cols[:, 0:1], cols[:, 1:2])
        n3 = Norm(c, "ff", x2, h, hT, cols[:, 2:3], cols[:, 3:4])
        V = Steps(s.sem("vector_steps"),
                  (1, ["b2s", "z0", "rot", "half2", "cosine", "part0", "part1", "factor0", "factor1", "rot0", "rot1", "rot_u", "rot_z"] +
                   n1.V + n2.V + ["u0", "u2"]),
                  (S, ["clip"], 2), (1, ["x2_0", "x2_1", "x2_2", "x2_3"] + n3.V + ["x2b", "xb"]), (4, ["x"]))
        A = Steps(s.sem("scalar_steps"), (1, ["omega", "decay", "sine", "half"] + n1.A + n2.A + ["u1", "u3"] + n3.A),
                  (4, [f"g{i}" for i in range(4)]))
        PE = Steps(s.sem("tensor_steps"), (1, n2.P + [f"u{i}" for i in range(4)]), (S, ["step"], 2),
                   (1, ["from0", "from1", "from2", "from3"] + n3.P), (4, [f"h{i}" for i in range(4)] + ["out"]))
        tp = [turn[:, i, :] for i in (0, 1)]
        four = lambda m: m.rearrange("p (i d) -> p i d", i=4)
        u3 = uT[:, :].rearrange("f (b s) -> f b s", b=B)
        block = s.block()

        @block.sync
        def _(sp):
            sp.dma_start(raw[:, 0:1], a[f"{name}_decay"]).then_inc(loaded, 16)
            sp.dma_start(raw[:, 1:2], a[f"{name}_freq"]).then_inc(loaded, 16)
            sp.dma_start(halves[:, :], a["c_halves"]).then_inc(loaded, 16)
            sp.dma_start(freq[:, :], a["c_freq"]).then_inc(loaded, 16)
            sp.dma_start(cols[:, :], a[f"{name}_cols"]).then_inc(loaded, 16)
            sp.dma_start(wto[:, :], a[f"{name}_W_toT"]).then_inc(loaded, 16)
            sp.dma_start(wfrom[:, :], a[f"{name}_W_fromT"]).then_inc(loaded, 16)
            sp.dma_start(w1[:, :], a[f"{name}_W1T"]).then_inc(loaded, 16)
            sp.dma_start(b1[:, :], a[f"{name}_b1"]).then_inc(loaded, 16)
            sp.dma_start(w2[:, :, :], a[f"{name}_W2T"].rearrange("(c p) d -> p c d", p=P)).then_inc(loaded, 16)
            sp.dma_start(b2[:, :], a[f"{name}_b2"].broadcast_to([P, D])).then_inc(loaded, 16)

        @block.tensor
        def _(pe):
            ln_tensor(c, pe, V, A, PE, tp, n2)
            pe.wait_ge(*V.at("in_T2"))
            pe.wait_ge(*A.at("in_T3"))
            for i in range(4):
                if i >= 2:
                    pe.wait_ge(*(A if i % 2 else V).at(f"u{i - 2}"))
                nc.tensor.matmul(big[0:F2, i % 2, :], wto[:, :], hT[:, 512 * i:512 * i + 512], start=True, stop=True)\
                    .then_inc(PE.did(f"u{i}"), 1)
            pe.wait_ge(*V.at("u2"))
            pe.wait_ge(*A.at("u3"))
            with pe.Fori(0, S // 2) as k:
                for u in (0, 1):
                    t = 2 * k + u
                    pe.wait_ge(*V.before("clip", t))
                    nc.tensor.matmul(step[0:F2, u, 0:B], rot_u[:, :], u3[:, :, bass.ds(t, 1)], start=True, stop=False)
                    nc.tensor.matmul(step[0:F2, u, 0:B], rot_z[:, :], z[:, :, bass.ds(t, 1)], start=False, stop=True)\
                        .then_inc(PE.did("step"), 1)
            pe.wait_ge(*V.at("clip", S - 1))
            for i in range(4):
                if i >= 2:
                    pe.wait_ge(*V.at(f"x2_{i - 2}"))
                for j in range(4):
                    for b in (0, 1):
                        last = nc.tensor.matmul(big[S * b:S * b + S, i % 2, P * j:P * j + P], z[:, 8 * i + 2 * j + b, 1:S + 1],
                                                wfrom[:, :], start=True, stop=True)
                last.then_inc(PE.did(f"from{i}"), 1)
            ln_tensor(c, pe, V, A, PE, tp, n3)
            pe.wait_ge(*V.at("ff_T2"))
            pe.wait_ge(*A.at("ff_T3"))
            with pe.Fori(0, 4) as i:
                for k in range(4):
                    pe.wait_ge(*(A.at(f"g{k - 2}", i) if k >= 2 else A.before(f"g{k + 2}", i)))
                    nc.tensor.matmul(tp[k % 2], w1[:, P * k:P * k + P], hT[:, bass.ds(512 * i, 512)], start=True, stop=True)\
                        .then_inc(PE.did(f"h{k}"), 1)
                pe.wait_ge(*A.at("g3", i))
                pe.wait_ge(*V.before("x", i))
                for j in range(4):
                    for k in range(4):
                        last = nc.tensor.matmul(big[:, 0, P * j:P * j + P], g[:, k, P * j:P * j + P], w2[:, k, :],
                                                start=(k == 0), stop=(k == 3))
                last.then_inc(PE.did("out"), 1)

        @block.vector
        def _(dve):
            dve.wait_ge(loaded, 176)
            nc.vector.tensor_scalar(b2s[:, :], b2[:, :], 0.1, None, ALU.mult).then_inc(V.did("b2s"), 1)
            nc.vector.memset(z[:, :, 0:1], 0.0).then_inc(V.did("z0"), 1)
            nc.vector.memset(rot[:, :], 0.0).then_inc(V.did("rot"), 1)
            dve.wait_ge(*A.at("half"))
            nc.vector.tensor_tensor(half2[:, :], half[:, :], half[:, :], ALU.mult).then_inc(V.did("half2"), 1)
            dve.wait_ge(*V.at("half2"))
            nc.vector.tensor_scalar(cosine[:, :], half2[:, :], -2.0, 1.0, ALU.mult, ALU.add).then_inc(V.did("cosine"), 1)
            nc.vector.tensor_tensor(part[:, 0:1], sine[:, :], halves[:, 1:2], ALU.mult).then_inc(V.did("part0"), 1)
            nc.vector.tensor_tensor(part[:, 1:2], sine[:, :], halves[:, 0:1], ALU.mult).then_inc(V.did("part1"), 1)
            dve.wait_ge(*V.at("part1"))
            nc.vector.scalar_tensor_tensor(out=factor[:, 0:1], in0=cosine[:, :], scalar=halves[:, 0:1], in1=part[:, 0:1],
                                           op0=ALU.mult, op1=ALU.subtract).then_inc(V.did("factor0"), 1)
            nc.vector.scalar_tensor_tensor(out=factor[:, 1:2], in0=cosine[:, :], scalar=halves[:, 1:2], in1=part[:, 1:2],
                                           op0=ALU.mult, op1=ALU.add).then_inc(V.did("factor1"), 1)
            dve.wait_ge(*V.at("factor1"))
            for i in (0, 1):
                nc.vector.tensor_scalar(rot[:, 32 * i:32 * i + 32], freq[:, :], factor[:, i:i + 1], None, ALU.mult)\
                    .then_inc(V.did(f"rot{i}"), 1)
            dve.wait_ge(*V.at("rot1"))
            nc.vector.tensor_scalar(rot_u[:, :], rot[:, :], 0.1, None, ALU.mult).then_inc(V.did("rot_u"), 1)
            nc.vector.tensor_scalar(rot_z[:, :], rot[:, :], decay[:, 0:1], None, ALU.mult).then_inc(V.did("rot_z"), 1)
            ln_vector(c, dve, V, A, PE, tp, n1)
            dve.wait_ge(*V.at("ln_xn"))
            ln_vector(c, dve, V, A, PE, tp, n2)
            for i in (0, 2):
                dve.wait_ge(*PE.at(f"u{i}"))
                nc.vector.tensor_copy(uT[:, 512 * i:512 * i + 512], big[0:F2, 0, :]).then_inc(V.did(f"u{i}"), 1)
            with dve.Fori(0, S // 2) as k:
                for u in (0, 1):
                    t = 2 * k + u
                    dve.wait_ge(*PE.at("step", t))
                    nc.vector.tensor_scalar(z[:, :, bass.ds(t + 1, 1)], step[0:F2, u, 0:B].unsqueeze(2), 10.0, -10.0,
                                            ALU.min, ALU.max).then_inc(V.did("clip"), 1)
            for i in range(4):
                dve.wait_ge(*PE.at(f"from{i}"))
                nc.vector.scalar_tensor_tensor(out=x2[:, 4 * i:4 * i + 4, :].rearrange("p i d -> p (i d)"), in0=big[:, i % 2, :],
                                               scalar=0.1, in1=c.xn[:, 4 * i:4 * i + 4, :].rearrange("p i d -> p (i d)"),
                                               op0=ALU.mult, op1=ALU.add).then_inc(V.did(f"x2_{i}"), 1)
            dve.wait_ge(*V.at("x2_3"))
            ln_vector(c, dve, V, A, PE, tp, n3)
            nc.vector.tensor_tensor(x2b[:, :, :], x2[:, :, :], b2s[:, :].unsqueeze(1).broadcast_to([P, NT, D]), ALU.add)\
                .then_inc(V.did("x2b"), 1)
            dve.wait_ge(*V.at("x2b"))
            nc.vector.tensor_tensor(c.x[:, :, :], c.x[:, :, :], x2b[:, :, :], ALU.add).then_inc(V.did("xb"), 1)
            dve.wait_ge(*V.at("xb"))
            with dve.Fori(0, 4) as i:
                dve.wait_ge(*PE.at("out", i))
                xs = c.x[:, bass.ds(4 * i, 4), :].rearrange("p i d -> p (i d)")
                nc.vector.scalar_tensor_tensor(out=xs, in0=big[:, 0, :], scalar=0.1, in1=xs, op0=ALU.mult, op1=ALU.add)\
                    .then_inc(V.did("x"), 1)

        @block.scalar
        def _(act):
            act.wait_ge(loaded, 176)
            nc.scalar.activation(omega[:, :], raw[:, 1:2], ACT.Tanh).then_inc(A.did("omega"), 1)
            nc.scalar.activation(decay[:, :], raw[:, 0:1], ACT.Sigmoid).then_inc(A.did("decay"), 1)
            act.wait_ge(*A.at("omega"))
            nc.scalar.activation(sine[:, :], omega[:, :], ACT.Sin, scale=0.1).then_inc(A.did("sine"), 1)
            nc.scalar.activation(half[:, :], omega[:, :], ACT.Sin, scale=0.05).then_inc(A.did("half"), 1)
            ln_scalar(c, act, V, A, PE, tp, n1)
            ln_scalar(c, act, V, A, PE, tp, n2)
            for i in (1, 3):
                act.wait_ge(*PE.at(f"u{i}"))
                nc.scalar.copy(uT[:, 512 * i:512 * i + 512], big[0:F2, 1, :]).then_inc(A.did(f"u{i}"), 1)
            ln_scalar(c, act, V, A, PE, tp, n3)
            with act.Fori(0, 4) as i:
                act.wait_ge(*PE.before("out", i))
                for k in range(4):
                    act.wait_ge(*PE.at(f"h{k}", i))
                    nc.scalar.activation(g[:, k, :], tp[k % 2], ACT.Gelu, bias=b1[:, k:k + 1]).then_inc(A.did(f"g{k}"), 1)


def capacity_experts(c, name):
    E, CAP, F = 16, TOK // 16, 512
    FC = F // P
    with Stage(c, name) as s:
        nc, a = c.nc, c.a
        wg = s.sb("wg", [P, E])
        earlier, ones = s.sb("earlier", [P, P]), s.sb("ones", [P, P])
        iota = s.sb("iota", [P, NT, E])
        lg, ex = s.sb("logits", [P, NT, E]), s.sb("exps", [P, NT, E])
        mx, total, gate = s.sb("mx", [P, NT]), s.sb("total", [P, NT]), s.sb("gate", [P, NT])
        top = s.sb("top", [P, NT, 8])
        topi = s.sb("topi", [P, NT, 8], U32)
        best = s.sb("best", [P, NT])
        hot = s.sb("hot", [P, NT, E])
        sums = s.sb("sums", [P, 2, NT, E])
        place, mine = s.sb("place", [P, NT, E]), s.sb("mine", [P, NT, E])
        loc, valid = s.sb("loc", [P, NT]), s.sb("valid", [P, NT])
        base, near, far = s.sb("base", [P, NT]), s.sb("near", [P, NT]), s.sb("far", [P, NT])
        to, frm = s.sb("to", [P, NT], U32), s.sb("frm", [P, NT], U32)
        weight = s.sb("weight", [P, NT])
        zero = s.sb("zero", [P, E, D])
        slots = s.sb("slots", [P, E, D])
        slotsT = s.sb("slotsT", [P, E * P])
        w1, w2 = s.sb("w1", [P, 2, F]), s.sb("w2", [P, 2, FC, D])
        hT = s.sb("hT", [P, 2, FC, P])
        done = s.sb("done", [P, E, D])
        got = s.sb("got", [P, NT, D])
        turn = s.ps("turn", [P, 2, 512])
        small = s.ps("small", [P, 2, 512])
        ph = s.ps("h", [P, 2, 512])
        po = s.ps("o", [P, 2, 512])
        loaded, zeroed, sent, read = s.sem("loaded"), s.sem("zeroed"), s.sem("sent"), s.sem("read")
        w_in = [s.sem("w_in0"), s.sem("w_in1")]
        stored, fetched = s.sem("stored"), s.sem("fetched")
        scans = [1, 2, 4, 8]
        V = Steps(s.sem("vector_steps"),
                  (1, ["zero", "ones"] + LN_V + ["logits", "mx", "less", "total", "gate"] + [f"top{i}" for i in range(NT)] +
                   [f"topi{i}" for i in range(NT)] + ["best", "hot", "sums"] +
                   [f"{w}{k}" for k in scans for w in ("head", "tail")] + ["place0", "place", "mine", "loc", "valid", "base", "near",
                    "far1", "far", "to", "near1", "near2", "frm", "weight", "sT0", "sT2"]),
                  (E, ["out"], 2), (1, ["weighted", "x"]))
        A = Steps(s.sem("scalar_steps"), (1, LN_A + ["exp", "sT1", "sT3"]), (E, ["relu"], 2))
        PE = Steps(s.sem("tensor_steps"), (1, LN_P + ["logits", "counts"] + [f"sT{i}" for i in range(4)]),
                   (E, ["h", "out"], 2))
        tp = [turn[:, i, :] for i in (0, 1)]
        e16 = lambda m: m.rearrange("p (t e) -> p t e", e=E)
        wide = lambda m: m[:, :].unsqueeze(2).broadcast_to([P, NT, E])
        dispatched, results = a["scratch_in"], a["scratch_out"]
        block = s.block()

        @block.sync
        def _(sp):
            sp.dma_start(wg[:, :], a[f"{name}_Wg"]).then_inc(loaded, 16)
            sp.dma_start(earlier[:, :], a["c_earlier"]).then_inc(loaded, 16)
            sp.dma_start(iota[:, :, :], a["c_sixteen"]).then_inc(loaded, 16)
            sp.wait_ge(*V.at("zero"))
            sp.dma_start(dispatched.rearrange("(e p) d -> p e d", p=P), zero[:, :, :]).then_inc(zeroed, 16)
            sp.wait_ge(sent, 16 * NT)
            sp.dma_start(slots[:, :, :], dispatched.rearrange("(e p) d -> p e d", p=P)).then_inc(read, 16)

            def load(e, u):
                sp.dma_start(w1[:, u, :], a[f"{name}_w1"][bass.ds(e, 1), :, :].rearrange("a d f -> (a d) f"))\
                    .then_inc(w_in[u], 16)
                sp.dma_start(w2[:, u, :, :], a[f"{name}_w2"][bass.ds(e, 1), :, :].rearrange("a (c p) d -> p (a c) d", p=P))\
                    .then_inc(w_in[u], 16)

            load(0, 0)
            load(1, 1)
            with sp.Fori(1, E // 2) as e2:
                for u in (0, 1):
                    sp.wait_ge(*PE.at("out", 2 * e2 + u - 2))
                    load(2 * e2 + u, u)
            sp.wait_ge(*V.at("out", E - 1))
            sp.dma_start(results.rearrange("(e p) d -> p e d", p=P), done[:, :, :]).then_inc(stored, 16)

        @block.gpsimd
        def _(pool):
            pool.wait_ge(*V.at("to"))
            pool.wait_ge(zeroed, 16)
            for t in range(NT):
                nc.gpsimd.indirect_dma_start(dispatched, bass.IndirectOffsetOnAxis(ap=to[:, t:t + 1], axis=0), c.xn[:, t, :], None,
                                             bounds_check=TOK - 1, oob_is_err=False).then_inc(sent, 16)
            pool.wait_ge(*V.at("frm"))
            pool.wait_ge(stored, 16)
            for t in range(NT):
                nc.gpsimd.indirect_dma_start(got[:, t, :], None, results, bass.IndirectOffsetOnAxis(ap=frm[:, t:t + 1], axis=0),
                                             bounds_check=TOK - 1, oob_is_err=False).then_inc(fetched, 16)

        @block.tensor
        def _(pe):
            ln_tensor(c, pe, V, A, PE, tp)
            pe.wait_ge(*V.at("ln_T2"))
            pe.wait_ge(*A.at("ln_T3"))
            pe.wait_ge(loaded, 48)
            for t in range(NT):
                last = nc.tensor.matmul(small[:, 0, E * t:E * t + E], c.xnT[:, P * t:P * t + P], wg[:, :], start=True, stop=True)
            last.then_inc(PE.did("logits"), 1)
            pe.wait_ge(*V.at("hot"))
            hots = hot[:, :, :].rearrange("p t e -> p (t e)")
            nc.tensor.matmul(small[:, 1, 0:NT * E], earlier[:, :], hots, start=True, stop=True)
            nc.tensor.matmul(small[:, 1, NT * E:2 * NT * E], ones[:, :], hots, start=True, stop=True)\
                .then_inc(PE.did("counts"), 1)
            pe.wait_ge(read, 16)
            for i in range(4):
                if i >= 2:
                    pe.wait_ge(*(A if i % 2 else V).at(f"sT{i - 2}"))
                for j in range(4):
                    last = nc.tensor.transpose(tp[i % 2][:, P * j:P * j + P], slots[:, 4 * i + j, :], c.ident[:, :])
                last.then_inc(PE.did(f"sT{i}"), 1)
            pe.wait_ge(*V.at("sT2"))
            pe.wait_ge(*A.at("sT3"))
            with pe.Fori(0, E // 2) as e2:
                for u in (0, 1):
                    e = 2 * e2 + u
                    pe.wait_ge(w_in[u], 32 * e2 + 32)
                    for k in range(FC):
                        last = nc.tensor.matmul(ph[:, u, P * k:P * k + P], w1[:, u, P * k:P * k + P], slotsT[:, bass.ds(P * e, P)],
                                                start=True, stop=True)
                    last.then_inc(PE.did("h"), 1)
                    pe.wait_ge(*V.before("out", e, 2))
                    pe.wait_ge(*A.at("relu", e))
                    for k in range(FC):
                        last = nc.tensor.matmul(po[:, u, 0:P], hT[:, u, k, :], w2[:, u, k, :], start=(k == 0), stop=(k == FC - 1))
                    last.then_inc(PE.did("out"), 1)

        @block.vector
        def _(dve):
            nc.vector.memset(zero[:, :, :], 0.0).then_inc(V.did("zero"), 1)
            nc.vector.memset(ones[:, :], 1.0).then_inc(V.did("ones"), 1)
            ln_vector(c, dve, V, A, PE, tp)
            dve.wait_ge(*PE.at("logits"))
            nc.vector.tensor_copy(lg[:, :, :], e16(small[:, 0, 0:NT * E])).then_inc(V.did("logits"), 1)
            dve.wait_ge(*V.at("logits"))
            nc.vector.tensor_reduce(mx[:, :], lg[:, :, :], AX.X, ALU.max).then_inc(V.did("mx"), 1)
            dve.wait_ge(*V.at("mx"))
            nc.vector.tensor_tensor(ex[:, :, :], lg[:, :, :], wide(mx), ALU.subtract).then_inc(V.did("less"), 1)
            dve.wait_ge(*A.at("exp"))
            nc.vector.tensor_reduce(total[:, :], ex[:, :, :], AX.X, ALU.add).then_inc(V.did("total"), 1)
            dve.wait_ge(*V.at("total"))
            nc.vector.reciprocal(gate[:, :], total[:, :]).then_inc(V.did("gate"), 1)
            for t in range(NT):
                nc.vector.max(top[:, t, :], lg[:, t, :]).then_inc(V.did(f"top{t}"), 1)
            dve.wait_ge(*V.at(f"top{NT - 1}"))
            for t in range(NT):
                nc.vector.max_index(topi[:, t, :], top[:, t, :], lg[:, t, :]).then_inc(V.did(f"topi{t}"), 1)
            dve.wait_ge(*V.at(f"topi{NT - 1}"))
            nc.vector.tensor_copy(best[:, :].unsqueeze(2), topi[:, :, 0:1]).then_inc(V.did("best"), 1)
            dve.wait_ge(*V.at("best"))
            dve.wait_ge(loaded, 48)
            nc.vector.tensor_tensor(hot[:, :, :], iota[:, :, :], wide(best), ALU.is_equal).then_inc(V.did("hot"), 1)
            dve.wait_ge(*PE.at("counts"))
            nc.vector.tensor_copy(sums[:, 0, :, :], e16(small[:, 1, NT * E:2 * NT * E])).then_inc(V.did("sums"), 1)
            prev = "sums"
            for n, k in enumerate(scans):
                src, dst = sums[:, n % 2, :, :], sums[:, (n + 1) % 2, :, :]
                dve.wait_ge(*V.at(prev))
                nc.vector.tensor_copy(dst[:, 0:k, :], src[:, 0:k, :]).then_inc(V.did(f"head{k}"), 1)
                nc.vector.tensor_tensor(dst[:, k:NT, :], src[:, k:NT, :], src[:, 0:NT - k, :], ALU.add)\
                    .then_inc(V.did(f"tail{k}"), 1)
                prev = f"tail{k}"
            dve.wait_ge(*V.at(prev))
            nc.vector.tensor_copy(place[:, 0:1, :], e16(small[:, 1, 0:NT * E])[:, 0:1, :]).then_inc(V.did("place0"), 1)
            nc.vector.tensor_tensor(place[:, 1:NT, :], e16(small[:, 1, 0:NT * E])[:, 1:NT, :], sums[:, 0, 0:NT - 1, :], ALU.add)\
                .then_inc(V.did("place"), 1)
            dve.wait_ge(*V.at("place"))
            nc.vector.tensor_tensor(mine[:, :, :], place[:, :, :], hot[:, :, :], ALU.mult).then_inc(V.did("mine"), 1)
            dve.wait_ge(*V.at("mine"))
            nc.vector.tensor_reduce(loc[:, :], mine[:, :, :], AX.X, ALU.add).then_inc(V.did("loc"), 1)
            dve.wait_ge(*V.at("loc"))
            nc.vector.tensor_scalar(valid[:, :], loc[:, :], float(CAP), None, ALU.is_lt).then_inc(V.did("valid"), 1)
            nc.vector.tensor_scalar(base[:, :], best[:, :], float(CAP), None, ALU.mult).then_inc(V.did("base"), 1)
            dve.wait_ge(*V.at("base"))
            nc.vector.tensor_tensor(near[:, :], base[:, :], loc[:, :], ALU.add).then_inc(V.did("near"), 1)
            nc.vector.tensor_scalar(far[:, :], loc[:, :], float(CAP), float(4 * TOK), ALU.is_ge, ALU.mult).then_inc(V.did("far1"), 1)
            dve.wait_ge(*V.at("far1"))
            nc.vector.tensor_tensor(mx[:, :], far[:, :], near[:, :], ALU.add).then_inc(V.did("far"), 1)
            dve.wait_ge(*V.at("far"))
            nc.vector.tensor_copy(to[:, :], mx[:, :]).then_inc(V.did("to"), 1)
            nc.vector.tensor_scalar(loc[:, :], loc[:, :], float(CAP - 1), None, ALU.min).then_inc(V.did("near1"), 1)
            dve.wait_ge(*V.at("near1"))
            nc.vector.tensor_tensor(total[:, :], base[:, :], loc[:, :], ALU.add).then_inc(V.did("near2"), 1)
            dve.wait_ge(*V.at("near2"))
            nc.vector.tensor_copy(frm[:, :], total[:, :]).then_inc(V.did("frm"), 1)
            nc.vector.tensor_tensor(weight[:, :], gate[:, :], valid[:, :], ALU.mult).then_inc(V.did("weight"), 1)
            for i in (0, 2):
                dve.wait_ge(*PE.at(f"sT{i}"))
                nc.vector.tensor_copy(slotsT[:, 512 * i:512 * i + 512], tp[0]).then_inc(V.did(f"sT{i}"), 1)
            with dve.Fori(0, E // 2) as e2:
                for u in (0, 1):
                    e = 2 * e2 + u
                    dve.wait_ge(*PE.at("out", e))
                    nc.vector.tensor_copy(done[:, bass.ds(e, 1), :], po[:, u, 0:P].unsqueeze(1)).then_inc(V.did("out"), 1)
            dve.wait_ge(fetched, 16 * NT)
            nc.vector.tensor_tensor(got[:, :, :], got[:, :, :], weight[:, :].unsqueeze(2).broadcast_to([P, NT, D]), ALU.mult)\
                .then_inc(V.did("weighted"), 1)
            dve.wait_ge(*V.at("weighted"))
            nc.vector.tensor_tensor(c.x[:, :, :], c.x[:, :, :], got[:, :, :], ALU.add).then_inc(V.did("x"), 1)

        @block.scalar
        def _(act):
            ln_scalar(c, act, V, A, PE, tp)
            act.wait_ge(*V.at("less"))
            nc.scalar.activation(ex[:, :, :], ex[:, :, :], ACT.Exp).then_inc(A.did("exp"), 1)
            for i in (1, 3):
                act.wait_ge(*PE.at(f"sT{i}"))
                nc.scalar.copy(slotsT[:, 512 * i:512 * i + 512], tp[1]).then_inc(A.did(f"sT{i}"), 1)
            with act.Fori(0, E // 2) as e2:
                for u in (0, 1):
                    e = 2 * e2 + u
                    act.wait_ge(*PE.at("h", e))
                    nc.scalar.activation(hT[:, u, :, :].rearrange("p c k -> p (c k)"), ph[:, u, :], ACT.Relu)\
                        .then_inc(A.did("relu"), 1)


def routed_experts(c, name):
    E, F = 8, 512
    FC = F // P
    with Stage(c, name) as s:
        nc, a = c.nc, c.a
        emb, emb2 = s.sb("emb", [P, E]), s.sb("emb2", [P, E])
        bonus = s.sb("bonus", [P, E])
        ones = s.sb("ones", [P, P])
        iota = s.sb("iota", [P, NT, E])
        sim, score = s.sb("sim", [P, NT, E]), s.sb("score", [P, NT, E])
        tn, te = s.sb("tn", [P, NT]), s.sb("te", [P, E])
        rt, re = s.sb("rt", [P, NT]), s.sb("re", [P, E])
        top, topi = s.sb("top", [P, NT, 8]), s.sb("topi", [P, NT, 8], U32)
        last_i, hit = s.sb("last_i", [P, NT]), s.sb("hit", [P, NT, E])
        best, besti = s.sb("best", [P, NT, 8]), s.sb("besti", [P, NT, 8], U32)
        bi = s.sb("bi", [P, NT, 2])
        gap, ex, den = s.sb("gap", [P, NT]), s.sb("ex", [P, NT]), s.sb("den", [P, NT])
        wt = s.sb("wt", [P, NT, 2])
        hit1, hit2 = s.sb("hit1", [P, NT, E]), s.sb("hit2", [P, NT, E])
        part1, part2 = s.sb("part1", [P, NT, E]), s.sb("part2", [P, NT, E])
        weights = s.sb("weights", [P, NT, E])
        weightsT = s.sb("weightsT", [E, TOK])
        b1, b1e = s.sb("b1", [P, E, FC]), s.sb("b1e", [P, 2, FC])
        b2 = s.sb("b2", [E, D])
        w1, w2 = s.sb("w1", [P, 2, F]), s.sb("w2", [P, 2, FC, D])
        g = s.sb("gelu", [P, 2, FC, 512])
        turn = s.ps("turn", [P, 2, 512])
        ph = s.ps("h", [P, 4, 512])
        po = s.ps("o", [P, 2, 512])
        loaded, w_in = s.sem("loaded"), [s.sem("w_in0"), s.sem("w_in1")]
        ROUTE = ["sim", "tn", "tn_eps", "rt", "te", "te_eps", "re", "s1", "s2", "s3"] + [f"top{t}" for t in range(NT)] + \
            [f"topi{t}" for t in range(NT)] + ["last", "hit", "s4"] + [f"best{t}" for t in range(NT)] + \
            [f"besti{t}" for t in range(NT)] + ["bi", "gap", "den", "w1", "w2", "hit1", "hit2", "part1", "part2", "weights"]
        V = Steps(s.sem("vector_steps"), (1, ["ones", "bonus"] + LN_V + ["emb2"] + ROUTE + ["wT0", "wT2"] +
                                          [f"b2_{i}" for i in range(4)]), (E, [f"x{i}" for i in range(4)], 2))
        A = Steps(s.sem("scalar_steps"), (1, LN_A + ["sq", "tn", "te", "exp", "wT1", "wT3"]),
                  (E, ["b1e"] + [f"g{i}{k}" for i in range(4) for k in range(FC)], 2))
        PE = Steps(s.sem("tensor_steps"), (1, LN_P + ["sim", "te"] + [f"wT{i}" for i in range(4)] + [f"b2_{i}" for i in range(4)]),
                   (E, sum([[f"h{i}{k}" for k in range(FC)] + [f"out{i}"] for i in range(4)], []), 2))
        tp = [turn[:, i, :] for i in (0, 1)]
        wide = lambda m: m.unsqueeze(2).broadcast_to([P, NT, E])
        each = lambda m: m[:, :].unsqueeze(1).broadcast_to([P, NT, E])
        block = s.block()

        @block.sync
        def _(sp):
            sp.dma_start(emb[:, :], a[f"{name}_embT"]).then_inc(loaded, 16)
            sp.dma_start(te[:, :], a[f"{name}_bonus"].broadcast_to([P, E])).then_inc(loaded, 16)
            sp.dma_start(iota[:, :, :], a["c_eight"]).then_inc(loaded, 16)
            sp.dma_start(b1[:, :, :], a[f"{name}_b1"]).then_inc(loaded, 16)
            sp.dma_start(b2[:, :], a[f"{name}_b2"]).then_inc(loaded, 16)

            def load(e, u):
                sp.dma_start(w1[:, u, :], a[f"{name}_W1"][bass.ds(e, 1), :, :].rearrange("a d f -> (a d) f"))\
                    .then_inc(w_in[u], 16)
                sp.dma_start(w2[:, u, :, :], a[f"{name}_W2"][bass.ds(e, 1), :, :].rearrange("a (c p) d -> p (a c) d", p=P))\
                    .then_inc(w_in[u], 16)

            load(0, 0)
            load(1, 1)
            with sp.Fori(1, E // 2) as e2:
                for u in (0, 1):
                    sp.wait_ge(*PE.at("out3", 2 * e2 + u - 2))
                    load(2 * e2 + u, u)

        @block.tensor
        def _(pe):
            ln_tensor(c, pe, V, A, PE, tp)
            pe.wait_ge(*V.at("ln_T2"))
            pe.wait_ge(*A.at("ln_T3"))
            pe.wait_ge(loaded, 80)
            for t in range(NT):
                last = nc.tensor.matmul(tp[0][:, E * t:E * t + E], c.xnT[:, P * t:P * t + P], emb[:, :], start=True, stop=True)
            last.then_inc(PE.did("sim"), 1)
            pe.wait_ge(*V.at("emb2"))
            nc.tensor.matmul(tp[1][:, 0:E], ones[:, :], emb2[:, :], start=True, stop=True).then_inc(PE.did("te"), 1)
            pe.wait_ge(*V.at("weights"))
            for i in range(4):
                if i >= 2:
                    pe.wait_ge(*(A if i % 2 else V).at(f"wT{i - 2}"))
                for j in range(4):
                    last = nc.tensor.transpose(tp[i % 2][0:E, P * j:P * j + P], weights[:, 4 * i + j, :], c.ident[:, :])
                last.then_inc(PE.did(f"wT{i}"), 1)
            pe.wait_ge(*V.at("wT2"))
            pe.wait_ge(*A.at("wT3"))
            for i in range(4):
                if i >= 2:
                    pe.wait_ge(*V.at(f"b2_{i - 2}"))
                for j in range(4):
                    t = 4 * i + j
                    last = nc.tensor.matmul(po[:, i % 2, P * j:P * j + P], weightsT[:, P * t:P * t + P], b2[:, :],
                                            start=True, stop=True)
                last.then_inc(PE.did(f"b2_{i}"), 1)
            with pe.Fori(0, E // 2) as e2:
                for u in (0, 1):
                    e = 2 * e2 + u
                    pe.wait_ge(w_in[u], 32 * e2 + 32)
                    for i in range(4):
                        for k in range(FC):
                            if i or u:
                                pe.wait_ge(*A.at(f"g{i - 1}{k}" if i else f"g3{k}", e if i else e - 1))
                            else:
                                pe.wait_ge(*A.before(f"g3{k}", e))
                            nc.tensor.matmul(ph[:, k, :], w1[:, u, P * k:P * k + P], c.xnT[:, 512 * i:512 * i + 512],
                                             start=True, stop=True).then_inc(PE.did(f"h{i}{k}"), 1)
                        pe.wait_ge(*A.at(f"g{i}{FC - 1}", e))
                        pe.wait_ge(*(V.at(f"x{i - 2}", e) if i >= 2 else V.before(f"x{i + 2}", e)))
                        for j in range(4):
                            for k in range(FC):
                                last = nc.tensor.matmul(po[:, i % 2, P * j:P * j + P], g[:, i % 2, k, P * j:P * j + P],
                                                        w2[:, u, k, :], start=(k == 0), stop=(k == FC - 1))
                        last.then_inc(PE.did(f"out{i}"), 1)

        @block.vector
        def _(dve):
            nc.vector.memset(ones[:, :], 1.0).then_inc(V.did("ones"), 1)
            dve.wait_ge(loaded, 80)
            nc.vector.tensor_scalar(bonus[:, :], te[:, :], 0.1, None, ALU.mult).then_inc(V.did("bonus"), 1)
            ln_vector(c, dve, V, A, PE, tp)
            nc.vector.tensor_tensor(emb2[:, :], emb[:, :], emb[:, :], ALU.mult).then_inc(V.did("emb2"), 1)
            dve.wait_ge(*PE.at("sim"))
            nc.vector.tensor_copy(sim[:, :, :], tp[0][:, 0:NT * E].rearrange("p (t e) -> p t e", e=E)).then_inc(V.did("sim"), 1)
            dve.wait_ge(*A.at("sq"))
            nc.vector.tensor_reduce(tn[:, :], c.sq[:, :, :], AX.X, ALU.add).then_inc(V.did("tn"), 1)
            dve.wait_ge(*A.at("tn"))
            nc.vector.tensor_scalar(tn[:, :], tn[:, :], 1e-8, None, ALU.add).then_inc(V.did("tn_eps"), 1)
            dve.wait_ge(*V.at("tn_eps"))
            nc.vector.reciprocal(rt[:, :], tn[:, :]).then_inc(V.did("rt"), 1)
            dve.wait_ge(*PE.at("te"))
            nc.vector.tensor_copy(te[:, :], tp[1][:, 0:E]).then_inc(V.did("te"), 1)
            dve.wait_ge(*A.at("te"))
            nc.vector.tensor_scalar(te[:, :], te[:, :], 1e-8, None, ALU.add).then_inc(V.did("te_eps"), 1)
            dve.wait_ge(*V.at("te_eps"))
            nc.vector.reciprocal(re[:, :], te[:, :]).then_inc(V.did("re"), 1)
            dve.wait_ge(*V.at("re"))
            nc.vector.tensor_tensor(score[:, :, :], sim[:, :, :], wide(rt[:, :]), ALU.mult).then_inc(V.did("s1"), 1)
            dve.wait_ge(*V.at("s1"))
            nc.vector.tensor_tensor(score[:, :, :], score[:, :, :], each(re), ALU.mult).then_inc(V.did("s2"), 1)
            dve.wait_ge(*V.at("s2"))
            nc.vector.tensor_tensor(score[:, :, :], score[:, :, :], each(bonus), ALU.add).then_inc(V.did("s3"), 1)
            for t in range(NT):
                nc.vector.max(top[:, t, :], sim[:, t, :]).then_inc(V.did(f"top{t}"), 1)
            dve.wait_ge(*V.at(f"top{NT - 1}"))
            for t in range(NT):
                nc.vector.max_index(topi[:, t, :], top[:, t, :], sim[:, t, :]).then_inc(V.did(f"topi{t}"), 1)
            dve.wait_ge(*V.at(f"topi{NT - 1}"))
            nc.vector.tensor_copy(last_i[:, :].unsqueeze(2), topi[:, :, 7:8]).then_inc(V.did("last"), 1)
            dve.wait_ge(*V.at("last"))
            nc.vector.tensor_tensor(hit[:, :, :], iota[:, :, :], wide(last_i[:, :]), ALU.is_equal).then_inc(V.did("hit"), 1)
            dve.wait_ge(*V.at("hit"))
            nc.vector.scalar_tensor_tensor(out=score[:, :, :], in0=hit[:, :, :], scalar=OUT, in1=score[:, :, :],
                                           op0=ALU.mult, op1=ALU.add).then_inc(V.did("s4"), 1)
            dve.wait_ge(*V.at("s4"))
            for t in range(NT):
                nc.vector.max(best[:, t, :], score[:, t, :]).then_inc(V.did(f"best{t}"), 1)
            dve.wait_ge(*V.at(f"best{NT - 1}"))
            for t in range(NT):
                nc.vector.max_index(besti[:, t, :], best[:, t, :], score[:, t, :]).then_inc(V.did(f"besti{t}"), 1)
            dve.wait_ge(*V.at(f"besti{NT - 1}"))
            nc.vector.tensor_copy(bi[:, :, :], besti[:, :, 0:2]).then_inc(V.did("bi"), 1)
            nc.vector.tensor_tensor(gap[:, :].unsqueeze(2), best[:, :, 1:2], best[:, :, 0:1], ALU.subtract).then_inc(V.did("gap"), 1)
            dve.wait_ge(*A.at("exp"))
            nc.vector.tensor_scalar(den[:, :], ex[:, :], 1.0, None, ALU.add).then_inc(V.did("den"), 1)
            dve.wait_ge(*V.at("den"))
            nc.vector.reciprocal(wt[:, :, 0:1], den[:, :].unsqueeze(2)).then_inc(V.did("w1"), 1)
            dve.wait_ge(*V.at("w1"))
            nc.vector.tensor_tensor(wt[:, :, 1:2], wt[:, :, 0:1], ex[:, :].unsqueeze(2), ALU.mult).then_inc(V.did("w2"), 1)
            nc.vector.tensor_tensor(hit1[:, :, :], iota[:, :, :], bi[:, :, 0:1].broadcast_to([P, NT, E]), ALU.is_equal)\
                .then_inc(V.did("hit1"), 1)
            nc.vector.tensor_tensor(hit2[:, :, :], iota[:, :, :], bi[:, :, 1:2].broadcast_to([P, NT, E]), ALU.is_equal)\
                .then_inc(V.did("hit2"), 1)
            dve.wait_ge(*V.at("hit2"))
            nc.vector.tensor_tensor(part1[:, :, :], hit1[:, :, :], wt[:, :, 0:1].broadcast_to([P, NT, E]), ALU.mult)\
                .then_inc(V.did("part1"), 1)
            nc.vector.tensor_tensor(part2[:, :, :], hit2[:, :, :], wt[:, :, 1:2].broadcast_to([P, NT, E]), ALU.mult)\
                .then_inc(V.did("part2"), 1)
            dve.wait_ge(*V.at("part2"))
            nc.vector.tensor_tensor(weights[:, :, :], part1[:, :, :], part2[:, :, :], ALU.add).then_inc(V.did("weights"), 1)
            for i in (0, 2):
                dve.wait_ge(*PE.at(f"wT{i}"))
                nc.vector.tensor_copy(weightsT[:, 512 * i:512 * i + 512], tp[0][0:E, :]).then_inc(V.did(f"wT{i}"), 1)
            for i in range(4):
                dve.wait_ge(*PE.at(f"b2_{i}"))
                xs = c.x[:, 4 * i:4 * i + 4, :].rearrange("p i d -> p (i d)")
                nc.vector.tensor_tensor(xs, po[:, i % 2, :], xs, ALU.add).then_inc(V.did(f"b2_{i}"), 1)
            dve.wait_ge(*V.at("b2_3"))
            with dve.Fori(0, E // 2) as e2:
                for u in (0, 1):
                    e = 2 * e2 + u
                    for i in range(4):
                        dve.wait_ge(*V.before(f"x{i}", e))
                        dve.wait_ge(*PE.at(f"out{i}", e))
                        for j in range(4):
                            xs = c.x[:, 4 * i + j, :]
                            last = nc.vector.scalar_tensor_tensor(out=xs, in0=po[:, i % 2, P * j:P * j + P],
                                                                  scalar=weights[:, 4 * i + j, bass.ds(e, 1)], in1=xs,
                                                                  op0=ALU.mult, op1=ALU.add)
                        last.then_inc(V.did(f"x{i}"), 1)

        @block.scalar
        def _(act):
            ln_scalar(c, act, V, A, PE, tp)
            act.wait_ge(*V.at("ln_xn"))
            nc.scalar.activation(c.sq[:, :, :], c.xn[:, :, :], ACT.Square).then_inc(A.did("sq"), 1)
            act.wait_ge(*V.at("tn"))
            nc.scalar.activation(tn[:, :], tn[:, :], ACT.Sqrt).then_inc(A.did("tn"), 1)
            act.wait_ge(*V.at("te"))
            nc.scalar.activation(te[:, :], te[:, :], ACT.Sqrt).then_inc(A.did("te"), 1)
            act.wait_ge(*V.at("gap"))
            nc.scalar.activation(ex[:, :], gap[:, :], ACT.Exp).then_inc(A.did("exp"), 1)
            for i in (1, 3):
                act.wait_ge(*PE.at(f"wT{i}"))
                nc.scalar.copy(weightsT[:, 512 * i:512 * i + 512], tp[1][0:E, :]).then_inc(A.did(f"wT{i}"), 1)
            with act.Fori(0, E // 2) as e2:
                for u in (0, 1):
                    e = 2 * e2 + u
                    act.wait_ge(*A.before("g33", e))
                    nc.scalar.copy(b1e[:, u, :], b1[:, bass.ds(e, 1), :].rearrange("p a k -> p (a k)")).then_inc(A.did("b1e"), 1)
                    act.wait_ge(*A.at("b1e", e))
                    for i in range(4):
                        for k in range(FC):
                            if k == 0:
                                act.wait_ge(*(PE.at(f"out{i - 2}", e) if i >= 2 else PE.before(f"out{i + 2}", e)))
                            act.wait_ge(*PE.at(f"h{i}{k}", e))
                            nc.scalar.activation(g[:, i % 2, k, :], ph[:, k, :], ACT.Gelu, bias=b1e[:, u, k:k + 1]).then_inc(A.did(f"g{i}{k}"), 1)


def selective_scan_layer(c, name):
    N, R, HALF = 16, 64, 2
    DT_MIN, DT_MAX = 0.001, 0.1
    with Stage(c, name) as s:
        nc, a = c.nc, c.a
        cols = s.sb("cols", [P, 2])
        win = s.sb("win", [P, 4 * D])
        taps, cb = s.sb("taps", [P, HALF, 4]), s.sb("cb", [P, HALF])
        wx, wdt = s.sb("wx", [P, HALF, R + 2 * N]), s.sb("wdt", [R, HALF * P])
        bdt, dp = s.sb("bdt", [P, HALF]), s.sb("dp", [P, HALF])
        la, na = s.sb("la", [P, HALF, N]), s.sb("na", [P, HALF, N])
        wo = s.sb("wo", [P, HALF, D])
        zeros = s.sb("zeros", [P, P])
        hT = s.sb("hT", [P, TOK])
        xi = s.sb("xi", [P, HALF, TOK])
        zs = s.sb("zs", [P, HALF, TOK])
        cv = s.sb("u", [P, HALF, TOK])
        dt = s.sb("dt", [P, HALF, TOK])
        xbc = s.sb("xbc", [R + 2 * N, TOK])
        bb, cc = s.sb("bb", [P, 2, TOK]), s.sb("cc", [P, 2, TOK])
        da, db = s.sb("da", [P, HALF, TOK]), s.sb("db", [P, HALF, TOK])
        ps = s.ps("all", [P, 8, 512])
        loaded, stored = s.sem("loaded"), s.sem("stored")
        b_in, c_in = [s.sem("b_in0"), s.sem("b_in1")], [s.sem("c_in0"), s.sem("c_in1")]
        n1 = Norm(c, turned=False)
        n2 = Norm(c, "in", c.xn, xi[:, 0, :].rearrange("p (t d) -> p t d", d=D), hT, cols[:, 0:1], cols[:, 1:2])
        quads = [(hf, i) for hf in range(HALF) for i in range(4)]
        V = Steps(s.sem("vector_steps"),
                  (1, ["zeros", "na", "da0"] + n1.V + n2.V + [f"xi{n}" for n in range(8)] +
                   [f"cv{hf}{k}" for hf in range(HALF) for k in (3, 2, 1, 0)] + ["xbc0", "xbc2"] +
                   [f"pre{n}" for n in range(8)] + ["low", "dt", "dtu"]),
                  (N, ["db0", "scan0", "db1", "scan1"], 2), (1, ["skip0", "gate0", "skip1", "gate1", "res"] + [f"x{i}" for i in range(4)]))
        A = Steps(s.sem("scalar_steps"),
                  (1, ["la"] + n1.A + n2.A + [f"z{n}" for n in range(8)] + ["u0", "u1", "xbc1", "xbc3", "e", "ln"]),
                  (N, ["da0", "da1"], 2))
        G = Steps(s.sem("gpsimd_steps"), (N, ["hc0", "hc1"], 2))
        PE = Steps(s.sem("tensor_steps"),
                   (1, n2.P + [f"in{n}" for n in range(16)] + [f"xbc{i}" for i in range(4)] + [f"dt{n}" for n in range(8)]),
                   (N, ["y0", "y1"], 2), (1, ["ysum"] + [f"out{i}" for i in range(4)]))
        tp = [ps[:, 6 + i, :] for i in (0, 1)]
        seq = lambda m: m.rearrange("p (b q) -> p b q", q=S)
        block = s.block()

        @block.sync
        def _(sp):
            for dst, src in ((cols[:, :], a[f"{name}_cols"]), (win[:, :], a[f"{name}_W_inT"]),
                             (taps[:, :, :], a[f"{name}_conv_w"].rearrange("(h p) k -> p h k", p=P)),
                             (wx[:, :, :], a[f"{name}_W_xT"].rearrange("(h p) n -> p h n", p=P)),
                             (wdt[:, :], a[f"{name}_W_dtT"]), (la[:, :, :], a[f"{name}_log_A"].rearrange("(h p) n -> p h n", p=P)),
                             (wo[:, :, :], a[f"{name}_W_outT"].rearrange("(h p) n -> p h n", p=P)),
                             (cb[:, :], a[f"{name}_vecs"][0]), (bdt[:, :], a[f"{name}_vecs"][1]), (dp[:, :], a[f"{name}_vecs"][2])):
                sp.dma_start(dst, src).then_inc(loaded, 16)
            sp.wait_ge(*V.at("xbc2"))
            sp.wait_ge(*A.at("xbc3"))
            sp.dma_start(a["scratch_rows"], xbc[R:R + 2 * N, :]).then_inc(stored, 16)
            sp.wait_ge(stored, 16)

            def load(n, u):
                sp.dma_start(bb[:, u, :], a["scratch_rows"][bass.ds(n, 1), :].broadcast_to([P, TOK])).then_inc(b_in[u], 16)
                sp.dma_start(cc[:, u, :], a["scratch_rows"][bass.ds(n + N, 1), :].broadcast_to([P, TOK])).then_inc(c_in[u], 16)

            load(0, 0)
            load(1, 1)
            with sp.Fori(1, N // 2) as n2_:
                for u in (0, 1):
                    sp.wait_ge(*G.at("hc1", 2 * n2_ + u - 2))
                    load(2 * n2_ + u, u)

        @block.tensor
        def _(pe):
            ln_tensor(c, pe, V, A, PE, tp, n2)
            pe.wait_ge(*V.at("in_T2"))
            pe.wait_ge(*A.at("in_T3"))
            pe.wait_ge(loaded, 160)
            order = [(blk, i) for pair in (0, 1) for i in range(4) for blk in (pair, 2 + pair)]
            for n, (blk, i) in enumerate(order):
                if n >= 4:
                    pe.wait_ge(*(V.at(f"xi{(n - 4) // 2}") if blk < 2 else A.at(f"z{(n - 4) // 2}")))
                nc.tensor.matmul(ps[:, (0 if blk < 2 else 2) + i % 2, :], win[:, P * blk:P * blk + P], hT[:, 512 * i:512 * i + 512],
                                 start=True, stop=True).then_inc(PE.did(f"in{n}"), 1)
            pe.wait_ge(*A.at("u1"))
            for i in range(4):
                if i >= 2:
                    pe.wait_ge(*(A if i % 2 else V).at(f"xbc{i - 2}"))
                for hf in range(HALF):
                    last = nc.tensor.matmul(ps[0:R + 2 * N, 4 + i % 2, :], wx[:, hf, :], cv[:, hf, 512 * i:512 * i + 512],
                                            start=(hf == 0), stop=(hf == 1))
                last.then_inc(PE.did(f"xbc{i}"), 1)
            pe.wait_ge(*V.at("xbc2"))
            pe.wait_ge(*A.at("xbc3"))
            for n, (hf, i) in enumerate(quads):
                if n >= 4:
                    pe.wait_ge(*V.at(f"pre{n - 4}"))
                nc.tensor.matmul(ps[:, n % 4, :], wdt[:, P * hf:P * hf + P], xbc[0:R, 512 * i:512 * i + 512],
                                 start=True, stop=True).then_inc(PE.did(f"dt{n}"), 1)
            pe.wait_ge(*V.at("dt"))
            for b in range(8):
                nc.tensor.matmul(ps[:, b, :], zeros[:, :], hT[:, 0:512], start=True, stop=False, skip_group_check=True)
            with pe.Fori(0, N // 2) as n2_:
                for u in (0, 1):
                    n = 2 * n2_ + u
                    for hf in range(HALF):
                        pe.wait_ge(*G.at(f"hc{hf}", n))
                        for i in range(4):
                            last = nc.tensor.matmul(ps[:, 4 * hf + i, :], c.ident[:, :], db[:, hf, 512 * i:512 * i + 512],
                                                    start=False, stop=False, skip_group_check=True)
                        last.then_inc(PE.did(f"y{hf}"), 1)
            for b in range(8):
                last = nc.tensor.matmul(ps[:, b, :], zeros[:, :], hT[:, 0:512], start=False, stop=True, skip_group_check=True)
            last.then_inc(PE.did("ysum"), 1)
            pe.wait_ge(*V.at("gate1"))
            for i in range(4):
                for j in range(4):
                    t = 4 * i + j
                    for hf in range(HALF):
                        last = nc.tensor.matmul(ps[:, i, P * j:P * j + P], xi[:, hf, P * t:P * t + P], wo[:, hf, :],
                                                start=(hf == 0), stop=(hf == 1))
                last.then_inc(PE.did(f"out{i}"), 1)

        @block.gpsimd
        def _(pool):
            with pool.Fori(0, N // 2) as n2_:
                for u in (0, 1):
                    n = 2 * n2_ + u
                    pool.wait_ge(c_in[u], 16 * n2_ + 16)
                    for hf in range(HALF):
                        pool.wait_ge(*V.at(f"scan{hf}", n))
                        nc.gpsimd.tensor_tensor(db[:, hf, :], db[:, hf, :], cc[:, u, :], ALU.mult).then_inc(G.did(f"hc{hf}"), 1)

        @block.vector
        def _(dve):
            nc.vector.memset(zeros[:, :], 0.0).then_inc(V.did("zeros"), 1)
            dve.wait_ge(*A.at("la"))
            nc.vector.tensor_scalar(na[:, :, :], la[:, :, :], -1.0, None, ALU.mult).then_inc(V.did("na"), 1)
            nc.vector.memset(da[:, :, :], 0.0).then_inc(V.did("da0"), 1)
            ln_vector(c, dve, V, A, PE, tp, n1)
            dve.wait_ge(*V.at("ln_xn"))
            ln_vector(c, dve, V, A, PE, tp, n2)
            order = [(hf, i) for hf in (0, 1) for i in range(4)]
            for n, (hf, i) in enumerate(order):
                dve.wait_ge(*PE.at(f"in{2 * n}"))
                nc.vector.tensor_copy(xi[:, hf, 512 * i:512 * i + 512], ps[:, i % 2, :]).then_inc(V.did(f"xi{n}"), 1)
            dve.wait_ge(*V.at("xi7"))
            for hf in range(HALF):
                x3, u3 = seq(xi[:, hf, :]), seq(cv[:, hf, :])
                nc.vector.tensor_scalar(cv[:, hf, :], xi[:, hf, :], taps[:, hf, 3:4], cb[:, hf:hf + 1], ALU.mult, ALU.add)\
                    .then_inc(V.did(f"cv{hf}3"), 1)
                for k in (2, 1, 0):
                    m = 3 - k
                    dve.wait_ge(*V.at(f"cv{hf}{k + 1}"))
                    nc.vector.scalar_tensor_tensor(out=u3[:, :, m:S], in0=x3[:, :, 0:S - m], scalar=taps[:, hf, k:k + 1],
                                                   in1=u3[:, :, m:S], op0=ALU.mult, op1=ALU.add).then_inc(V.did(f"cv{hf}{k}"), 1)
            for i in (0, 2):
                dve.wait_ge(*PE.at(f"xbc{i}"))
                nc.vector.tensor_copy(xbc[:, 512 * i:512 * i + 512], ps[0:R + 2 * N, 4, :]).then_inc(V.did(f"xbc{i}"), 1)
            for n, (hf, i) in enumerate(quads):
                dve.wait_ge(*PE.at(f"dt{n}"))
                nc.vector.tensor_scalar(dt[:, hf, 512 * i:512 * i + 512], ps[:, n % 4, :], bdt[:, hf:hf + 1], 0.0, ALU.add, ALU.min)\
                    .then_inc(V.did(f"pre{n}"), 1)
            dve.wait_ge(*A.at("ln"))
            nc.vector.tensor_scalar(dt[:, :, :], dt[:, :, :], DT_MIN, DT_MIN, ALU.add, ALU.max).then_inc(V.did("low"), 1)
            dve.wait_ge(*V.at("low"))
            nc.vector.tensor_scalar(dt[:, :, :], dt[:, :, :], DT_MAX, None, ALU.min).then_inc(V.did("dt"), 1)
            dve.wait_ge(*V.at("dt"))
            nc.vector.tensor_tensor(xi[:, :, :], dt[:, :, :], cv[:, :, :], ALU.mult).then_inc(V.did("dtu"), 1)
            with dve.Fori(0, N // 2) as n2_:
                for u in (0, 1):
                    n = 2 * n2_ + u
                    dve.wait_ge(b_in[u], 16 * n2_ + 16)
                    for hf in range(HALF):
                        dve.wait_ge(*PE.before(f"y{hf}", n))
                        dve.wait_ge(*V.before("scan1", n))
                        nc.vector.tensor_tensor(db[:, hf, :], xi[:, hf, :], bb[:, u, :], ALU.mult).then_inc(V.did(f"db{hf}"), 1)
                        dve.wait_ge(*V.at(f"db{hf}", n))
                        dve.wait_ge(*A.at(f"da{hf}", n))
                        nc.vector.tensor_tensor_scan(db[:, hf, :], da[:, hf, :], db[:, hf, :], 0.0, ALU.mult, ALU.add)\
                            .then_inc(V.did(f"scan{hf}"), 1)
            for hf in range(HALF):
                dve.wait_ge(*PE.at("ysum"))
                nc.vector.scalar_tensor_tensor(out=db[:, hf, :], in0=cv[:, hf, :], scalar=dp[:, hf:hf + 1],
                                               in1=ps[:, 4 * hf:4 * hf + 4, :].rearrange("p i n -> p (i n)"),
                                               op0=ALU.mult, op1=ALU.add).then_inc(V.did(f"skip{hf}"), 1)
                dve.wait_ge(*V.at(f"skip{hf}"))
                nc.vector.tensor_tensor(xi[:, hf, :], db[:, hf, :], zs[:, hf, :], ALU.mult).then_inc(V.did(f"gate{hf}"), 1)
            nc.vector.tensor_tensor(c.x[:, :, :], c.x[:, :, :], c.xn[:, :, :], ALU.add).then_inc(V.did("res"), 1)
            dve.wait_ge(*V.at("res"))
            for i in range(4):
                dve.wait_ge(*PE.at(f"out{i}"))
                xs = c.x[:, 4 * i:4 * i + 4, :].rearrange("p i d -> p (i d)")
                nc.vector.tensor_tensor(xs, ps[:, i, :], xs, ALU.add).then_inc(V.did(f"x{i}"), 1)

        @block.scalar
        def _(act):
            act.wait_ge(loaded, 160)
            nc.scalar.activation(la[:, :, :], la[:, :, :], ACT.Exp).then_inc(A.did("la"), 1)
            ln_scalar(c, act, V, A, PE, tp, n1)
            ln_scalar(c, act, V, A, PE, tp, n2)
            for n, (hf, i) in enumerate(quads):
                act.wait_ge(*PE.at(f"in{2 * n + 1}"))
                nc.scalar.activation(zs[:, hf, 512 * i:512 * i + 512], ps[:, 2 + i % 2, :], ACT.Silu).then_inc(A.did(f"z{n}"), 1)
            for hf in range(HALF):
                act.wait_ge(*V.at(f"cv{hf}0"))
                nc.scalar.activation(cv[:, hf, :], cv[:, hf, :], ACT.Silu).then_inc(A.did(f"u{hf}"), 1)
            for i in (1, 3):
                act.wait_ge(*PE.at(f"xbc{i}"))
                nc.scalar.copy(xbc[:, 512 * i:512 * i + 512], ps[0:R + 2 * N, 5, :]).then_inc(A.did(f"xbc{i}"), 1)
            act.wait_ge(*V.at("pre7"))
            nc.scalar.activation(dt[:, :, :], dt[:, :, :], ACT.Exp).then_inc(A.did("e"), 1)
            act.wait_ge(*A.at("e"))
            nc.scalar.activation(dt[:, :, :], dt[:, :, :], ACT.Ln, bias=1.0).then_inc(A.did("ln"), 1)
            act.wait_ge(*V.at("dt"))
            with act.Fori(0, N // 2) as n2_:
                for u in (0, 1):
                    n = 2 * n2_ + u
                    for hf in range(HALF):
                        act.wait_ge(*V.before(f"scan{hf}", n))
                        nc.scalar.activation(seq(da[:, hf, :])[:, :, 1:S], seq(dt[:, hf, :])[:, :, 1:S], ACT.Exp,
                                             scale=na[:, hf, bass.ds(n, 1)]).then_inc(A.did(f"da{hf}"), 1)


def chosen_adapters(c, name):
    E, HID, R = 8, 32, 64
    with Stage(c, name) as s:
        nc, a = c.nc, c.a
        wd1, bd1 = s.sb("wd1", [P, 2 * P]), s.sb("bd1", [P, 2])
        wd2, bd2 = s.sb("wd2", [P, 2, D]), s.sb("bd2", [P, E])
        wad, bad = s.sb("wad", [P, 4 * P]), s.sb("bad", [P, 4])
        wau, bau = s.sb("wau", [P, 4, D]), s.sb("bau", [E, D])
        wb, bb = s.sb("wb", [P, D]), s.sb("bb", [P, D])
        rank, diag = s.sb("rank", [P, E, B]), s.sb("diag", [E, E])
        ones = s.sb("ones", [P, P])
        hid = s.sb("hid", [P, 2, 512])
        diff, sq = s.sb("diff", [P, 2, 512]), s.sb("sq", [P, 2, 512])
        loss = s.sb("loss", [P, E, B])
        full = s.sb("full", [P, E, B])
        least, vote, most = s.sb("least", [P, B]), s.sb("vote", [P, E, B]), s.sb("most", [P, B])
        hot = s.sb("hot", [P, E, B])
        mask = s.sb("mask", [P, 4, B])
        own, hot8 = s.sb("own", [E, E, B]), s.sb("hot8", [E, B])
        xg, hg = s.sb("xg", [P, 512]), s.sb("hg", [E, 512])
        ad, adm = s.sb("ad", [P, 4, 512]), s.sb("adm", [P, 4, 512])
        turn = s.ps("turn", [P, 2, 512])
        ps = s.ps("ps", [P, 6, 512])
        loaded = s.sem("loaded")
        V = Steps(s.sem("vector_steps"), (1, LN_V + ["ones", "bb"]),
                  (4, sum([[f"diff{e}", f"loss{e}"] for e in range(E)], [])),
                  (1, ["full", "least", "vote", "votes", "most", "hot", "mask0", "mask1", "own", "hot8"]),
                  (4, ["hg"] + [f"adm{k}" for k in range(4)] + ["x"]))
        A = Steps(s.sem("scalar_steps"), (1, LN_A), (4, ["hid0", "hid1"] + [f"sq{e}" for e in range(E)]),
                  (4, ["xg"] + [f"ad{k}" for k in range(4)]))
        PE = Steps(s.sem("tensor_steps"), (1, LN_P), (4, ["hid0", "hid1"] + [f"rec{e}" for e in range(E)]),
                   (1, ["full"]), (4, [f"ad{k}" for k in range(4)] + ["out"]))
        tp = [turn[:, i, :] for i in (0, 1)]
        seq = lambda m: m.rearrange("p (b q) -> p b q", q=S)
        block = s.block()

        @block.sync
        def _(sp):
            for dst, src in ((wd1, "wd1"), (bd1, "bd1"), (bd2, "bd2"), (wad, "wad"), (bad, "bad"), (bau, "bau"), (wb, "wb")):
                sp.dma_start(dst[:, :], a[f"{name}_{src}"]).then_inc(loaded, 16)
            sp.dma_start(wd2[:, :, :], a[f"{name}_wd2"].rearrange("(c p) d -> p c d", p=P)).then_inc(loaded, 16)
            sp.dma_start(wau[:, :, :], a[f"{name}_wau"].rearrange("(c p) d -> p c d", p=P)).then_inc(loaded, 16)
            sp.dma_start(bb[:, :], a[f"{name}_bb"].broadcast_to([P, D])).then_inc(loaded, 16)
            sp.dma_start(rank[:, :, :], a["c_rank"]).then_inc(loaded, 16)
            sp.dma_start(diag[:, :], a["c_ident"][0:E, 0:E]).then_inc(loaded, 16)

        @block.tensor
        def _(pe):
            ln_tensor(c, pe, V, A, PE, tp)
            pe.wait_ge(*V.at("ln_T2"))
            pe.wait_ge(*A.at("ln_T3"))
            pe.wait_ge(loaded, 192)
            with pe.Fori(0, 4) as i:
                pe.wait_ge(*A.before("sq7", i))
                for k in (0, 1):
                    nc.tensor.matmul(ps[:, k, :], wd1[:, P * k:P * k + P], c.xnT[:, bass.ds(512 * i, 512)], start=True, stop=True)\
                        .then_inc(PE.did(f"hid{k}"), 1)
                for e in range(E):
                    if e % 4 == 0:
                        pe.wait_ge(*A.at(f"hid{e // 4}", i))
                    pe.wait_ge(*(V.at(f"diff{e - 4}", i) if e >= 4 else V.before(f"diff{e + 4}", i)))
                    lo = HID * (e % 4)
                    nc.tensor.matmul(ps[:, 2 + e % 4, :], wd2[lo:lo + HID, e // 4, :], hid[lo:lo + HID, e // 4, :],
                                     start=True, stop=True, tile_position=(lo, 0)).then_inc(PE.did(f"rec{e}"), 1)
            pe.wait_ge(*V.at("loss7", 3))
            nc.tensor.matmul(ps[:, 0, 0:E * B], ones[:, :], loss[:, :, :].rearrange("p e b -> p (e b)"), start=True, stop=True)\
                .then_inc(PE.did("full"), 1)
            pe.wait_ge(*V.at("hot8"))
            with pe.Fori(0, 4) as i:
                for k in range(4):
                    pe.wait_ge(*A.before(f"ad{k}", i))
                    nc.tensor.matmul(ps[:, k, :], wad[:, P * k:P * k + P], c.xnT[:, bass.ds(512 * i, 512)], start=True, stop=True)\
                        .then_inc(PE.did(f"ad{k}"), 1)
                pe.wait_ge(*A.at("xg", i))
                pe.wait_ge(*V.at("adm3", i))
                for j in range(4):
                    part = slice(P * j, P * j + P)
                    nc.tensor.matmul(ps[:, 4, part], xg[:, part], wb[:, :], start=True, stop=False)
                    for k in range(4):
                        nc.tensor.matmul(ps[:, 4, part], adm[:, k, part], wau[:, k, :], start=False, stop=False)
                    last = nc.tensor.matmul(ps[:, 4, part], hg[:, part], bau[:, :], start=False, stop=True)
                last.then_inc(PE.did("out"), 1)

        @block.vector
        def _(dve):
            ln_vector(c, dve, V, A, PE, tp)
            dve.wait_ge(loaded, 192)
            nc.vector.memset(ones[:, :], 1.0).then_inc(V.did("ones"), 1)
            nc.vector.tensor_tensor(c.x[:, :, :], c.x[:, :, :], bb[:, :].unsqueeze(1).broadcast_to([P, NT, D]), ALU.add)\
                .then_inc(V.did("bb"), 1)
            dve.wait_ge(*A.at("ln_T3"))
            dve.wait_ge(*V.at("ln_T2"))
            with dve.Fori(0, 4) as i:
                for e in range(E):
                    dve.wait_ge(*(A.at(f"sq{e - 2}", i) if e >= 2 else A.before(f"sq{e + 6}", i)))
                    dve.wait_ge(*PE.at(f"rec{e}", i))
                    nc.vector.scalar_tensor_tensor(out=diff[:, e % 2, :], in0=ps[:, 2 + e % 4, :], scalar=bd2[:, e:e + 1],
                                                   in1=c.xnT[:, bass.ds(512 * i, 512)], op0=ALU.add, op1=ALU.subtract)\
                        .then_inc(V.did(f"diff{e}"), 1)
                    dve.wait_ge(*A.at(f"sq{e}", i))
                    nc.vector.tensor_reduce(loss[:, e, bass.ds(8 * i, 8)], seq(sq[:, e % 2, :]), AX.X, ALU.add)\
                        .then_inc(V.did(f"loss{e}"), 1)
            dve.wait_ge(*PE.at("full"))
            nc.vector.tensor_copy(full[:, :, :], ps[:, 0, 0:E * B].rearrange("p (e b) -> p e b", e=E)).then_inc(V.did("full"), 1)
            dve.wait_ge(*V.at("full"))
            nc.vector.tensor_reduce(least[:, :], full[:, :, :].rearrange("p e b -> p b e"), AX.X, ALU.min).then_inc(V.did("least"), 1)
            dve.wait_ge(*V.at("least"))
            nc.vector.tensor_tensor(vote[:, :, :], full[:, :, :], least[:, :].unsqueeze(1).broadcast_to([P, E, B]), ALU.is_equal)\
                .then_inc(V.did("vote"), 1)
            dve.wait_ge(*V.at("vote"))
            nc.vector.tensor_tensor(vote[:, :, :], vote[:, :, :], rank[:, :, :], ALU.mult).then_inc(V.did("votes"), 1)
            dve.wait_ge(*V.at("votes"))
            nc.vector.tensor_reduce(most[:, :], vote[:, :, :].rearrange("p e b -> p b e"), AX.X, ALU.max).then_inc(V.did("most"), 1)
            dve.wait_ge(*V.at("most"))
            nc.vector.tensor_tensor(hot[:, :, :], vote[:, :, :], most[:, :].unsqueeze(1).broadcast_to([P, E, B]), ALU.is_equal)\
                .then_inc(V.did("hot"), 1)
            dve.wait_ge(*V.at("hot"))
            pairs = hot[:, :, :].rearrange("p (k e) b -> p k e b", e=2)
            for e in (0, 1):
                nc.vector.tensor_copy(mask[R * e:R * e + R, :, :], pairs[R * e:R * e + R, :, e, :]).then_inc(V.did(f"mask{e}"), 1)
            nc.vector.tensor_tensor(own[:, :, :], hot[0:E, :, :], diag[:, :].unsqueeze(2).broadcast_to([E, E, B]), ALU.mult)\
                .then_inc(V.did("own"), 1)
            dve.wait_ge(*V.at("own"))
            nc.vector.tensor_reduce(hot8[:, :], own[:, :, :].rearrange("p e b -> p b e"), AX.X, ALU.add).then_inc(V.did("hot8"), 1)
            dve.wait_ge(*V.at("hot8"))
            with dve.Fori(0, 4) as i:
                dve.wait_ge(*V.before("x", i))
                nc.vector.tensor_copy(seq(hg[:, :]), hot8[:, bass.ds(8 * i, 8)].unsqueeze(2).broadcast_to([E, 8, S]))\
                    .then_inc(V.did("hg"), 1)
                for k in range(4):
                    dve.wait_ge(*A.at(f"ad{k}", i))
                    nc.vector.tensor_tensor(seq(adm[:, k, :]), seq(ad[:, k, :]),
                                            mask[:, k, bass.ds(8 * i, 8)].unsqueeze(2).broadcast_to([P, 8, S]), ALU.mult)\
                        .then_inc(V.did(f"adm{k}"), 1)
                dve.wait_ge(*PE.at("out", i))
                xs = c.x[:, bass.ds(4 * i, 4), :].rearrange("p i d -> p (i d)")
                nc.vector.tensor_tensor(xs, ps[:, 4, :], xs, ALU.add).then_inc(V.did("x"), 1)

        @block.scalar
        def _(act):
            ln_scalar(c, act, V, A, PE, tp)
            act.wait_ge(loaded, 192)
            with act.Fori(0, 4) as i:
                act.wait_ge(*V.before("loss7", i))
                for k in (0, 1):
                    act.wait_ge(*PE.at(f"hid{k}", i))
                    nc.scalar.activation(hid[:, k, :], ps[:, k, :], ACT.Relu, bias=bd1[:, k:k + 1]).then_inc(A.did(f"hid{k}"), 1)
                for e in range(E):
                    if e >= 2:
                        act.wait_ge(*V.at(f"loss{e - 2}", i))
                    act.wait_ge(*V.at(f"diff{e}", i))
                    nc.scalar.activation(sq[:, e % 2, :], diff[:, e % 2, :], ACT.Square).then_inc(A.did(f"sq{e}"), 1)
            with act.Fori(0, 4) as i:
                act.wait_ge(*V.before("x", i))
                nc.scalar.copy(xg[:, :], c.xnT[:, bass.ds(512 * i, 512)]).then_inc(A.did("xg"), 1)
                for k in range(4):
                    act.wait_ge(*PE.at(f"ad{k}", i))
                    nc.scalar.activation(ad[:, k, :], ps[:, k, :], ACT.Relu, bias=bad[:, k:k + 1]).then_inc(A.did(f"ad{k}"), 1)


BLK = 16
Q_V = ["amax", "scale", "rscale", "y", "a7", "a6", "a5", "b4", "b3", "b2", "b1", "q", "signed", "out"]
Q_A = ["abs", "sign"]


class Quant:

    def __init__(self, s, tag, n):
        self.n = n
        self.scale, self.rscale = s.sb(f"{tag}_scale", [P, n]), s.sb(f"{tag}_rscale", [P, n])
        self.y, self.ay, self.sign = (s.sb(f"{tag}_{k}", [P, n * BLK]) for k in ("y", "ay", "sign"))
        self.a, self.b = s.sb(f"{tag}_a", [P, n * BLK]), s.sb(f"{tag}_b", [P, n * BLK])


def quant_vector(c, dve, q, V, A, tag, t, src, dst):
    nc = c.nc
    blocks = lambda m: m.rearrange("p (n k) -> p n k", k=BLK)
    wide = lambda m: m[:, :].unsqueeze(2).broadcast_to([P, q.n, BLK])
    step = lambda n: (V.did(f"{tag}_{n}"), 1)

    def then(n):
        dve.wait_ge(*V.at(f"{tag}_{n}", t))

    nc.vector.tensor_reduce(q.scale[:, :], blocks(src), AX.X, ALU.max, apply_absolute_value=True).then_inc(*step("amax"))
    then("amax")
    nc.vector.tensor_scalar(q.scale[:, :], q.scale[:, :], 1.0 / 6.0, 1e-12, ALU.mult, ALU.max).then_inc(*step("scale"))
    then("scale")
    nc.vector.reciprocal(q.rscale[:, :], q.scale[:, :]).then_inc(*step("rscale"))
    then("rscale")
    nc.vector.tensor_tensor(blocks(q.y[:, :]), blocks(src), wide(q.rscale), ALU.mult).then_inc(*step("y"))
    dve.wait_ge(*A.at(f"{tag}_abs", t))
    nc.vector.tensor_scalar(q.a[:, :], q.ay[:, :], 5.0, 2.0, ALU.is_gt, ALU.mult).then_inc(*step("a7"))
    then("a7")
    nc.vector.scalar_tensor_tensor(out=q.a[:, :], in0=q.ay[:, :], scalar=3.5, in1=q.a[:, :], op0=ALU.is_gt, op1=ALU.add)\
        .then_inc(*step("a6"))
    then("a6")
    nc.vector.scalar_tensor_tensor(out=q.a[:, :], in0=q.ay[:, :], scalar=2.5, in1=q.a[:, :], op0=ALU.is_gt, op1=ALU.add)\
        .then_inc(*step("a5"))
    nc.vector.tensor_scalar(q.b[:, :], q.ay[:, :], 1.75, None, ALU.is_gt).then_inc(*step("b4"))
    for n, middle in (("b3", 1.25), ("b2", 0.75), ("b1", 0.25)):
        then(f"b{int(n[1]) + 1}")
        nc.vector.scalar_tensor_tensor(out=q.b[:, :], in0=q.ay[:, :], scalar=middle, in1=q.b[:, :], op0=ALU.is_gt,
                                       op1=ALU.add).then_inc(*step(n))
    then("b1")
    nc.vector.scalar_tensor_tensor(out=q.a[:, :], in0=q.b[:, :], scalar=0.5, in1=q.a[:, :], op0=ALU.mult, op1=ALU.add)\
        .then_inc(*step("q"))
    then("q")
    dve.wait_ge(*A.at(f"{tag}_sign", t))
    nc.vector.tensor_tensor(q.a[:, :], q.a[:, :], q.sign[:, :], ALU.mult).then_inc(*step("signed"))
    then("signed")
    nc.vector.tensor_tensor(blocks(dst), blocks(q.a[:, :]), wide(q.scale), ALU.mult).then_inc(*step("out"))


def quant_scalar(c, act, q, V, A, tag, t):
    nc = c.nc
    act.wait_ge(*V.at(f"{tag}_y", t))
    nc.scalar.activation(q.ay[:, :], q.y[:, :], ACT.Abs).then_inc(A.did(f"{tag}_abs"), 1)
    nc.scalar.activation(q.sign[:, :], q.y[:, :], ACT.Sign).then_inc(A.did(f"{tag}_sign"), 1)


def quantised_ffn(c, name):
    I = 352
    IC = -(-I // P)
    IP = IC * P
    rest = I - (IC - 1) * P
    wide_ = [P, P, rest]
    with Stage(c, name) as s:
        nc, a = c.nc, c.a
        w = s.sb("w", [P, 2 * IP + I])
        wguT = s.sb("wguT", [P, 2, IP])
        wdT = s.sb("wdT", [P, IC, D])
        xq = s.sb("xq", [P, NT, D])
        xqT = s.sb("xqT", [P, TOK])
        qw, qx, qh = Quant(s, "qw", (2 * IP + I) // BLK), Quant(s, "qx", TOK // BLK), Quant(s, "qh", 4 * I // BLK)
        xg = s.sb("xg", [P, 512])
        gate = s.sb("gate", [P, 4, I])
        hh, hq = s.sb("hh", [P, 4, I]), s.sb("hq", [P, 4, I])
        hT = s.sb("hT", [P, IC, 512])
        ps = s.ps("all", [P, 8, 512])
        loaded = s.sem("loaded")
        V = Steps(s.sem("vector_steps"), (1, named("w", Q_V) + ["wgT", "wdT"] + Norm(c, turned=False).V + named("x", Q_V) + ["xT0", "xT2"]),
                  (4, [f"h{j}" for j in range(4)] + named("h", Q_V) + ["hT0", "hT2", "x"]))
        A = Steps(s.sem("scalar_steps"), (1, named("w", Q_A) + ["wuT"] + Norm(c, turned=False).A + named("x", Q_A) + ["xT1", "xT3"]),
                  (4, ["xg"] + [f"silu{j}" for j in range(4)] + named("h", Q_A) + ["hT1"]))
        PE = Steps(s.sem("tensor_steps"), (1, ["wgT", "wuT", "wdT"] + [f"xT{i}" for i in range(4)]),
                   (4, [f"gu{j}" for j in range(4)] + [f"hT{k}" for k in range(IC)] + ["out"]))
        n1 = Norm(c, turned=False)
        flat = lambda m: m[:, :, :].rearrange("p i k -> p (i k)")
        block = s.block()

        @block.sync
        def _(sp):
            sp.dma_start(w[:, :], a[f"{name}_w"]).then_inc(loaded, 16)

        @block.tensor
        def _(pe):
            pe.wait_ge(*V.at("w_out"))
            for m, n in ((0, "wgT"), (1, "wuT")):
                for k in range(IC):
                    last = nc.tensor.transpose(ps[:, m, P * k:P * k + P], w[:, IP * m + P * k:IP * m + P * k + P], c.ident[:, :])
                last.then_inc(PE.did(n), 1)
            for k in range(IC):
                last = nc.tensor.transpose(ps[0:wide_[k], 2, P * k:P * k + P], w[:, 2 * IP + P * k:2 * IP + P * k + wide_[k]],
                                           c.ident[:, :])
            last.then_inc(PE.did("wdT"), 1)
            pe.wait_ge(*V.at("x_out"))
            for i in range(4):
                if i >= 2:
                    pe.wait_ge(*(A if i % 2 else V).at(f"xT{i - 2}"))
                for j in range(4):
                    last = nc.tensor.transpose(ps[:, 6 + i % 2, P * j:P * j + P], xq[:, 4 * i + j, :], c.ident[:, :])
                last.then_inc(PE.did(f"xT{i}"), 1)
            with pe.Fori(0, 4) as i:
                pe.wait_ge(*A.at("xg", i))
                for j in range(4):
                    if j >= 2:
                        pe.wait_ge(*V.at(f"h{j - 2}", i))
                    for m in (0, 1):
                        last = nc.tensor.matmul(ps[:, 2 * m + j % 2, 0:I], xg[:, P * j:P * j + P], wguT[:, m, 0:I],
                                                start=True, stop=True)
                    last.then_inc(PE.did(f"gu{j}"), 1)
                pe.wait_ge(*V.at("h_out", i))
                for k in range(IC):
                    for j in range(4):
                        last = nc.tensor.transpose(ps[0:wide_[k], 4 + k, P * j:P * j + P], hq[:, j, P * k:P * k + wide_[k]],
                                                   c.ident[:, :])
                    last.then_inc(PE.did(f"hT{k}"), 1)
                pe.wait_ge(*A.at("hT1", i))
                pe.wait_ge(*V.at("hT2", i))
                for j in range(4):
                    for k in range(IC):
                        last = nc.tensor.matmul(ps[:, 7, P * j:P * j + P], hT[0:wide_[k], k, P * j:P * j + P],
                                                wdT[0:wide_[k], k, :], start=(k == 0), stop=(k == IC - 1))
                last.then_inc(PE.did("out"), 1)

        @block.vector
        def _(dve):
            dve.wait_ge(loaded, 16)
            quant_vector(c, dve, qw, V, A, "w", 0, w[:, :], w[:, :])
            dve.wait_ge(*PE.at("wgT"))
            nc.vector.tensor_copy(wguT[:, 0, :], ps[:, 0, 0:IP]).then_inc(V.did("wgT"), 1)
            dve.wait_ge(*PE.at("wdT"))
            nc.vector.tensor_copy(wdT[:, 0:2, :].rearrange("p k d -> p (k d)"), ps[:, 2, 0:2 * P])
            nc.vector.tensor_copy(wdT[0:rest, 2, :], ps[0:rest, 2, 2 * P:3 * P]).then_inc(V.did("wdT"), 1)
            ln_vector(c, dve, V, A, PE, None, n1)
            dve.wait_ge(*V.at("ln_xn"))
            quant_vector(c, dve, qx, V, A, "x", 0, flat(c.xn), flat(xq))
            for i in (0, 2):
                dve.wait_ge(*PE.at(f"xT{i}"))
                nc.vector.tensor_copy(xqT[:, 512 * i:512 * i + 512], ps[:, 6, :]).then_inc(V.did(f"xT{i}"), 1)
            with dve.Fori(0, 4) as i:
                dve.wait_ge(*V.before("x", i))
                for j in range(4):
                    dve.wait_ge(*A.at(f"silu{j}", i))
                    nc.vector.tensor_tensor(hh[:, j, :], gate[:, j, :], ps[:, 2 + j % 2, 0:I], ALU.mult).then_inc(V.did(f"h{j}"), 1)
                dve.wait_ge(*V.at("h3", i))
                quant_vector(c, dve, qh, V, A, "h", i, flat(hh), flat(hq))
                for k in (0, 2):
                    dve.wait_ge(*PE.at(f"hT{k}", i))
                    nc.vector.tensor_copy(hT[0:wide_[k], k, :], ps[0:wide_[k], 4 + k, :]).then_inc(V.did(f"hT{k}"), 1)
                dve.wait_ge(*PE.at("out", i))
                xs = c.x[:, bass.ds(4 * i, 4), :].rearrange("p i d -> p (i d)")
                nc.vector.tensor_tensor(xs, ps[:, 7, :], xs, ALU.add).then_inc(V.did("x"), 1)

        @block.scalar
        def _(act):
            quant_scalar(c, act, qw, V, A, "w", 0)
            act.wait_ge(*PE.at("wuT"))
            nc.scalar.copy(wguT[:, 1, :], ps[:, 1, 0:IP]).then_inc(A.did("wuT"), 1)
            ln_scalar(c, act, V, A, PE, None, n1)
            quant_scalar(c, act, qx, V, A, "x", 0)
            for i in (1, 3):
                act.wait_ge(*PE.at(f"xT{i}"))
                nc.scalar.copy(xqT[:, 512 * i:512 * i + 512], ps[:, 7, :]).then_inc(A.did(f"xT{i}"), 1)
            act.wait_ge(*V.at("xT2"))
            act.wait_ge(*A.at("xT3"))
            with act.Fori(0, 4) as i:
                act.wait_ge(*V.before("x", i))
                nc.scalar.copy(xg[:, :], xqT[:, bass.ds(512 * i, 512)]).then_inc(A.did("xg"), 1)
                for j in range(4):
                    act.wait_ge(*PE.at(f"gu{j}", i))
                    nc.scalar.activation(gate[:, j, :], ps[:, j % 2, 0:I], ACT.Silu).then_inc(A.did(f"silu{j}"), 1)
                quant_scalar(c, act, qh, V, A, "h", i)
                act.wait_ge(*PE.at("hT1", i))
                nc.scalar.copy(hT[:, 1, :], ps[:, 5, :]).then_inc(A.did("hT1"), 1)


def many_head_cross_attention(c, name):
    NG = -(-KC // 4)
    wide_ = [min(512, KEYS - 512 * m) for m in range(NG)]
    part = [min(4, KC - 4 * m) for m in range(NG)]
    chunk = [min(P, KEYS - P * j) for j in range(KC)]
    with Stage(c, name) as s:
        nc, a = c.nc, c.a
        wq, wk, wv, wo = (s.sb(n, [P, D]) for n in ("wq", "wk", "wv", "wo"))
        hb, which, delta = s.sb("hb", [P, 4]), s.sb("which", [P, 8, P]), s.sb("delta", [P, S])
        mask, shift = s.sb("mask", [P, KEYS], U8), s.sb("shift", [P, KEYS])
        qT = s.sb("qT", [P, TOK])
        qd = s.sb("qd", [P, 4, S])
        ctx, ctxT = s.sb("ctx", [P, 2, KC, D]), s.sb("ctxT", [P, KEYS])
        kT, v = s.sb("kT", [P, KEYS]), s.sb("v", [P, KC, D])
        sc = s.sb("sc", [P, 2, 4, KEYS])
        tops, top = s.sb("tops", [P, 4, 2, NG]), s.sb("top", [P, 4, 2])
        ntop, rows, rinv = s.sb("ntop", [P, 4, 2]), s.sb("rows", [P, 4, 2]), s.sb("rinv", [P, 8])
        vinv = s.sb("vinv", [P, 8])
        diag = s.sb("diag", [P, 8, S])
        pT = s.sb("pT", [P, 2, KC, P])
        own, sums, yT = s.sb("own", [P, 4, S]), s.sb("sums", [P, S]), s.sb("yT", [P, S])
        ps = s.ps("scores", [P, 4, 512])
        turn = s.ps("turn", [P, 2, 512])
        pv = s.ps("pv", [P, 512])
        misc = s.ps("misc", [P, 512])
        loaded, ctx_in = s.sem("loaded"), [s.sem("ctx_in0"), s.sem("ctx_in1")]
        tiles = [(j, g) for j in (0, 1) for g in range(4)]
        V_OF, A_OF = (0,), (1, 2, 3)
        pTs = lambda who: [f"pT{j}{g}{m}" for j, g in tiles for m in who]
        turns = lambda j, who: [f"pT{j}{g}{m}" for g in range(4) for m in who]
        scored = lambda j: [f"m{j}{m}{g}" for m in range(NG) for g in range(4)] + [f"top{j}", f"ntop{j}"]
        V = Steps(s.sem("vector_steps"), (1, ["shift"] + LN_V + [f"q{i}" for i in range(4)]),
                  (B, ["ctxT0", "ctxT2", "kT0", "kT2", "v0", "v2", "qd"] + scored(0) +
                   sum([[f"m1{m}{g}" for g in range(4)] + [f"pT0{m}{k}" for k in V_OF] for m in range(NG)], []) + ["top1", "ntop1"] +
                   turns(1, V_OF) + ["rinv", "vinv", "diag", "own", "sums", "yT", "x"], 2))
        A = Steps(s.sem("scalar_steps"), (1, LN_A),
                  (B, ["ctxT1", "ctxT3", "kT1", "kT3", "v1", "v3"] +
                   [f"exp0{g}" for g in range(4)] + turns(0, A_OF) + [f"exp1{g}" for g in range(4)] + turns(1, A_OF), 2))
        tpv = lambda j, g: [f"pT{j}{g}{m}" for m in range(NG)] + [f"pv{j}{g}"]
        PE = Steps(s.sem("tensor_steps"), (1, LN_P + [f"q{i}" for i in range(4)]),
                   (B, [f"ctxT{m}" for m in range(NG)] + [f"kT{m}" for m in range(NG)] + [f"v{m}" for m in range(NG)] +
                    [f"s0{m}" for m in range(NG)] + sum([[f"s1{m}"] + tpv(0, m) for m in range(4)], []) +
                    sum([tpv(1, g) for g in range(4)], []) + ["norm", "out"], 2))
        tp = [turn[:, i, :] for i in (0, 1)]
        block = s.block()

        @block.sync
        def _(sp):
            for dst, src in ((wq, "wq"), (wk, "wk"), (wv, "wv"), (wo, "wo")):
                sp.dma_start(dst[:, :], a[f"{name}_{src}"]).then_inc(loaded, 16)
            sp.dma_start(hb[:, :], a["c_heads"]).then_inc(loaded, 16)
            sp.dma_start(which[:, :, :], a["c_which"]).then_inc(loaded, 16)
            sp.dma_start(delta[:, :], a["c_delta"]).then_inc(loaded, 16)
            for h in (0, 1):
                sp.dma_start(mask[S * h:S * h + S, :], a["mask_all"]).then_inc(loaded, 16)

            def load(n, u):
                keys = a["ctx"][bass.ds(n, 1), :, :].rearrange("a k d -> (a k) d")
                sp.dma_start(ctx[:, u, 0:KC - 1, :], keys[0:(KC - 1) * P, :].rearrange("(j p) d -> p j d", p=P))\
                    .then_inc(ctx_in[u], 16)
                sp.dma_start(ctx[0:KREST, u, KC - 1, :], keys[(KC - 1) * P:KEYS, :]).then_inc(ctx_in[u], 16)

            load(0, 0)
            load(1, 1)
            with sp.Fori(1, B // 2) as t:
                for u in (0, 1):
                    sp.wait_ge(*PE.at("ctxT3", 2 * t + u - 2))
                    load(2 * t + u, u)

        @block.tensor
        def _(pe):
            ln_tensor(c, pe, V, A, PE, tp)
            pe.wait_ge(*V.at("ln_T2"))
            pe.wait_ge(*A.at("ln_T3"))
            pe.wait_ge(loaded, 144)
            for i in range(4):
                nc.tensor.matmul(ps[:, i, :], wq[:, :], c.xnT[:, 512 * i:512 * i + 512], start=True, stop=True)\
                    .then_inc(PE.did(f"q{i}"), 1)
            with pe.Fori(0, B // 2) as t:
                for u in (0, 1):
                    n = 2 * t + u

                    def copied(what, m):
                        pe.wait_ge(*(A if m % 2 else V).at(f"{what}{m}", n))

                    pe.wait_ge(ctx_in[u], 32 * t + 32)
                    pe.wait_ge(*V.before("x", n))
                    for m in range(NG):
                        if m >= 2:
                            copied("ctxT", m - 2)
                        for k in range(part[m]):
                            j = 4 * m + k
                            last = nc.tensor.transpose(tp[m % 2][:, P * k:P * k + chunk[j]], ctx[0:chunk[j], u, j, :],
                                                       c.ident[0:chunk[j], 0:chunk[j]])
                        last.then_inc(PE.did(f"ctxT{m}"), 1)
                    for m in range(NG):
                        copied("ctxT", m)
                        nc.tensor.matmul(ps[:, m, 0:wide_[m]], wk[:, :], ctxT[:, 512 * m:512 * m + wide_[m]], start=True, stop=True)\
                            .then_inc(PE.did(f"kT{m}"), 1)
                    for m in range(NG):
                        if m >= 2:
                            copied("v", m - 2)
                        for k in range(part[m]):
                            j = 4 * m + k
                            last = nc.tensor.matmul(tp[m % 2][0:chunk[j], P * k:P * k + P], ctxT[:, P * j:P * j + chunk[j]],
                                                    wv[:, :], start=True, stop=True)
                        last.then_inc(PE.did(f"v{m}"), 1)
                    pe.wait_ge(*V.at("qd", n))
                    copied("kT", NG - 1)

                    def scores(j, m):
                        for g in range(4):
                            if m:
                                pe.wait_ge(*V.at(f"m{j}{m - 1}{g}", n))
                            elif j:
                                pe.wait_ge(*V.at(f"m0{NG - 1}{g}", n))
                            last = nc.tensor.matmul(ps[:, g, 0:wide_[m]],
                                                    qd[32 * g:32 * g + 32, 2 * j:2 * j + 2, :].rearrange("p h q -> p (h q)"),
                                                    kT[32 * g:32 * g + 32, 512 * m:512 * m + wide_[m]], start=True, stop=True,
                                                    tile_position=(32 * g, 0))
                        last.then_inc(PE.did(f"s{j}{m}"), 1)

                    def turn_copied(j, g, m):
                        pe.wait_ge(*(V if m in V_OF else A).at(f"pT{j}{g}{m}", n))

                    def values(j, g):
                        pe.wait_ge(*A.at(f"exp{j}{g}", n))
                        tile = 4 * j + g
                        for m in range(NG):
                            if m >= 2:
                                turn_copied(j, g, m - 2)
                            elif tile:
                                turn_copied(*tiles[tile - 1], m + 2)
                            else:
                                copied("v", m + 2)
                            for k in range(part[m]):
                                i = 4 * m + k
                                last = nc.tensor.transpose(tp[m % 2][0:chunk[i], P * k:P * k + P],
                                                           sc[:, j, g, P * i:P * i + chunk[i]], c.ident[:, :])
                            last.then_inc(PE.did(f"pT{j}{g}{m}"), 1)
                        turn_copied(j, g, NG - 2)
                        turn_copied(j, g, NG - 1)
                        for i in range(KC):
                            last = nc.tensor.matmul(pv[32 * g:32 * g + 32, P * j:P * j + P], v[0:chunk[i], i, 32 * g:32 * g + 32],
                                                    pT[0:chunk[i], g % 2, i, :], start=(i == 0), stop=(i == KC - 1),
                                                    tile_position=(0, 32 * g))
                        last.then_inc(PE.did(f"pv{j}{g}"), 1)

                    for m in range(NG):
                        scores(0, m)
                    for m in range(NG):
                        scores(1, m)
                        values(0, m)
                    for g in range(4):
                        values(1, g)
                    pe.wait_ge(*V.at("diag", n))
                    for r in range(8):
                        last = nc.tensor.matmul(misc[:, 0:S], which[:, r, :], diag[:, r, :], start=(r == 0), stop=(r == 7))
                    last.then_inc(PE.did("norm"), 1)
                    pe.wait_ge(*V.at("yT", n))
                    nc.tensor.matmul(misc[S * u:S * u + S, P:2 * P], yT[:, :], wo[:, :], start=True, stop=True)\
                        .then_inc(PE.did("out"), 1)

        @block.vector
        def _(dve):
            dve.wait_ge(loaded, 144)
            nc.vector.tensor_scalar(shift[:, :], mask[:, :], OUT, None, ALU.mult).then_inc(V.did("shift"), 1)
            ln_vector(c, dve, V, A, PE, tp)
            for i in range(4):
                dve.wait_ge(*PE.at(f"q{i}"))
                nc.vector.tensor_scalar(qT[:, 512 * i:512 * i + 512], ps[:, i, :], DH ** -0.5, None, ALU.mult)\
                    .then_inc(V.did(f"q{i}"), 1)
            dve.wait_ge(*V.at("q3"))
            with dve.Fori(0, B // 2) as t:
                for u in (0, 1):
                    n = 2 * t + u
                    for m in (0, 2):
                        dve.wait_ge(*PE.at(f"ctxT{m}", n))
                        nc.vector.tensor_copy(ctxT[:, 512 * m:512 * m + wide_[m]], tp[0]).then_inc(V.did(f"ctxT{m}"), 1)
                    for m in (0, 2):
                        dve.wait_ge(*PE.at(f"kT{m}", n))
                        nc.vector.tensor_copy(kT[:, 512 * m:512 * m + wide_[m]], ps[:, m, :]).then_inc(V.did(f"kT{m}"), 1)
                    for m in (0, 2):
                        dve.wait_ge(*PE.at(f"v{m}", n))
                        nc.vector.tensor_copy(v[:, 4 * m:4 * m + 4, :].rearrange("p j d -> p (j d)"), tp[0])\
                            .then_inc(V.did(f"v{m}"), 1)
                    nc.vector.tensor_tensor(qd[:, :, :], qT[:, bass.ds(S * n, S)].unsqueeze(1).broadcast_to([P, 4, S]),
                                            hb[:, :].unsqueeze(2).broadcast_to([P, 4, S]), ALU.mult).then_inc(V.did("qd"), 1)

                    def add_mask(j, m):
                        dve.wait_ge(*PE.at(f"s{j}{m}", n))
                        nc.vector.memset(c.pause[:, :], 0.0)
                        for g in range(4):
                            span = slice(512 * m, 512 * m + wide_[m])
                            nc.vector.tensor_tensor_reduce(out=sc[:, j, g, span], in0=ps[:, g, 0:wide_[m]], in1=shift[:, span],
                                                           scale=1.0, scalar=3 * OUT, op0=ALU.add, op1=ALU.max,
                                                           accum_out=tops[:, g, j, m:m + 1]).then_inc(V.did(f"m{j}{m}{g}"), 1)

                    def copy_turn(j, g):
                        for m in V_OF:
                            dve.wait_ge(*PE.at(f"pT{j}{g}{m}", n))
                            nc.vector.tensor_copy(pT[:, g % 2, 4 * m:4 * m + 4, :].rearrange("p j q -> p (j q)"), tp[m % 2])\
                                .then_inc(V.did(f"pT{j}{g}{m}"), 1)

                    def largest(j):
                        dve.wait_ge(*V.at(f"m{j}{NG - 1}3", n))
                        nc.vector.tensor_reduce(top[:, :, j:j + 1].rearrange("p g j -> p (g j)"), tops[:, :, j, :], AX.X, ALU.max)\
                            .then_inc(V.did(f"top{j}"), 1)
                        dve.wait_ge(*V.at(f"top{j}", n))
                        nc.vector.tensor_scalar(ntop[:, :, j:j + 1], top[:, :, j:j + 1], -1.0, None, ALU.mult)\
                            .then_inc(V.did(f"ntop{j}"), 1)

                    for m in range(NG):
                        add_mask(0, m)
                    largest(0)
                    for m in range(NG):
                        add_mask(1, m)
                        copy_turn(0, m)
                    largest(1)
                    for g in range(4):
                        copy_turn(1, g)
                    dve.wait_ge(*A.at("exp13", n))
                    flat = lambda w: w[:, :, :].rearrange("p g j -> p (g j)")
                    nc.vector.reciprocal(rinv[:, :], flat(rows)).then_inc(V.did("rinv"), 1)
                    dve.wait_ge(*V.at("rinv", n))
                    nc.vector.scalar_tensor_tensor(out=vinv[:, :], in0=flat(ntop), scalar=-0.5 * OUT, in1=rinv[:, :],
                                                   op0=ALU.is_lt, op1=ALU.mult).then_inc(V.did("vinv"), 1)
                    dve.wait_ge(*V.at("vinv", n))
                    nc.vector.tensor_tensor(diag[:, :, :], vinv[:, :].unsqueeze(2).broadcast_to([P, 8, S]),
                                            delta[:, :].unsqueeze(1).broadcast_to([P, 8, S]), ALU.mult).then_inc(V.did("diag"), 1)
                    dve.wait_ge(*PE.at("pv13", n))
                    nc.vector.tensor_tensor(own[:, :, :], pv[:, 0:4 * S].rearrange("p (h q) -> p h q", h=4),
                                            hb[:, :].unsqueeze(2).broadcast_to([P, 4, S]), ALU.mult).then_inc(V.did("own"), 1)
                    dve.wait_ge(*V.at("own", n))
                    nc.vector.tensor_reduce(sums[:, :], own[:, :, :].rearrange("p h q -> p q h"), AX.X, ALU.add)\
                        .then_inc(V.did("sums"), 1)
                    dve.wait_ge(*V.at("sums", n))
                    dve.wait_ge(*PE.at("norm", n))
                    nc.vector.tensor_tensor(yT[:, :], sums[:, :], misc[:, 0:S], ALU.mult).then_inc(V.did("yT"), 1)
                    dve.wait_ge(*PE.at("out", n))
                    half = slice(S * u, S * u + S)
                    xs = c.x[half, bass.ds(t, 1), :].rearrange("p a d -> p (a d)")
                    nc.vector.tensor_tensor(xs, misc[half, P:2 * P], xs, ALU.add).then_inc(V.did("x"), 1)

        @block.scalar
        def _(act):
            ln_scalar(c, act, V, A, PE, tp)
            with act.Fori(0, B // 2) as t:
                for u in (0, 1):
                    n = 2 * t + u
                    for m in (1, 3):
                        act.wait_ge(*PE.at(f"ctxT{m}", n))
                        nc.scalar.copy(ctxT[:, 512 * m:512 * m + wide_[m]], tp[1][:, 0:wide_[m]]).then_inc(A.did(f"ctxT{m}"), 1)
                    for m in (1, 3):
                        act.wait_ge(*PE.at(f"kT{m}", n))
                        nc.scalar.copy(kT[:, 512 * m:512 * m + wide_[m]], ps[:, m, 0:wide_[m]]).then_inc(A.did(f"kT{m}"), 1)

                    def put(dst, m, src):
                        k = min(P, KEYS - 512 * m)
                        nc.scalar.copy(dst[0:k, 4 * m:4 * m + part[m], :].rearrange("p j d -> p (j d)"), src[0:k, 0:P * part[m]])\
                            .then_inc(A.did(put.step), 1)

                    for m in (1, 3):
                        act.wait_ge(*PE.at(f"v{m}", n))
                        put.step = f"v{m}"
                        put(v, m, tp[1])

                    def exps(j):
                        act.wait_ge(*V.at(f"ntop{j}", n))
                        for g in range(4):
                            nc.scalar.activation(sc[:, j, g, :], sc[:, j, g, :], ACT.Exp, bias=ntop[:, g, j:j + 1], scale=1.0,
                                                 accum_out=rows[:, g, j:j + 1]).then_inc(A.did(f"exp{j}{g}"), 1)

                    def copy_turn(j, g):
                        for m in A_OF:
                            act.wait_ge(*PE.at(f"pT{j}{g}{m}", n))
                            put.step = f"pT{j}{g}{m}"
                            put(pT[:, g % 2, :, :], m, tp[m % 2])

                    exps(0)
                    for g in range(4):
                        copy_turn(0, g)
                    exps(1)
                    for g in range(4):
                        copy_turn(1, g)


def build(nc, a):
    with ExitStack() as ctx:
        c = Core(nc, ctx, a)
        start(c)
        if 0 in STAGES:
            cross_attention(c, "L0_xattn", "mask_keys", 1)
        if 1 in STAGES:
            spectral_layer(c, "L0_attn")
        if 2 in STAGES:
            capacity_experts(c, "L0_ffn")
        if 3 in STAGES:
            causal_cross_attention(c, "L1_xattn")
        if 4 in STAGES:
            two_step_attention(c, "L1_attn")
        if 5 in STAGES:
            routed_experts(c, "L1_ffn")
        if 6 in STAGES:
            many_head_cross_attention(c, "L2_xattn")
        if 7 in STAGES:
            selective_scan_layer(c, "L2_attn")
        if 8 in STAGES:
            chosen_adapters(c, "L2_ffn")
        if 9 in STAGES:
            cross_attention(c, "L3_xattn", "mask_pairs", S)
        if 10 in STAGES:
            self_attention(c, "L3_attn")
        if 11 in STAGES:
            quantised_ffn(c, "L3_ffn")
        finish(c)


def constants():
    p = np.arange(P)
    same = p[:, None] // S == p[None, :] // S
    f = np.float32
    half = DH // 2
    angle = np.arange(S, dtype=f)[None, :] * (f(1) / f(10000) ** ((p % half).astype(f) / f(half)))[:, None]
    return {
        "c_heads": (p[:, None] % 32 // DH == np.arange(4)).astype(f),
        "c_which": (p[None, None, :] // DH == 2 * np.arange(8)[None, :, None] + p[:, None, None] // S).astype(f),
        "c_delta": (p[:, None] % S == np.arange(S)).astype(f),
        "c_later": ((p[:, None] % S == np.arange(S)) & (np.arange(S) > 0)).astype(f),
        "c_causal": np.where(np.arange(S) <= p[:, None] % S, 0, OUT).astype(f),
        "c_strict": np.where(np.arange(S) < p[:, None] % S, 0, OUT).astype(f),
        "c_halves": np.stack([p < 32, (p >= 32) & (p < 64)], axis=1).astype(f),
        "c_freq": ((p[:, None] % 32 == np.arange(32)) & (p[:, None] < 64)).astype(f),
        "c_earlier": (p[:, None] < p[None, :]).astype(f),
        "c_sixteen": np.broadcast_to(np.arange(16, dtype=f), (P, NT, 16)),
        "c_rank": np.broadcast_to((8 - np.arange(8, dtype=f))[None, :, None], (P, 8, B)),
        "c_eight": np.broadcast_to(np.arange(8, dtype=f), (P, NT, 8)),
        "c_cos": np.cos(angle).astype(f),
        "c_sin": (np.sin(angle) * np.where(p % DH < half, -1, 1)[:, None]).astype(f),
        "c_ident": np.eye(P, dtype=f),
        "c_pair_causal": np.where(same & (p[None, :] <= p[:, None]), 0, OUT).astype(f),
    }


def kernel(**inputs):
    import concourse.bacc as bacc
    from concourse.bass_utils import run_bass_kernel_spmd

    i = {k: np.asarray(v) for k, v in inputs.items()}
    arrays = {
        "x": i["x"].reshape(TOK, D),
        "ctx": i["ctx_1024"],
        "mask_keys": i["mask_BxS2_ik0"].reshape(B, 1, KEYS),
        "mask_pairs": i["mask_BxSxS2_bk1"],
    }
    for n in ("L0_xattn", "L3_xattn"):
        arrays.update({f"{n}_Wq": i[f"{n}_Wq"], f"{n}_WkT": i[f"{n}_Wk"].T, f"{n}_Wv": i[f"{n}_Wv"],
                       f"{n}_bq": i[f"{n}_bq"].reshape(D, 1), f"{n}_bk": i[f"{n}_bk"].reshape(D, 1),
                       f"{n}_bv": i[f"{n}_bv"].reshape(1, D)})
    arrays.update({"L1_xattn_Wq": i["L1_xattn_Wq"], "L1_xattn_WqT": i["L1_xattn_Wq"].T})
    arrays.update({
        "L1_attn_w": np.stack([i["L1_attn_W_attn"][:, :D], i["L1_attn_W_attn"][:, D:], i["L1_attn_W_k2"]]),
        "L1_attn_bias": np.stack([i["L1_attn_b_attn"][:D], i["L1_attn_b_attn"][D:], i["L1_attn_b_k2"]], axis=1),
        "L1_attn_W_proj": i["L1_attn_W_proj"], "L1_attn_b_proj": i["L1_attn_b_proj"].reshape(1, D),
    })
    swapped = np.arange(D).reshape(H, 2, DH // 2)[:, ::-1].reshape(D)
    wq, wk, wv = i["L3_attn_w_qkv"].reshape(3, D, D)
    arrays.update({"L3_attn_w": np.stack([wq.T, wq[swapped].T, wk.T, wk[swapped].T, wv.T]),
                   "L3_attn_wo": i["L3_attn_w_out"].T})
    twice = lambda v: np.concatenate([v, v, np.zeros_like(v), np.zeros_like(v)]).reshape(-1, 1)
    filled = lambda w: np.concatenate([w, np.zeros((P - w.shape[0],) + w.shape[1:], w.dtype)])
    arrays.update({
        "L0_attn_cols": np.stack([i[f"L0_attn_{n}"] for n in ("ln1_g", "ln1_b", "ln3_g", "ln3_b")], axis=1),
        "L0_attn_W_toT": filled(i["L0_attn_W_to"]).T, "L0_attn_W_fromT": filled(i["L0_attn_W_from"].T),
        "L0_attn_decay": twice(i["L0_attn_log_decay"]), "L0_attn_freq": twice(i["L0_attn_frequencies"]),
        "L0_attn_W1T": i["L0_attn_W_ffn1"].T, "L0_attn_b1": i["L0_attn_b_ffn1"].reshape(4, P).T,
        "L0_attn_W2T": i["L0_attn_W_ffn2"].T, "L0_attn_b2": i["L0_attn_b_ffn2"].reshape(1, D),
        "L0_ffn_Wg": i["L0_ffn_Wg"], "L0_ffn_w1": i["L0_ffn_w1"], "L0_ffn_w2": i["L0_ffn_w2"],
    })
    arrays.update({
        "L1_ffn_embT": i["L1_ffn_uzman_embeddings"].T, "L1_ffn_bonus": i["L1_ffn_onbellek_durumu"].reshape(1, -1),
        "L1_ffn_b1": i["L1_ffn_b1"].reshape(8, 4, P).transpose(2, 0, 1), "L1_ffn_b2": i["L1_ffn_b2"], "L1_ffn_W1": i["L1_ffn_W1"], "L1_ffn_W2": i["L1_ffn_W2"],
        "L2_attn_cols": np.stack([i["L2_attn_ln_w"], i["L2_attn_ln_b"]], axis=1),
        "L2_attn_W_inT": i["L2_attn_W_in"].T, "L2_attn_conv_w": i["L2_attn_conv_w"].reshape(2 * D, 4),
        "L2_attn_W_xT": i["L2_attn_W_x"].T, "L2_attn_W_dtT": i["L2_attn_W_dt"].T, "L2_attn_log_A": i["L2_attn_log_A"],
        "L2_attn_W_outT": i["L2_attn_W_out"].T,
        "L2_attn_vecs": np.stack([i[f"L2_attn_{n}"].reshape(2, P).T for n in ("conv_b", "b_dt", "D_param")]),
    })
    side_by_side = lambda w: w.transpose(1, 0, 2).reshape(D, -1)
    adapter = {n: i[f"L2_ffn_{n}"] for n in ("W_base", "b_base", "Wd1", "bd1", "Wd2", "bd2", "Wa_down", "ba_down", "Wa_up", "ba_up")}
    arrays.update({
        "L2_ffn_wd1": side_by_side(adapter["Wd1"]), "L2_ffn_bd1": adapter["bd1"].reshape(2, P).T,
        "L2_ffn_wd2": adapter["Wd2"].reshape(2 * P, D), "L2_ffn_bd2": adapter["bd2"].T,
        "L2_ffn_wad": side_by_side(adapter["Wa_down"]), "L2_ffn_bad": adapter["ba_down"].reshape(4, P).T,
        "L2_ffn_wau": adapter["Wa_up"].reshape(4 * P, D), "L2_ffn_bau": adapter["ba_up"],
        "L2_ffn_wb": adapter["W_base"], "L2_ffn_bb": adapter["b_base"].reshape(1, D),
    })
    rows = lambda w: np.concatenate([w, np.zeros((384 - w.shape[0], D), w.dtype)]).reshape(3, P, D).transpose(1, 0, 2).reshape(P, -1)
    arrays["L3_ffn_w"] = np.concatenate([rows(i["L3_ffn_w_gate"]), rows(i["L3_ffn_w_up"]), i["L3_ffn_w_down"]], axis=1)
    arrays.update({f"L2_xattn_w{n}": i[f"L2_xattn_W_{n}"].T for n in "qkvo"})
    arrays["mask_all"] = i["mask_1x1xSxS2_bk1"].reshape(S, KEYS)
    arrays.update(constants())

    nc = bacc.Bacc("TRN2", target_bir_lowering=False, num_devices=1)
    arrays = {f"in_{k}": np.ascontiguousarray(v) for k, v in arrays.items()}
    a = {k[3:]: nc.dram_tensor(k, v.shape, mybir.dt.from_np(v.dtype), kind="ExternalInput").ap()
         for k, v in arrays.items()}
    a["out"] = nc.dram_tensor("out", (TOK, D), F32, kind="ExternalOutput").ap()
    a["scratch_in"] = nc.dram_tensor("scratch_in", (TOK, D), F32).ap()
    a["scratch_out"] = nc.dram_tensor("scratch_out", (TOK, D), F32).ap()
    a["scratch_rows"] = nc.dram_tensor("scratch_rows", (32, TOK), F32).ap()
    build(nc, a)
    r = run_bass_kernel_spmd(nc, [arrays], core_ids=[0])
    return r.results[0]["out"].reshape(B, S, D)
```

```python
from contextlib import ExitStack

import numpy as np

import concourse.bass as bass
from concourse import mybir

STAGES = tuple(range(12))

F32 = mybir.dt.float32
I32 = mybir.dt.int32
U32 = mybir.dt.uint32
U8 = mybir.dt.uint8
ALU = mybir.AluOpType
ACT = mybir.ActivationFunctionType
AX = mybir.AxisListType

P = 128
B, S, D = 32, 64, 128
TOK = B * S
NT = TOK // P
KEYS = 1601
KC = -(-KEYS // P)
KREST = KEYS - (KC - 1) * P
SPANS = [(k, min(512, KEYS - k)) for k in range(0, KEYS, 512)]
H, DH = 16, 8
EPS = 1e-5
OUT = -2.0 ** 100


class Steps:

    def __init__(self, sem, *parts):
        self.sem, self.where, self.order, self.next = sem, {}, [], 0
        base = 0
        for times, names, *copies in parts:
            for i, n in enumerate(names):
                assert n not in self.where, n
                self.where[n] = (base + i + 1, len(names))
            self.order += names * (copies[0] if copies else 1)
            base += times * len(names)

    def at(self, name, t=0):
        first, per = self.where[name]
        return self.sem, t * per + first

    def before(self, name, t, rounds=1):
        first, per = self.where[name]
        assert first - rounds * per >= 1, name
        return self.sem, t * per + (first - rounds * per)

    def did(self, name):
        assert self.order[self.next] == name, (self.order[self.next], name)
        self.next += 1
        return self.sem


class RoundSteps(Steps):

    def __init__(self, sem, names, body):
        super().__init__(sem, (1, names), (1, body))
        self.body, self.start = body, len(names)

    def inc(self, name):
        skipped = 0
        while self.order[self.next] != name:
            assert self.next >= self.start, (self.order[self.next], name)
            skipped += 1
            self.advance()
        self.advance()
        return self.sem, 1 + skipped

    def advance(self):
        self.next = self.next + 1 if self.next + 1 < len(self.order) else self.start

    def did(self, name):
        sem, amount = self.inc(name)
        assert amount == 1, name
        return sem


class Core:

    def __init__(self, nc, ctx, a):
        self.nc, self.a = nc, a
        self.sb = lambda name, shape, dt=F32: ctx.enter_context(nc.sbuf_tensor(name, shape, dt))
        self.x = self.sb("x", [P, NT, D])
        self.xn = self.sb("xn", [P, NT, D])
        self.xnT = self.sb("xnT", [P, TOK])
        self.ident = self.sb("ident", [P, P])
        self.eps = self.sb("eps", [P, 1])
        self.pause = self.sb("pause", [P, 1])
        self.sum = self.sb("ln_sum", [P, NT])
        self.mean = self.sb("ln_mean", [P, NT])
        self.sq = self.sb("ln_sq", [P, NT, D])
        self.var = self.sb("ln_var", [P, NT])
        self.std = self.sb("ln_std", [P, NT])
        self.rstd = self.sb("ln_rstd", [P, NT])


class Stage:

    def __init__(self, core, name):
        self.core, self.nc, self.name, self.ctx = core, core.nc, name, ExitStack()

    def __enter__(self):
        return self

    def __exit__(self, *exc):
        return self.ctx.__exit__(*exc)

    def sb(self, name, shape, dt=F32):
        return self.ctx.enter_context(self.nc.sbuf_tensor(f"{self.name}_{name}", shape, dt))

    def ps(self, name, shape):
        return self.ctx.enter_context(self.nc.psum_tensor(f"{self.name}_ps_{name}", shape, F32))

    def sem(self, name):
        return self.ctx.enter_context(self.nc.semaphore(f"{self.name}_{name}"))

    def block(self):
        return self.ctx.enter_context(self.nc.Block())


class Norm:

    def __init__(self, c, tag="ln", x=None, xn=None, xnT=None, gain=None, bias=None, turned=True):
        self.x, self.xn = (c.x, c.xn) if x is None else (x, xn)
        self.xnT = c.xnT if xnT is None else xnT
        self.tag, self.gain, self.bias, self.turned = tag, gain, bias, turned
        turns = [0, 1, 2, 3] if turned else []
        name = lambda n: f"{tag}_{n}"
        self.V = [name(n) for n in ["sum", "mean", "centred", "var", "rstd", "xn"] + [f"T{i}" for i in turns[::2]]]
        self.A = [name(n) for n in ["sq", "std"] + [f"T{i}" for i in turns[1::2]]]
        self.P = [name(f"PT{i}") for i in turns]


LN_V = ["ln_sum", "ln_mean", "ln_centred", "ln_var", "ln_rstd", "ln_xn", "ln_T0", "ln_T2"]
LN_A = ["ln_sq", "ln_std", "ln_T1", "ln_T3"]
LN_P = ["ln_PT0", "ln_PT1", "ln_PT2", "ln_PT3"]


def ln_vector(c, dve, V, A, PE, tp, n=None):
    nc, n = c.nc, n or Norm(c)
    g = n.tag

    def wide(m):
        return m[:, :].unsqueeze(2).broadcast_to([P, NT, D])

    nc.vector.tensor_reduce(c.sum[:, :], n.x[:, :, :], AX.X, ALU.add).then_inc(V.did(f"{g}_sum"), 1)
    dve.wait_ge(*V.at(f"{g}_sum"))
    nc.vector.tensor_scalar(c.mean[:, :], c.sum[:, :], 1.0 / D, None, ALU.mult).then_inc(V.did(f"{g}_mean"), 1)
    dve.wait_ge(*V.at(f"{g}_mean"))
    nc.vector.tensor_tensor(n.xn[:, :, :], n.x[:, :, :], wide(c.mean), ALU.subtract).then_inc(V.did(f"{g}_centred"), 1)
    dve.wait_ge(*A.at(f"{g}_sq"))
    nc.vector.tensor_reduce(c.var[:, :], c.sq[:, :, :], AX.X, ALU.add).then_inc(V.did(f"{g}_var"), 1)
    dve.wait_ge(*A.at(f"{g}_std"))
    nc.vector.reciprocal(c.rstd[:, :], c.std[:, :]).then_inc(V.did(f"{g}_rstd"), 1)
    dve.wait_ge(*V.at(f"{g}_rstd"))
    nc.vector.tensor_tensor(n.xn[:, :, :], n.xn[:, :, :], wide(c.rstd), ALU.mult).then_inc(V.did(f"{g}_xn"), 1)
    for i in (0, 2) if n.turned else ():
        dve.wait_ge(*PE.at(f"{g}_PT{i}"))
        dst = n.xnT[:, 512 * i:512 * i + 512]
        if n.gain is None:
            nc.vector.tensor_copy(dst, tp[0]).then_inc(V.did(f"{g}_T{i}"), 1)
        else:
            nc.vector.tensor_scalar(dst, tp[0], n.gain, n.bias, ALU.mult, ALU.add).then_inc(V.did(f"{g}_T{i}"), 1)


def ln_scalar(c, act, V, A, PE, tp, n=None):
    nc, n = c.nc, n or Norm(c)
    g = n.tag
    act.wait_ge(*V.at(f"{g}_centred"))
    nc.scalar.activation(c.sq[:, :, :], n.xn[:, :, :], ACT.Square).then_inc(A.did(f"{g}_sq"), 1)
    act.wait_ge(*V.at(f"{g}_var"))
    nc.scalar.activation(c.std[:, :], c.var[:, :], ACT.Sqrt, bias=c.eps[:, 0:1], scale=1.0 / D)\
        .then_inc(A.did(f"{g}_std"), 1)
    for i in (1, 3) if n.turned else ():
        act.wait_ge(*PE.at(f"{g}_PT{i}"))
        dst = n.xnT[:, 512 * i:512 * i + 512]
        if n.gain is None:
            nc.scalar.copy(dst, tp[1]).then_inc(A.did(f"{g}_T{i}"), 1)
        else:
            nc.scalar.activation(dst, tp[1], ACT.Identity, bias=n.bias, scale=n.gain).then_inc(A.did(f"{g}_T{i}"), 1)


def ln_tensor(c, pe, V, A, PE, tp, n=None):
    nc, n = c.nc, n or Norm(c)
    g = n.tag
    pe.wait_ge(*V.at(f"{g}_xn"))
    for i in range(4):
        if i == 2:
            pe.wait_ge(*V.at(f"{g}_T0"))
        if i == 3:
            pe.wait_ge(*A.at(f"{g}_T1"))
        for j in range(4):
            last = nc.tensor.transpose(tp[i % 2][:, P * j:P * j + P], n.xn[:, 4 * i + j, :], c.ident[:, :])
        last.then_inc(PE.did(f"{g}_PT{i}"), 1)


def start(c):
    with Stage(c, "start") as s:
        nc, a = c.nc, c.a
        loaded, eps_set = s.sem("loaded"), s.sem("eps_set")
        block = s.block()

        @block.sync
        def _(sp):
            sp.dma_start(c.x[:, :, :], a["x"].rearrange("(t p) d -> p t d", p=P)).then_inc(loaded, 16)
            sp.dma_start(c.ident[:, :], a["c_ident"]).then_inc(loaded, 16)
            sp.wait_ge(loaded, 32)

        @block.vector
        def _(dve):
            nc.vector.memset(c.eps[:, :], EPS).then_inc(eps_set, 1)
            dve.wait_ge(eps_set, 1)


def finish(c):
    with Stage(c, "finish") as s:
        stored = s.sem("stored")
        block = s.block()

        @block.sync
        def _(sp):
            sp.dma_start(c.a["out"].rearrange("(t p) d -> p t d", p=P), c.x[:, :, :]).then_inc(stored, 16)
            sp.wait_ge(stored, 16)


def cross_attention(c, name, mask_name, mask_rows):
    NG = -(-KC // 4)
    TILE = [(b, g) for b in (0, 1) for g in range(NG)]
    with Stage(c, name) as s:
        nc, a = c.nc, c.a
        wq, wkT, wv = s.sb("wq", [P, D]), s.sb("wkT", [P, D]), s.sb("wv", [P, D])
        bq, bk, bv = s.sb("bq", [P, 1]), s.sb("bk", [P, 1]), s.sb("bv", [P, D])
        qT = s.sb("qT", [P, TOK])
        qkT = s.sb("qkT", [P, TOK])
        q1 = s.sb("q1", [P, P])
        qk1 = s.sb("qk1", [P, P])
        qbk = s.sb("qbk", [P, 1])
        mask = s.sb("mask", [P, 2, KEYS], I32 if mask_rows == 1 else U8)
        out_ = s.sb("out_keys", [P, KEYS])
        shift = s.sb("shift", [P, KEYS])
        ctx = s.sb("ctx", [P, 2, 2, KC, D])
        ctxT = s.sb("ctxT", [P, 2, KEYS])
        sc = s.sb("sc", [P, KEYS])
        probs = s.sb("probs", [P, KEYS])
        probsT = s.sb("probsT", [P, KC, P])
        mx, nmx = s.sb("mx", [P, 1]), s.sb("nmx", [P, 1])
        rows, rinv = s.sb("rows", [P, 1]), s.sb("rinv", [P, 1])
        oT, o = s.sb("oT", [P, P]), s.sb("o", [P, D])
        turn = s.ps("turn", [P, 2, 512])
        scores = s.ps("scores", [P, 4, 512])
        mixed = s.ps("mixed", [P, 512])
        small = s.ps("small", [P, 512])
        weights, first = s.sem("weights"), s.sem("first")
        ctx_in = [s.sem("ctx_in0"), s.sem("ctx_in1")]
        mask_in = [s.sem("mask_in0"), s.sem("mask_in1")]
        V = Steps(s.sem("vector_steps"), (1, LN_V + [f"q{i}" for i in range(4)]),
                  (NT, ["tile_q", "qbk", "ind"] + [f"ctxT{b}{g}" for b, g in TILE if g % 2 == 0] +
                   ["masked", "nmax"] + [f"pT{g}" for g in range(0, NG, 2)] + ["oT", "rinv", "out", "x"], 2))
        A = Steps(s.sem("scalar_steps"), (1, LN_A + [f"qk{i}" for i in range(4)]),
                  (NT, ["tile_qk", "shift"] + [f"ctxT{b}{g}" for b, g in TILE if g % 2] + ["exp"] +
                   [f"pT{g}" for g in range(1, NG, 2)], 2))
        PE = Steps(s.sem("tensor_steps"), (1, LN_P + [x for i in range(4) for x in (f"q{i}", f"qk{i}")]),
                   (NT, ["qbk"] + [f"ctxT{b}{g}" for b, g in TILE] + ["scores"] +
                    [f"pT{g}" for g in range(NG)] + ["oT", "out"], 2))
        tp = [turn[:, i, :] for i in (0, 1)]
        flat = scores[:, :, :].rearrange("p a n -> p (a n)")[:, 0:KEYS]
        wide = [min(512, KEYS - 512 * g) for g in range(NG)]
        block = s.block()

        @block.sync
        def _(sp):
            for dst, src in ((wq, "Wq"), (wkT, "WkT"), (wv, "Wv"), (bq, "bq"), (bk, "bk")):
                sp.dma_start(dst[:, :], a[f"{name}_{src}"]).then_inc(weights, 16)
            sp.dma_start(bv[:, :], a[f"{name}_bv"].broadcast_to([P, D])).then_inc(weights, 16)

            def load(t, u):
                for b in (0, 1):
                    keys = a["ctx"][bass.ds(2 * t + b, 1), :, :].rearrange("a k d -> (a k) d")
                    sp.dma_start(ctx[:, u, b, 0:KC - 1, :], keys[0:(KC - 1) * P, :].rearrange("(j p) d -> p j d", p=P))\
                        .then_inc(ctx_in[u], 16)
                    sp.dma_start(ctx[0:KREST, u, b, KC - 1, :], keys[(KC - 1) * P:KEYS, :]).then_inc(ctx_in[u], 16)
                    m = a[mask_name][bass.ds(2 * t + b, 1), :, :].rearrange("a q k -> (a q) k")
                    if mask_rows == 1:
                        m = m.broadcast_to([S, KEYS])
                    sp.dma_start(mask[S * b:S * b + S, u, :], m).then_inc(mask_in[u], 16)

            load(0, 0)
            load(1, 1)
            with sp.Fori(1, NT // 2) as t2:
                for u in (0, 1):
                    sp.wait_ge(*PE.at("oT", 2 * t2 + u - 2))
                    load(2 * t2 + u, u)

        @block.tensor
        def _(pe):
            ln_tensor(c, pe, V, A, PE, tp)
            pe.wait_ge(weights, 96)
            pe.wait_ge(*V.at("ln_T2"))
            pe.wait_ge(*A.at("ln_T3"))
            for i in range(4):
                nc.tensor.matmul(scores[:, i, :], wq[:, :], c.xnT[:, 512 * i:512 * i + 512], start=True, stop=True)\
                    .then_inc(PE.did(f"q{i}"), 1)
                pe.wait_ge(*V.at(f"q{i}"))
                if i >= 2:
                    pe.wait_ge(*A.at(f"qk{i - 2}"))
                nc.tensor.matmul(tp[i % 2], wkT[:, :], qT[:, 512 * i:512 * i + 512], start=True, stop=True)\
                    .then_inc(PE.did(f"qk{i}"), 1)
            with pe.Fori(0, NT // 2) as t2:
                for u in (0, 1):
                    t = 2 * t2 + u
                    pe.wait_ge(*V.at("tile_q", t))
                    nc.tensor.matmul(small[:, 0:1], q1[:, :], bk[:, :], start=True, stop=True).then_inc(PE.did("qbk"), 1)
                    pe.wait_ge(*A.at("tile_qk", t))
                    pe.wait_ge(ctx_in[u], 64 * t2 + 64)
                    for n, (b, g) in enumerate(TILE):
                        if n >= 2:
                            pe.wait_ge(*(A if g % 2 else V).at("ctxT%d%d" % TILE[n - 2], t))
                        for j in range(4 * g, min(4 * g + 4, KC)):
                            k = min(P, KEYS - P * j)
                            last = nc.tensor.transpose(tp[g % 2][:, P * (j % 4):P * (j % 4) + k], ctx[0:k, u, b, j, :],
                                                       c.ident[0:k, 0:k])
                        last.then_inc(PE.did(f"ctxT{b}{g}"), 1)
                    pe.wait_ge(*V.at(f"ctxT1{NG - 2}", t))
                    pe.wait_ge(*A.at(f"ctxT1{NG - 1}", t))
                    for b in (0, 1):
                        for g in range(NG):
                            last = nc.tensor.matmul(scores[S * b:S * b + S, g, 0:wide[g]], qk1[:, S * b:S * b + S],
                                                    ctxT[:, b, 512 * g:512 * g + wide[g]], start=True, stop=True)
                    last.then_inc(PE.did("scores"), 1)
                    pe.wait_ge(*A.at("exp", t))
                    for g in range(NG):
                        if g >= 2:
                            pe.wait_ge(*(A if g % 2 else V).at(f"pT{g - 2}", t))
                        for j in range(4 * g, min(4 * g + 4, KC)):
                            k = min(P, KEYS - P * j)
                            last = nc.tensor.transpose(tp[g % 2][0:k, P * (j % 4):P * (j % 4) + P], probs[:, P * j:P * j + k],
                                                       c.ident[:, :])
                        last.then_inc(PE.did(f"pT{g}"), 1)
                    pe.wait_ge(*V.at(f"pT{NG - 2}", t))
                    pe.wait_ge(*A.at(f"pT{NG - 1}", t))
                    for b in (0, 1):
                        for j in range(KC):
                            k = min(P, KEYS - P * j)
                            last = nc.tensor.matmul(mixed[:, S * b:S * b + S], ctx[0:k, u, b, j, :],
                                                    probsT[0:k, j, S * b:S * b + S], start=(j == 0), stop=(j == KC - 1))
                    last.then_inc(PE.did("oT"), 1)
                    pe.wait_ge(*V.at("oT", t))
                    nc.tensor.matmul(small[:, P:2 * P], oT[:, :], wv[:, :], start=True, stop=True).then_inc(PE.did("out"), 1)

        @block.vector
        def _(dve):
            ln_vector(c, dve, V, A, PE, tp)
            dve.wait_ge(weights, 96)
            for i in range(4):
                dve.wait_ge(*PE.at(f"q{i}"))
                nc.vector.tensor_scalar(qT[:, 512 * i:512 * i + 512], scores[:, i, :], bq[:, 0:1], D ** -0.5,
                                        ALU.add, ALU.mult).then_inc(V.did(f"q{i}"), 1)
            with dve.Fori(0, NT // 2) as t2:
                for u in (0, 1):
                    t = 2 * t2 + u
                    nc.vector.tensor_copy(q1[:, :], qT[:, bass.ds(P * t, P)]).then_inc(V.did("tile_q"), 1)
                    dve.wait_ge(*PE.at("qbk", t))
                    nc.vector.tensor_copy(qbk[:, :], small[:, 0:1]).then_inc(V.did("qbk"), 1)
                    dve.wait_ge(mask_in[u], 32 * t2 + 32)
                    if mask_rows == 1:
                        nc.vector.tensor_scalar(out_[:, :], mask[:, u, :], 0.0, None, ALU.is_equal).then_inc(V.did("ind"), 1)
                    else:
                        nc.vector.tensor_copy(out_[:, :], mask[:, u, :]).then_inc(V.did("ind"), 1)
                    for b, g in TILE:
                        if g % 2 == 0:
                            dve.wait_ge(*PE.at(f"ctxT{b}{g}", t))
                            nc.vector.tensor_copy(ctxT[:, b, 512 * g:512 * g + wide[g]], tp[0][:, 0:wide[g]])\
                                .then_inc(V.did(f"ctxT{b}{g}"), 1)
                    dve.wait_ge(*A.at("shift", t))
                    dve.wait_ge(*PE.at("scores", t))
                    nc.vector.memset(c.pause[:, :], 0.0)
                    nc.vector.tensor_tensor_reduce(out=sc[:, :], in0=flat, in1=shift[:, :], scale=1.0, scalar=3 * OUT,
                                                   op0=ALU.add, op1=ALU.max, accum_out=mx[:, :]).then_inc(V.did("masked"), 1)
                    dve.wait_ge(*V.at("masked", t))
                    nc.vector.tensor_scalar(nmx[:, :], mx[:, :], -1.0, None, ALU.mult).then_inc(V.did("nmax"), 1)
                    for g in range(0, NG, 2):
                        dve.wait_ge(*PE.at(f"pT{g}", t))
                        nc.vector.tensor_copy(probsT[:, 4 * g:4 * g + 4, :].rearrange("p j q -> p (j q)"), tp[0])\
                            .then_inc(V.did(f"pT{g}"), 1)
                    dve.wait_ge(*PE.at("oT", t))
                    nc.vector.tensor_copy(oT[:, :], mixed[:, 0:P]).then_inc(V.did("oT"), 1)
                    nc.vector.reciprocal(rinv[:, :], rows[:, :]).then_inc(V.did("rinv"), 1)
                    dve.wait_ge(*V.at("rinv", t))
                    dve.wait_ge(*PE.at("out", t))
                    nc.vector.scalar_tensor_tensor(out=o[:, :], in0=small[:, P:2 * P], scalar=rinv[:, 0:1], in1=bv[:, :],
                                                   op0=ALU.mult, op1=ALU.add).then_inc(V.did("out"), 1)
                    dve.wait_ge(*V.at("out", t))
                    xt = c.x[:, bass.ds(t, 1), :].rearrange("p a d -> p (a d)")
                    nc.vector.tensor_tensor(xt, xt, o[:, :], ALU.add).then_inc(V.did("x"), 1)

        @block.scalar
        def _(act):
            ln_scalar(c, act, V, A, PE, tp)
            for i in range(4):
                act.wait_ge(*PE.at(f"qk{i}"))
                nc.scalar.copy(qkT[:, 512 * i:512 * i + 512], tp[i % 2]).then_inc(A.did(f"qk{i}"), 1)
            with act.Fori(0, NT // 2) as t2:
                for u in (0, 1):
                    t = 2 * t2 + u
                    act.wait_ge(*V.at("tile_q", t))
                    nc.scalar.copy(qk1[:, :], qkT[:, bass.ds(P * t, P)]).then_inc(A.did("tile_qk"), 1)
                    act.wait_ge(*V.at("ind", t))
                    nc.scalar.activation(shift[:, :], out_[:, :], ACT.Identity, bias=qbk[:, 0:1], scale=OUT)\
                        .then_inc(A.did("shift"), 1)
                    for b, g in TILE:
                        if g % 2:
                            act.wait_ge(*PE.at(f"ctxT{b}{g}", t))
                            nc.scalar.copy(ctxT[:, b, 512 * g:512 * g + wide[g]], tp[1][:, 0:wide[g]])\
                                .then_inc(A.did(f"ctxT{b}{g}"), 1)
                    act.wait_ge(*V.at("nmax", t))
                    nc.scalar.activation(probs[:, :], sc[:, :], ACT.Exp, bias=nmx[:, 0:1], scale=1.0, accum_out=rows[:, :])\
                        .then_inc(A.did("exp"), 1)
                    for g in range(1, NG, 2):
                        act.wait_ge(*PE.at(f"pT{g}", t))
                        k = P if g < NG - 1 else KREST
                        j = min(4 * g + 4, KC)
                        nc.scalar.copy(probsT[0:k, 4 * g:j, :].rearrange("p j q -> p (j q)"), tp[1][0:k, 0:P * (j - 4 * g)])\
                            .then_inc(A.did(f"pT{g}"), 1)


def causal_cross_attention(c, name):
    with Stage(c, name) as s:
        nc, a = c.nc, c.a
        G = NT // 4
        w, wT = s.sb("w", [P, D]), s.sb("wT", [P, D])
        mask = s.sb("mask", [P, P])
        keys_all = s.sb("keys_all", [P, NT, D])
        keys = s.sb("keys", [P, 4, D])
        keysT = s.sb("keysT", [P, 512])
        q, qk = s.sb("q", [P, 512]), s.sb("qk", [P, 512])
        sc, probsT = s.sb("sc", [P, 4, P]), s.sb("probsT", [P, 4, P])
        mx, rows, rinv = s.sb("mx", [P, 4]), s.sb("rows", [P, 4]), s.sb("rinv", [P, 4])
        oT, o = s.sb("oT", [P, 4, P]), s.sb("o", [P, 4, D])
        turn = s.ps("turn", [P, 2, 512])
        pq, pqk, psc = s.ps("q", [P, 512]), s.ps("qk", [P, 512]), s.ps("sc", [P, 512])
        po, pout = s.ps("oT", [P, 512]), s.ps("out", [P, 512])
        loaded = s.sem("loaded")
        V = Steps(s.sem("vector_steps"), (1, LN_V), (G, ["keysT", "q", "masked", "max", "less", "rows", "rinv", "probs",
                                                        "oT", "x"]))
        A = Steps(s.sem("scalar_steps"), (1, LN_A), (G, ["keys", "qk", "exp", "probsT"]))
        PE = Steps(s.sem("tensor_steps"), (1, LN_P), (G, ["keysT", "q", "qk", "scores", "probsT", "oT", "out"]))
        tp = [turn[:, i, :] for i in (0, 1)]
        four = lambda m: m.rearrange("p (i k) -> p i k", i=4)
        wide = lambda m: m[:, :].unsqueeze(2).broadcast_to([P, 4, P])
        block = s.block()

        @block.sync
        def _(sp):
            sp.dma_start(w[:, :], a[f"{name}_Wq"]).then_inc(loaded, 16)
            sp.dma_start(wT[:, :], a[f"{name}_WqT"]).then_inc(loaded, 16)
            sp.dma_start(mask[:, :], a["c_pair_causal"]).then_inc(loaded, 16)
            for b in (0, 1):
                src = a["ctx"].rearrange("(t b) k d -> b k t d", b=2)[b, 0:S, :, :]
                sp.dma_start(keys_all[S * b:S * b + S, :, :], src).then_inc(loaded, 16)

        @block.tensor
        def _(pe):
            ln_tensor(c, pe, V, A, PE, tp)
            pe.wait_ge(*V.at("ln_T2"))
            pe.wait_ge(*A.at("ln_T3"))
            with pe.Fori(0, G) as g:
                pe.wait_ge(*A.at("keys", g))
                for i in range(4):
                    last = nc.tensor.transpose(tp[0][:, P * i:P * i + P], keys[:, i, :], c.ident[:, :])
                last.then_inc(PE.did("keysT"), 1)
                nc.tensor.matmul(pq[:, :], wT[:, :], c.xnT[:, bass.ds(512 * g, 512)], start=True, stop=True)\
                    .then_inc(PE.did("q"), 1)
                pe.wait_ge(*V.at("q", g))
                nc.tensor.matmul(pqk[:, :], w[:, :], q[:, :], start=True, stop=True).then_inc(PE.did("qk"), 1)
                pe.wait_ge(*A.at("qk", g))
                for i in range(4):
                    last = nc.tensor.matmul(psc[:, P * i:P * i + P], qk[:, P * i:P * i + P], keysT[:, P * i:P * i + P],
                                            start=True, stop=True)
                last.then_inc(PE.did("scores"), 1)
                pe.wait_ge(*V.at("probs", g))
                for i in range(4):
                    last = nc.tensor.transpose(tp[1][:, P * i:P * i + P], sc[:, i, :], c.ident[:, :])
                last.then_inc(PE.did("probsT"), 1)
                pe.wait_ge(*A.at("probsT", g))
                for i in range(4):
                    last = nc.tensor.matmul(po[:, P * i:P * i + P], keys[:, i, :], probsT[:, i, :], start=True, stop=True)
                last.then_inc(PE.did("oT"), 1)
                pe.wait_ge(*V.at("oT", g))
                for i in range(4):
                    last = nc.tensor.matmul(pout[:, P * i:P * i + P], oT[:, i, :], wT[:, :], start=True, stop=True)
                last.then_inc(PE.did("out"), 1)

        @block.vector
        def _(dve):
            ln_vector(c, dve, V, A, PE, tp)
            with dve.Fori(0, G) as g:
                dve.wait_ge(*PE.at("keysT", g))
                nc.vector.tensor_copy(keysT[:, :], tp[0]).then_inc(V.did("keysT"), 1)
                dve.wait_ge(*PE.at("q", g))
                nc.vector.tensor_scalar(q[:, :], pq[:, :], D ** -0.5, None, ALU.mult).then_inc(V.did("q"), 1)
                dve.wait_ge(*PE.at("scores", g))
                nc.vector.tensor_tensor(sc[:, :, :], four(psc[:, :]), mask[:, :].unsqueeze(1).broadcast_to([P, 4, P]),
                                        ALU.add).then_inc(V.did("masked"), 1)
                dve.wait_ge(*V.at("masked", g))
                nc.vector.tensor_reduce(mx[:, :], sc[:, :, :], AX.X, ALU.max).then_inc(V.did("max"), 1)
                dve.wait_ge(*V.at("max", g))
                nc.vector.tensor_tensor(sc[:, :, :], sc[:, :, :], wide(mx), ALU.subtract).then_inc(V.did("less"), 1)
                dve.wait_ge(*A.at("exp", g))
                nc.vector.tensor_reduce(rows[:, :], sc[:, :, :], AX.X, ALU.add).then_inc(V.did("rows"), 1)
                dve.wait_ge(*V.at("rows", g))
                nc.vector.reciprocal(rinv[:, :], rows[:, :]).then_inc(V.did("rinv"), 1)
                dve.wait_ge(*V.at("rinv", g))
                nc.vector.tensor_tensor(sc[:, :, :], sc[:, :, :], wide(rinv), ALU.mult).then_inc(V.did("probs"), 1)
                dve.wait_ge(*PE.at("oT", g))
                nc.vector.tensor_copy(oT[:, :, :], four(po[:, :])).then_inc(V.did("oT"), 1)
                dve.wait_ge(*PE.at("out", g))
                xg = c.x[:, bass.ds(4 * g, 4), :]
                nc.vector.tensor_tensor(xg, four(pout[:, :]), xg, ALU.add).then_inc(V.did("x"), 1)

        @block.scalar
        def _(act):
            ln_scalar(c, act, V, A, PE, tp)
            act.wait_ge(loaded, 80)
            with act.Fori(0, G) as g:
                act.wait_ge(*PE.before("oT", g))
                nc.scalar.copy(keys[:, :, :], keys_all[:, bass.ds(4 * g, 4), :]).then_inc(A.did("keys"), 1)
                act.wait_ge(*PE.at("qk", g))
                nc.scalar.copy(qk[:, :], pqk[:, :]).then_inc(A.did("qk"), 1)
                act.wait_ge(*V.at("less", g))
                nc.scalar.activation(sc[:, :, :], sc[:, :, :], ACT.Exp).then_inc(A.did("exp"), 1)
                act.wait_ge(*PE.at("probsT", g))
                nc.scalar.copy(probsT[:, :, :], four(tp[1])).then_inc(A.did("probsT"), 1)


MH_V = ["spread", "masked", "max", "less", "rows", "rinv", "diag", "own", "sum", "scale"]
MH_A = ["exp", "pT0", "pT1"]
MH_P = ["scores", "pT0", "pT1", "norm", "pv"]


def named(tag, names):
    return [f"{tag}_{n}" for n in names]


class Heads:

    def __init__(self, s):
        self.hb = s.sb("hb", [P, 4])
        self.which = s.sb("which", [P, 8, P])
        self.delta = s.sb("delta", [P, S])
        self.qd = s.sb("qd", [P, 2, 4, S])
        self.sc = s.sb("sc", [P, 16, S])
        self.mx, self.rows, self.rinv = s.sb("mx", [P, 16]), s.sb("rows", [P, 16]), s.sb("rinv", [P, 16])
        self.diag = s.sb("diag", [P, 16, S])
        self.pT = s.sb("pT", [P, 8, P])
        self.own = s.sb("own", [P, 2, 4, S])
        self.sum = s.sb("sum", [P, 2, S])
        self.ps = s.ps("scores", [P, 4, 512])
        self.turn = s.ps("turn", [P, 2, 512])

    def load(self, eng, a, sem):
        eng.dma_start(self.hb[:, :], a["c_heads"]).then_inc(sem, 16)
        eng.dma_start(self.which[:, :, :], a["c_which"]).then_inc(sem, 16)
        eng.dma_start(self.delta[:, :], a["c_delta"]).then_inc(sem, 16)


def heads_vector(c, dve, h, V, A, PE, tag, t, q, mask, delta, out, before):
    nc = c.nc
    for w in before:
        dve.wait_ge(*w)
    nc.vector.tensor_tensor(h.qd[:, :, :, :], q.rearrange("p (b q) -> p b q", b=2).unsqueeze(2).broadcast_to([P, 2, 4, S]),
                            h.hb[:, :].unsqueeze(1).unsqueeze(3).broadcast_to([P, 2, 4, S]), ALU.mult)\
        .then_inc(V.did(f"{tag}_spread"), 1)
    dve.wait_ge(*PE.at(f"{tag}_scores", t))
    four = h.ps[:, :, 0:256].rearrange("p g (r k) -> p g r k", k=S)
    sc4 = h.sc[:, :, :].rearrange("p (g r) k -> p g r k", g=4)
    if mask is not None:
        nc.vector.tensor_tensor(sc4, four, mask[:, :].unsqueeze(1).unsqueeze(1).broadcast_to([P, 4, 4, S]), ALU.add)\
            .then_inc(V.did(f"{tag}_masked"), 1)
    else:
        nc.vector.tensor_copy(sc4, four).then_inc(V.did(f"{tag}_masked"), 1)
    dve.wait_ge(*V.at(f"{tag}_masked", t))
    nc.vector.tensor_reduce(h.mx[:, :], h.sc[:, :, :], AX.X, ALU.max).then_inc(V.did(f"{tag}_max"), 1)
    dve.wait_ge(*V.at(f"{tag}_max", t))
    nc.vector.tensor_tensor(h.sc[:, :, :], h.sc[:, :, :], h.mx[:, :].unsqueeze(2).broadcast_to([P, 16, S]), ALU.subtract)\
        .then_inc(V.did(f"{tag}_less"), 1)
    dve.wait_ge(*A.at(f"{tag}_exp", t))
    nc.vector.tensor_reduce(h.rows[:, :], h.sc[:, :, :], AX.X, ALU.add).then_inc(V.did(f"{tag}_rows"), 1)
    dve.wait_ge(*V.at(f"{tag}_rows", t))
    nc.vector.reciprocal(h.rinv[:, :], h.rows[:, :]).then_inc(V.did(f"{tag}_rinv"), 1)
    dve.wait_ge(*V.at(f"{tag}_rinv", t))
    nc.vector.tensor_tensor(h.diag[:, :, :], h.rinv[:, :].unsqueeze(2).broadcast_to([P, 16, S]),
                            delta[:, :].unsqueeze(1).broadcast_to([P, 16, S]), ALU.mult).then_inc(V.did(f"{tag}_diag"), 1)
    dve.wait_ge(*PE.at(f"{tag}_pv", t))
    nc.vector.tensor_tensor(h.own[:, :, :, :], h.ps[:, 0:2, 0:256].rearrange("p b (h q) -> p b h q", h=4),
                            h.hb[:, :].unsqueeze(1).unsqueeze(3).broadcast_to([P, 2, 4, S]), ALU.mult)\
        .then_inc(V.did(f"{tag}_own"), 1)
    dve.wait_ge(*V.at(f"{tag}_own", t))
    nc.vector.tensor_reduce(h.sum[:, :, :], h.own[:, :, :, :].rearrange("p b h q -> p b q h"), AX.X, ALU.add)\
        .then_inc(V.did(f"{tag}_sum"), 1)
    dve.wait_ge(*V.at(f"{tag}_sum", t))
    nc.vector.tensor_tensor(out, h.sum[:, :, :].rearrange("p b q -> p (b q)"), h.ps[:, 2, 0:P], ALU.mult)\
        .then_inc(V.did(f"{tag}_scale"), 1)


def heads_scalar(c, act, h, V, A, PE, tag, t):
    nc = c.nc
    act.wait_ge(*V.at(f"{tag}_less", t))
    nc.scalar.activation(h.sc[:, :, :], h.sc[:, :, :], ACT.Exp).then_inc(A.did(f"{tag}_exp"), 1)
    for i in (0, 1):
        act.wait_ge(*PE.at(f"{tag}_pT{i}", t))
        nc.scalar.copy(h.pT[:, 4 * i:4 * i + 4, :].rearrange("p r q -> p (r q)"), h.turn[:, i, :])\
            .then_inc(A.did(f"{tag}_pT{i}"), 1)


def heads_tensor(c, pe, h, V, A, PE, tag, t, k, v, before):
    nc = c.nc
    pe.wait_ge(*V.at(f"{tag}_spread", t))
    for w in before:
        pe.wait_ge(*w)
    for j in (0, 1):
        for b in (0, 1):
            for g in range(4):
                last = nc.tensor.matmul(h.ps[:, g, P * j + S * b:P * j + S * b + S],
                                        h.qd[32 * g:32 * g + 32, b, 2 * j:2 * j + 2, :].rearrange("p h q -> p (h q)"),
                                        k[32 * g:32 * g + 32, S * b:S * b + S], start=True, stop=True)
    last.then_inc(PE.did(f"{tag}_scores"), 1)
    pe.wait_ge(*A.at(f"{tag}_exp", t))
    for i in (0, 1):
        for r in range(4):
            last = nc.tensor.transpose(h.turn[:, i, P * r:P * r + P],
                                       h.sc[:, 8 * i + 2 * r:8 * i + 2 * r + 2, :].rearrange("p b k -> p (b k)"), c.ident[:, :])
        last.then_inc(PE.did(f"{tag}_pT{i}"), 1)
    pe.wait_ge(*A.at(f"{tag}_pT1", t))
    pe.wait_ge(*V.at(f"{tag}_diag", t))
    for r in range(8):
        last = nc.tensor.matmul(h.ps[:, 2, 0:P], h.which[:, r, :],
                                h.diag[:, 2 * r:2 * r + 2, :].rearrange("p b q -> p (b q)"), start=(r == 0), stop=(r == 7))
    last.then_inc(PE.did(f"{tag}_norm"), 1)
    for b in (0, 1):
        for g in range(4):
            last = nc.tensor.matmul(h.ps[32 * g:32 * g + 32, b, 0:256], v[S * b:S * b + S, 32 * g:32 * g + 32],
                                    h.pT[S * b:S * b + S, 2 * g:2 * g + 2, :].rearrange("p r q -> p (r q)"),
                                    start=True, stop=True, tile_position=(S * b, 32 * g))
    last.then_inc(PE.did(f"{tag}_pv"), 1)


def self_attention(c, name):
    with Stage(c, name) as s:
        nc, a = c.nc, c.a
        h = Heads(s)
        w = s.sb("w", [P, 5, D])
        wo = s.sb("wo", [P, D])
        cos, sin = s.sb("cos", [P, S]), s.sb("sin", [P, S])
        xg = s.sb("xg", [P, 512])
        straight, turned = s.sb("straight", [P, 2, 512]), s.sb("turned", [P, 2, 512])
        qT, kT, v, yT = s.sb("qT", [P, 512]), s.sb("kT", [P, 512]), s.sb("v", [P, 4, D]), s.sb("yT", [P, 4, P])
        pa, pb = s.ps("a", [P, 512]), s.ps("b", [P, 512])
        loaded = s.sem("loaded")
        tags = [f"t{i}" for i in range(4)]
        G = NT // 4
        V = Steps(s.sem("vector_steps"), (1, LN_V),
                  (G, ["q_cos", "q_sin", "q", "k_cos", "k_sin", "k"] + sum([named(n, MH_V) for n in tags], []) + ["x"]))
        A = Steps(s.sem("scalar_steps"), (1, LN_A), (G, ["xg", "v"] + sum([named(n, MH_A) for n in tags], [])))
        PE = Steps(s.sem("tensor_steps"), (1, LN_P), (G, ["q", "k", "v"] + sum([named(n, MH_P) for n in tags], []) + ["out"]))
        tp = [h.turn[:, i, :] for i in (0, 1)]
        eight = lambda m: m.rearrange("p (b q) -> p b q", q=S)
        wide = lambda m: m[:, :].unsqueeze(1).broadcast_to([P, 8, S])
        block = s.block()

        @block.sync
        def _(sp):
            h.load(sp, a, loaded)
            sp.dma_start(w[:, :, :], a[f"{name}_w"].rearrange("n p d -> p n d")).then_inc(loaded, 16)
            sp.dma_start(wo[:, :], a[f"{name}_wo"]).then_inc(loaded, 16)
            sp.dma_start(cos[:, :], a["c_cos"]).then_inc(loaded, 16)
            sp.dma_start(sin[:, :], a["c_sin"]).then_inc(loaded, 16)

        @block.tensor
        def _(pe):
            ln_tensor(c, pe, V, A, PE, tp)
            pe.wait_ge(loaded, 112)
            with pe.Fori(0, G) as g:
                pe.wait_ge(*A.at("xg", g))
                nc.tensor.matmul(pa[:, :], w[:, 0, :], xg[:, :], start=True, stop=True)
                nc.tensor.matmul(pb[:, :], w[:, 1, :], xg[:, :], start=True, stop=True).then_inc(PE.did("q"), 1)
                pe.wait_ge(*V.at("q_sin", g))
                nc.tensor.matmul(pa[:, :], w[:, 2, :], xg[:, :], start=True, stop=True)
                nc.tensor.matmul(pb[:, :], w[:, 3, :], xg[:, :], start=True, stop=True).then_inc(PE.did("k"), 1)
                pe.wait_ge(*V.at("k_sin", g))
                for i in range(4):
                    last = nc.tensor.matmul(pa[:, P * i:P * i + P], xg[:, P * i:P * i + P], w[:, 4, :], start=True, stop=True)
                last.then_inc(PE.did("v"), 1)
                for i, tag in enumerate(tags):
                    heads_tensor(c, pe, h, V, A, PE, tag, g, kT[:, P * i:P * i + P], v[:, i, :], [V.at("k", g), A.at("v", g)])
                pe.wait_ge(*V.at("t3_scale", g))
                for i in range(4):
                    last = nc.tensor.matmul(pb[:, P * i:P * i + P], yT[:, i, :], wo[:, :], start=True, stop=True)
                last.then_inc(PE.did("out"), 1)

        @block.vector
        def _(dve):
            ln_vector(c, dve, V, A, PE, tp)
            with dve.Fori(0, G) as g:
                for m, (n, dst, scale) in enumerate((("q", qT, DH ** -0.5), ("k", kT, 1.0))):
                    dve.wait_ge(*PE.at(n, g))
                    nc.vector.scalar_tensor_tensor(out=eight(straight[:, m, :]), in0=eight(pa[:, :]), scalar=scale,
                                                   in1=wide(cos), op0=ALU.mult, op1=ALU.mult).then_inc(V.did(f"{n}_cos"), 1)
                    nc.vector.scalar_tensor_tensor(out=eight(turned[:, m, :]), in0=eight(pb[:, :]), scalar=scale,
                                                   in1=wide(sin), op0=ALU.mult, op1=ALU.mult).then_inc(V.did(f"{n}_sin"), 1)
                    dve.wait_ge(*V.at(f"{n}_sin", g))
                    nc.vector.tensor_tensor(dst[:, :], straight[:, m, :], turned[:, m, :], ALU.add).then_inc(V.did(n), 1)
                for i, tag in enumerate(tags):
                    heads_vector(c, dve, h, V, A, PE, tag, g, qT[:, P * i:P * i + P], None, h.delta, yT[:, i, :], [V.at("q", g)])
                dve.wait_ge(*PE.at("out", g))
                xs = c.x[:, bass.ds(4 * g, 4), :]
                nc.vector.tensor_tensor(xs, pb[:, :].rearrange("p (i d) -> p i d", i=4), xs, ALU.add).then_inc(V.did("x"), 1)

        @block.scalar
        def _(act):
            ln_scalar(c, act, V, A, PE, tp)
            with act.Fori(0, G) as g:
                act.wait_ge(*V.at("ln_T2"))
                act.wait_ge(*V.before("x", g))
                nc.scalar.copy(xg[:, :], c.xnT[:, bass.ds(512 * g, 512)]).then_inc(A.did("xg"), 1)
                act.wait_ge(*PE.at("v", g))
                nc.scalar.copy(v[:, :, :], pa[:, :].rearrange("p (i d) -> p i d", i=4)).then_inc(A.did("v"), 1)
                for i, tag in enumerate(tags):
                    heads_scalar(c, act, h, V, A, PE, tag, g)


def two_step_attention(c, name):
    with Stage(c, name) as s:
        nc, a = c.nc, c.a
        h = Heads(s)
        w, wp = s.sb("w", [P, 3, D]), s.sb("wp", [P, D])
        bias = s.sb("bias", [P, 3])
        bp, bp2 = s.sb("bp", [P, D]), s.sb("bp2", [P, D])
        causal, strict = s.sb("causal", [P, S]), s.sb("strict", [P, S])
        later = s.sb("later", [P, S])
        vg = s.sb("vg", [P, 4, D])
        qT, kT, k2T = s.sb("qT", [P, 512]), s.sb("kT", [P, 512]), s.sb("k2T", [P, 512])
        xg = s.sb("xg", [P, 512])
        yT, y2T, sumT = s.sb("yT", [P, P]), s.sb("y2T", [P, P]), s.sb("sumT", [P, 4, P])
        eT, e = s.sb("eT", [P, 2, S]), s.sb("e", [P, D])
        pa, pb = s.ps("a", [P, 512]), s.ps("b", [P, 512])
        loaded = s.sem("loaded")
        G = NT // 4
        tags = [f"t{i}" for i in range(4)]
        V = Steps(s.sem("vector_steps"), (1, LN_V + ["bp2", "eT"]),
                  (G, ["q", "k2"] + sum([named(n, MH_V) + [f"{n}_err"] + named(n + "b", MH_V) + [f"{n}_total"] for n in
                                         ("u0", "u1", "u2", "u3")], []) + ["bias", "x"]))
        A = Steps(s.sem("scalar_steps"), (1, LN_A),
                  (G, ["xg", "vg", "k"] + sum([named(n, MH_A) + [f"{n}_e"] + named(n + "b", MH_A) for n in
                                               ("u0", "u1", "u2", "u3")], [])))
        PE = Steps(s.sem("tensor_steps"), (1, LN_P),
                   (G, ["q", "k", "k2"] + sum([named(n, MH_P) + [f"{n}_e"] + named(n + "b", MH_P) for n in
                                               ("u0", "u1", "u2", "u3")], []) + ["out"]))
        tags = ["u0", "u1", "u2", "u3"]
        tp = [h.turn[:, i, :] for i in (0, 1)]
        four = lambda m: m.rearrange("p (i d) -> p i d", i=4)
        block = s.block()

        @block.sync
        def _(sp):
            h.load(sp, a, loaded)
            sp.dma_start(w[:, :, :], a[f"{name}_w"].rearrange("n p d -> p n d")).then_inc(loaded, 16)
            sp.dma_start(bias[:, :], a[f"{name}_bias"]).then_inc(loaded, 16)
            sp.dma_start(wp[:, :], a[f"{name}_W_proj"]).then_inc(loaded, 16)
            sp.dma_start(bp[:, :], a[f"{name}_b_proj"].broadcast_to([P, D])).then_inc(loaded, 16)
            sp.dma_start(causal[:, :], a["c_causal"]).then_inc(loaded, 16)
            sp.dma_start(strict[:, :], a["c_strict"]).then_inc(loaded, 16)
            sp.dma_start(later[:, :], a["c_later"]).then_inc(loaded, 16)

        @block.tensor
        def _(pe):
            ln_tensor(c, pe, V, A, PE, tp)
            pe.wait_ge(loaded, 160)
            with pe.Fori(0, G) as g:
                pe.wait_ge(*A.at("xg", g))
                nc.tensor.matmul(pa[:, :], w[:, 0, :], xg[:, :], start=True, stop=True).then_inc(PE.did("q"), 1)
                pe.wait_ge(*V.before("x", g))
                nc.tensor.matmul(pb[:, :], w[:, 1, :], xg[:, :], start=True, stop=True).then_inc(PE.did("k"), 1)
                pe.wait_ge(*V.at("q", g))
                nc.tensor.matmul(pa[:, :], w[:, 2, :], xg[:, :], start=True, stop=True).then_inc(PE.did("k2"), 1)
                for i, tag in enumerate(tags):
                    part = slice(P * i, P * i + P)
                    heads_tensor(c, pe, h, V, A, PE, tag, g, kT[:, part], vg[:, i, :], [A.at("k", g)])
                    pe.wait_ge(*V.at(f"{tag}_err", g))
                    nc.tensor.transpose(pa[:, 0:P], eT[:, :, :].rearrange("p b q -> p (b q)"), c.ident[:, :])\
                        .then_inc(PE.did(f"{tag}_e"), 1)
                    heads_tensor(c, pe, h, V, A, PE, tag + "b", g, k2T[:, part], e[:, :], [A.at(f"{tag}_e", g)])
                pe.wait_ge(*V.at("u3_total", g))
                for i in range(4):
                    last = nc.tensor.matmul(pb[:, P * i:P * i + P], sumT[:, i, :], wp[:, :], start=True, stop=True)
                last.then_inc(PE.did("out"), 1)

        @block.vector
        def _(dve):
            ln_vector(c, dve, V, A, PE, tp)
            dve.wait_ge(loaded, 160)
            nc.vector.tensor_tensor(bp2[:, :], bp[:, :], bp[:, :], ALU.add).then_inc(V.did("bp2"), 1)
            nc.vector.memset(eT[:, :, S - 1:S], 0.0).then_inc(V.did("eT"), 1)
            with dve.Fori(0, G) as g:
                dve.wait_ge(*PE.at("q", g))
                nc.vector.tensor_scalar(qT[:, :], pa[:, :], bias[:, 0:1], DH ** -0.5, ALU.add, ALU.mult)\
                    .then_inc(V.did("q"), 1)
                dve.wait_ge(*PE.at("k2", g))
                nc.vector.tensor_scalar(k2T[:, :], pa[:, :], bias[:, 2:3], None, ALU.add).then_inc(V.did("k2"), 1)
                for i, tag in enumerate(tags):
                    part = slice(P * i, P * i + P)
                    heads_vector(c, dve, h, V, A, PE, tag, g, qT[:, part], causal, h.delta, yT[:, :], [V.at("q", g)])
                    dve.wait_ge(*V.at(f"{tag}_scale", g))
                    v2, y2 = (m.rearrange("p (b q) -> p b q", b=2) for m in (xg[:, part], yT[:, :]))
                    nc.vector.tensor_tensor(eT[:, :, 0:S - 1], v2[:, :, 1:S], y2[:, :, 0:S - 1], ALU.subtract)\
                        .then_inc(V.did(f"{tag}_err"), 1)
                    heads_vector(c, dve, h, V, A, PE, tag + "b", g, qT[:, part], strict, later, y2T[:, :], [])
                    dve.wait_ge(*V.at(f"{tag}b_scale", g))
                    nc.vector.tensor_tensor(sumT[:, i, :], yT[:, :], y2T[:, :], ALU.add).then_inc(V.did(f"{tag}_total"), 1)
                xs = c.x[:, bass.ds(4 * g, 4), :]
                nc.vector.tensor_tensor(xs, xs, bp2[:, :].unsqueeze(1).broadcast_to([P, 4, D]), ALU.add)\
                    .then_inc(V.did("bias"), 1)
                dve.wait_ge(*V.at("bias", g))
                dve.wait_ge(*PE.at("out", g))
                nc.vector.tensor_tensor(xs, four(pb[:, :]), xs, ALU.add).then_inc(V.did("x"), 1)

        @block.scalar
        def _(act):
            ln_scalar(c, act, V, A, PE, tp)
            with act.Fori(0, G) as g:
                act.wait_ge(*V.before("x", g))
                nc.scalar.copy(xg[:, :], c.xnT[:, bass.ds(512 * g, 512)]).then_inc(A.did("xg"), 1)
                nc.scalar.copy(vg[:, :, :], c.xn[:, bass.ds(4 * g, 4), :]).then_inc(A.did("vg"), 1)
                act.wait_ge(*PE.at("k", g))
                nc.scalar.activation(kT[:, :], pb[:, :], ACT.Identity, bias=bias[:, 1:2]).then_inc(A.did("k"), 1)
                for i, tag in enumerate(tags):
                    heads_scalar(c, act, h, V, A, PE, tag, g)
                    act.wait_ge(*PE.at(f"{tag}_e", g))
                    nc.scalar.copy(e[:, :], pa[:, 0:P]).then_inc(A.did(f"{tag}_e"), 1)
                    heads_scalar(c, act, h, V, A, PE, tag + "b", g)


def spectral_layer(c, name):
    F2 = P
    with Stage(c, name) as s:
        nc, a = c.nc, c.a
        cols = s.sb("cols", [P, 4])
        wto, wfrom = s.sb("wto", [P, F2]), s.sb("wfrom", [F2, D])
        w1, b1 = s.sb("w1", [P, 4 * D]), s.sb("b1", [P, 4])
        w2, b2 = s.sb("w2", [P, 4, D]), s.sb("b2", [P, D])
        b2s = s.sb("b2s", [P, D])
        halves, freq = s.sb("halves", [F2, 2]), s.sb("freq", [F2, 32])
        raw = s.sb("raw", [F2, 2])
        decay, omega = s.sb("decay", [F2, 1]), s.sb("omega", [F2, 1])
        sine, half = s.sb("sine", [F2, 1]), s.sb("half", [F2, 1])
        half2, cosine = s.sb("half2", [F2, 1]), s.sb("cosine", [F2, 1])
        part = s.sb("part", [F2, 2])
        factor = s.sb("factor", [F2, 2])
        rot = s.sb("rot", [F2, F2])
        rot_u, rot_z = s.sb("rot_u", [F2, F2]), s.sb("rot_z", [F2, F2])
        h, hT = s.sb("h", [P, NT, D]), s.sb("hT", [P, TOK])
        uT = s.sb("uT", [F2, TOK])
        z = s.sb("z", [F2, B, S + 1])
        x2, x2b = s.sb("x2", [P, NT, D]), s.sb("x2b", [P, NT, D])
        g = s.sb("gelu", [P, 4, 512])
        turn = s.ps("turn", [P, 2, 512])
        step = s.ps("step", [P, 2, 512])
        big = s.ps("big", [P, 2, 512])
        loaded = s.sem("loaded")
        n1 = Norm(c, turned=False)
        n2 = Norm(c, "in", c.xn, h, hT, cols[:, 0:1], cols[:, 1:2])
        n3 = Norm(c, "ff", x2, h, hT, cols[:, 2:3], cols[:, 3:4])
        V = Steps(s.sem("vector_steps"),
                  (1, ["b2s", "z0", "rot", "half2", "cosine", "part0", "part1", "factor0", "factor1", "rot0", "rot1", "rot_u", "rot_z"] +
                   n1.V + n2.V + ["u0", "u2"]),
                  (S, ["clip"], 2), (1, ["x2_0", "x2_1", "x2_2", "x2_3"] + n3.V + ["x2b", "xb"]), (4, ["x"]))
        A = Steps(s.sem("scalar_steps"), (1, ["omega", "decay", "sine", "half"] + n1.A + n2.A + ["u1", "u3"] + n3.A),
                  (4, [f"g{i}" for i in range(4)]))
        PE = Steps(s.sem("tensor_steps"), (1, n2.P + [f"u{i}" for i in range(4)]), (S, ["step"], 2),
                   (1, ["from0", "from1", "from2", "from3"] + n3.P), (4, [f"h{i}" for i in range(4)] + ["out"]))
        tp = [turn[:, i, :] for i in (0, 1)]
        four = lambda m: m.rearrange("p (i d) -> p i d", i=4)
        u3 = uT[:, :].rearrange("f (b s) -> f b s", b=B)
        block = s.block()

        @block.sync
        def _(sp):
            sp.dma_start(raw[:, 0:1], a[f"{name}_decay"]).then_inc(loaded, 16)
            sp.dma_start(raw[:, 1:2], a[f"{name}_freq"]).then_inc(loaded, 16)
            sp.dma_start(halves[:, :], a["c_halves"]).then_inc(loaded, 16)
            sp.dma_start(freq[:, :], a["c_freq"]).then_inc(loaded, 16)
            sp.dma_start(cols[:, :], a[f"{name}_cols"]).then_inc(loaded, 16)
            sp.dma_start(wto[:, :], a[f"{name}_W_toT"]).then_inc(loaded, 16)
            sp.dma_start(wfrom[:, :], a[f"{name}_W_fromT"]).then_inc(loaded, 16)
            sp.dma_start(w1[:, :], a[f"{name}_W1T"]).then_inc(loaded, 16)
            sp.dma_start(b1[:, :], a[f"{name}_b1"]).then_inc(loaded, 16)
            sp.dma_start(w2[:, :, :], a[f"{name}_W2T"].rearrange("(c p) d -> p c d", p=P)).then_inc(loaded, 16)
            sp.dma_start(b2[:, :], a[f"{name}_b2"].broadcast_to([P, D])).then_inc(loaded, 16)

        @block.tensor
        def _(pe):
            ln_tensor(c, pe, V, A, PE, tp, n2)
            pe.wait_ge(*V.at("in_T2"))
            pe.wait_ge(*A.at("in_T3"))
            for i in range(4):
                if i >= 2:
                    pe.wait_ge(*(A if i % 2 else V).at(f"u{i - 2}"))
                nc.tensor.matmul(big[0:F2, i % 2, :], wto[:, :], hT[:, 512 * i:512 * i + 512], start=True, stop=True)\
                    .then_inc(PE.did(f"u{i}"), 1)
            pe.wait_ge(*V.at("u2"))
            pe.wait_ge(*A.at("u3"))
            with pe.Fori(0, S // 2) as k:
                for u in (0, 1):
                    t = 2 * k + u
                    pe.wait_ge(*V.before("clip", t))
                    nc.tensor.matmul(step[0:F2, u, 0:B], rot_u[:, :], u3[:, :, bass.ds(t, 1)], start=True, stop=False)
                    nc.tensor.matmul(step[0:F2, u, 0:B], rot_z[:, :], z[:, :, bass.ds(t, 1)], start=False, stop=True)\
                        .then_inc(PE.did("step"), 1)
            pe.wait_ge(*V.at("clip", S - 1))
            for i in range(4):
                if i >= 2:
                    pe.wait_ge(*V.at(f"x2_{i - 2}"))
                for j in range(4):
                    for b in (0, 1):
                        last = nc.tensor.matmul(big[S * b:S * b + S, i % 2, P * j:P * j + P], z[:, 8 * i + 2 * j + b, 1:S + 1],
                                                wfrom[:, :], start=True, stop=True)
                last.then_inc(PE.did(f"from{i}"), 1)
            ln_tensor(c, pe, V, A, PE, tp, n3)
            pe.wait_ge(*V.at("ff_T2"))
            pe.wait_ge(*A.at("ff_T3"))
            with pe.Fori(0, 4) as i:
                for k in range(4):
                    pe.wait_ge(*(A.at(f"g{k - 2}", i) if k >= 2 else A.before(f"g{k + 2}", i)))
                    nc.tensor.matmul(tp[k % 2], w1[:, P * k:P * k + P], hT[:, bass.ds(512 * i, 512)], start=True, stop=True)\
                        .then_inc(PE.did(f"h{k}"), 1)
                pe.wait_ge(*A.at("g3", i))
                pe.wait_ge(*V.before("x", i))
                for j in range(4):
                    for k in range(4):
                        last = nc.tensor.matmul(big[:, 0, P * j:P * j + P], g[:, k, P * j:P * j + P], w2[:, k, :],
                                                start=(k == 0), stop=(k == 3))
                last.then_inc(PE.did("out"), 1)

        @block.vector
        def _(dve):
            dve.wait_ge(loaded, 176)
            nc.vector.tensor_scalar(b2s[:, :], b2[:, :], 0.1, None, ALU.mult).then_inc(V.did("b2s"), 1)
            nc.vector.memset(z[:, :, 0:1], 0.0).then_inc(V.did("z0"), 1)
            nc.vector.memset(rot[:, :], 0.0).then_inc(V.did("rot"), 1)
            dve.wait_ge(*A.at("half"))
            nc.vector.tensor_tensor(half2[:, :], half[:, :], half[:, :], ALU.mult).then_inc(V.did("half2"), 1)
            dve.wait_ge(*V.at("half2"))
            nc.vector.tensor_scalar(cosine[:, :], half2[:, :], -2.0, 1.0, ALU.mult, ALU.add).then_inc(V.did("cosine"), 1)
            nc.vector.tensor_tensor(part[:, 0:1], sine[:, :], halves[:, 1:2], ALU.mult).then_inc(V.did("part0"), 1)
            nc.vector.tensor_tensor(part[:, 1:2], sine[:, :], halves[:, 0:1], ALU.mult).then_inc(V.did("part1"), 1)
            dve.wait_ge(*V.at("part1"))
            nc.vector.scalar_tensor_tensor(out=factor[:, 0:1], in0=cosine[:, :], scalar=halves[:, 0:1], in1=part[:, 0:1],
                                           op0=ALU.mult, op1=ALU.subtract).then_inc(V.did("factor0"), 1)
            nc.vector.scalar_tensor_tensor(out=factor[:, 1:2], in0=cosine[:, :], scalar=halves[:, 1:2], in1=part[:, 1:2],
                                           op0=ALU.mult, op1=ALU.add).then_inc(V.did("factor1"), 1)
            dve.wait_ge(*V.at("factor1"))
            for i in (0, 1):
                nc.vector.tensor_scalar(rot[:, 32 * i:32 * i + 32], freq[:, :], factor[:, i:i + 1], None, ALU.mult)\
                    .then_inc(V.did(f"rot{i}"), 1)
            dve.wait_ge(*V.at("rot1"))
            nc.vector.tensor_scalar(rot_u[:, :], rot[:, :], 0.1, None, ALU.mult).then_inc(V.did("rot_u"), 1)
            nc.vector.tensor_scalar(rot_z[:, :], rot[:, :], decay[:, 0:1], None, ALU.mult).then_inc(V.did("rot_z"), 1)
            ln_vector(c, dve, V, A, PE, tp, n1)
            dve.wait_ge(*V.at("ln_xn"))
            ln_vector(c, dve, V, A, PE, tp, n2)
            for i in (0, 2):
                dve.wait_ge(*PE.at(f"u{i}"))
                nc.vector.tensor_copy(uT[:, 512 * i:512 * i + 512], big[0:F2, 0, :]).then_inc(V.did(f"u{i}"), 1)
            with dve.Fori(0, S // 2) as k:
                for u in (0, 1):
                    t = 2 * k + u
                    dve.wait_ge(*PE.at("step", t))
                    nc.vector.tensor_scalar(z[:, :, bass.ds(t + 1, 1)], step[0:F2, u, 0:B].unsqueeze(2), 10.0, -10.0,
                                            ALU.min, ALU.max).then_inc(V.did("clip"), 1)
            for i in range(4):
                dve.wait_ge(*PE.at(f"from{i}"))
                nc.vector.scalar_tensor_tensor(out=x2[:, 4 * i:4 * i + 4, :].rearrange("p i d -> p (i d)"), in0=big[:, i % 2, :],
                                               scalar=0.1, in1=c.xn[:, 4 * i:4 * i + 4, :].rearrange("p i d -> p (i d)"),
                                               op0=ALU.mult, op1=ALU.add).then_inc(V.did(f"x2_{i}"), 1)
            dve.wait_ge(*V.at("x2_3"))
            ln_vector(c, dve, V, A, PE, tp, n3)
            nc.vector.tensor_tensor(x2b[:, :, :], x2[:, :, :], b2s[:, :].unsqueeze(1).broadcast_to([P, NT, D]), ALU.add)\
                .then_inc(V.did("x2b"), 1)
            dve.wait_ge(*V.at("x2b"))
            nc.vector.tensor_tensor(c.x[:, :, :], c.x[:, :, :], x2b[:, :, :], ALU.add).then_inc(V.did("xb"), 1)
            dve.wait_ge(*V.at("xb"))
            with dve.Fori(0, 4) as i:
                dve.wait_ge(*PE.at("out", i))
                xs = c.x[:, bass.ds(4 * i, 4), :].rearrange("p i d -> p (i d)")
                nc.vector.scalar_tensor_tensor(out=xs, in0=big[:, 0, :], scalar=0.1, in1=xs, op0=ALU.mult, op1=ALU.add)\
                    .then_inc(V.did("x"), 1)

        @block.scalar
        def _(act):
            act.wait_ge(loaded, 176)
            nc.scalar.activation(omega[:, :], raw[:, 1:2], ACT.Tanh).then_inc(A.did("omega"), 1)
            nc.scalar.activation(decay[:, :], raw[:, 0:1], ACT.Sigmoid).then_inc(A.did("decay"), 1)
            act.wait_ge(*A.at("omega"))
            nc.scalar.activation(sine[:, :], omega[:, :], ACT.Sin, scale=0.1).then_inc(A.did("sine"), 1)
            nc.scalar.activation(half[:, :], omega[:, :], ACT.Sin, scale=0.05).then_inc(A.did("half"), 1)
            ln_scalar(c, act, V, A, PE, tp, n1)
            ln_scalar(c, act, V, A, PE, tp, n2)
            for i in (1, 3):
                act.wait_ge(*PE.at(f"u{i}"))
                nc.scalar.copy(uT[:, 512 * i:512 * i + 512], big[0:F2, 1, :]).then_inc(A.did(f"u{i}"), 1)
            ln_scalar(c, act, V, A, PE, tp, n3)
            with act.Fori(0, 4) as i:
                act.wait_ge(*PE.before("out", i))
                for k in range(4):
                    act.wait_ge(*PE.at(f"h{k}", i))
                    nc.scalar.activation(g[:, k, :], tp[k % 2], ACT.Gelu, bias=b1[:, k:k + 1]).then_inc(A.did(f"g{k}"), 1)


def capacity_experts(c, name):
    E, CAP, F = 16, TOK // 16, 512
    FC = F // P
    with Stage(c, name) as s:
        nc, a = c.nc, c.a
        wg = s.sb("wg", [P, E])
        earlier, ones = s.sb("earlier", [P, P]), s.sb("ones", [P, P])
        iota = s.sb("iota", [P, NT, E])
        lg, ex = s.sb("logits", [P, NT, E]), s.sb("exps", [P, NT, E])
        mx, total, gate = s.sb("mx", [P, NT]), s.sb("total", [P, NT]), s.sb("gate", [P, NT])
        top = s.sb("top", [P, NT, 8])
        topi = s.sb("topi", [P, NT, 8], U32)
        best = s.sb("best", [P, NT])
        hot = s.sb("hot", [P, NT, E])
        sums = s.sb("sums", [P, 2, NT, E])
        place, mine = s.sb("place", [P, NT, E]), s.sb("mine", [P, NT, E])
        loc, valid = s.sb("loc", [P, NT]), s.sb("valid", [P, NT])
        base, near, far = s.sb("base", [P, NT]), s.sb("near", [P, NT]), s.sb("far", [P, NT])
        to, frm = s.sb("to", [P, NT], U32), s.sb("frm", [P, NT], U32)
        weight = s.sb("weight", [P, NT])
        zero = s.sb("zero", [P, E, D])
        slots = s.sb("slots", [P, E, D])
        slotsT = s.sb("slotsT", [P, E * P])
        w1, w2 = s.sb("w1", [P, 2, F]), s.sb("w2", [P, 2, FC, D])
        hT = s.sb("hT", [P, 2, FC, P])
        done = s.sb("done", [P, E, D])
        got = s.sb("got", [P, NT, D])
        turn = s.ps("turn", [P, 2, 512])
        small = s.ps("small", [P, 2, 512])
        ph = s.ps("h", [P, 2, 512])
        po = s.ps("o", [P, 2, 512])
        loaded, zeroed, sent, read = s.sem("loaded"), s.sem("zeroed"), s.sem("sent"), s.sem("read")
        w_in = [s.sem("w_in0"), s.sem("w_in1")]
        stored, fetched = s.sem("stored"), s.sem("fetched")
        scans = [1, 2, 4, 8]
        V = Steps(s.sem("vector_steps"),
                  (1, ["zero", "ones"] + LN_V + ["logits", "mx", "less", "total", "gate"] + [f"top{i}" for i in range(NT)] +
                   [f"topi{i}" for i in range(NT)] + ["best", "hot", "sums"] +
                   [f"{w}{k}" for k in scans for w in ("head", "tail")] + ["place0", "place", "mine", "loc", "valid", "base", "near",
                    "far1", "far", "to", "near1", "near2", "frm", "weight", "sT0", "sT2"]),
                  (E, ["out"], 2), (1, ["weighted", "x"]))
        A = Steps(s.sem("scalar_steps"), (1, LN_A + ["exp", "sT1", "sT3"]), (E, ["relu"], 2))
        PE = Steps(s.sem("tensor_steps"), (1, LN_P + ["logits", "counts"] + [f"sT{i}" for i in range(4)]),
                   (E, ["h", "out"], 2))
        tp = [turn[:, i, :] for i in (0, 1)]
        e16 = lambda m: m.rearrange("p (t e) -> p t e", e=E)
        wide = lambda m: m[:, :].unsqueeze(2).broadcast_to([P, NT, E])
        dispatched, results = a["scratch_in"], a["scratch_out"]
        block = s.block()

        @block.sync
        def _(sp):
            sp.dma_start(wg[:, :], a[f"{name}_Wg"]).then_inc(loaded, 16)
            sp.dma_start(earlier[:, :], a["c_earlier"]).then_inc(loaded, 16)
            sp.dma_start(iota[:, :, :], a["c_sixteen"]).then_inc(loaded, 16)
            sp.wait_ge(*V.at("zero"))
            sp.dma_start(dispatched.rearrange("(e p) d -> p e d", p=P), zero[:, :, :]).then_inc(zeroed, 16)
            sp.wait_ge(sent, 16 * NT)
            sp.dma_start(slots[:, :, :], dispatched.rearrange("(e p) d -> p e d", p=P)).then_inc(read, 16)

            def load(e, u):
                sp.dma_start(w1[:, u, :], a[f"{name}_w1"][bass.ds(e, 1), :, :].rearrange("a d f -> (a d) f"))\
                    .then_inc(w_in[u], 16)
                sp.dma_start(w2[:, u, :, :], a[f"{name}_w2"][bass.ds(e, 1), :, :].rearrange("a (c p) d -> p (a c) d", p=P))\
                    .then_inc(w_in[u], 16)

            load(0, 0)
            load(1, 1)
            with sp.Fori(1, E // 2) as e2:
                for u in (0, 1):
                    sp.wait_ge(*PE.at("out", 2 * e2 + u - 2))
                    load(2 * e2 + u, u)
            sp.wait_ge(*V.at("out", E - 1))
            sp.dma_start(results.rearrange("(e p) d -> p e d", p=P), done[:, :, :]).then_inc(stored, 16)

        @block.gpsimd
        def _(pool):
            pool.wait_ge(*V.at("to"))
            pool.wait_ge(zeroed, 16)
            for t in range(NT):
                nc.gpsimd.indirect_dma_start(dispatched, bass.IndirectOffsetOnAxis(ap=to[:, t:t + 1], axis=0), c.xn[:, t, :], None,
                                             bounds_check=TOK - 1, oob_is_err=False).then_inc(sent, 16)
            pool.wait_ge(*V.at("frm"))
            pool.wait_ge(stored, 16)
            for t in range(NT):
                nc.gpsimd.indirect_dma_start(got[:, t, :], None, results, bass.IndirectOffsetOnAxis(ap=frm[:, t:t + 1], axis=0),
                                             bounds_check=TOK - 1, oob_is_err=False).then_inc(fetched, 16)

        @block.tensor
        def _(pe):
            ln_tensor(c, pe, V, A, PE, tp)
            pe.wait_ge(*V.at("ln_T2"))
            pe.wait_ge(*A.at("ln_T3"))
            pe.wait_ge(loaded, 48)
            for t in range(NT):
                last = nc.tensor.matmul(small[:, 0, E * t:E * t + E], c.xnT[:, P * t:P * t + P], wg[:, :], start=True, stop=True)
            last.then_inc(PE.did("logits"), 1)
            pe.wait_ge(*V.at("hot"))
            hots = hot[:, :, :].rearrange("p t e -> p (t e)")
            nc.tensor.matmul(small[:, 1, 0:NT * E], earlier[:, :], hots, start=True, stop=True)
            nc.tensor.matmul(small[:, 1, NT * E:2 * NT * E], ones[:, :], hots, start=True, stop=True)\
                .then_inc(PE.did("counts"), 1)
            pe.wait_ge(read, 16)
            for i in range(4):
                if i >= 2:
                    pe.wait_ge(*(A if i % 2 else V).at(f"sT{i - 2}"))
                for j in range(4):
                    last = nc.tensor.transpose(tp[i % 2][:, P * j:P * j + P], slots[:, 4 * i + j, :], c.ident[:, :])
                last.then_inc(PE.did(f"sT{i}"), 1)
            pe.wait_ge(*V.at("sT2"))
            pe.wait_ge(*A.at("sT3"))
            with pe.Fori(0, E // 2) as e2:
                for u in (0, 1):
                    e = 2 * e2 + u
                    pe.wait_ge(w_in[u], 32 * e2 + 32)
                    for k in range(FC):
                        last = nc.tensor.matmul(ph[:, u, P * k:P * k + P], w1[:, u, P * k:P * k + P], slotsT[:, bass.ds(P * e, P)],
                                                start=True, stop=True)
                    last.then_inc(PE.did("h"), 1)
                    pe.wait_ge(*V.before("out", e, 2))
                    pe.wait_ge(*A.at("relu", e))
                    for k in range(FC):
                        last = nc.tensor.matmul(po[:, u, 0:P], hT[:, u, k, :], w2[:, u, k, :], start=(k == 0), stop=(k == FC - 1))
                    last.then_inc(PE.did("out"), 1)

        @block.vector
        def _(dve):
            nc.vector.memset(zero[:, :, :], 0.0).then_inc(V.did("zero"), 1)
            nc.vector.memset(ones[:, :], 1.0).then_inc(V.did("ones"), 1)
            ln_vector(c, dve, V, A, PE, tp)
            dve.wait_ge(*PE.at("logits"))
            nc.vector.tensor_copy(lg[:, :, :], e16(small[:, 0, 0:NT * E])).then_inc(V.did("logits"), 1)
            dve.wait_ge(*V.at("logits"))
            nc.vector.tensor_reduce(mx[:, :], lg[:, :, :], AX.X, ALU.max).then_inc(V.did("mx"), 1)
            dve.wait_ge(*V.at("mx"))
            nc.vector.tensor_tensor(ex[:, :, :], lg[:, :, :], wide(mx), ALU.subtract).then_inc(V.did("less"), 1)
            dve.wait_ge(*A.at("exp"))
            nc.vector.tensor_reduce(total[:, :], ex[:, :, :], AX.X, ALU.add).then_inc(V.did("total"), 1)
            dve.wait_ge(*V.at("total"))
            nc.vector.reciprocal(gate[:, :], total[:, :]).then_inc(V.did("gate"), 1)
            for t in range(NT):
                nc.vector.max(top[:, t, :], lg[:, t, :]).then_inc(V.did(f"top{t}"), 1)
            dve.wait_ge(*V.at(f"top{NT - 1}"))
            for t in range(NT):
                nc.vector.max_index(topi[:, t, :], top[:, t, :], lg[:, t, :]).then_inc(V.did(f"topi{t}"), 1)
            dve.wait_ge(*V.at(f"topi{NT - 1}"))
            nc.vector.tensor_copy(best[:, :].unsqueeze(2), topi[:, :, 0:1]).then_inc(V.did("best"), 1)
            dve.wait_ge(*V.at("best"))
            dve.wait_ge(loaded, 48)
            nc.vector.tensor_tensor(hot[:, :, :], iota[:, :, :], wide(best), ALU.is_equal).then_inc(V.did("hot"), 1)
            dve.wait_ge(*PE.at("counts"))
            nc.vector.tensor_copy(sums[:, 0, :, :], e16(small[:, 1, NT * E:2 * NT * E])).then_inc(V.did("sums"), 1)
            prev = "sums"
            for n, k in enumerate(scans):
                src, dst = sums[:, n % 2, :, :], sums[:, (n + 1) % 2, :, :]
                dve.wait_ge(*V.at(prev))
                nc.vector.tensor_copy(dst[:, 0:k, :], src[:, 0:k, :]).then_inc(V.did(f"head{k}"), 1)
                nc.vector.tensor_tensor(dst[:, k:NT, :], src[:, k:NT, :], src[:, 0:NT - k, :], ALU.add)\
                    .then_inc(V.did(f"tail{k}"), 1)
                prev = f"tail{k}"
            dve.wait_ge(*V.at(prev))
            nc.vector.tensor_copy(place[:, 0:1, :], e16(small[:, 1, 0:NT * E])[:, 0:1, :]).then_inc(V.did("place0"), 1)
            nc.vector.tensor_tensor(place[:, 1:NT, :], e16(small[:, 1, 0:NT * E])[:, 1:NT, :], sums[:, 0, 0:NT - 1, :], ALU.add)\
                .then_inc(V.did("place"), 1)
            dve.wait_ge(*V.at("place"))
            nc.vector.tensor_tensor(mine[:, :, :], place[:, :, :], hot[:, :, :], ALU.mult).then_inc(V.did("mine"), 1)
            dve.wait_ge(*V.at("mine"))
            nc.vector.tensor_reduce(loc[:, :], mine[:, :, :], AX.X, ALU.add).then_inc(V.did("loc"), 1)
            dve.wait_ge(*V.at("loc"))
            nc.vector.tensor_scalar(valid[:, :], loc[:, :], float(CAP), None, ALU.is_lt).then_inc(V.did("valid"), 1)
            nc.vector.tensor_scalar(base[:, :], best[:, :], float(CAP), None, ALU.mult).then_inc(V.did("base"), 1)
            dve.wait_ge(*V.at("base"))
            nc.vector.tensor_tensor(near[:, :], base[:, :], loc[:, :], ALU.add).then_inc(V.did("near"), 1)
            nc.vector.tensor_scalar(far[:, :], loc[:, :], float(CAP), float(4 * TOK), ALU.is_ge, ALU.mult).then_inc(V.did("far1"), 1)
            dve.wait_ge(*V.at("far1"))
            nc.vector.tensor_tensor(mx[:, :], far[:, :], near[:, :], ALU.add).then_inc(V.did("far"), 1)
            dve.wait_ge(*V.at("far"))
            nc.vector.tensor_copy(to[:, :], mx[:, :]).then_inc(V.did("to"), 1)
            nc.vector.tensor_scalar(loc[:, :], loc[:, :], float(CAP - 1), None, ALU.min).then_inc(V.did("near1"), 1)
            dve.wait_ge(*V.at("near1"))
            nc.vector.tensor_tensor(total[:, :], base[:, :], loc[:, :], ALU.add).then_inc(V.did("near2"), 1)
            dve.wait_ge(*V.at("near2"))
            nc.vector.tensor_copy(frm[:, :], total[:, :]).then_inc(V.did("frm"), 1)
            nc.vector.tensor_tensor(weight[:, :], gate[:, :], valid[:, :], ALU.mult).then_inc(V.did("weight"), 1)
            for i in (0, 2):
                dve.wait_ge(*PE.at(f"sT{i}"))
                nc.vector.tensor_copy(slotsT[:, 512 * i:512 * i + 512], tp[0]).then_inc(V.did(f"sT{i}"), 1)
            with dve.Fori(0, E // 2) as e2:
                for u in (0, 1):
                    e = 2 * e2 + u
                    dve.wait_ge(*PE.at("out", e))
                    nc.vector.tensor_copy(done[:, bass.ds(e, 1), :], po[:, u, 0:P].unsqueeze(1)).then_inc(V.did("out"), 1)
            dve.wait_ge(fetched, 16 * NT)
            nc.vector.tensor_tensor(got[:, :, :], got[:, :, :], weight[:, :].unsqueeze(2).broadcast_to([P, NT, D]), ALU.mult)\
                .then_inc(V.did("weighted"), 1)
            dve.wait_ge(*V.at("weighted"))
            nc.vector.tensor_tensor(c.x[:, :, :], c.x[:, :, :], got[:, :, :], ALU.add).then_inc(V.did("x"), 1)

        @block.scalar
        def _(act):
            ln_scalar(c, act, V, A, PE, tp)
            act.wait_ge(*V.at("less"))
            nc.scalar.activation(ex[:, :, :], ex[:, :, :], ACT.Exp).then_inc(A.did("exp"), 1)
            for i in (1, 3):
                act.wait_ge(*PE.at(f"sT{i}"))
                nc.scalar.copy(slotsT[:, 512 * i:512 * i + 512], tp[1]).then_inc(A.did(f"sT{i}"), 1)
            with act.Fori(0, E // 2) as e2:
                for u in (0, 1):
                    e = 2 * e2 + u
                    act.wait_ge(*PE.at("h", e))
                    nc.scalar.activation(hT[:, u, :, :].rearrange("p c k -> p (c k)"), ph[:, u, :], ACT.Relu)\
                        .then_inc(A.did("relu"), 1)


def routed_experts(c, name):
    E, F = 8, 512
    FC = F // P
    with Stage(c, name) as s:
        nc, a = c.nc, c.a
        emb, emb2 = s.sb("emb", [P, E]), s.sb("emb2", [P, E])
        bonus = s.sb("bonus", [P, E])
        ones = s.sb("ones", [P, P])
        iota = s.sb("iota", [P, NT, E])
        sim, score = s.sb("sim", [P, NT, E]), s.sb("score", [P, NT, E])
        tn, te = s.sb("tn", [P, NT]), s.sb("te", [P, E])
        rt, re = s.sb("rt", [P, NT]), s.sb("re", [P, E])
        top, topi = s.sb("top", [P, NT, 8]), s.sb("topi", [P, NT, 8], U32)
        last_i, hit = s.sb("last_i", [P, NT]), s.sb("hit", [P, NT, E])
        best, besti = s.sb("best", [P, NT, 8]), s.sb("besti", [P, NT, 8], U32)
        bi = s.sb("bi", [P, NT, 2])
        gap, ex, den = s.sb("gap", [P, NT]), s.sb("ex", [P, NT]), s.sb("den", [P, NT])
        wt = s.sb("wt", [P, NT, 2])
        hit1, hit2 = s.sb("hit1", [P, NT, E]), s.sb("hit2", [P, NT, E])
        part1, part2 = s.sb("part1", [P, NT, E]), s.sb("part2", [P, NT, E])
        weights = s.sb("weights", [P, NT, E])
        weightsT = s.sb("weightsT", [E, TOK])
        b1, b1e = s.sb("b1", [P, E, FC]), s.sb("b1e", [P, 2, FC])
        b2 = s.sb("b2", [E, D])
        w1, w2 = s.sb("w1", [P, 2, F]), s.sb("w2", [P, 2, FC, D])
        g = s.sb("gelu", [P, 2, FC, 512])
        turn = s.ps("turn", [P, 2, 512])
        ph = s.ps("h", [P, 4, 512])
        po = s.ps("o", [P, 2, 512])
        loaded, w_in = s.sem("loaded"), [s.sem("w_in0"), s.sem("w_in1")]
        ROUTE = ["sim", "tn", "tn_eps", "rt", "te", "te_eps", "re", "s1", "s2", "s3"] + [f"top{t}" for t in range(NT)] + \
            [f"topi{t}" for t in range(NT)] + ["last", "hit", "s4"] + [f"best{t}" for t in range(NT)] + \
            [f"besti{t}" for t in range(NT)] + ["bi", "gap", "den", "w1", "w2", "hit1", "hit2", "part1", "part2", "weights"]
        V = Steps(s.sem("vector_steps"), (1, ["ones", "bonus"] + LN_V + ["emb2"] + ROUTE + ["wT0", "wT2"] +
                                          [f"b2_{i}" for i in range(4)]), (E, [f"x{i}" for i in range(4)], 2))
        A = Steps(s.sem("scalar_steps"), (1, LN_A + ["sq", "tn", "te", "exp", "wT1", "wT3"]),
                  (E, ["b1e"] + [f"g{i}{k}" for i in range(4) for k in range(FC)], 2))
        PE = Steps(s.sem("tensor_steps"), (1, LN_P + ["sim", "te"] + [f"wT{i}" for i in range(4)] + [f"b2_{i}" for i in range(4)]),
                   (E, sum([[f"h{i}{k}" for k in range(FC)] + [f"out{i}"] for i in range(4)], []), 2))
        tp = [turn[:, i, :] for i in (0, 1)]
        wide = lambda m: m.unsqueeze(2).broadcast_to([P, NT, E])
        each = lambda m: m[:, :].unsqueeze(1).broadcast_to([P, NT, E])
        block = s.block()

        @block.sync
        def _(sp):
            sp.dma_start(emb[:, :], a[f"{name}_embT"]).then_inc(loaded, 16)
            sp.dma_start(te[:, :], a[f"{name}_bonus"].broadcast_to([P, E])).then_inc(loaded, 16)
            sp.dma_start(iota[:, :, :], a["c_eight"]).then_inc(loaded, 16)
            sp.dma_start(b1[:, :, :], a[f"{name}_b1"]).then_inc(loaded, 16)
            sp.dma_start(b2[:, :], a[f"{name}_b2"]).then_inc(loaded, 16)

            def load(e, u):
                sp.dma_start(w1[:, u, :], a[f"{name}_W1"][bass.ds(e, 1), :, :].rearrange("a d f -> (a d) f"))\
                    .then_inc(w_in[u], 16)
                sp.dma_start(w2[:, u, :, :], a[f"{name}_W2"][bass.ds(e, 1), :, :].rearrange("a (c p) d -> p (a c) d", p=P))\
                    .then_inc(w_in[u], 16)

            load(0, 0)
            load(1, 1)
            with sp.Fori(1, E // 2) as e2:
                for u in (0, 1):
                    sp.wait_ge(*PE.at("out3", 2 * e2 + u - 2))
                    load(2 * e2 + u, u)

        @block.tensor
        def _(pe):
            ln_tensor(c, pe, V, A, PE, tp)
            pe.wait_ge(*V.at("ln_T2"))
            pe.wait_ge(*A.at("ln_T3"))
            pe.wait_ge(loaded, 80)
            for t in range(NT):
                last = nc.tensor.matmul(tp[0][:, E * t:E * t + E], c.xnT[:, P * t:P * t + P], emb[:, :], start=True, stop=True)
            last.then_inc(PE.did("sim"), 1)
            pe.wait_ge(*V.at("emb2"))
            nc.tensor.matmul(tp[1][:, 0:E], ones[:, :], emb2[:, :], start=True, stop=True).then_inc(PE.did("te"), 1)
            pe.wait_ge(*V.at("weights"))
            for i in range(4):
                if i >= 2:
                    pe.wait_ge(*(A if i % 2 else V).at(f"wT{i - 2}"))
                for j in range(4):
                    last = nc.tensor.transpose(tp[i % 2][0:E, P * j:P * j + P], weights[:, 4 * i + j, :], c.ident[:, :])
                last.then_inc(PE.did(f"wT{i}"), 1)
            pe.wait_ge(*V.at("wT2"))
            pe.wait_ge(*A.at("wT3"))
            for i in range(4):
                if i >= 2:
                    pe.wait_ge(*V.at(f"b2_{i - 2}"))
                for j in range(4):
                    t = 4 * i + j
                    last = nc.tensor.matmul(po[:, i % 2, P * j:P * j + P], weightsT[:, P * t:P * t + P], b2[:, :],
                                            start=True, stop=True)
                last.then_inc(PE.did(f"b2_{i}"), 1)
            with pe.Fori(0, E // 2) as e2:
                for u in (0, 1):
                    e = 2 * e2 + u
                    pe.wait_ge(w_in[u], 32 * e2 + 32)
                    for i in range(4):
                        for k in range(FC):
                            if i or u:
                                pe.wait_ge(*A.at(f"g{i - 1}{k}" if i else f"g3{k}", e if i else e - 1))
                            else:
                                pe.wait_ge(*A.before(f"g3{k}", e))
                            nc.tensor.matmul(ph[:, k, :], w1[:, u, P * k:P * k + P], c.xnT[:, 512 * i:512 * i + 512],
                                             start=True, stop=True).then_inc(PE.did(f"h{i}{k}"), 1)
                        pe.wait_ge(*A.at(f"g{i}{FC - 1}", e))
                        pe.wait_ge(*(V.at(f"x{i - 2}", e) if i >= 2 else V.before(f"x{i + 2}", e)))
                        for j in range(4):
                            for k in range(FC):
                                last = nc.tensor.matmul(po[:, i % 2, P * j:P * j + P], g[:, i % 2, k, P * j:P * j + P],
                                                        w2[:, u, k, :], start=(k == 0), stop=(k == FC - 1))
                        last.then_inc(PE.did(f"out{i}"), 1)

        @block.vector
        def _(dve):
            nc.vector.memset(ones[:, :], 1.0).then_inc(V.did("ones"), 1)
            dve.wait_ge(loaded, 80)
            nc.vector.tensor_scalar(bonus[:, :], te[:, :], 0.1, None, ALU.mult).then_inc(V.did("bonus"), 1)
            ln_vector(c, dve, V, A, PE, tp)
            nc.vector.tensor_tensor(emb2[:, :], emb[:, :], emb[:, :], ALU.mult).then_inc(V.did("emb2"), 1)
            dve.wait_ge(*PE.at("sim"))
            nc.vector.tensor_copy(sim[:, :, :], tp[0][:, 0:NT * E].rearrange("p (t e) -> p t e", e=E)).then_inc(V.did("sim"), 1)
            dve.wait_ge(*A.at("sq"))
            nc.vector.tensor_reduce(tn[:, :], c.sq[:, :, :], AX.X, ALU.add).then_inc(V.did("tn"), 1)
            dve.wait_ge(*A.at("tn"))
            nc.vector.tensor_scalar(tn[:, :], tn[:, :], 1e-8, None, ALU.add).then_inc(V.did("tn_eps"), 1)
            dve.wait_ge(*V.at("tn_eps"))
            nc.vector.reciprocal(rt[:, :], tn[:, :]).then_inc(V.did("rt"), 1)
            dve.wait_ge(*PE.at("te"))
            nc.vector.tensor_copy(te[:, :], tp[1][:, 0:E]).then_inc(V.did("te"), 1)
            dve.wait_ge(*A.at("te"))
            nc.vector.tensor_scalar(te[:, :], te[:, :], 1e-8, None, ALU.add).then_inc(V.did("te_eps"), 1)
            dve.wait_ge(*V.at("te_eps"))
            nc.vector.reciprocal(re[:, :], te[:, :]).then_inc(V.did("re"), 1)
            dve.wait_ge(*V.at("re"))
            nc.vector.tensor_tensor(score[:, :, :], sim[:, :, :], wide(rt[:, :]), ALU.mult).then_inc(V.did("s1"), 1)
            dve.wait_ge(*V.at("s1"))
            nc.vector.tensor_tensor(score[:, :, :], score[:, :, :], each(re), ALU.mult).then_inc(V.did("s2"), 1)
            dve.wait_ge(*V.at("s2"))
            nc.vector.tensor_tensor(score[:, :, :], score[:, :, :], each(bonus), ALU.add).then_inc(V.did("s3"), 1)
            for t in range(NT):
                nc.vector.max(top[:, t, :], sim[:, t, :]).then_inc(V.did(f"top{t}"), 1)
            dve.wait_ge(*V.at(f"top{NT - 1}"))
            for t in range(NT):
                nc.vector.max_index(topi[:, t, :], top[:, t, :], sim[:, t, :]).then_inc(V.did(f"topi{t}"), 1)
            dve.wait_ge(*V.at(f"topi{NT - 1}"))
            nc.vector.tensor_copy(last_i[:, :].unsqueeze(2), topi[:, :, 7:8]).then_inc(V.did("last"), 1)
            dve.wait_ge(*V.at("last"))
            nc.vector.tensor_tensor(hit[:, :, :], iota[:, :, :], wide(last_i[:, :]), ALU.is_equal).then_inc(V.did("hit"), 1)
            dve.wait_ge(*V.at("hit"))
            nc.vector.scalar_tensor_tensor(out=score[:, :, :], in0=hit[:, :, :], scalar=OUT, in1=score[:, :, :],
                                           op0=ALU.mult, op1=ALU.add).then_inc(V.did("s4"), 1)
            dve.wait_ge(*V.at("s4"))
            for t in range(NT):
                nc.vector.max(best[:, t, :], score[:, t, :]).then_inc(V.did(f"best{t}"), 1)
            dve.wait_ge(*V.at(f"best{NT - 1}"))
            for t in range(NT):
                nc.vector.max_index(besti[:, t, :], best[:, t, :], score[:, t, :]).then_inc(V.did(f"besti{t}"), 1)
            dve.wait_ge(*V.at(f"besti{NT - 1}"))
            nc.vector.tensor_copy(bi[:, :, :], besti[:, :, 0:2]).then_inc(V.did("bi"), 1)
            nc.vector.tensor_tensor(gap[:, :].unsqueeze(2), best[:, :, 1:2], best[:, :, 0:1], ALU.subtract).then_inc(V.did("gap"), 1)
            dve.wait_ge(*A.at("exp"))
            nc.vector.tensor_scalar(den[:, :], ex[:, :], 1.0, None, ALU.add).then_inc(V.did("den"), 1)
            dve.wait_ge(*V.at("den"))
            nc.vector.reciprocal(wt[:, :, 0:1], den[:, :].unsqueeze(2)).then_inc(V.did("w1"), 1)
            dve.wait_ge(*V.at("w1"))
            nc.vector.tensor_tensor(wt[:, :, 1:2], wt[:, :, 0:1], ex[:, :].unsqueeze(2), ALU.mult).then_inc(V.did("w2"), 1)
            nc.vector.tensor_tensor(hit1[:, :, :], iota[:, :, :], bi[:, :, 0:1].broadcast_to([P, NT, E]), ALU.is_equal)\
                .then_inc(V.did("hit1"), 1)
            nc.vector.tensor_tensor(hit2[:, :, :], iota[:, :, :], bi[:, :, 1:2].broadcast_to([P, NT, E]), ALU.is_equal)\
                .then_inc(V.did("hit2"), 1)
            dve.wait_ge(*V.at("hit2"))
            nc.vector.tensor_tensor(part1[:, :, :], hit1[:, :, :], wt[:, :, 0:1].broadcast_to([P, NT, E]), ALU.mult)\
                .then_inc(V.did("part1"), 1)
            nc.vector.tensor_tensor(part2[:, :, :], hit2[:, :, :], wt[:, :, 1:2].broadcast_to([P, NT, E]), ALU.mult)\
                .then_inc(V.did("part2"), 1)
            dve.wait_ge(*V.at("part2"))
            nc.vector.tensor_tensor(weights[:, :, :], part1[:, :, :], part2[:, :, :], ALU.add).then_inc(V.did("weights"), 1)
            for i in (0, 2):
                dve.wait_ge(*PE.at(f"wT{i}"))
                nc.vector.tensor_copy(weightsT[:, 512 * i:512 * i + 512], tp[0][0:E, :]).then_inc(V.did(f"wT{i}"), 1)
            for i in range(4):
                dve.wait_ge(*PE.at(f"b2_{i}"))
                xs = c.x[:, 4 * i:4 * i + 4, :].rearrange("p i d -> p (i d)")
                nc.vector.tensor_tensor(xs, po[:, i % 2, :], xs, ALU.add).then_inc(V.did(f"b2_{i}"), 1)
            dve.wait_ge(*V.at("b2_3"))
            with dve.Fori(0, E // 2) as e2:
                for u in (0, 1):
                    e = 2 * e2 + u
                    for i in range(4):
                        dve.wait_ge(*V.before(f"x{i}", e))
                        dve.wait_ge(*PE.at(f"out{i}", e))
                        for j in range(4):
                            xs = c.x[:, 4 * i + j, :]
                            last = nc.vector.scalar_tensor_tensor(out=xs, in0=po[:, i % 2, P * j:P * j + P],
                                                                  scalar=weights[:, 4 * i + j, bass.ds(e, 1)], in1=xs,
                                                                  op0=ALU.mult, op1=ALU.add)
                        last.then_inc(V.did(f"x{i}"), 1)

        @block.scalar
        def _(act):
            ln_scalar(c, act, V, A, PE, tp)
            act.wait_ge(*V.at("ln_xn"))
            nc.scalar.activation(c.sq[:, :, :], c.xn[:, :, :], ACT.Square).then_inc(A.did("sq"), 1)
            act.wait_ge(*V.at("tn"))
            nc.scalar.activation(tn[:, :], tn[:, :], ACT.Sqrt).then_inc(A.did("tn"), 1)
            act.wait_ge(*V.at("te"))
            nc.scalar.activation(te[:, :], te[:, :], ACT.Sqrt).then_inc(A.did("te"), 1)
            act.wait_ge(*V.at("gap"))
            nc.scalar.activation(ex[:, :], gap[:, :], ACT.Exp).then_inc(A.did("exp"), 1)
            for i in (1, 3):
                act.wait_ge(*PE.at(f"wT{i}"))
                nc.scalar.copy(weightsT[:, 512 * i:512 * i + 512], tp[1][0:E, :]).then_inc(A.did(f"wT{i}"), 1)
            with act.Fori(0, E // 2) as e2:
                for u in (0, 1):
                    e = 2 * e2 + u
                    act.wait_ge(*A.before("g33", e))
                    nc.scalar.copy(b1e[:, u, :], b1[:, bass.ds(e, 1), :].rearrange("p a k -> p (a k)")).then_inc(A.did("b1e"), 1)
                    act.wait_ge(*A.at("b1e", e))
                    for i in range(4):
                        for k in range(FC):
                            if k == 0:
                                act.wait_ge(*(PE.at(f"out{i - 2}", e) if i >= 2 else PE.before(f"out{i + 2}", e)))
                            act.wait_ge(*PE.at(f"h{i}{k}", e))
                            nc.scalar.activation(g[:, i % 2, k, :], ph[:, k, :], ACT.Gelu, bias=b1e[:, u, k:k + 1]).then_inc(A.did(f"g{i}{k}"), 1)


def selective_scan_layer(c, name):
    N, R, HALF = 16, 64, 2
    DT_MIN, DT_MAX = 0.001, 0.1
    with Stage(c, name) as s:
        nc, a = c.nc, c.a
        cols = s.sb("cols", [P, 2])
        win = s.sb("win", [P, 4 * D])
        taps, cb = s.sb("taps", [P, HALF, 4]), s.sb("cb", [P, HALF])
        wx, wdt = s.sb("wx", [P, HALF, R + 2 * N]), s.sb("wdt", [R, HALF * P])
        bdt, dp = s.sb("bdt", [P, HALF]), s.sb("dp", [P, HALF])
        la, na = s.sb("la", [P, HALF, N]), s.sb("na", [P, HALF, N])
        wo = s.sb("wo", [P, HALF, D])
        zeros = s.sb("zeros", [P, P])
        hT = s.sb("hT", [P, TOK])
        xi = s.sb("xi", [P, HALF, TOK])
        zs = s.sb("zs", [P, HALF, TOK])
        cv = s.sb("u", [P, HALF, TOK])
        dt = s.sb("dt", [P, HALF, TOK])
        xbc = s.sb("xbc", [R + 2 * N, TOK])
        bb, cc = s.sb("bb", [P, 2, TOK]), s.sb("cc", [P, 2, TOK])
        da, db = s.sb("da", [P, HALF, TOK]), s.sb("db", [P, HALF, TOK])
        ps = s.ps("all", [P, 8, 512])
        loaded, stored = s.sem("loaded"), s.sem("stored")
        b_in, c_in = [s.sem("b_in0"), s.sem("b_in1")], [s.sem("c_in0"), s.sem("c_in1")]
        n1 = Norm(c, turned=False)
        n2 = Norm(c, "in", c.xn, xi[:, 0, :].rearrange("p (t d) -> p t d", d=D), hT, cols[:, 0:1], cols[:, 1:2])
        quads = [(hf, i) for hf in range(HALF) for i in range(4)]
        V = Steps(s.sem("vector_steps"),
                  (1, ["zeros", "na", "da0"] + n1.V + n2.V + [f"xi{n}" for n in range(8)] +
                   [f"cv{hf}{k}" for hf in range(HALF) for k in (3, 2, 1, 0)] + ["xbc0", "xbc2"] +
                   [f"pre{n}" for n in range(8)] + ["low", "dt", "dtu"]),
                  (N, ["db0", "scan0", "db1", "scan1"], 2), (1, ["skip0", "gate0", "skip1", "gate1", "res"] + [f"x{i}" for i in range(4)]))
        A = Steps(s.sem("scalar_steps"),
                  (1, ["la"] + n1.A + n2.A + [f"z{n}" for n in range(8)] + ["u0", "u1", "xbc1", "xbc3", "e", "ln"]),
                  (N, ["da0", "da1"], 2))
        G = Steps(s.sem("gpsimd_steps"), (N, ["hc0", "hc1"], 2))
        PE = Steps(s.sem("tensor_steps"),
                   (1, n2.P + [f"in{n}" for n in range(16)] + [f"xbc{i}" for i in range(4)] + [f"dt{n}" for n in range(8)]),
                   (N, ["y0", "y1"], 2), (1, ["ysum"] + [f"out{i}" for i in range(4)]))
        tp = [ps[:, 6 + i, :] for i in (0, 1)]
        seq = lambda m: m.rearrange("p (b q) -> p b q", q=S)
        block = s.block()

        @block.sync
        def _(sp):
            for dst, src in ((cols[:, :], a[f"{name}_cols"]), (win[:, :], a[f"{name}_W_inT"]),
                             (taps[:, :, :], a[f"{name}_conv_w"].rearrange("(h p) k -> p h k", p=P)),
                             (wx[:, :, :], a[f"{name}_W_xT"].rearrange("(h p) n -> p h n", p=P)),
                             (wdt[:, :], a[f"{name}_W_dtT"]), (la[:, :, :], a[f"{name}_log_A"].rearrange("(h p) n -> p h n", p=P)),
                             (wo[:, :, :], a[f"{name}_W_outT"].rearrange("(h p) n -> p h n", p=P)),
                             (cb[:, :], a[f"{name}_vecs"][0]), (bdt[:, :], a[f"{name}_vecs"][1]), (dp[:, :], a[f"{name}_vecs"][2])):
                sp.dma_start(dst, src).then_inc(loaded, 16)
            sp.wait_ge(*V.at("xbc2"))
            sp.wait_ge(*A.at("xbc3"))
            sp.dma_start(a["scratch_rows"], xbc[R:R + 2 * N, :]).then_inc(stored, 16)
            sp.wait_ge(stored, 16)

            def load(n, u):
                sp.dma_start(bb[:, u, :], a["scratch_rows"][bass.ds(n, 1), :].broadcast_to([P, TOK])).then_inc(b_in[u], 16)
                sp.dma_start(cc[:, u, :], a["scratch_rows"][bass.ds(n + N, 1), :].broadcast_to([P, TOK])).then_inc(c_in[u], 16)

            load(0, 0)
            load(1, 1)
            with sp.Fori(1, N // 2) as n2_:
                for u in (0, 1):
                    sp.wait_ge(*G.at("hc1", 2 * n2_ + u - 2))
                    load(2 * n2_ + u, u)

        @block.tensor
        def _(pe):
            ln_tensor(c, pe, V, A, PE, tp, n2)
            pe.wait_ge(*V.at("in_T2"))
            pe.wait_ge(*A.at("in_T3"))
            pe.wait_ge(loaded, 160)
            order = [(blk, i) for pair in (0, 1) for i in range(4) for blk in (pair, 2 + pair)]
            for n, (blk, i) in enumerate(order):
                if n >= 4:
                    pe.wait_ge(*(V.at(f"xi{(n - 4) // 2}") if blk < 2 else A.at(f"z{(n - 4) // 2}")))
                nc.tensor.matmul(ps[:, (0 if blk < 2 else 2) + i % 2, :], win[:, P * blk:P * blk + P], hT[:, 512 * i:512 * i + 512],
                                 start=True, stop=True).then_inc(PE.did(f"in{n}"), 1)
            pe.wait_ge(*A.at("u1"))
            for i in range(4):
                if i >= 2:
                    pe.wait_ge(*(A if i % 2 else V).at(f"xbc{i - 2}"))
                for hf in range(HALF):
                    last = nc.tensor.matmul(ps[0:R + 2 * N, 4 + i % 2, :], wx[:, hf, :], cv[:, hf, 512 * i:512 * i + 512],
                                            start=(hf == 0), stop=(hf == 1))
                last.then_inc(PE.did(f"xbc{i}"), 1)
            pe.wait_ge(*V.at("xbc2"))
            pe.wait_ge(*A.at("xbc3"))
            for n, (hf, i) in enumerate(quads):
                if n >= 4:
                    pe.wait_ge(*V.at(f"pre{n - 4}"))
                nc.tensor.matmul(ps[:, n % 4, :], wdt[:, P * hf:P * hf + P], xbc[0:R, 512 * i:512 * i + 512],
                                 start=True, stop=True).then_inc(PE.did(f"dt{n}"), 1)
            pe.wait_ge(*V.at("dt"))
            for b in range(8):
                nc.tensor.matmul(ps[:, b, :], zeros[:, :], hT[:, 0:512], start=True, stop=False, skip_group_check=True)
            with pe.Fori(0, N // 2) as n2_:
                for u in (0, 1):
                    n = 2 * n2_ + u
                    for hf in range(HALF):
                        pe.wait_ge(*G.at(f"hc{hf}", n))
                        for i in range(4):
                            last = nc.tensor.matmul(ps[:, 4 * hf + i, :], c.ident[:, :], db[:, hf, 512 * i:512 * i + 512],
                                                    start=False, stop=False, skip_group_check=True)
                        last.then_inc(PE.did(f"y{hf}"), 1)
            for b in range(8):
                last = nc.tensor.matmul(ps[:, b, :], zeros[:, :], hT[:, 0:512], start=False, stop=True, skip_group_check=True)
            last.then_inc(PE.did("ysum"), 1)
            pe.wait_ge(*V.at("gate1"))
            for i in range(4):
                for j in range(4):
                    t = 4 * i + j
                    for hf in range(HALF):
                        last = nc.tensor.matmul(ps[:, i, P * j:P * j + P], xi[:, hf, P * t:P * t + P], wo[:, hf, :],
                                                start=(hf == 0), stop=(hf == 1))
                last.then_inc(PE.did(f"out{i}"), 1)

        @block.gpsimd
        def _(pool):
            with pool.Fori(0, N // 2) as n2_:
                for u in (0, 1):
                    n = 2 * n2_ + u
                    pool.wait_ge(c_in[u], 16 * n2_ + 16)
                    for hf in range(HALF):
                        pool.wait_ge(*V.at(f"scan{hf}", n))
                        nc.gpsimd.tensor_tensor(db[:, hf, :], db[:, hf, :], cc[:, u, :], ALU.mult).then_inc(G.did(f"hc{hf}"), 1)

        @block.vector
        def _(dve):
            nc.vector.memset(zeros[:, :], 0.0).then_inc(V.did("zeros"), 1)
            dve.wait_ge(*A.at("la"))
            nc.vector.tensor_scalar(na[:, :, :], la[:, :, :], -1.0, None, ALU.mult).then_inc(V.did("na"), 1)
            nc.vector.memset(da[:, :, :], 0.0).then_inc(V.did("da0"), 1)
            ln_vector(c, dve, V, A, PE, tp, n1)
            dve.wait_ge(*V.at("ln_xn"))
            ln_vector(c, dve, V, A, PE, tp, n2)
            order = [(hf, i) for hf in (0, 1) for i in range(4)]
            for n, (hf, i) in enumerate(order):
                dve.wait_ge(*PE.at(f"in{2 * n}"))
                nc.vector.tensor_copy(xi[:, hf, 512 * i:512 * i + 512], ps[:, i % 2, :]).then_inc(V.did(f"xi{n}"), 1)
            dve.wait_ge(*V.at("xi7"))
            for hf in range(HALF):
                x3, u3 = seq(xi[:, hf, :]), seq(cv[:, hf, :])
                nc.vector.tensor_scalar(cv[:, hf, :], xi[:, hf, :], taps[:, hf, 3:4], cb[:, hf:hf + 1], ALU.mult, ALU.add)\
                    .then_inc(V.did(f"cv{hf}3"), 1)
                for k in (2, 1, 0):
                    m = 3 - k
                    dve.wait_ge(*V.at(f"cv{hf}{k + 1}"))
                    nc.vector.scalar_tensor_tensor(out=u3[:, :, m:S], in0=x3[:, :, 0:S - m], scalar=taps[:, hf, k:k + 1],
                                                   in1=u3[:, :, m:S], op0=ALU.mult, op1=ALU.add).then_inc(V.did(f"cv{hf}{k}"), 1)
            for i in (0, 2):
                dve.wait_ge(*PE.at(f"xbc{i}"))
                nc.vector.tensor_copy(xbc[:, 512 * i:512 * i + 512], ps[0:R + 2 * N, 4, :]).then_inc(V.did(f"xbc{i}"), 1)
            for n, (hf, i) in enumerate(quads):
                dve.wait_ge(*PE.at(f"dt{n}"))
                nc.vector.tensor_scalar(dt[:, hf, 512 * i:512 * i + 512], ps[:, n % 4, :], bdt[:, hf:hf + 1], 0.0, ALU.add, ALU.min)\
                    .then_inc(V.did(f"pre{n}"), 1)
            dve.wait_ge(*A.at("ln"))
            nc.vector.tensor_scalar(dt[:, :, :], dt[:, :, :], DT_MIN, DT_MIN, ALU.add, ALU.max).then_inc(V.did("low"), 1)
            dve.wait_ge(*V.at("low"))
            nc.vector.tensor_scalar(dt[:, :, :], dt[:, :, :], DT_MAX, None, ALU.min).then_inc(V.did("dt"), 1)
            dve.wait_ge(*V.at("dt"))
            nc.vector.tensor_tensor(xi[:, :, :], dt[:, :, :], cv[:, :, :], ALU.mult).then_inc(V.did("dtu"), 1)
            with dve.Fori(0, N // 2) as n2_:
                for u in (0, 1):
                    n = 2 * n2_ + u
                    dve.wait_ge(b_in[u], 16 * n2_ + 16)
                    for hf in range(HALF):
                        dve.wait_ge(*PE.before(f"y{hf}", n))
                        dve.wait_ge(*V.before("scan1", n))
                        nc.vector.tensor_tensor(db[:, hf, :], xi[:, hf, :], bb[:, u, :], ALU.mult).then_inc(V.did(f"db{hf}"), 1)
                        dve.wait_ge(*V.at(f"db{hf}", n))
                        dve.wait_ge(*A.at(f"da{hf}", n))
                        nc.vector.tensor_tensor_scan(db[:, hf, :], da[:, hf, :], db[:, hf, :], 0.0, ALU.mult, ALU.add)\
                            .then_inc(V.did(f"scan{hf}"), 1)
            for hf in range(HALF):
                dve.wait_ge(*PE.at("ysum"))
                nc.vector.scalar_tensor_tensor(out=db[:, hf, :], in0=cv[:, hf, :], scalar=dp[:, hf:hf + 1],
                                               in1=ps[:, 4 * hf:4 * hf + 4, :].rearrange("p i n -> p (i n)"),
                                               op0=ALU.mult, op1=ALU.add).then_inc(V.did(f"skip{hf}"), 1)
                dve.wait_ge(*V.at(f"skip{hf}"))
                nc.vector.tensor_tensor(xi[:, hf, :], db[:, hf, :], zs[:, hf, :], ALU.mult).then_inc(V.did(f"gate{hf}"), 1)
            nc.vector.tensor_tensor(c.x[:, :, :], c.x[:, :, :], c.xn[:, :, :], ALU.add).then_inc(V.did("res"), 1)
            dve.wait_ge(*V.at("res"))
            for i in range(4):
                dve.wait_ge(*PE.at(f"out{i}"))
                xs = c.x[:, 4 * i:4 * i + 4, :].rearrange("p i d -> p (i d)")
                nc.vector.tensor_tensor(xs, ps[:, i, :], xs, ALU.add).then_inc(V.did(f"x{i}"), 1)

        @block.scalar
        def _(act):
            act.wait_ge(loaded, 160)
            nc.scalar.activation(la[:, :, :], la[:, :, :], ACT.Exp).then_inc(A.did("la"), 1)
            ln_scalar(c, act, V, A, PE, tp, n1)
            ln_scalar(c, act, V, A, PE, tp, n2)
            for n, (hf, i) in enumerate(quads):
                act.wait_ge(*PE.at(f"in{2 * n + 1}"))
                nc.scalar.activation(zs[:, hf, 512 * i:512 * i + 512], ps[:, 2 + i % 2, :], ACT.Silu).then_inc(A.did(f"z{n}"), 1)
            for hf in range(HALF):
                act.wait_ge(*V.at(f"cv{hf}0"))
                nc.scalar.activation(cv[:, hf, :], cv[:, hf, :], ACT.Silu).then_inc(A.did(f"u{hf}"), 1)
            for i in (1, 3):
                act.wait_ge(*PE.at(f"xbc{i}"))
                nc.scalar.copy(xbc[:, 512 * i:512 * i + 512], ps[0:R + 2 * N, 5, :]).then_inc(A.did(f"xbc{i}"), 1)
            act.wait_ge(*V.at("pre7"))
            nc.scalar.activation(dt[:, :, :], dt[:, :, :], ACT.Exp).then_inc(A.did("e"), 1)
            act.wait_ge(*A.at("e"))
            nc.scalar.activation(dt[:, :, :], dt[:, :, :], ACT.Ln, bias=1.0).then_inc(A.did("ln"), 1)
            act.wait_ge(*V.at("dt"))
            with act.Fori(0, N // 2) as n2_:
                for u in (0, 1):
                    n = 2 * n2_ + u
                    for hf in range(HALF):
                        act.wait_ge(*V.before(f"scan{hf}", n))
                        nc.scalar.activation(seq(da[:, hf, :])[:, :, 1:S], seq(dt[:, hf, :])[:, :, 1:S], ACT.Exp,
                                             scale=na[:, hf, bass.ds(n, 1)]).then_inc(A.did(f"da{hf}"), 1)


def chosen_adapters(c, name):
    E, HID, R = 8, 32, 64
    with Stage(c, name) as s:
        nc, a = c.nc, c.a
        wd1, bd1 = s.sb("wd1", [P, 2 * P]), s.sb("bd1", [P, 2])
        wd2, bd2 = s.sb("wd2", [P, 2, D]), s.sb("bd2", [P, E])
        wad, bad = s.sb("wad", [P, 4 * P]), s.sb("bad", [P, 4])
        wau, bau = s.sb("wau", [P, 4, D]), s.sb("bau", [E, D])
        wb, bb = s.sb("wb", [P, D]), s.sb("bb", [P, D])
        rank, diag = s.sb("rank", [P, E, B]), s.sb("diag", [E, E])
        ones = s.sb("ones", [P, P])
        hid = s.sb("hid", [P, 2, 512])
        diff, sq = s.sb("diff", [P, 2, 512]), s.sb("sq", [P, 2, 512])
        loss = s.sb("loss", [P, E, B])
        full = s.sb("full", [P, E, B])
        least, vote, most = s.sb("least", [P, B]), s.sb("vote", [P, E, B]), s.sb("most", [P, B])
        hot = s.sb("hot", [P, E, B])
        mask = s.sb("mask", [P, 4, B])
        own, hot8 = s.sb("own", [E, E, B]), s.sb("hot8", [E, B])
        xg, hg = s.sb("xg", [P, 512]), s.sb("hg", [E, 512])
        ad, adm = s.sb("ad", [P, 4, 512]), s.sb("adm", [P, 4, 512])
        turn = s.ps("turn", [P, 2, 512])
        ps = s.ps("ps", [P, 6, 512])
        loaded = s.sem("loaded")
        V = Steps(s.sem("vector_steps"), (1, LN_V + ["ones", "bb"]),
                  (4, sum([[f"diff{e}", f"loss{e}"] for e in range(E)], [])),
                  (1, ["full", "least", "vote", "votes", "most", "hot", "mask0", "mask1", "own", "hot8"]),
                  (4, ["hg"] + [f"adm{k}" for k in range(4)] + ["x"]))
        A = Steps(s.sem("scalar_steps"), (1, LN_A), (4, ["hid0", "hid1"] + [f"sq{e}" for e in range(E)]),
                  (4, ["xg"] + [f"ad{k}" for k in range(4)]))
        PE = Steps(s.sem("tensor_steps"), (1, LN_P), (4, ["hid0", "hid1"] + [f"rec{e}" for e in range(E)]),
                   (1, ["full"]), (4, [f"ad{k}" for k in range(4)] + ["out"]))
        tp = [turn[:, i, :] for i in (0, 1)]
        seq = lambda m: m.rearrange("p (b q) -> p b q", q=S)
        block = s.block()

        @block.sync
        def _(sp):
            for dst, src in ((wd1, "wd1"), (bd1, "bd1"), (bd2, "bd2"), (wad, "wad"), (bad, "bad"), (bau, "bau"), (wb, "wb")):
                sp.dma_start(dst[:, :], a[f"{name}_{src}"]).then_inc(loaded, 16)
            sp.dma_start(wd2[:, :, :], a[f"{name}_wd2"].rearrange("(c p) d -> p c d", p=P)).then_inc(loaded, 16)
            sp.dma_start(wau[:, :, :], a[f"{name}_wau"].rearrange("(c p) d -> p c d", p=P)).then_inc(loaded, 16)
            sp.dma_start(bb[:, :], a[f"{name}_bb"].broadcast_to([P, D])).then_inc(loaded, 16)
            sp.dma_start(rank[:, :, :], a["c_rank"]).then_inc(loaded, 16)
            sp.dma_start(diag[:, :], a["c_ident"][0:E, 0:E]).then_inc(loaded, 16)

        @block.tensor
        def _(pe):
            ln_tensor(c, pe, V, A, PE, tp)
            pe.wait_ge(*V.at("ln_T2"))
            pe.wait_ge(*A.at("ln_T3"))
            pe.wait_ge(loaded, 192)
            with pe.Fori(0, 4) as i:
                pe.wait_ge(*A.before("sq7", i))
                for k in (0, 1):
                    nc.tensor.matmul(ps[:, k, :], wd1[:, P * k:P * k + P], c.xnT[:, bass.ds(512 * i, 512)], start=True, stop=True)\
                        .then_inc(PE.did(f"hid{k}"), 1)
                for e in range(E):
                    if e % 4 == 0:
                        pe.wait_ge(*A.at(f"hid{e // 4}", i))
                    pe.wait_ge(*(V.at(f"diff{e - 4}", i) if e >= 4 else V.before(f"diff{e + 4}", i)))
                    lo = HID * (e % 4)
                    nc.tensor.matmul(ps[:, 2 + e % 4, :], wd2[lo:lo + HID, e // 4, :], hid[lo:lo + HID, e // 4, :],
                                     start=True, stop=True, tile_position=(lo, 0)).then_inc(PE.did(f"rec{e}"), 1)
            pe.wait_ge(*V.at("loss7", 3))
            nc.tensor.matmul(ps[:, 0, 0:E * B], ones[:, :], loss[:, :, :].rearrange("p e b -> p (e b)"), start=True, stop=True)\
                .then_inc(PE.did("full"), 1)
            pe.wait_ge(*V.at("hot8"))
            with pe.Fori(0, 4) as i:
                for k in range(4):
                    pe.wait_ge(*A.before(f"ad{k}", i))
                    nc.tensor.matmul(ps[:, k, :], wad[:, P * k:P * k + P], c.xnT[:, bass.ds(512 * i, 512)], start=True, stop=True)\
                        .then_inc(PE.did(f"ad{k}"), 1)
                pe.wait_ge(*A.at("xg", i))
                pe.wait_ge(*V.at("adm3", i))
                for j in range(4):
                    part = slice(P * j, P * j + P)
                    nc.tensor.matmul(ps[:, 4, part], xg[:, part], wb[:, :], start=True, stop=False)
                    for k in range(4):
                        nc.tensor.matmul(ps[:, 4, part], adm[:, k, part], wau[:, k, :], start=False, stop=False)
                    last = nc.tensor.matmul(ps[:, 4, part], hg[:, part], bau[:, :], start=False, stop=True)
                last.then_inc(PE.did("out"), 1)

        @block.vector
        def _(dve):
            ln_vector(c, dve, V, A, PE, tp)
            dve.wait_ge(loaded, 192)
            nc.vector.memset(ones[:, :], 1.0).then_inc(V.did("ones"), 1)
            nc.vector.tensor_tensor(c.x[:, :, :], c.x[:, :, :], bb[:, :].unsqueeze(1).broadcast_to([P, NT, D]), ALU.add)\
                .then_inc(V.did("bb"), 1)
            dve.wait_ge(*A.at("ln_T3"))
            dve.wait_ge(*V.at("ln_T2"))
            with dve.Fori(0, 4) as i:
                for e in range(E):
                    dve.wait_ge(*(A.at(f"sq{e - 2}", i) if e >= 2 else A.before(f"sq{e + 6}", i)))
                    dve.wait_ge(*PE.at(f"rec{e}", i))
                    nc.vector.scalar_tensor_tensor(out=diff[:, e % 2, :], in0=ps[:, 2 + e % 4, :], scalar=bd2[:, e:e + 1],
                                                   in1=c.xnT[:, bass.ds(512 * i, 512)], op0=ALU.add, op1=ALU.subtract)\
                        .then_inc(V.did(f"diff{e}"), 1)
                    dve.wait_ge(*A.at(f"sq{e}", i))
                    nc.vector.tensor_reduce(loss[:, e, bass.ds(8 * i, 8)], seq(sq[:, e % 2, :]), AX.X, ALU.add)\
                        .then_inc(V.did(f"loss{e}"), 1)
            dve.wait_ge(*PE.at("full"))
            nc.vector.tensor_copy(full[:, :, :], ps[:, 0, 0:E * B].rearrange("p (e b) -> p e b", e=E)).then_inc(V.did("full"), 1)
            dve.wait_ge(*V.at("full"))
            nc.vector.tensor_reduce(least[:, :], full[:, :, :].rearrange("p e b -> p b e"), AX.X, ALU.min).then_inc(V.did("least"), 1)
            dve.wait_ge(*V.at("least"))
            nc.vector.tensor_tensor(vote[:, :, :], full[:, :, :], least[:, :].unsqueeze(1).broadcast_to([P, E, B]), ALU.is_equal)\
                .then_inc(V.did("vote"), 1)
            dve.wait_ge(*V.at("vote"))
            nc.vector.tensor_tensor(vote[:, :, :], vote[:, :, :], rank[:, :, :], ALU.mult).then_inc(V.did("votes"), 1)
            dve.wait_ge(*V.at("votes"))
            nc.vector.tensor_reduce(most[:, :], vote[:, :, :].rearrange("p e b -> p b e"), AX.X, ALU.max).then_inc(V.did("most"), 1)
            dve.wait_ge(*V.at("most"))
            nc.vector.tensor_tensor(hot[:, :, :], vote[:, :, :], most[:, :].unsqueeze(1).broadcast_to([P, E, B]), ALU.is_equal)\
                .then_inc(V.did("hot"), 1)
            dve.wait_ge(*V.at("hot"))
            pairs = hot[:, :, :].rearrange("p (k e) b -> p k e b", e=2)
            for e in (0, 1):
                nc.vector.tensor_copy(mask[R * e:R * e + R, :, :], pairs[R * e:R * e + R, :, e, :]).then_inc(V.did(f"mask{e}"), 1)
            nc.vector.tensor_tensor(own[:, :, :], hot[0:E, :, :], diag[:, :].unsqueeze(2).broadcast_to([E, E, B]), ALU.mult)\
                .then_inc(V.did("own"), 1)
            dve.wait_ge(*V.at("own"))
            nc.vector.tensor_reduce(hot8[:, :], own[:, :, :].rearrange("p e b -> p b e"), AX.X, ALU.add).then_inc(V.did("hot8"), 1)
            dve.wait_ge(*V.at("hot8"))
            with dve.Fori(0, 4) as i:
                dve.wait_ge(*V.before("x", i))
                nc.vector.tensor_copy(seq(hg[:, :]), hot8[:, bass.ds(8 * i, 8)].unsqueeze(2).broadcast_to([E, 8, S]))\
                    .then_inc(V.did("hg"), 1)
                for k in range(4):
                    dve.wait_ge(*A.at(f"ad{k}", i))
                    nc.vector.tensor_tensor(seq(adm[:, k, :]), seq(ad[:, k, :]),
                                            mask[:, k, bass.ds(8 * i, 8)].unsqueeze(2).broadcast_to([P, 8, S]), ALU.mult)\
                        .then_inc(V.did(f"adm{k}"), 1)
                dve.wait_ge(*PE.at("out", i))
                xs = c.x[:, bass.ds(4 * i, 4), :].rearrange("p i d -> p (i d)")
                nc.vector.tensor_tensor(xs, ps[:, 4, :], xs, ALU.add).then_inc(V.did("x"), 1)

        @block.scalar
        def _(act):
            ln_scalar(c, act, V, A, PE, tp)
            act.wait_ge(loaded, 192)
            with act.Fori(0, 4) as i:
                act.wait_ge(*V.before("loss7", i))
                for k in (0, 1):
                    act.wait_ge(*PE.at(f"hid{k}", i))
                    nc.scalar.activation(hid[:, k, :], ps[:, k, :], ACT.Relu, bias=bd1[:, k:k + 1]).then_inc(A.did(f"hid{k}"), 1)
                for e in range(E):
                    if e >= 2:
                        act.wait_ge(*V.at(f"loss{e - 2}", i))
                    act.wait_ge(*V.at(f"diff{e}", i))
                    nc.scalar.activation(sq[:, e % 2, :], diff[:, e % 2, :], ACT.Square).then_inc(A.did(f"sq{e}"), 1)
            with act.Fori(0, 4) as i:
                act.wait_ge(*V.before("x", i))
                nc.scalar.copy(xg[:, :], c.xnT[:, bass.ds(512 * i, 512)]).then_inc(A.did("xg"), 1)
                for k in range(4):
                    act.wait_ge(*PE.at(f"ad{k}", i))
                    nc.scalar.activation(ad[:, k, :], ps[:, k, :], ACT.Relu, bias=bad[:, k:k + 1]).then_inc(A.did(f"ad{k}"), 1)


BLK = 16
Q_V = ["amax", "scale", "rscale", "y", "a7", "a6", "a5", "b4", "b3", "b2", "b1", "q", "signed", "out"]
Q_A = ["abs", "sign"]


class Quant:

    def __init__(self, s, tag, n):
        self.n = n
        self.scale, self.rscale = s.sb(f"{tag}_scale", [P, n]), s.sb(f"{tag}_rscale", [P, n])
        self.y, self.ay, self.sign = (s.sb(f"{tag}_{k}", [P, n * BLK]) for k in ("y", "ay", "sign"))
        self.a, self.b = s.sb(f"{tag}_a", [P, n * BLK]), s.sb(f"{tag}_b", [P, n * BLK])


def quant_vector(c, dve, q, V, A, tag, t, src, dst):
    nc = c.nc
    blocks = lambda m: m.rearrange("p (n k) -> p n k", k=BLK)
    wide = lambda m: m[:, :].unsqueeze(2).broadcast_to([P, q.n, BLK])
    step = lambda n: (V.did(f"{tag}_{n}"), 1)

    def then(n):
        dve.wait_ge(*V.at(f"{tag}_{n}", t))

    nc.vector.tensor_reduce(q.scale[:, :], blocks(src), AX.X, ALU.max, apply_absolute_value=True).then_inc(*step("amax"))
    then("amax")
    nc.vector.tensor_scalar(q.scale[:, :], q.scale[:, :], 1.0 / 6.0, 1e-12, ALU.mult, ALU.max).then_inc(*step("scale"))
    then("scale")
    nc.vector.reciprocal(q.rscale[:, :], q.scale[:, :]).then_inc(*step("rscale"))
    then("rscale")
    nc.vector.tensor_tensor(blocks(q.y[:, :]), blocks(src), wide(q.rscale), ALU.mult).then_inc(*step("y"))
    dve.wait_ge(*A.at(f"{tag}_abs", t))
    nc.vector.tensor_scalar(q.a[:, :], q.ay[:, :], 5.0, 2.0, ALU.is_gt, ALU.mult).then_inc(*step("a7"))
    then("a7")
    nc.vector.scalar_tensor_tensor(out=q.a[:, :], in0=q.ay[:, :], scalar=3.5, in1=q.a[:, :], op0=ALU.is_gt, op1=ALU.add)\
        .then_inc(*step("a6"))
    then("a6")
    nc.vector.scalar_tensor_tensor(out=q.a[:, :], in0=q.ay[:, :], scalar=2.5, in1=q.a[:, :], op0=ALU.is_gt, op1=ALU.add)\
        .then_inc(*step("a5"))
    nc.vector.tensor_scalar(q.b[:, :], q.ay[:, :], 1.75, None, ALU.is_gt).then_inc(*step("b4"))
    for n, middle in (("b3", 1.25), ("b2", 0.75), ("b1", 0.25)):
        then(f"b{int(n[1]) + 1}")
        nc.vector.scalar_tensor_tensor(out=q.b[:, :], in0=q.ay[:, :], scalar=middle, in1=q.b[:, :], op0=ALU.is_gt,
                                       op1=ALU.add).then_inc(*step(n))
    then("b1")
    nc.vector.scalar_tensor_tensor(out=q.a[:, :], in0=q.b[:, :], scalar=0.5, in1=q.a[:, :], op0=ALU.mult, op1=ALU.add)\
        .then_inc(*step("q"))
    then("q")
    dve.wait_ge(*A.at(f"{tag}_sign", t))
    nc.vector.tensor_tensor(q.a[:, :], q.a[:, :], q.sign[:, :], ALU.mult).then_inc(*step("signed"))
    then("signed")
    nc.vector.tensor_tensor(blocks(dst), blocks(q.a[:, :]), wide(q.scale), ALU.mult).then_inc(*step("out"))


def quant_scalar(c, act, q, V, A, tag, t):
    nc = c.nc
    act.wait_ge(*V.at(f"{tag}_y", t))
    nc.scalar.activation(q.ay[:, :], q.y[:, :], ACT.Abs).then_inc(A.did(f"{tag}_abs"), 1)
    nc.scalar.activation(q.sign[:, :], q.y[:, :], ACT.Sign).then_inc(A.did(f"{tag}_sign"), 1)


def quantised_ffn(c, name):
    I = 352
    IC = -(-I // P)
    IP = IC * P
    rest = I - (IC - 1) * P
    wide_ = [P, P, rest]
    with Stage(c, name) as s:
        nc, a = c.nc, c.a
        w = s.sb("w", [P, 2 * IP + I])
        wguT = s.sb("wguT", [P, 2, IP])
        wdT = s.sb("wdT", [P, IC, D])
        xq = s.sb("xq", [P, NT, D])
        xqT = s.sb("xqT", [P, TOK])
        qw, qx, qh = Quant(s, "qw", (2 * IP + I) // BLK), Quant(s, "qx", TOK // BLK), Quant(s, "qh", 4 * I // BLK)
        xg = s.sb("xg", [P, 512])
        gate = s.sb("gate", [P, 4, I])
        hh, hq = s.sb("hh", [P, 4, I]), s.sb("hq", [P, 4, I])
        hT = s.sb("hT", [P, IC, 512])
        ps = s.ps("all", [P, 8, 512])
        loaded = s.sem("loaded")
        V = Steps(s.sem("vector_steps"), (1, named("w", Q_V) + ["wgT", "wdT"] + Norm(c, turned=False).V + named("x", Q_V) + ["xT0", "xT2"]),
                  (4, [f"h{j}" for j in range(4)] + named("h", Q_V) + ["hT0", "hT2", "x"]))
        A = Steps(s.sem("scalar_steps"), (1, named("w", Q_A) + ["wuT"] + Norm(c, turned=False).A + named("x", Q_A) + ["xT1", "xT3"]),
                  (4, ["xg"] + [f"silu{j}" for j in range(4)] + named("h", Q_A) + ["hT1"]))
        PE = Steps(s.sem("tensor_steps"), (1, ["wgT", "wuT", "wdT"] + [f"xT{i}" for i in range(4)]),
                   (4, [f"gu{j}" for j in range(4)] + [f"hT{k}" for k in range(IC)] + ["out"]))
        n1 = Norm(c, turned=False)
        flat = lambda m: m[:, :, :].rearrange("p i k -> p (i k)")
        block = s.block()

        @block.sync
        def _(sp):
            sp.dma_start(w[:, :], a[f"{name}_w"]).then_inc(loaded, 16)

        @block.tensor
        def _(pe):
            pe.wait_ge(*V.at("w_out"))
            for m, n in ((0, "wgT"), (1, "wuT")):
                for k in range(IC):
                    last = nc.tensor.transpose(ps[:, m, P * k:P * k + P], w[:, IP * m + P * k:IP * m + P * k + P], c.ident[:, :])
                last.then_inc(PE.did(n), 1)
            for k in range(IC):
                last = nc.tensor.transpose(ps[0:wide_[k], 2, P * k:P * k + P], w[:, 2 * IP + P * k:2 * IP + P * k + wide_[k]],
                                           c.ident[:, :])
            last.then_inc(PE.did("wdT"), 1)
            pe.wait_ge(*V.at("x_out"))
            for i in range(4):
                if i >= 2:
                    pe.wait_ge(*(A if i % 2 else V).at(f"xT{i - 2}"))
                for j in range(4):
                    last = nc.tensor.transpose(ps[:, 6 + i % 2, P * j:P * j + P], xq[:, 4 * i + j, :], c.ident[:, :])
                last.then_inc(PE.did(f"xT{i}"), 1)
            with pe.Fori(0, 4) as i:
                pe.wait_ge(*A.at("xg", i))
                for j in range(4):
                    if j >= 2:
                        pe.wait_ge(*V.at(f"h{j - 2}", i))
                    for m in (0, 1):
                        last = nc.tensor.matmul(ps[:, 2 * m + j % 2, 0:I], xg[:, P * j:P * j + P], wguT[:, m, 0:I],
                                                start=True, stop=True)
                    last.then_inc(PE.did(f"gu{j}"), 1)
                pe.wait_ge(*V.at("h_out", i))
                for k in range(IC):
                    for j in range(4):
                        last = nc.tensor.transpose(ps[0:wide_[k], 4 + k, P * j:P * j + P], hq[:, j, P * k:P * k + wide_[k]],
                                                   c.ident[:, :])
                    last.then_inc(PE.did(f"hT{k}"), 1)
                pe.wait_ge(*A.at("hT1", i))
                pe.wait_ge(*V.at("hT2", i))
                for j in range(4):
                    for k in range(IC):
                        last = nc.tensor.matmul(ps[:, 7, P * j:P * j + P], hT[0:wide_[k], k, P * j:P * j + P],
                                                wdT[0:wide_[k], k, :], start=(k == 0), stop=(k == IC - 1))
                last.then_inc(PE.did("out"), 1)

        @block.vector
        def _(dve):
            dve.wait_ge(loaded, 16)
            quant_vector(c, dve, qw, V, A, "w", 0, w[:, :], w[:, :])
            dve.wait_ge(*PE.at("wgT"))
            nc.vector.tensor_copy(wguT[:, 0, :], ps[:, 0, 0:IP]).then_inc(V.did("wgT"), 1)
            dve.wait_ge(*PE.at("wdT"))
            nc.vector.tensor_copy(wdT[:, 0:2, :].rearrange("p k d -> p (k d)"), ps[:, 2, 0:2 * P])
            nc.vector.tensor_copy(wdT[0:rest, 2, :], ps[0:rest, 2, 2 * P:3 * P]).then_inc(V.did("wdT"), 1)
            ln_vector(c, dve, V, A, PE, None, n1)
            dve.wait_ge(*V.at("ln_xn"))
            quant_vector(c, dve, qx, V, A, "x", 0, flat(c.xn), flat(xq))
            for i in (0, 2):
                dve.wait_ge(*PE.at(f"xT{i}"))
                nc.vector.tensor_copy(xqT[:, 512 * i:512 * i + 512], ps[:, 6, :]).then_inc(V.did(f"xT{i}"), 1)
            with dve.Fori(0, 4) as i:
                dve.wait_ge(*V.before("x", i))
                for j in range(4):
                    dve.wait_ge(*A.at(f"silu{j}", i))
                    nc.vector.tensor_tensor(hh[:, j, :], gate[:, j, :], ps[:, 2 + j % 2, 0:I], ALU.mult).then_inc(V.did(f"h{j}"), 1)
                dve.wait_ge(*V.at("h3", i))
                quant_vector(c, dve, qh, V, A, "h", i, flat(hh), flat(hq))
                for k in (0, 2):
                    dve.wait_ge(*PE.at(f"hT{k}", i))
                    nc.vector.tensor_copy(hT[0:wide_[k], k, :], ps[0:wide_[k], 4 + k, :]).then_inc(V.did(f"hT{k}"), 1)
                dve.wait_ge(*PE.at("out", i))
                xs = c.x[:, bass.ds(4 * i, 4), :].rearrange("p i d -> p (i d)")
                nc.vector.tensor_tensor(xs, ps[:, 7, :], xs, ALU.add).then_inc(V.did("x"), 1)

        @block.scalar
        def _(act):
            quant_scalar(c, act, qw, V, A, "w", 0)
            act.wait_ge(*PE.at("wuT"))
            nc.scalar.copy(wguT[:, 1, :], ps[:, 1, 0:IP]).then_inc(A.did("wuT"), 1)
            ln_scalar(c, act, V, A, PE, None, n1)
            quant_scalar(c, act, qx, V, A, "x", 0)
            for i in (1, 3):
                act.wait_ge(*PE.at(f"xT{i}"))
                nc.scalar.copy(xqT[:, 512 * i:512 * i + 512], ps[:, 7, :]).then_inc(A.did(f"xT{i}"), 1)
            act.wait_ge(*V.at("xT2"))
            act.wait_ge(*A.at("xT3"))
            with act.Fori(0, 4) as i:
                act.wait_ge(*V.before("x", i))
                nc.scalar.copy(xg[:, :], xqT[:, bass.ds(512 * i, 512)]).then_inc(A.did("xg"), 1)
                for j in range(4):
                    act.wait_ge(*PE.at(f"gu{j}", i))
                    nc.scalar.activation(gate[:, j, :], ps[:, j % 2, 0:I], ACT.Silu).then_inc(A.did(f"silu{j}"), 1)
                quant_scalar(c, act, qh, V, A, "h", i)
                act.wait_ge(*PE.at("hT1", i))
                nc.scalar.copy(hT[:, 1, :], ps[:, 5, :]).then_inc(A.did("hT1"), 1)


def many_head_cross_attention(c, name):
    TILES = H // 2
    NG = len(SPANS)
    wide_ = [w for _, w in SPANS]
    part = [min(4, KC - 4 * m) for m in range(NG)]
    chunk = [min(P, KEYS - P * j) for j in range(KC)]
    HALF = 1024
    halves = ((0, HALF), (HALF, KEYS))
    with Stage(c, name) as s:
        nc, a = c.nc, c.a
        wq, wk, wv, wo = (s.sb(n, [P, D]) for n in ("wq", "wk", "wv", "wo"))
        heads, own_dims, delta = s.sb("heads", [P, H]), s.sb("own_dims", [P, D]), s.sb("delta", [P, S])
        mask, shift = s.sb("mask", [P, KEYS], U8), s.sb("shift", [P, KEYS])
        qT = s.sb("qT", [P, TOK])
        qd = s.sb("qd", [P, 2, TILES, 2, S])
        ctx, ctxT = s.sb("ctx", [P, 2, KC, D]), s.sb("ctxT", [P, KEYS])
        kT, v = s.sb("kT", [P, 2, KEYS]), s.sb("v", [P, 2, KC, D])
        sc = s.sb("sc", [P, 4, KEYS])
        tops, top = s.sb("tops", [P, 2]), s.sb("top", [P, 1])
        ntop, rows = s.sb("ntop", [P, 2, TILES]), s.sb("rows", [P, 2, TILES])
        rinv, vinv, coef = s.sb("rinv", [P, TILES]), s.sb("vinv", [P, TILES]), s.sb("coef", [P, D])
        pT = s.sb("pT", [P, 2, KC, P])
        place = s.sb("place", [P, TILES, D])
        pvs = s.sb("pvs", [P, TILES, P])
        own, yT, pause = s.sb("own", [P, D]), s.sb("yT", [P, S]), s.sb("pause", [P, 2])
        ps = s.ps("scores", [P, 2048])
        turn = s.ps("turn", [P, 2, 512])
        prep = s.ps("prep", [P, 512])
        pv = s.ps("pv", [P, 512])
        tile_pv, sums = pv[:, 0:P], pv[:, P:2 * P]
        loaded, ctx_in = s.sem("loaded"), [s.sem("ctx_in0"), s.sem("ctx_in1")]
        qd_made = s.sem("qd_made")
        slots = lambda f: sum([f(t) for t in range(TILES)], [])
        PREPS = [f"{w}{t}" for t in range(6) for w in "ab"]
        PIECE = dict(zip(PREPS, [(what, m) for what in ("ctxT", "kT", "v") for m in range(NG)]))
        V = RoundSteps(s.sem("vector_steps"), ["shift", "zero"] + LN_V + [f"q{i}" for i in range(4)], slots(
            lambda t: [f"mA{t}"] + (["rinv", "vinv", "coef"] if t == 0 else []) + [f"pv{t}", f"T{t}2", f"T{t}3"] + ["own"] * (t == 0) +
            ([f"b{t}"] if t < 6 else []) + ["yT"] * (t == 6) + ["x"] * (t == 7) + [f"mB{t}", f"top{t}", f"ntop{t}"]))
        A = RoundSteps(s.sem("scalar_steps"), LN_A,
                       slots(lambda t: [f"T{t}0", f"T{t}1"] + ([f"a{t}"] if t < 6 else []) + [f"exp{t}"]))
        PE = RoundSteps(s.sem("tensor_steps"), LN_P + [f"q{i}" for i in range(4)], slots(
            lambda t: [f"T{t}0", f"T{t}1", f"a{t}", f"SA{t}", f"PV{t}", f"T{t}2", f"T{t}3"] + ["sums"] * (t == 0) +
            ([f"b{t}"] if t < 6 else []) + [f"SB{t}"]))
        tp = [turn[:, i, :] for i in (0, 1)]
        block = s.block()

        def copier(step):
            return V if step[0] == "b" else A

        def rounds(engine, body):
            body(0, 0, 0)
            body(1, 1, 0)
            with engine.Fori(0, B // 2 - 1) as t:
                for i in (0, 1):
                    body(2 * t + (2 + i), i, t + 1)
            body(B, 0, B // 2)
            body(B + 1, 1, B // 2)

        def kind(r):
            fixed = isinstance(r, int)
            return not fixed or r >= 2, not fixed or 1 <= r <= B, not fixed or r < B

        def put(engine_copy, dst, src, m, sem_inc):
            k = min(P, KEYS - 512 * m)
            engine_copy(dst[0:k, 4 * m:4 * m + part[m], :].rearrange("p j d -> p (j d)"), src[0:k, 0:P * part[m]])\
                .then_inc(*sem_inc)

        def copy_prep(engine_copy, step, par, sem_inc):
            what, m = PIECE[step]
            if what == "v":
                put(engine_copy, v[:, par, :, :], prep, m, sem_inc)
            else:
                dst = ctxT if what == "ctxT" else kT[:, par, :]
                engine_copy(dst[:, 512 * m:512 * m + wide_[m]], prep[:, 0:wide_[m]]).then_inc(*sem_inc)

        @block.sync
        def _(sp):
            for dst, src in ((wq, "wq"), (wk, "wk"), (wv, "wv"), (wo, "wo")):
                sp.dma_start(dst[:, :], a[f"{name}_{src}"]).then_inc(loaded, 16)
            sp.dma_start(heads[:, :], a["c_sixteen_heads"]).then_inc(loaded, 16)
            sp.dma_start(own_dims[:, :], a["c_own_dims"]).then_inc(loaded, 16)
            sp.dma_start(delta[:, :], a["c_delta"]).then_inc(loaded, 16)
            sp.dma_start(place[:, :, :], a["c_place"]).then_inc(loaded, 16)
            for h in (0, 1):
                sp.dma_start(mask[S * h:S * h + S, :], a["mask_all"]).then_inc(loaded, 16)

            def load(n, u):
                keys = a["ctx"][bass.ds(n, 1), :, :].rearrange("a k d -> (a k) d")
                sp.dma_start(ctx[:, u, 0:KC - 1, :], keys[0:(KC - 1) * P, :].rearrange("(j p) d -> p j d", p=P))\
                    .then_inc(ctx_in[u], 16)
                sp.dma_start(ctx[0:KREST, u, KC - 1, :], keys[(KC - 1) * P:KEYS, :]).then_inc(ctx_in[u], 16)

            load(0, 0)
            load(1, 1)
            with sp.Fori(0, B // 2 - 1) as t:
                for u in (0, 1):
                    sp.wait_ge(*PE.at("b1", 2 * t + u))
                    load(2 * t + (2 + u), u)

        @block.gpsimd
        def _(pool):
            pool.wait_ge(loaded, 160)
            pool.wait_ge(*V.at("q3"))

            def body(r, par, pair):
                if not kind(r)[2]:
                    return
                if kind(r)[0]:
                    pool.wait_ge(*PE.at("SB5", r - 1))
                nc.gpsimd.tensor_tensor(qd[:, par, :, :, :].rearrange("p k h q -> p (k h) q"),
                                        qT[:, bass.ds(S * r, S)].unsqueeze(1).broadcast_to([P, H, S]),
                                        heads[:, :].unsqueeze(2).broadcast_to([P, H, S]), ALU.mult).then_inc(qd_made, 1)

            rounds(pool, body)

        @block.tensor
        def _(pe):
            ln_tensor(c, pe, V, A, PE, tp)
            pe.wait_ge(*V.at("ln_T2"))
            pe.wait_ge(*A.at("ln_T3"))
            pe.wait_ge(loaded, 160)
            for i in range(4):
                nc.tensor.matmul(ps[:, 512 * i:512 * i + 512], wq[:, :], c.xnT[:, 512 * i:512 * i + 512], start=True, stop=True)\
                    .then_inc(*PE.inc(f"q{i}"))

            def body(r, par, pair):
                last_fin, tiles, coming = kind(r)
                cur = 1 - par

                def turns(t, m):
                    if m < 2:
                        pe.wait_ge(*(A.at(f"exp{t - 1}", r) if t else A.at("exp7", r - 1)))
                        if t:
                            pe.wait_ge(*V.at(f"T{t - 1}{m + 2}", r))
                        elif last_fin:
                            pe.wait_ge(*V.at(f"T7{m + 2}", r - 1))
                    else:
                        pe.wait_ge(*A.at(f"T{t}{m - 2}", r))
                    for i in range(4 * m, 4 * m + part[m]):
                        last = nc.tensor.transpose(tp[m % 2][0:chunk[i], P * (i - 4 * m):P * (i - 4 * m) + P],
                                                   sc[:, t % 4, P * i:P * i + chunk[i]], c.ident[:, :])
                    last.then_inc(*PE.inc(f"T{t}{m}"))

                def scores(t, half):
                    k, buf = (t + 2, cur) if t < 6 else (t - 6, par)
                    if t == 6 and half == 0:
                        pe.wait_ge(*V.at("b3", r))
                        pe.wait_ge(*A.at("a3", r))
                        pe.wait_ge(qd_made, r + 1)
                    step = "AB"[half]
                    if t and (tiles or t == 7):
                        pe.wait_ge(*V.at(f"m{step}{t - 1}", r))
                    elif t == 0:
                        pe.wait_ge(*V.at(f"m{step}7", r - 1))
                    for m in (2 * half, 2 * half + 1):
                        last = nc.tensor.matmul(ps[:, 512 * m:512 * m + wide_[m]],
                                                qd[:, buf, k, :, :].rearrange("p h q -> p (h q)"),
                                                kT[:, buf, 512 * m:512 * m + wide_[m]], start=True, stop=True)
                    last.then_inc(*PE.inc(f"S{step}{t}"))

                def values(t):
                    k, buf = (t - 1, cur) if t else (TILES - 1, par)
                    pe.wait_ge(*A.at(f"T{k}1", r if t else r - 1))
                    pe.wait_ge(*V.at(f"T{k}3", r if t else r - 1))
                    if t == 1 and last_fin:
                        pe.wait_ge(*V.at("own", r))
                    elif t > 1:
                        pe.wait_ge(*V.at(f"pv{t - 1}", r))
                    elif t == 0:
                        pe.wait_ge(*V.at("pv7", r - 1))
                    for i in range(KC):
                        q = i % 4
                        last = nc.tensor.matmul(pv[32 * q:32 * q + 16, 0:P], v[0:chunk[i], buf, i, 16 * k:16 * k + 16],
                                                pT[0:chunk[i], k % 2, i, :], start=(i < 4), stop=(i >= KC - 4),
                                                tile_position=(0, 32 * q))
                    last.then_inc(*PE.inc(f"PV{t}"))

                def add_tiles():
                    pe.wait_ge(*V.at("pv0", r))
                    for k in range(TILES):
                        last = nc.tensor.matmul(sums, pvs[:, k, :], place[:, k, :], start=(k == 0), stop=(k == TILES - 1))
                    last.then_inc(*PE.inc("sums"))

                def prepare(step):
                    before = PREPS.index(step) - 1
                    if before >= 0:
                        pe.wait_ge(*copier(PREPS[before]).at(PREPS[before], r))
                    else:
                        pe.wait_ge(ctx_in[par], 32 * pair + 32)
                        if kind(r)[0] and not (isinstance(r, int) and r < 3):
                            pe.wait_ge(*V.at("x", r - 1))
                    what, m = PIECE[step]
                    if what == "kT":
                        nc.tensor.matmul(prep[:, 0:wide_[m]], wk[:, :], ctxT[:, 512 * m:512 * m + wide_[m]], start=True, stop=True)\
                            .then_inc(*PE.inc(step))
                        return
                    for j in range(4 * m, 4 * m + part[m]):
                        at = P * (j - 4 * m)
                        if what == "ctxT":
                            last = nc.tensor.transpose(prep[:, at:at + chunk[j]], ctx[0:chunk[j], par, j, :],
                                                       c.ident[0:chunk[j], 0:chunk[j]])
                        else:
                            last = nc.tensor.matmul(prep[0:chunk[j], at:at + P], ctxT[:, P * j:P * j + chunk[j]], wv[:, :],
                                                    start=True, stop=True)
                    last.then_inc(*PE.inc(step))

                for t in range(TILES):
                    if tiles:
                        turns(t, 0)
                        turns(t, 1)
                    if t < 6 and coming:
                        prepare(f"a{t}")
                    if t == 6 and last_fin:
                        pe.wait_ge(*V.at("own", r))
                        if coming:
                            pe.wait_ge(*V.at("b5", r))
                        nc.tensor.matmul(prep[:, 0:S], own[:, :], delta[:, :], start=True, stop=True).then_inc(*PE.inc("a6"))
                    if t == 7 and last_fin:
                        pe.wait_ge(*V.at("yT", r))
                        nc.tensor.matmul(prep[S * par:S * par + S, 0:D], yT[:, :], wo[:, :], start=True, stop=True)\
                            .then_inc(*PE.inc("a7"))
                    if (t < 6 and tiles) or (t >= 6 and coming):
                        scores(t, 0)
                    if (t == 0 and last_fin) or (t and tiles):
                        values(t)
                    if tiles:
                        turns(t, 2)
                        turns(t, 3)
                    if t == 0 and last_fin:
                        add_tiles()
                    if t < 6 and coming:
                        prepare(f"b{t}")
                    if (t < 6 and tiles) or (t >= 6 and coming):
                        scores(t, 1)

            rounds(pe, body)

        @block.vector
        def _(dve):
            dve.wait_ge(loaded, 160)
            nc.vector.tensor_scalar(shift[:, :], mask[:, :], OUT, None, ALU.mult).then_inc(*V.inc("shift"))
            nc.vector.memset(pv[:, :], 0.0).then_inc(*V.inc("zero"))
            ln_vector(c, dve, V, A, PE, tp)
            for i in range(4):
                dve.wait_ge(*PE.at(f"q{i}"))
                nc.vector.tensor_scalar(qT[:, 512 * i:512 * i + 512], ps[:, 512 * i:512 * i + 512], DH ** -0.5, None, ALU.mult)\
                    .then_inc(*V.inc(f"q{i}"))

            def body(r, par, pair):
                last_fin, tiles, coming = kind(r)
                cur = 1 - par

                def masked(t, half):
                    k = (t + 2) % TILES
                    step, span = "AB"[half], slice(*halves[half])
                    dve.wait_ge(*PE.at(f"S{step}{t}", r))
                    nc.vector.memset(pause[:, half:half + 1], 0.0)
                    nc.vector.tensor_tensor_reduce(out=sc[:, k % 4, span], in0=ps[:, span], in1=shift[:, span],
                                                   scale=1.0, scalar=3 * OUT, op0=ALU.add, op1=ALU.max,
                                                   accum_out=tops[:, half:half + 1]).then_inc(*V.inc(f"m{step}{t}"))

                for t in range(TILES):
                    scored = (t < 6 and tiles) or (t >= 6 and coming)
                    if scored:
                        masked(t, 0)
                    if t == 0 and last_fin:
                        dve.wait_ge(*A.at("exp6", r - 1))
                        nc.vector.reciprocal(rinv[:, :], rows[:, par, :]).then_inc(*V.inc("rinv"))
                        dve.wait_ge(*V.at("rinv", r))
                        nc.vector.scalar_tensor_tensor(out=vinv[:, :], in0=ntop[:, par, :], scalar=-0.5 * OUT, in1=rinv[:, :],
                                                       op0=ALU.is_lt, op1=ALU.mult).then_inc(*V.inc("vinv"))
                        dve.wait_ge(*V.at("vinv", r))
                        nc.vector.tensor_tensor(coef[:, :].rearrange("p (k d) -> p k d", k=TILES),
                                                vinv[:, :].unsqueeze(2).broadcast_to([P, TILES, 16]),
                                                own_dims[:, :].rearrange("p (k d) -> p k d", k=TILES), ALU.mult)\
                            .then_inc(*V.inc("coef"))
                    if (t == 0 and last_fin) or (t and tiles):
                        dve.wait_ge(*PE.at(f"PV{t}", r))
                        nc.vector.tensor_copy(pvs[:, (t - 1) % TILES, :], tile_pv).then_inc(*V.inc(f"pv{t}"))
                    if tiles:
                        for m in (2, 3):
                            dve.wait_ge(*PE.at(f"T{t}{m}", r))
                            put(nc.vector.tensor_copy, pT[:, t % 2, :, :], tp[m % 2], m, V.inc(f"T{t}{m}"))
                    if t == 0 and last_fin:
                        dve.wait_ge(*V.at("coef", r))
                        dve.wait_ge(*PE.at("sums", r))
                        nc.vector.tensor_tensor(own[:, :], sums, coef[:, :], ALU.mult).then_inc(*V.inc("own"))
                    if t < 6 and coming:
                        dve.wait_ge(*PE.at(f"b{t}", r))
                        copy_prep(nc.vector.tensor_copy, f"b{t}", par, V.inc(f"b{t}"))
                    if t == 6 and last_fin:
                        dve.wait_ge(*PE.at("a6", r))
                        nc.vector.tensor_copy(yT[:, :], prep[:, 0:S]).then_inc(*V.inc("yT"))
                    if t == 7 and last_fin:
                        dve.wait_ge(*PE.at("a7", r))
                        half = slice(S * par, S * par + S)
                        xs = c.x[half, bass.ds(pair - 1, 1), :].rearrange("p a d -> p (a d)")
                        nc.vector.tensor_tensor(xs, prep[half, 0:D], xs, ALU.add).then_inc(*V.inc("x"))
                    if scored:
                        buf = cur if t < 6 else par
                        k = (t + 2) % TILES
                        masked(t, 1)
                        dve.wait_ge(*V.at(f"mB{t}", r))
                        nc.vector.tensor_reduce(top[:, :], tops[:, :], AX.X, ALU.max).then_inc(*V.inc(f"top{t}"))
                        dve.wait_ge(*V.at(f"top{t}", r))
                        nc.vector.tensor_scalar(ntop[:, buf, k:k + 1], top[:, :], -1.0, None, ALU.mult).then_inc(*V.inc(f"ntop{t}"))

            rounds(dve, body)

        @block.scalar
        def _(act):
            ln_scalar(c, act, V, A, PE, tp)

            def body(r, par, pair):
                last_fin, tiles, coming = kind(r)
                cur = 1 - par
                for t in range(TILES):
                    if tiles:
                        for m in (0, 1):
                            act.wait_ge(*PE.at(f"T{t}{m}", r))
                            put(nc.scalar.copy, pT[:, t % 2, :, :], tp[m % 2], m, A.inc(f"T{t}{m}"))
                    if t < 6 and coming:
                        act.wait_ge(*PE.at(f"a{t}", r))
                        copy_prep(nc.scalar.copy, f"a{t}", par, A.inc(f"a{t}"))
                    if (t < 7 and tiles) or (t == 7 and coming):
                        k, buf = (t + 1, cur) if t < 7 else (0, par)
                        act.wait_ge(*(V.at(f"ntop{t - 1}", r) if t else V.at("ntop7", r - 1)))
                        nc.scalar.activation(sc[:, k % 4, :], sc[:, k % 4, :], ACT.Exp, bias=ntop[:, buf, k:k + 1], scale=1.0,
                                             accum_out=rows[:, buf, k:k + 1]).then_inc(*A.inc(f"exp{t}"))

            rounds(act, body)


def build(nc, a):
    with ExitStack() as ctx:
        c = Core(nc, ctx, a)
        start(c)
        if 0 in STAGES:
            cross_attention(c, "L0_xattn", "mask_keys", 1)
        if 1 in STAGES:
            spectral_layer(c, "L0_attn")
        if 2 in STAGES:
            capacity_experts(c, "L0_ffn")
        if 3 in STAGES:
            causal_cross_attention(c, "L1_xattn")
        if 4 in STAGES:
            two_step_attention(c, "L1_attn")
        if 5 in STAGES:
            routed_experts(c, "L1_ffn")
        if 6 in STAGES:
            many_head_cross_attention(c, "L2_xattn")
        if 7 in STAGES:
            selective_scan_layer(c, "L2_attn")
        if 8 in STAGES:
            chosen_adapters(c, "L2_ffn")
        if 9 in STAGES:
            cross_attention(c, "L3_xattn", "mask_pairs", S)
        if 10 in STAGES:
            self_attention(c, "L3_attn")
        if 11 in STAGES:
            quantised_ffn(c, "L3_ffn")
        finish(c)


def constants():
    p = np.arange(P)
    same = p[:, None] // S == p[None, :] // S
    f = np.float32
    half = DH // 2
    angle = np.arange(S, dtype=f)[None, :] * (f(1) / f(10000) ** ((p % half).astype(f) / f(half)))[:, None]
    return {
        "c_heads": (p[:, None] % 32 // DH == np.arange(4)).astype(f),
        "c_sixteen_heads": (p[:, None] // DH == np.arange(H)).astype(f),
        "c_own_dims": (p[:, None] // S == p[None, :] // DH % 2).astype(f),
        "c_place": ((p[:, None, None] % 32 < 16) & (p[None, None, :] == 16 * np.arange(8)[None, :, None] + p[:, None, None] % 32)).astype(f),
        "c_which": (p[None, None, :] // DH == 2 * np.arange(8)[None, :, None] + p[:, None, None] // S).astype(f),
        "c_delta": (p[:, None] % S == np.arange(S)).astype(f),
        "c_later": ((p[:, None] % S == np.arange(S)) & (np.arange(S) > 0)).astype(f),
        "c_causal": np.where(np.arange(S) <= p[:, None] % S, 0, OUT).astype(f),
        "c_strict": np.where(np.arange(S) < p[:, None] % S, 0, OUT).astype(f),
        "c_halves": np.stack([p < 32, (p >= 32) & (p < 64)], axis=1).astype(f),
        "c_freq": ((p[:, None] % 32 == np.arange(32)) & (p[:, None] < 64)).astype(f),
        "c_earlier": (p[:, None] < p[None, :]).astype(f),
        "c_sixteen": np.broadcast_to(np.arange(16, dtype=f), (P, NT, 16)),
        "c_rank": np.broadcast_to((8 - np.arange(8, dtype=f))[None, :, None], (P, 8, B)),
        "c_eight": np.broadcast_to(np.arange(8, dtype=f), (P, NT, 8)),
        "c_cos": np.cos(angle).astype(f),
        "c_sin": (np.sin(angle) * np.where(p % DH < half, -1, 1)[:, None]).astype(f),
        "c_ident": np.eye(P, dtype=f),
        "c_pair_causal": np.where(same & (p[None, :] <= p[:, None]), 0, OUT).astype(f),
    }


def kernel(**inputs):
    import concourse.bacc as bacc
    from concourse.bass_utils import run_bass_kernel_spmd

    i = {k: np.asarray(v) for k, v in inputs.items()}
    arrays = {
        "x": i["x"].reshape(TOK, D),
        "ctx": i["ctx_1024"],
        "mask_keys": i["mask_BxS2_ik0"].reshape(B, 1, KEYS),
        "mask_pairs": i["mask_BxSxS2_bk1"],
    }
    for n in ("L0_xattn", "L3_xattn"):
        arrays.update({f"{n}_Wq": i[f"{n}_Wq"], f"{n}_WkT": i[f"{n}_Wk"].T, f"{n}_Wv": i[f"{n}_Wv"],
                       f"{n}_bq": i[f"{n}_bq"].reshape(D, 1), f"{n}_bk": i[f"{n}_bk"].reshape(D, 1),
                       f"{n}_bv": i[f"{n}_bv"].reshape(1, D)})
    arrays.update({"L1_xattn_Wq": i["L1_xattn_Wq"], "L1_xattn_WqT": i["L1_xattn_Wq"].T})
    arrays.update({
        "L1_attn_w": np.stack([i["L1_attn_W_attn"][:, :D], i["L1_attn_W_attn"][:, D:], i["L1_attn_W_k2"]]),
        "L1_attn_bias": np.stack([i["L1_attn_b_attn"][:D], i["L1_attn_b_attn"][D:], i["L1_attn_b_k2"]], axis=1),
        "L1_attn_W_proj": i["L1_attn_W_proj"], "L1_attn_b_proj": i["L1_attn_b_proj"].reshape(1, D),
    })
    swapped = np.arange(D).reshape(H, 2, DH // 2)[:, ::-1].reshape(D)
    wq, wk, wv = i["L3_attn_w_qkv"].reshape(3, D, D)
    arrays.update({"L3_attn_w": np.stack([wq.T, wq[swapped].T, wk.T, wk[swapped].T, wv.T]),
                   "L3_attn_wo": i["L3_attn_w_out"].T})
    twice = lambda v: np.concatenate([v, v, np.zeros_like(v), np.zeros_like(v)]).reshape(-1, 1)
    filled = lambda w: np.concatenate([w, np.zeros((P - w.shape[0],) + w.shape[1:], w.dtype)])
    arrays.update({
        "L0_attn_cols": np.stack([i[f"L0_attn_{n}"] for n in ("ln1_g", "ln1_b", "ln3_g", "ln3_b")], axis=1),
        "L0_attn_W_toT": filled(i["L0_attn_W_to"]).T, "L0_attn_W_fromT": filled(i["L0_attn_W_from"].T),
        "L0_attn_decay": twice(i["L0_attn_log_decay"]), "L0_attn_freq": twice(i["L0_attn_frequencies"]),
        "L0_attn_W1T": i["L0_attn_W_ffn1"].T, "L0_attn_b1": i["L0_attn_b_ffn1"].reshape(4, P).T,
        "L0_attn_W2T": i["L0_attn_W_ffn2"].T, "L0_attn_b2": i["L0_attn_b_ffn2"].reshape(1, D),
        "L0_ffn_Wg": i["L0_ffn_Wg"], "L0_ffn_w1": i["L0_ffn_w1"], "L0_ffn_w2": i["L0_ffn_w2"],
    })
    arrays.update({
        "L1_ffn_embT": i["L1_ffn_uzman_embeddings"].T, "L1_ffn_bonus": i["L1_ffn_onbellek_durumu"].reshape(1, -1),
        "L1_ffn_b1": i["L1_ffn_b1"].reshape(8, 4, P).transpose(2, 0, 1), "L1_ffn_b2": i["L1_ffn_b2"], "L1_ffn_W1": i["L1_ffn_W1"], "L1_ffn_W2": i["L1_ffn_W2"],
        "L2_attn_cols": np.stack([i["L2_attn_ln_w"], i["L2_attn_ln_b"]], axis=1),
        "L2_attn_W_inT": i["L2_attn_W_in"].T, "L2_attn_conv_w": i["L2_attn_conv_w"].reshape(2 * D, 4),
        "L2_attn_W_xT": i["L2_attn_W_x"].T, "L2_attn_W_dtT": i["L2_attn_W_dt"].T, "L2_attn_log_A": i["L2_attn_log_A"],
        "L2_attn_W_outT": i["L2_attn_W_out"].T,
        "L2_attn_vecs": np.stack([i[f"L2_attn_{n}"].reshape(2, P).T for n in ("conv_b", "b_dt", "D_param")]),
    })
    side_by_side = lambda w: w.transpose(1, 0, 2).reshape(D, -1)
    adapter = {n: i[f"L2_ffn_{n}"] for n in ("W_base", "b_base", "Wd1", "bd1", "Wd2", "bd2", "Wa_down", "ba_down", "Wa_up", "ba_up")}
    arrays.update({
        "L2_ffn_wd1": side_by_side(adapter["Wd1"]), "L2_ffn_bd1": adapter["bd1"].reshape(2, P).T,
        "L2_ffn_wd2": adapter["Wd2"].reshape(2 * P, D), "L2_ffn_bd2": adapter["bd2"].T,
        "L2_ffn_wad": side_by_side(adapter["Wa_down"]), "L2_ffn_bad": adapter["ba_down"].reshape(4, P).T,
        "L2_ffn_wau": adapter["Wa_up"].reshape(4 * P, D), "L2_ffn_bau": adapter["ba_up"],
        "L2_ffn_wb": adapter["W_base"], "L2_ffn_bb": adapter["b_base"].reshape(1, D),
    })
    rows = lambda w: np.concatenate([w, np.zeros((384 - w.shape[0], D), w.dtype)]).reshape(3, P, D).transpose(1, 0, 2).reshape(P, -1)
    arrays["L3_ffn_w"] = np.concatenate([rows(i["L3_ffn_w_gate"]), rows(i["L3_ffn_w_up"]), i["L3_ffn_w_down"]], axis=1)
    arrays.update({f"L2_xattn_w{n}": i[f"L2_xattn_W_{n}"].T for n in "qkvo"})
    arrays["mask_all"] = i["mask_1x1xSxS2_bk1"].reshape(S, KEYS)
    arrays.update(constants())

    nc = bacc.Bacc("TRN2", target_bir_lowering=False, num_devices=1)
    arrays = {f"in_{k}": np.ascontiguousarray(v) for k, v in arrays.items()}
    a = {k[3:]: nc.dram_tensor(k, v.shape, mybir.dt.from_np(v.dtype), kind="ExternalInput").ap()
         for k, v in arrays.items()}
    a["out"] = nc.dram_tensor("out", (TOK, D), F32, kind="ExternalOutput").ap()
    a["scratch_in"] = nc.dram_tensor("scratch_in", (TOK, D), F32).ap()
    a["scratch_out"] = nc.dram_tensor("scratch_out", (TOK, D), F32).ap()
    a["scratch_rows"] = nc.dram_tensor("scratch_rows", (32, TOK), F32).ap()
    build(nc, a)
    r = run_bass_kernel_spmd(nc, [arrays], core_ids=[0])
    return r.results[0]["out"].reshape(B, S, D)
```

```python
from contextlib import ExitStack

import numpy as np

import concourse.bass as bass
from concourse import mybir

F32 = mybir.dt.float32
BF16 = mybir.dt.bfloat16
I32 = mybir.dt.int32
U32 = mybir.dt.uint32
U8 = mybir.dt.uint8
ALU = mybir.AluOpType
ACT = mybir.ActivationFunctionType
AX = mybir.AxisListType

P = 128
B, S, D = 32, 64, 128
TOK = B * S
NT = TOK // P
KEYS = 1601
KC = -(-KEYS // P)
KREST = KEYS - (KC - 1) * P
SPANS = [(k, min(512, KEYS - k)) for k in range(0, KEYS, 512)]
H, DH = 16, 8
EPS = 1e-5
OUT = -2.0 ** 100


class Steps:

    def __init__(self, sem, *parts):
        self.sem, self.where, self.order, self.next = sem, {}, [], 0
        base = 0
        for times, names, *copies in parts:
            for i, n in enumerate(names):
                assert n not in self.where, n
                self.where[n] = (base + i + 1, len(names))
            self.order += names * (copies[0] if copies else 1)
            base += times * len(names)

    def at(self, name, t=0):
        first, per = self.where[name]
        return self.sem, t * per + first

    def before(self, name, t, rounds=1):
        first, per = self.where[name]
        assert first - rounds * per >= 1, name
        return self.sem, t * per + (first - rounds * per)

    def did(self, name):
        assert self.order[self.next] == name, (self.order[self.next], name)
        self.next += 1
        return self.sem


class RoundSteps(Steps):

    def __init__(self, sem, names, body):
        super().__init__(sem, (1, names), (1, body))
        self.body, self.start = body, len(names)

    def inc(self, name):
        skipped = 0
        while self.order[self.next] != name:
            assert self.next >= self.start, (self.order[self.next], name)
            skipped += 1
            self.advance()
        self.advance()
        return self.sem, 1 + skipped

    def advance(self):
        self.next = self.next + 1 if self.next + 1 < len(self.order) else self.start

    def did(self, name):
        sem, amount = self.inc(name)
        assert amount == 1, name
        return sem


class Core:

    def __init__(self, nc, ctx, a):
        self.nc, self.a = nc, a
        self.sb = lambda name, shape, dt=F32: ctx.enter_context(nc.sbuf_tensor(name, shape, dt))
        self.x = self.sb("x", [P, NT, D])
        self.xn = self.sb("xn", [P, NT, D])
        self.xnT = self.sb("xnT", [P, TOK])
        self.ident = self.sb("ident", [P, P])
        self.eps = self.sb("eps", [P, 1])
        self.ahead = self.sb("ahead", [P, 1])
        self.pause = self.sb("pause", [P, 1])
        self.sum = self.sb("ln_sum", [P, NT])
        self.mean = self.sb("ln_mean", [P, NT])
        self.sq = self.sb("ln_sq", [P, NT, D])
        self.var = self.sb("ln_var", [P, NT])
        self.std = self.sb("ln_std", [P, NT])
        self.rstd = self.sb("ln_rstd", [P, NT])


class Stage:

    def __init__(self, core, name):
        self.core, self.nc, self.name, self.ctx = core, core.nc, name, ExitStack()

    def __enter__(self):
        return self

    def __exit__(self, *exc):
        return self.ctx.__exit__(*exc)

    def sb(self, name, shape, dt=F32):
        return self.ctx.enter_context(self.nc.sbuf_tensor(f"{self.name}_{name}", shape, dt))

    def ps(self, name, shape):
        return self.ctx.enter_context(self.nc.psum_tensor(f"{self.name}_ps_{name}", shape, F32))

    def sem(self, name):
        return self.ctx.enter_context(self.nc.semaphore(f"{self.name}_{name}"))

    def block(self):
        return self.ctx.enter_context(self.nc.Block())


class Norm:

    def __init__(self, c, tag="ln", x=None, xn=None, xnT=None, gain=None, bias=None, turned=True):
        self.x, self.xn = (c.x, c.xn) if x is None else (x, xn)
        self.xnT = c.xnT if xnT is None else xnT
        self.tag, self.gain, self.bias, self.turned = tag, gain, bias, turned
        turns = [0, 1, 2, 3] if turned else []
        name = lambda n: f"{tag}_{n}"
        self.V = [name(n) for n in LN_STEPS_V + [f"T{i}" for i in turns[::2]]]
        self.A = [name(n) for n in LN_STEPS_A + [f"T{i}" for i in turns[1::2]]]
        self.P = [name(f"PT{i}") for i in turns]


LN_STEPS_V = ["sum0", "mean0", "centred0", "sum", "mean", "centred", "var0", "var", "rstd0", "xn0", "rstd", "xn"]
LN_STEPS_A = ["sq0", "sq", "std0", "std"]
LN_V = ["ln_" + n for n in LN_STEPS_V + ["T0", "T2"]]
LN_A = ["ln_" + n for n in LN_STEPS_A + ["T1", "T3"]]
LN_P = ["ln_PT0", "ln_PT1", "ln_PT2", "ln_PT3"]


def ln_vector(c, dve, V, A, PE, tp, n=None):
    nc, n = c.nc, n or Norm(c)
    g = n.tag

    halves = (("0", slice(0, NT // 2)), ("", slice(NT // 2, NT)))

    def wide(m, at):
        return m[:, at].unsqueeze(2).broadcast_to([P, NT // 2, D])

    for h, at in halves:
        nc.vector.tensor_reduce(c.sum[:, at], n.x[:, at, :], AX.X, ALU.add).then_inc(V.did(f"{g}_sum{h}"), 1)
        dve.wait_ge(*V.at(f"{g}_sum{h}"))
        nc.vector.tensor_scalar(c.mean[:, at], c.sum[:, at], 1.0 / D, None, ALU.mult).then_inc(V.did(f"{g}_mean{h}"), 1)
        dve.wait_ge(*V.at(f"{g}_mean{h}"))
        nc.vector.tensor_tensor(n.xn[:, at, :], n.x[:, at, :], wide(c.mean, at), ALU.subtract)\
            .then_inc(V.did(f"{g}_centred{h}"), 1)
    for h, at in halves:
        dve.wait_ge(*A.at(f"{g}_sq{h}"))
        nc.vector.tensor_reduce(c.var[:, at], c.sq[:, at, :], AX.X, ALU.add).then_inc(V.did(f"{g}_var{h}"), 1)
    for h, at in halves:
        dve.wait_ge(*A.at(f"{g}_std{h}"))
        nc.vector.reciprocal(c.rstd[:, at], c.std[:, at]).then_inc(V.did(f"{g}_rstd{h}"), 1)
        dve.wait_ge(*V.at(f"{g}_rstd{h}"))
        nc.vector.tensor_tensor(n.xn[:, at, :], n.xn[:, at, :], wide(c.rstd, at), ALU.mult).then_inc(V.did(f"{g}_xn{h}"), 1)
    for i in (0, 2) if n.turned else ():
        dve.wait_ge(*PE.at(f"{g}_PT{i}"))
        dst = n.xnT[:, 512 * i:512 * i + 512]
        if n.gain is None:
            nc.vector.tensor_copy(dst, tp[0]).then_inc(V.did(f"{g}_T{i}"), 1)
        else:
            nc.vector.tensor_scalar(dst, tp[0], n.gain, n.bias, ALU.mult, ALU.add).then_inc(V.did(f"{g}_T{i}"), 1)


def ln_scalar(c, act, V, A, PE, tp, n=None):
    nc, n = c.nc, n or Norm(c)
    g = n.tag
    if g == "ln":
        nc.scalar.activation(c.ahead[:, :], c.eps[:, :], ACT.Sqrt)
    halves = (("0", slice(0, NT // 2)), ("", slice(NT // 2, NT)))
    for h, at in halves:
        act.wait_ge(*V.at(f"{g}_centred{h}"))
        nc.scalar.activation(c.sq[:, at, :], n.xn[:, at, :], ACT.Square).then_inc(A.did(f"{g}_sq{h}"), 1)
    for h, at in halves:
        act.wait_ge(*V.at(f"{g}_var{h}"))
        nc.scalar.activation(c.std[:, at], c.var[:, at], ACT.Sqrt, bias=c.eps[:, 0:1], scale=1.0 / D)\
            .then_inc(A.did(f"{g}_std{h}"), 1)
    for i in (1, 3) if n.turned else ():
        act.wait_ge(*PE.at(f"{g}_PT{i}"))
        dst = n.xnT[:, 512 * i:512 * i + 512]
        if n.gain is None:
            nc.scalar.copy(dst, tp[1]).then_inc(A.did(f"{g}_T{i}"), 1)
        else:
            nc.scalar.activation(dst, tp[1], ACT.Identity, bias=n.bias, scale=n.gain).then_inc(A.did(f"{g}_T{i}"), 1)


def ln_tensor(c, pe, V, A, PE, tp, n=None):
    nc, n = c.nc, n or Norm(c)
    g = n.tag
    pe.wait_ge(*V.at(f"{g}_xn0"))
    for i in range(4):
        if i == 2:
            pe.wait_ge(*V.at(f"{g}_xn"))
            pe.wait_ge(*V.at(f"{g}_T0"))
        if i == 3:
            pe.wait_ge(*A.at(f"{g}_T1"))
        for j in range(4):
            last = nc.tensor.transpose(tp[i % 2][:, P * j:P * j + P], n.xn[:, 4 * i + j, :], c.ident[:, :])
        last.then_inc(PE.did(f"{g}_PT{i}"), 1)


def start(c):
    with Stage(c, "start") as s:
        nc, a = c.nc, c.a
        loaded, eps_set = s.sem("loaded"), s.sem("eps_set")
        block = s.block()

        @block.sync
        def _(sp):
            sp.dma_start(c.x[:, :, :], a["x"].rearrange("(t p) d -> p t d", p=P)).then_inc(loaded, 16)
            sp.dma_start(c.ident[:, :], a["c_ident"]).then_inc(loaded, 16)
            sp.wait_ge(loaded, 32)

        @block.vector
        def _(dve):
            nc.vector.memset(c.eps[:, :], EPS).then_inc(eps_set, 1)
            dve.wait_ge(eps_set, 1)


def finish(c):
    with Stage(c, "finish") as s:
        stored = s.sem("stored")
        block = s.block()

        @block.sync
        def _(sp):
            sp.dma_start(c.a["out"].rearrange("(t p) d -> p t d", p=P), c.x[:, :, :]).then_inc(stored, 16)
            sp.wait_ge(stored, 16)


def cross_attention(c, name, mask_name, mask_rows):
    NG = len(SPANS)
    TILE = [(b, g) for b in (0, 1) for g in range(NG)]
    wide = [w for _, w in SPANS]
    indicated = mask_rows != 1
    with Stage(c, name) as s:
        nc, a = c.nc, c.a
        wq, wkT, wv = s.sb("wq", [P, D]), s.sb("wkT", [P, D]), s.sb("wv", [P, D])
        bq, bk, bv = s.sb("bq", [P, 1]), s.sb("bk", [P, 1]), s.sb("bv", [P, D])
        qT, qkT = (m[:, :, :].rearrange("p t d -> p (t d)") for m in (c.sq, c.xn))
        qk1 = s.sb("qk1", [P, 3, P])
        qbk, qbk1 = s.sb("qbk", [P, NT]), s.sb("qbk1", [P, 1])
        mask = s.sb("mask", [P, 3, KEYS], U8 if indicated else I32)
        out_ = None if indicated else s.sb("out_keys", [P, KEYS])
        shift = s.sb("shift", [P, KEYS])
        ctx = s.sb("ctx", [P, 3, 2, KC, D])
        ctxT = s.sb("ctxT", [P, 2, KEYS])
        sc = s.sb("sc", [P, KEYS])
        probsT = s.sb("probsT", [P, KC, P])
        mx, nmx = s.sb("mx", [P, 1]), s.sb("nmx", [P, 1])
        rows, rinv = s.sb("rows", [P, 3]), s.sb("rinv", [P, 1])
        o, oT, pause = s.sb("o", [P, D]), s.sb("oT", [P, P]), s.sb("pause", [P, 1])
        turn = s.ps("turn", [P, 2, 512])
        scores = s.ps("scores", [P, 4, 512])
        mixed = s.ps("mixed", [P, D])
        small = s.ps("small", [P, 512])
        weights = s.sem("weights")
        ctx_in = [[s.sem(f"ctx_in{u}{b}") for b in (0, 1)] for u in range(3)]
        mask_in = [s.sem(f"mask_in{u}") for u in range(3)]
        tile_made = s.sem("tile_made")
        out_made = s.sem("out_made")
        V_PT, A_PT = (0, 2), (1, 3)
        V = RoundSteps(s.sem("vector_steps"), LN_V + [f"q{i}" for i in range(4)] + ["qbk", "xbv"],
                       [f"ctxT1{g}" for g in range(NG)] + ["oT"] + [f"pT{g}" for g in V_PT] + ["x", "rinv", "o"] +
                       ["masked", "nmax"])
        A = RoundSteps(s.sem("scalar_steps"), LN_A + [f"qk{i}" for i in range(4)],
                       [f"ctxT0{g}" for g in range(NG)] + ["exp"] + [f"pT{g}" for g in A_PT] + ["qbk", "shift"])
        PE = RoundSteps(s.sem("tensor_steps"), LN_P + [f"q{i}" for i in range(4)] + [f"qk{i}" for i in range(4)] + ["qbk"],
                        [f"ctxT{b}{g}" for b, g in TILE] + ["oT"] + [f"pT{g}" for g in range(NG)] +
                        ["out", "mixed", "scores"])
        tp = [turn[:, i, :] for i in (0, 1)]
        flat = scores[:, :, :].rearrange("p a n -> p (a n)")[:, 0:KEYS]
        block = s.block()

        def rounds(engine, body):
            for r in range(3):
                body(r, r, 0)
            with engine.Fori(0, (NT - 4) // 3) as t:
                for i in range(3):
                    body(3 * t + (3 + i), i, t + 1)
            for r in range(NT - 1, NT + 2):
                body(r, r % 3, r // 3)

        def kind(r):
            fixed = isinstance(r, int)
            return not fixed or r >= 2, not fixed or 1 <= r <= NT, not fixed or r < NT

        @block.sync
        def _(sp):
            for dst, src in ((wq, "Wq"), (wkT, "WkT"), (wv, "Wv"), (bq, "bq"), (bk, "bk")):
                sp.dma_start(dst[:, :], a[f"{name}_{src}"]).then_inc(weights, 16)
            sp.dma_start(bv[:, :], a[f"{name}_bv"].broadcast_to([P, D])).then_inc(weights, 16)

            def load(t, u):
                for b in (0, 1):
                    keys = a["ctx"][bass.ds(2 * t + b, 1), :, :].rearrange("a k d -> (a k) d")
                    sp.dma_start(ctx[:, u, b, 0:KC - 1, :], keys[0:(KC - 1) * P, :].rearrange("(j p) d -> p j d", p=P))\
                        .then_inc(ctx_in[u][b], 16)
                    sp.dma_start(ctx[0:KREST, u, b, KC - 1, :], keys[(KC - 1) * P:KEYS, :]).then_inc(ctx_in[u][b], 16)
                for b in (0, 1):
                    m = a[mask_name][bass.ds(2 * t + b, 1), :, :].rearrange("a q k -> (a q) k")
                    if mask_rows == 1:
                        m = m.broadcast_to([S, KEYS])
                    sp.dma_start(mask[S * b:S * b + S, u, :], m).then_inc(mask_in[u], 16)

            def reload(r, u, n):
                sp.wait_ge(*PE.at("mixed", r))
                sp.wait_ge(*A.at("shift", r - 1))
                if not indicated:
                    sp.wait_ge(out_made, r)
                load(n, u)

            for u in range(3):
                load(u, u)
            with sp.Fori(0, (NT - 4) // 3) as t:
                for u in range(3):
                    reload(3 * t + (1 + u), u, 3 * t + (3 + u))
            reload(NT - 3, 0, NT - 1)

        @block.gpsimd
        def _(pool):
            pool.wait_ge(*A.at("qk3"))

            def body(r, u, third):
                if not kind(r)[2]:
                    return
                if kind(r)[0]:
                    pool.wait_ge(*PE.at("scores", r - 2))
                if not indicated:
                    pool.wait_ge(mask_in[u], 32 * third + 32)
                    if kind(r)[1]:
                        pool.wait_ge(*A.at("shift", r - 1))
                nc.gpsimd.tensor_copy(qk1[:, u, :], qkT[:, bass.ds(P * r, P)]).then_inc(tile_made, 1)
                if not indicated:
                    nc.gpsimd.tensor_scalar(out_[:, :], mask[:, u, :], 0.0, None, ALU.is_equal).then_inc(out_made, 1)

            rounds(pool, body)

        @block.tensor
        def _(pe):
            ln_tensor(c, pe, V, A, PE, tp)
            pe.wait_ge(weights, 96)
            pe.wait_ge(*V.at("ln_T2"))
            pe.wait_ge(*A.at("ln_T3"))
            for i in range(4):
                nc.tensor.matmul(scores[:, i, :], wq[:, :], c.xnT[:, 512 * i:512 * i + 512], start=True, stop=True)\
                    .then_inc(PE.did(f"q{i}"), 1)
            for i in range(4):
                pe.wait_ge(*V.at(f"q{i}"))
                if i >= 2:
                    pe.wait_ge(*A.at(f"qk{i - 2}"))
                nc.tensor.matmul(tp[i % 2], wkT[:, :], qT[:, 512 * i:512 * i + 512], start=True, stop=True)\
                    .then_inc(PE.did(f"qk{i}"), 1)
            for t in range(NT):
                last = nc.tensor.matmul(small[:, t:t + 1], qT[:, P * t:P * t + P], bk[:, :], start=True, stop=True)
            last.then_inc(PE.did("qbk"), 1)

            def body(r, u, third):
                finishing, using, scoring = kind(r)

                def turn_context(b):
                    pe.wait_ge(ctx_in[u][b], 32 * third + 32)
                    for g in range(NG):
                        if g >= 2:
                            pe.wait_ge(*(V if b else A).at(f"ctxT{b}{g - 2}", r))
                        elif b:
                            pe.wait_ge(*A.at(f"ctxT0{g + 2}", r))
                        elif finishing:
                            pe.wait_ge(*(V, A)[g].at(f"pT{g + 2}", r - 1))
                        elif using:
                            pe.wait_ge(*V.at(f"ctxT1{g + 2}", r - 1))
                        else:
                            pe.wait_ge(*A.at(f"qk{g + 2}"))
                        for j in range(4 * g, min(4 * g + 4, KC)):
                            k = min(P, KEYS - P * j)
                            last = nc.tensor.transpose(tp[g % 2][:, P * (j % 4):P * (j % 4) + k], ctx[0:k, u, b, j, :],
                                                       c.ident[0:k, 0:k])
                        last.then_inc(*PE.inc(f"ctxT{b}{g}"))

                if scoring:
                    turn_context(0)
                    turn_context(1)
                if finishing:
                    pe.wait_ge(*V.at("o", r - 1))
                    nc.tensor.transpose(small[:, 0:P], o[:, :], c.ident[:, :]).then_inc(*PE.inc("oT"))
                if using:
                    for g in range(NG):
                        pe.wait_ge(*A.at("exp", r))
                        if g >= 2:
                            pe.wait_ge(*(V, A)[g % 2].at(f"pT{g - 2}", r))
                        elif scoring:
                            pe.wait_ge(*V.at(f"ctxT1{g + 2}", r))
                        else:
                            pe.wait_ge(*(V, A)[g].at(f"pT{g + 2}", r - 1))
                        for j in range(4 * g, min(4 * g + 4, KC)):
                            k = min(P, KEYS - P * j)
                            last = nc.tensor.transpose(tp[g % 2][0:k, P * (j % 4):P * (j % 4) + P], sc[:, P * j:P * j + k],
                                                       c.ident[:, :])
                        last.then_inc(*PE.inc(f"pT{g}"))
                if finishing:
                    pe.wait_ge(*V.at("oT", r))
                    nc.tensor.matmul(small[:, P:2 * P], oT[:, :], wv[:, :], start=True, stop=True).then_inc(*PE.inc("out"))
                if using:
                    if finishing:
                        pe.wait_ge(*V.at("o", r - 1))
                    for j in range(KC):
                        if j % 4 == 0:
                            pe.wait_ge(*(V, A)[j // 4 % 2].at(f"pT{j // 4}", r))
                        k = min(P, KEYS - P * j)
                        for b in (0, 1):
                            last = nc.tensor.matmul(mixed[S * b:S * b + S, :], probsT[0:k, j, S * b:S * b + S],
                                                    ctx[0:k, (u + 2) % 3, b, j, :], start=(j == 0), stop=(j == KC - 1),
                                                    tile_position=(0, S * b))
                    last.then_inc(*PE.inc("mixed"))
                if scoring:
                    pe.wait_ge(tile_made, r + 1)
                    pe.wait_ge(*V.at(f"ctxT1{NG - 1}", r))
                    pe.wait_ge(*A.at(f"ctxT0{NG - 1}", r))
                    if using:
                        pe.wait_ge(*V.at("masked", r - 1))
                    for g in range(NG):
                        for b in (0, 1):
                            last = nc.tensor.matmul(scores[S * b:S * b + S, g, 0:wide[g]], qk1[:, u, S * b:S * b + S],
                                                    ctxT[:, b, 512 * g:512 * g + wide[g]], start=True, stop=True,
                                                    tile_position=(0, S * b))
                    last.then_inc(*PE.inc("scores"))

            rounds(pe, body)

        @block.vector
        def _(dve):
            ln_vector(c, dve, V, A, PE, tp)
            dve.wait_ge(weights, 96)
            for i in range(4):
                dve.wait_ge(*PE.at(f"q{i}"))
                nc.vector.tensor_scalar(qT[:, 512 * i:512 * i + 512], scores[:, i, :], bq[:, 0:1], D ** -0.5,
                                        ALU.add, ALU.mult).then_inc(V.did(f"q{i}"), 1)
            dve.wait_ge(*PE.at("qbk"))
            nc.vector.tensor_copy(qbk[:, :], small[:, 0:NT]).then_inc(V.did("qbk"), 1)
            nc.vector.tensor_tensor(c.x[:, :, :], c.x[:, :, :], bv[:, :].unsqueeze(1).broadcast_to([P, NT, D]), ALU.add)\
                .then_inc(V.did("xbv"), 1)
            dve.wait_ge(*V.at("xbv"))

            def body(r, u, third):
                finishing, using, scoring = kind(r)
                if scoring:
                    for g in range(NG):
                        dve.wait_ge(*PE.at(f"ctxT1{g}", r))
                        nc.vector.tensor_copy(ctxT[:, 1, 512 * g:512 * g + wide[g]], tp[g % 2][:, 0:wide[g]])\
                            .then_inc(*V.inc(f"ctxT1{g}"))
                if finishing:
                    dve.wait_ge(*PE.at("oT", r))
                    nc.vector.tensor_copy(oT[:, :], small[:, 0:P]).then_inc(*V.inc("oT"))
                if using:
                    for g in V_PT:
                        dve.wait_ge(*PE.at(f"pT{g}", r))
                        nc.vector.tensor_copy(probsT[:, 4 * g:4 * g + 4, :].rearrange("p j q -> p (j q)"), tp[0])\
                            .then_inc(*V.inc(f"pT{g}"))
                if finishing:
                    dve.wait_ge(*PE.at("out", r))
                    xt = c.x[:, bass.ds(r - 2, 1), :].rearrange("p a d -> p (a d)")
                    nc.vector.tensor_tensor(xt, small[:, P:2 * P], xt, ALU.add).then_inc(*V.inc("x"))
                if using:
                    nc.vector.reciprocal(rinv[:, :], rows[:, (u + 2) % 3:(u + 2) % 3 + 1]).then_inc(*V.inc("rinv"))
                    dve.wait_ge(*V.at("rinv", r))
                    dve.wait_ge(*PE.at("mixed", r))
                    nc.vector.tensor_scalar(o[:, :], mixed[:, :], rinv[:, 0:1], None, ALU.mult).then_inc(*V.inc("o"))
                if scoring:
                    dve.wait_ge(*A.at("shift", r))
                    dve.wait_ge(*PE.at("scores", r))
                    nc.vector.memset(pause[:, :], 0.0)
                    nc.vector.tensor_tensor_reduce(out=sc[:, :], in0=flat, in1=shift[:, :], scale=1.0, scalar=3 * OUT,
                                                   op0=ALU.add, op1=ALU.max, accum_out=mx[:, :]).then_inc(*V.inc("masked"))
                    dve.wait_ge(*V.at("masked", r))
                    nc.vector.tensor_scalar(nmx[:, :], mx[:, :], -1.0, None, ALU.mult).then_inc(*V.inc("nmax"))

            rounds(dve, body)

        @block.scalar
        def _(act):
            ln_scalar(c, act, V, A, PE, tp)
            for i in range(4):
                act.wait_ge(*PE.at(f"qk{i}"))
                nc.scalar.copy(qkT[:, 512 * i:512 * i + 512], tp[i % 2]).then_inc(A.did(f"qk{i}"), 1)
            act.wait_ge(*V.at("qbk"))

            def body(r, u, third):
                finishing, using, scoring = kind(r)
                if scoring:
                    for g in range(NG):
                        act.wait_ge(*PE.at(f"ctxT0{g}", r))
                        nc.scalar.copy(ctxT[:, 0, 512 * g:512 * g + wide[g]], tp[g % 2][:, 0:wide[g]])\
                            .then_inc(*A.inc(f"ctxT0{g}"))
                if using:
                    act.wait_ge(*V.at("nmax", r - 1))
                    nc.scalar.activation(sc[:, :], sc[:, :], ACT.Exp, bias=nmx[:, 0:1], scale=1.0,
                                         accum_out=rows[:, (u + 2) % 3:(u + 2) % 3 + 1]).then_inc(*A.inc("exp"))
                if using:
                    for g in A_PT:
                        act.wait_ge(*PE.at(f"pT{g}", r))
                        k = P if g < NG - 1 else KREST
                        j = min(4 * g + 4, KC)
                        nc.scalar.copy(probsT[0:k, 4 * g:j, :].rearrange("p j q -> p (j q)"), tp[1][0:k, 0:P * (j - 4 * g)])\
                            .then_inc(*A.inc(f"pT{g}"))
                if scoring:
                    act.wait_ge(mask_in[u], 32 * third + 32)
                    if not indicated:
                        act.wait_ge(out_made, r + 1)
                    if using:
                        act.wait_ge(*V.at("masked", r - 1))
                    nc.scalar.copy(qbk1[:, :], qbk[:, bass.ds(r, 1)]).then_inc(*A.inc("qbk"))
                    act.wait_ge(*A.at("qbk", r))
                    nc.scalar.activation(shift[:, :], mask[:, u, :] if indicated else out_[:, :], ACT.Identity,
                                         bias=qbk1[:, 0:1], scale=OUT).then_inc(*A.inc("shift"))

            rounds(act, body)


def causal_cross_attention(c, name):
    with Stage(c, name) as s:
        nc, a = c.nc, c.a
        G = NT // 4
        w, wT = s.sb("w", [P, D]), s.sb("wT", [P, D])
        mask = s.sb("mask", [P, P])
        keys_all = s.sb("keys_all", [P, NT, D])
        keys = s.sb("keys", [P, 4, D])
        keysT = s.sb("keysT", [P, 512])
        q, qk = s.sb("q", [P, 512]), s.sb("qk", [P, 512])
        sc, probsT = s.sb("sc", [P, 4, P]), s.sb("probsT", [P, 4, P])
        mx, rows, rinv = s.sb("mx", [P, 4]), s.sb("rows", [P, 4]), s.sb("rinv", [P, 4])
        oT, o = s.sb("oT", [P, 4, P]), s.sb("o", [P, 4, D])
        turn = s.ps("turn", [P, 2, 512])
        pq, pqk, psc = s.ps("q", [P, 512]), s.ps("qk", [P, 512]), s.ps("sc", [P, 512])
        po, pout = s.ps("oT", [P, 512]), s.ps("out", [P, 512])
        loaded = s.sem("loaded")
        V = Steps(s.sem("vector_steps"), (1, LN_V), (G, ["keysT", "q", "masked", "max", "less", "rows", "rinv", "probs",
                                                        "oT", "x"]))
        A = Steps(s.sem("scalar_steps"), (1, LN_A), (G, ["keys", "qk", "exp", "probsT"]))
        PE = Steps(s.sem("tensor_steps"), (1, LN_P), (G, ["keysT", "q", "qk", "scores", "probsT", "oT", "out"]))
        tp = [turn[:, i, :] for i in (0, 1)]
        four = lambda m: m.rearrange("p (i k) -> p i k", i=4)
        wide = lambda m: m[:, :].unsqueeze(2).broadcast_to([P, 4, P])
        block = s.block()

        @block.sync
        def _(sp):
            sp.dma_start(w[:, :], a[f"{name}_Wq"]).then_inc(loaded, 16)
            sp.dma_start(wT[:, :], a[f"{name}_WqT"]).then_inc(loaded, 16)
            sp.dma_start(mask[:, :], a["c_pair_causal"]).then_inc(loaded, 16)
            for b in (0, 1):
                src = a["ctx"].rearrange("(t b) k d -> b k t d", b=2)[b, 0:S, :, :]
                sp.dma_start(keys_all[S * b:S * b + S, :, :], src).then_inc(loaded, 16)

        @block.tensor
        def _(pe):
            ln_tensor(c, pe, V, A, PE, tp)
            pe.wait_ge(*V.at("ln_T2"))
            pe.wait_ge(*A.at("ln_T3"))
            with pe.Fori(0, G) as g:
                pe.wait_ge(*A.at("keys", g))
                for i in range(4):
                    last = nc.tensor.transpose(tp[0][:, P * i:P * i + P], keys[:, i, :], c.ident[:, :])
                last.then_inc(PE.did("keysT"), 1)
                nc.tensor.matmul(pq[:, :], wT[:, :], c.xnT[:, bass.ds(512 * g, 512)], start=True, stop=True)\
                    .then_inc(PE.did("q"), 1)
                pe.wait_ge(*V.at("q", g))
                nc.tensor.matmul(pqk[:, :], w[:, :], q[:, :], start=True, stop=True).then_inc(PE.did("qk"), 1)
                pe.wait_ge(*A.at("qk", g))
                for i in range(4):
                    last = nc.tensor.matmul(psc[:, P * i:P * i + P], qk[:, P * i:P * i + P], keysT[:, P * i:P * i + P],
                                            start=True, stop=True)
                last.then_inc(PE.did("scores"), 1)
                pe.wait_ge(*V.at("probs", g))
                for i in range(4):
                    last = nc.tensor.transpose(tp[1][:, P * i:P * i + P], sc[:, i, :], c.ident[:, :])
                last.then_inc(PE.did("probsT"), 1)
                pe.wait_ge(*A.at("probsT", g))
                for i in range(4):
                    last = nc.tensor.matmul(po[:, P * i:P * i + P], keys[:, i, :], probsT[:, i, :], start=True, stop=True)
                last.then_inc(PE.did("oT"), 1)
                pe.wait_ge(*V.at("oT", g))
                for i in range(4):
                    last = nc.tensor.matmul(pout[:, P * i:P * i + P], oT[:, i, :], wT[:, :], start=True, stop=True)
                last.then_inc(PE.did("out"), 1)

        @block.vector
        def _(dve):
            ln_vector(c, dve, V, A, PE, tp)
            with dve.Fori(0, G) as g:
                dve.wait_ge(*PE.at("keysT", g))
                nc.vector.tensor_copy(keysT[:, :], tp[0]).then_inc(V.did("keysT"), 1)
                dve.wait_ge(*PE.at("q", g))
                nc.vector.tensor_scalar(q[:, :], pq[:, :], D ** -0.5, None, ALU.mult).then_inc(V.did("q"), 1)
                dve.wait_ge(*PE.at("scores", g))
                nc.vector.tensor_tensor(sc[:, :, :], four(psc[:, :]), mask[:, :].unsqueeze(1).broadcast_to([P, 4, P]),
                                        ALU.add).then_inc(V.did("masked"), 1)
                dve.wait_ge(*V.at("masked", g))
                nc.vector.tensor_reduce(mx[:, :], sc[:, :, :], AX.X, ALU.max).then_inc(V.did("max"), 1)
                dve.wait_ge(*V.at("max", g))
                nc.vector.tensor_tensor(sc[:, :, :], sc[:, :, :], wide(mx), ALU.subtract).then_inc(V.did("less"), 1)
                dve.wait_ge(*A.at("exp", g))
                nc.vector.tensor_reduce(rows[:, :], sc[:, :, :], AX.X, ALU.add).then_inc(V.did("rows"), 1)
                dve.wait_ge(*V.at("rows", g))
                nc.vector.reciprocal(rinv[:, :], rows[:, :]).then_inc(V.did("rinv"), 1)
                dve.wait_ge(*V.at("rinv", g))
                nc.vector.tensor_tensor(sc[:, :, :], sc[:, :, :], wide(rinv), ALU.mult).then_inc(V.did("probs"), 1)
                dve.wait_ge(*PE.at("oT", g))
                nc.vector.tensor_copy(oT[:, :, :], four(po[:, :])).then_inc(V.did("oT"), 1)
                dve.wait_ge(*PE.at("out", g))
                xg = c.x[:, bass.ds(4 * g, 4), :]
                nc.vector.tensor_tensor(xg, four(pout[:, :]), xg, ALU.add).then_inc(V.did("x"), 1)

        @block.scalar
        def _(act):
            ln_scalar(c, act, V, A, PE, tp)
            act.wait_ge(loaded, 80)
            with act.Fori(0, G) as g:
                act.wait_ge(*PE.before("oT", g))
                nc.scalar.copy(keys[:, :, :], keys_all[:, bass.ds(4 * g, 4), :]).then_inc(A.did("keys"), 1)
                act.wait_ge(*PE.at("qk", g))
                nc.scalar.copy(qk[:, :], pqk[:, :]).then_inc(A.did("qk"), 1)
                act.wait_ge(*V.at("less", g))
                nc.scalar.activation(sc[:, :, :], sc[:, :, :], ACT.Exp).then_inc(A.did("exp"), 1)
                act.wait_ge(*PE.at("probsT", g))
                nc.scalar.copy(probsT[:, :, :], four(tp[1])).then_inc(A.did("probsT"), 1)


def in_turn(names, scored, valued, last):
    steps = []
    for k, n in enumerate(names):
        steps += of(n, *scored) + (valued(names[k - 1]) if k else []) + of(n, *last)
    return steps + valued(names[-1])


def of(tag, *names):
    return [f"{tag}_{n}" for n in names]


class Heads:

    def __init__(self, s):
        self.hb = s.sb("hb", [P, 4])
        self.which = s.sb("which", [P, 8, P])
        self.delta = s.sb("delta", [P, S])
        self.heads = s.sb("heads", [P, H])
        self.sets = [HeadsBuffers(s, f"{i}") for i in (0, 1)]

    def load(self, eng, a, sem):
        eng.dma_start(self.hb[:, :], a["c_heads"]).then_inc(sem, 16)
        eng.dma_start(self.which[:, :, :], a["c_which"]).then_inc(sem, 16)
        eng.dma_start(self.delta[:, :], a["c_delta"]).then_inc(sem, 16)
        eng.dma_start(self.heads[:, :], a["c_sixteen_heads"]).then_inc(sem, 16)


class HeadsBuffers:
    def __init__(self, s, i):
        self.qd = s.sb("qd" + i, [P, 2, H, S])
        self.sc = s.sb("sc" + i, [P, 16, S])
        self.mx, self.rows, self.rinv = (s.sb(n + i, [P, 16]) for n in ("mx", "rows", "rinv"))
        self.diag = s.sb("diag" + i, [P, 16, S])
        self.pT = s.sb("pT" + i, [P, 8, P])
        self.own = s.sb("own" + i, [P, 2, 4, S])
        self.sum = s.sb("sum" + i, [P, 2, S])
        self.norm = s.sb("norm" + i, [P, P])
        self.ps = s.ps("scores" + i, [P, 2, 512])
        self.turn = s.ps("turn" + i, [P, 512])


def heads_spread(c, h, b, made, q):
    for n in (0, 1):
        last = c.nc.gpsimd.tensor_tensor(b.qd[:, n, :, :], q[:, S * n:S * n + S].unsqueeze(1).broadcast_to([P, H, S]),
                                         h.heads[:, :].unsqueeze(2).broadcast_to([P, H, S]), ALU.mult)
    last.then_inc(made, 1)


def heads_masked(c, dve, b, V, PE, tag, t, mask):
    nc = c.nc
    dve.wait_ge(*PE.at(f"{tag}_scores", t))
    scores = b.ps[:, :, :].rearrange("p n (r k) -> p (n r) k", k=S)
    if mask is not None:
        nc.vector.tensor_tensor(b.sc[:, :, :], scores, mask[:, :].unsqueeze(1).broadcast_to([P, 16, S]), ALU.add)\
            .then_inc(V.did(f"{tag}_masked"), 1)
        dve.wait_ge(*V.at(f"{tag}_masked", t))
        scores = b.sc[:, :, :]
    nc.vector.tensor_reduce(b.mx[:, :], scores, AX.X, ALU.max).then_inc(V.did(f"{tag}_max"), 1)
    dve.wait_ge(*V.at(f"{tag}_max", t))
    nc.vector.tensor_tensor(b.sc[:, :, :], scores, b.mx[:, :].unsqueeze(2).broadcast_to([P, 16, S]), ALU.subtract)\
        .then_inc(V.did(f"{tag}_less"), 1)


def heads_norms(c, dve, b, V, A, tag, t, delta):
    nc = c.nc
    dve.wait_ge(*A.at(f"{tag}_exp", t))
    nc.vector.tensor_reduce(b.rows[:, :], b.sc[:, :, :], AX.X, ALU.add).then_inc(V.did(f"{tag}_rows"), 1)
    dve.wait_ge(*V.at(f"{tag}_rows", t))
    nc.vector.reciprocal(b.rinv[:, :], b.rows[:, :]).then_inc(V.did(f"{tag}_rinv"), 1)
    dve.wait_ge(*V.at(f"{tag}_rinv", t))
    nc.vector.tensor_tensor(b.diag[:, :, :], b.rinv[:, :].unsqueeze(2).broadcast_to([P, 16, S]),
                            delta[:, :].unsqueeze(1).broadcast_to([P, 16, S]), ALU.mult).then_inc(V.did(f"{tag}_diag"), 1)


def heads_result(c, dve, h, b, V, PE, tag, t, out):
    nc = c.nc
    dve.wait_ge(*PE.at(f"{tag}_pv", t))
    nc.vector.tensor_tensor(b.own[:, :, :, :], b.ps[:, :, 0:256].rearrange("p b (h q) -> p b h q", h=4),
                            h.hb[:, :].unsqueeze(1).unsqueeze(3).broadcast_to([P, 2, 4, S]), ALU.mult)\
        .then_inc(V.did(f"{tag}_own"), 1)
    nc.vector.tensor_copy(b.norm[:, :], b.ps[:, 0, 256:256 + P]).then_inc(V.did(f"{tag}_norm"), 1)
    dve.wait_ge(*V.at(f"{tag}_own", t))
    nc.vector.tensor_reduce(b.sum[:, :, :], b.own[:, :, :, :].rearrange("p b h q -> p b q h"), AX.X, ALU.add)\
        .then_inc(V.did(f"{tag}_sum"), 1)
    dve.wait_ge(*V.at(f"{tag}_sum", t))
    nc.vector.tensor_tensor(out, b.sum[:, :, :].rearrange("p b q -> p (b q)"), b.norm[:, :], ALU.mult)\
        .then_inc(V.did(f"{tag}_scale"), 1)


def heads_exp(c, act, b, V, A, tag, t):
    act.wait_ge(*V.at(f"{tag}_less", t))
    c.nc.scalar.activation(b.sc[:, :, :], b.sc[:, :, :], ACT.Exp).then_inc(A.did(f"{tag}_exp"), 1)


def heads_turned(c, act, b, A, PE, tag, t):
    for i in (0, 1):
        act.wait_ge(*PE.at(f"{tag}_pT{i}", t))
        c.nc.scalar.copy(b.pT[:, 4 * i:4 * i + 4, :].rearrange("p r q -> p (r q)"), b.turn[:, :]).then_inc(A.did(f"{tag}_pT{i}"), 1)


def heads_scores(c, b, PE, tag, k):
    for r in range(H // 2):
        for n in (0, 1):
            at = (2 * r + n) * S
            last = c.nc.tensor.matmul(b.ps[:, at // 512, at % 512:at % 512 + S],
                                      b.qd[:, n, 2 * r:2 * r + 2, :].rearrange("p h q -> p (h q)"),
                                      k[:, S * n:S * n + S], start=True, stop=True)
    last.then_inc(PE.did(f"{tag}_scores"), 1)


def heads_values(c, pe, h, b, V, A, PE, tag, t, v):
    nc = c.nc

    def norm(rs):
        for r in rs:
            last = nc.tensor.matmul(b.ps[:, 0, 256:256 + P], h.which[:, r, :],
                                    b.diag[:, 2 * r:2 * r + 2, :].rearrange("p b q -> p (b q)"), start=(r == 0), stop=(r == 7))
        return last

    pe.wait_ge(*A.at(f"{tag}_exp", t))
    for i in (0, 1):
        if i:
            pe.wait_ge(*V.at(f"{tag}_diag", t))
            norm(range(4))
            pe.wait_ge(*A.at(f"{tag}_pT0", t))
        for r in range(4):
            last = nc.tensor.transpose(b.turn[:, P * r:P * r + P],
                                       b.sc[:, 8 * i + 2 * r:8 * i + 2 * r + 2, :].rearrange("p b k -> p (b k)"), c.ident[:, :])
        last.then_inc(PE.did(f"{tag}_pT{i}"), 1)
    norm(range(4, 7))
    pe.wait_ge(*A.at(f"{tag}_pT1", t))
    norm([7]).then_inc(PE.did(f"{tag}_norm"), 1)
    for n in (0, 1):
        for g in range(4):
            last = nc.tensor.matmul(b.ps[32 * g:32 * g + 32, n, 0:256], v[S * n:S * n + S, 32 * g:32 * g + 32],
                                    b.pT[S * n:S * n + S, 2 * g:2 * g + 2, :].rearrange("p r q -> p (r q)"),
                                    start=True, stop=True, tile_position=(S * n, 32 * g))
    last.then_inc(PE.did(f"{tag}_pv"), 1)


def self_attention(c, name):
    with Stage(c, name) as s:
        nc, a = c.nc, c.a
        h = Heads(s)
        w = s.sb("w", [P, 5, D])
        wo = s.sb("wo", [P, D])
        cos, sin = s.sb("cos", [P, S]), s.sb("sin", [P, S])
        xg = s.sb("xg", [P, 512])
        straight, turned = s.sb("straight", [P, 2, 512]), s.sb("turned", [P, 2, 512])
        qT, kT, v, yT = s.sb("qT", [P, 512]), s.sb("kT", [P, 512]), s.sb("v", [P, 4, D]), s.sb("yT", [P, 4, P])
        pa, pb = s.ps("a", [P, 512]), s.ps("b", [P, 512])
        loaded, spread = s.sem("loaded"), s.sem("spread")
        tags = [f"t{i}" for i in range(4)]
        G = NT // 4
        V = Steps(s.sem("vector_steps"), (1, LN_V),
                  (G, ["q_cos", "q_sin", "q", "k_cos", "k_sin", "k"] +
                   in_turn(tags, ["max", "less"], lambda n: of(n, "own", "norm", "sum", "scale"),
                           ["rows", "rinv", "diag"]) + ["x"]))
        A = Steps(s.sem("scalar_steps"), (1, LN_A), (G, ["xg", "v"] + in_turn(
            tags, [], lambda n: of(n, "pT0", "pT1"), ["exp"])))
        PE = Steps(s.sem("tensor_steps"), (1, LN_P), (G, ["q", "k", "v"] + in_turn(
            tags, ["scores"], lambda n: of(n, "pT0", "pT1", "norm", "pv"), []) + ["out"]))
        tp = [b.turn[:, :] for b in h.sets]
        tiles = list(enumerate(tags))
        eight = lambda m: m.rearrange("p (b q) -> p b q", q=S)
        wide = lambda m: m[:, :].unsqueeze(1).broadcast_to([P, 8, S])
        block = s.block()

        @block.sync
        def _(sp):
            h.load(sp, a, loaded)
            sp.dma_start(w[:, :, :], a[f"{name}_w"].rearrange("n p d -> p n d")).then_inc(loaded, 16)
            sp.dma_start(wo[:, :], a[f"{name}_wo"]).then_inc(loaded, 16)
            sp.dma_start(cos[:, :], a["c_cos"]).then_inc(loaded, 16)
            sp.dma_start(sin[:, :], a["c_sin"]).then_inc(loaded, 16)

        @block.gpsimd
        def _(pool):
            pool.wait_ge(loaded, 128)
            with pool.Fori(0, G) as g:
                pool.wait_ge(*V.at("q", g))
                for k, tag in enumerate(tags):
                    if k >= 2:
                        pool.wait_ge(*PE.at(f"{tags[k - 2]}_scores", g))
                    heads_spread(c, h, h.sets[k % 2], spread, qT[:, P * k:P * k + P])

        @block.tensor
        def _(pe):
            ln_tensor(c, pe, V, A, PE, tp)
            pe.wait_ge(loaded, 128)
            with pe.Fori(0, G) as g:
                pe.wait_ge(*A.at("xg", g))
                nc.tensor.matmul(pa[:, :], w[:, 0, :], xg[:, :], start=True, stop=True)
                nc.tensor.matmul(pb[:, :], w[:, 1, :], xg[:, :], start=True, stop=True).then_inc(PE.did("q"), 1)
                pe.wait_ge(*V.at("q_sin", g))
                nc.tensor.matmul(pa[:, :], w[:, 2, :], xg[:, :], start=True, stop=True)
                nc.tensor.matmul(pb[:, :], w[:, 3, :], xg[:, :], start=True, stop=True).then_inc(PE.did("k"), 1)
                pe.wait_ge(*V.at("k_sin", g))
                for i in range(4):
                    last = nc.tensor.matmul(pa[:, P * i:P * i + P], xg[:, P * i:P * i + P], w[:, 4, :], start=True, stop=True)
                last.then_inc(PE.did("v"), 1)
                pe.wait_ge(*V.at("k", g))
                for i, tag in tiles:
                    pe.wait_ge(spread, 4 * g + (i + 1))
                    if i >= 2:
                        pe.wait_ge(*V.at(f"{tags[i - 2]}_norm", g))
                    heads_scores(c, h.sets[i % 2], PE, tag, kT[:, P * i:P * i + P])
                    if i == 1:
                        pe.wait_ge(*A.at("v", g))
                    if i:
                        heads_values(c, pe, h, h.sets[(i - 1) % 2], V, A, PE, tags[i - 1], g, v[:, i - 1, :])
                heads_values(c, pe, h, h.sets[1], V, A, PE, tags[3], g, v[:, 3, :])
                pe.wait_ge(*V.at("t3_scale", g))
                for i in range(4):
                    last = nc.tensor.matmul(pb[:, P * i:P * i + P], yT[:, i, :], wo[:, :], start=True, stop=True)
                last.then_inc(PE.did("out"), 1)

        @block.vector
        def _(dve):
            ln_vector(c, dve, V, A, PE, tp)
            with dve.Fori(0, G) as g:
                for m, (n, dst, scale) in enumerate((("q", qT, DH ** -0.5), ("k", kT, 1.0))):
                    dve.wait_ge(*PE.at(n, g))
                    nc.vector.scalar_tensor_tensor(out=eight(straight[:, m, :]), in0=eight(pa[:, :]), scalar=scale,
                                                   in1=wide(cos), op0=ALU.mult, op1=ALU.mult).then_inc(V.did(f"{n}_cos"), 1)
                    nc.vector.scalar_tensor_tensor(out=eight(turned[:, m, :]), in0=eight(pb[:, :]), scalar=scale,
                                                   in1=wide(sin), op0=ALU.mult, op1=ALU.mult).then_inc(V.did(f"{n}_sin"), 1)
                    dve.wait_ge(*V.at(f"{n}_sin", g))
                    nc.vector.tensor_tensor(dst[:, :], straight[:, m, :], turned[:, m, :], ALU.add).then_inc(V.did(n), 1)
                result = lambda i: heads_result(c, dve, h, h.sets[i % 2], V, PE, tags[i], g, yT[:, i, :])
                for i, tag in tiles:
                    heads_masked(c, dve, h.sets[i % 2], V, PE, tag, g, None)
                    if i:
                        result(i - 1)
                    heads_norms(c, dve, h.sets[i % 2], V, A, tag, g, h.delta)
                result(3)
                dve.wait_ge(*PE.at("out", g))
                xs = c.x[:, bass.ds(4 * g, 4), :]
                nc.vector.tensor_tensor(xs, pb[:, :].rearrange("p (i d) -> p i d", i=4), xs, ALU.add).then_inc(V.did("x"), 1)

        @block.scalar
        def _(act):
            ln_scalar(c, act, V, A, PE, tp)
            with act.Fori(0, G) as g:
                act.wait_ge(*V.at("ln_T2"))
                act.wait_ge(*V.before("x", g))
                nc.scalar.copy(xg[:, :], c.xnT[:, bass.ds(512 * g, 512)]).then_inc(A.did("xg"), 1)
                act.wait_ge(*PE.at("v", g))
                nc.scalar.copy(v[:, :, :], pa[:, :].rearrange("p (i d) -> p i d", i=4)).then_inc(A.did("v"), 1)
                for i, tag in tiles:
                    if i:
                        heads_turned(c, act, h.sets[(i - 1) % 2], A, PE, tags[i - 1], g)
                    heads_exp(c, act, h.sets[i % 2], V, A, tag, g)
                heads_turned(c, act, h.sets[1], A, PE, tags[3], g)


def two_step_attention(c, name):
    with Stage(c, name) as s:
        nc, a = c.nc, c.a
        h = Heads(s)
        w, wp = s.sb("w", [P, 3, D]), s.sb("wp", [P, D])
        bias = s.sb("bias", [P, 3])
        bp, bp2 = s.sb("bp", [P, D]), s.sb("bp2", [P, D])
        causal, strict = s.sb("causal", [P, S]), s.sb("strict", [P, S])
        later = s.sb("later", [P, S])
        vg = s.sb("vg", [P, 4, D])
        qT, kT, k2T = s.sb("qT", [P, 512]), s.sb("kT", [P, 512]), s.sb("k2T", [P, 512])
        xg = s.sb("xg", [P, 512])
        yT, y2T, sumT = s.sb("yT", [P, 4, P]), s.sb("y2T", [P, 2, P]), s.sb("sumT", [P, 4, P])
        eT, e = s.sb("eT", [P, 2, 2, S]), s.sb("e", [P, 2, D])
        pa, pb = s.ps("a", [P, 512]), s.ps("b", [P, 512])
        loaded, spread = s.sem("loaded"), s.sem("spread")
        G = NT // 4
        turn = [(i, second) for pair in (0, 2) for second in (False, True) for i in (pair, pair + 1)]
        tags = [f"u{i}" + "b" * second for i, second in turn]
        extra = lambda n: [f"{n}_total"] if n[-1] == "b" else [f"{n}_err"]
        V = Steps(s.sem("vector_steps"), (1, LN_V + ["bp2", "eT"]),
                  (G, ["q", "k2"] + in_turn(tags, ["masked", "max", "less"],
                                            lambda n: of(n, "own", "norm", "sum", "scale") + extra(n), ["rows", "rinv", "diag"]) +
                   ["bias", "x"]))
        A = Steps(s.sem("scalar_steps"), (1, LN_A), (G, ["xg", "vg", "k"] + in_turn(
            tags, [], lambda n: (of(n[:-1], "e") if n[-1] == "b" else []) + of(n, "pT0", "pT1"), ["exp"])))
        PE = Steps(s.sem("tensor_steps"), (1, LN_P), (G, ["q", "k", "k2"] + in_turn(
            tags, ["scores"], lambda n: (of(n[:-1], "e") if n[-1] == "b" else []) + of(n, "pT0", "pT1", "norm", "pv"), []) +
            ["out"]))
        tp = [b.turn[:, :] for b in h.sets]
        K = len(turn)
        is_second = lambda k: turn[k][1]
        four = lambda m: m.rearrange("p (i d) -> p i d", i=4)
        block = s.block()

        @block.sync
        def _(sp):
            h.load(sp, a, loaded)
            sp.dma_start(w[:, :, :], a[f"{name}_w"].rearrange("n p d -> p n d")).then_inc(loaded, 16)
            sp.dma_start(bias[:, :], a[f"{name}_bias"]).then_inc(loaded, 16)
            sp.dma_start(wp[:, :], a[f"{name}_W_proj"]).then_inc(loaded, 16)
            sp.dma_start(bp[:, :], a[f"{name}_b_proj"].broadcast_to([P, D])).then_inc(loaded, 16)
            sp.dma_start(causal[:, :], a["c_causal"]).then_inc(loaded, 16)
            sp.dma_start(strict[:, :], a["c_strict"]).then_inc(loaded, 16)
            sp.dma_start(later[:, :], a["c_later"]).then_inc(loaded, 16)

        @block.gpsimd
        def _(pool):
            pool.wait_ge(loaded, 176)
            with pool.Fori(0, G) as g:
                pool.wait_ge(*V.at("q", g))
                for k, tag in enumerate(tags):
                    if k >= 2:
                        pool.wait_ge(*PE.at(f"{tags[k - 2]}_scores", g))
                    heads_spread(c, h, h.sets[k % 2], spread, qT[:, P * turn[k][0]:P * turn[k][0] + P])

        @block.tensor
        def _(pe):
            ln_tensor(c, pe, V, A, PE, tp)
            pe.wait_ge(loaded, 176)
            with pe.Fori(0, G) as g:
                pe.wait_ge(*A.at("xg", g))
                nc.tensor.matmul(pa[:, :], w[:, 0, :], xg[:, :], start=True, stop=True).then_inc(PE.did("q"), 1)
                pe.wait_ge(*V.before("x", g))
                nc.tensor.matmul(pb[:, :], w[:, 1, :], xg[:, :], start=True, stop=True).then_inc(PE.did("k"), 1)
                pe.wait_ge(*V.at("q", g))
                nc.tensor.matmul(pa[:, :], w[:, 2, :], xg[:, :], start=True, stop=True).then_inc(PE.did("k2"), 1)

                def values(k):
                    i, second = turn[k]
                    if second:
                        pe.wait_ge(*V.at(f"u{i}_err", g))
                        if i:
                            pe.wait_ge(*A.at(f"u{i - 1}_e", g))
                        nc.tensor.transpose(pa[:, 0:P], eT[:, i % 2, :, :].rearrange("p b q -> p (b q)"), c.ident[:, :])\
                            .then_inc(PE.did(f"u{i}_e"), 1)
                        pe.wait_ge(*A.at(f"u{i}_e", g))
                    heads_values(c, pe, h, h.sets[k % 2], V, A, PE, tags[k], g, e[:, i % 2, :] if second else vg[:, i, :])

                pe.wait_ge(*A.at("k", g))
                pe.wait_ge(*V.at("k2", g))
                for k in range(K):
                    i, second = turn[k]
                    pe.wait_ge(spread, K * g + (k + 1))
                    if k >= 2:
                        pe.wait_ge(*V.at(f"{tags[k - 2]}_norm", g))
                    heads_scores(c, h.sets[k % 2], PE, tags[k], (k2T if second else kT)[:, P * i:P * i + P])
                    if k:
                        values(k - 1)
                values(K - 1)
                pe.wait_ge(*V.at("u3b_total", g))
                for i in range(4):
                    last = nc.tensor.matmul(pb[:, P * i:P * i + P], sumT[:, i, :], wp[:, :], start=True, stop=True)
                last.then_inc(PE.did("out"), 1)

        @block.vector
        def _(dve):
            ln_vector(c, dve, V, A, PE, tp)
            dve.wait_ge(loaded, 176)
            nc.vector.tensor_tensor(bp2[:, :], bp[:, :], bp[:, :], ALU.add).then_inc(V.did("bp2"), 1)
            nc.vector.memset(eT[:, :, :, S - 1:S], 0.0).then_inc(V.did("eT"), 1)
            with dve.Fori(0, G) as g:
                dve.wait_ge(*PE.at("q", g))
                nc.vector.tensor_scalar(qT[:, :], pa[:, :], bias[:, 0:1], DH ** -0.5, ALU.add, ALU.mult)\
                    .then_inc(V.did("q"), 1)
                dve.wait_ge(*PE.at("k2", g))
                nc.vector.tensor_scalar(k2T[:, :], pa[:, :], bias[:, 2:3], None, ALU.add).then_inc(V.did("k2"), 1)

                def result(k):
                    i, second = turn[k]
                    y = y2T[:, i % 2, :] if second else yT[:, i, :]
                    heads_result(c, dve, h, h.sets[k % 2], V, PE, tags[k], g, y)
                    dve.wait_ge(*V.at(f"{tags[k]}_scale", g))
                    if second:
                        nc.vector.tensor_tensor(sumT[:, i, :], yT[:, i, :], y, ALU.add).then_inc(V.did(f"{tags[k]}_total"), 1)
                    else:
                        v2, y2 = (m.rearrange("p (b q) -> p b q", b=2) for m in (xg[:, P * i:P * i + P], y))
                        nc.vector.tensor_tensor(eT[:, i % 2, :, 0:S - 1], v2[:, :, 1:S], y2[:, :, 0:S - 1], ALU.subtract)\
                            .then_inc(V.did(f"{tags[k]}_err"), 1)

                for k in range(K):
                    second = is_second(k)
                    heads_masked(c, dve, h.sets[k % 2], V, PE, tags[k], g, strict if second else causal)
                    if k:
                        result(k - 1)
                    heads_norms(c, dve, h.sets[k % 2], V, A, tags[k], g, later if second else h.delta)
                result(K - 1)
                xs = c.x[:, bass.ds(4 * g, 4), :]
                nc.vector.tensor_tensor(xs, xs, bp2[:, :].unsqueeze(1).broadcast_to([P, 4, D]), ALU.add)\
                    .then_inc(V.did("bias"), 1)
                dve.wait_ge(*V.at("bias", g))
                dve.wait_ge(*PE.at("out", g))
                nc.vector.tensor_tensor(xs, four(pb[:, :]), xs, ALU.add).then_inc(V.did("x"), 1)

        @block.scalar
        def _(act):
            ln_scalar(c, act, V, A, PE, tp)
            with act.Fori(0, G) as g:
                act.wait_ge(*V.before("x", g))
                nc.scalar.copy(xg[:, :], c.xnT[:, bass.ds(512 * g, 512)]).then_inc(A.did("xg"), 1)
                nc.scalar.copy(vg[:, :, :], c.xn[:, bass.ds(4 * g, 4), :]).then_inc(A.did("vg"), 1)
                act.wait_ge(*PE.at("k", g))
                nc.scalar.activation(kT[:, :], pb[:, :], ACT.Identity, bias=bias[:, 1:2]).then_inc(A.did("k"), 1)

                def turned(k):
                    i, second = turn[k]
                    if second:
                        act.wait_ge(*PE.at(f"u{i}_e", g))
                        nc.scalar.copy(e[:, i % 2, :], pa[:, 0:P]).then_inc(A.did(f"u{i}_e"), 1)
                    heads_turned(c, act, h.sets[k % 2], A, PE, tags[k], g)

                for k in range(K):
                    if k:
                        turned(k - 1)
                    heads_exp(c, act, h.sets[k % 2], V, A, tags[k], g)
                turned(K - 1)


def spectral_layer(c, name):
    F2 = P
    with Stage(c, name) as s:
        nc, a = c.nc, c.a
        cols = s.sb("cols", [P, 4])
        wto, wfrom = s.sb("wto", [P, F2]), s.sb("wfrom", [F2, D])
        w1, b1 = s.sb("w1", [P, 4 * D]), s.sb("b1", [P, 4])
        w2, b2 = s.sb("w2", [P, 4, D]), s.sb("b2", [P, D])
        b2s = s.sb("b2s", [P, D])
        halves, freq = s.sb("halves", [F2, 2]), s.sb("freq", [F2, 32])
        raw = s.sb("raw", [F2, 2])
        decay, omega = s.sb("decay", [F2, 1]), s.sb("omega", [F2, 1])
        sine, half = s.sb("sine", [F2, 1]), s.sb("half", [F2, 1])
        half2, cosine = s.sb("half2", [F2, 1]), s.sb("cosine", [F2, 1])
        part = s.sb("part", [F2, 2])
        factor = s.sb("factor", [F2, 2])
        rot = s.sb("rot", [F2, F2])
        rot_u, rot_z = s.sb("rot_u", [F2, F2]), s.sb("rot_z", [F2, F2])
        h, hT = s.sb("h", [P, NT, D]), s.sb("hT", [P, TOK])
        uT = s.sb("uT", [F2, TOK])
        z = s.sb("z", [F2, B, S + 1])
        x2, x2b = s.sb("x2", [P, NT, D]), s.sb("x2b", [P, NT, D])
        g = s.sb("gelu", [P, 4, 512])
        turn = s.ps("turn", [P, 2, 512])
        step = s.ps("step", [P, 2, 512])
        big = s.ps("big", [P, 2, 512])
        loaded = s.sem("loaded")
        n1 = Norm(c, turned=False)
        n2 = Norm(c, "in", c.xn, h, hT, cols[:, 0:1], cols[:, 1:2])
        n3 = Norm(c, "ff", x2, h, hT, cols[:, 2:3], cols[:, 3:4])
        V = Steps(s.sem("vector_steps"),
                  (1, ["b2s", "z0", "rot", "half2", "cosine", "part0", "part1", "factor0", "factor1", "rot0", "rot1", "rot_u", "rot_z"] +
                   n1.V + n2.V + ["u0", "u2"]),
                  (S, ["clip"], 2), (1, ["x2_0", "x2_1", "x2_2", "x2_3"] + n3.V + ["x2b", "xb"]), (4, ["x"]))
        A = Steps(s.sem("scalar_steps"), (1, ["omega", "decay", "sine", "half"] + n1.A + n2.A + ["u1", "u3"] + n3.A),
                  (4, [f"g{i}" for i in range(4)]))
        PE = Steps(s.sem("tensor_steps"), (1, n2.P + [f"u{i}" for i in range(4)]), (S, ["step"], 2),
                   (1, ["from0", "from1", "from2", "from3"] + n3.P), (4, [f"h{i}" for i in range(4)] + ["out"]))
        tp = [turn[:, i, :] for i in (0, 1)]
        four = lambda m: m.rearrange("p (i d) -> p i d", i=4)
        u3 = uT[:, :].rearrange("f (b s) -> f b s", b=B)
        block = s.block()

        @block.sync
        def _(sp):
            sp.dma_start(raw[:, 0:1], a[f"{name}_decay"]).then_inc(loaded, 16)
            sp.dma_start(raw[:, 1:2], a[f"{name}_freq"]).then_inc(loaded, 16)
            sp.dma_start(halves[:, :], a["c_halves"]).then_inc(loaded, 16)
            sp.dma_start(freq[:, :], a["c_freq"]).then_inc(loaded, 16)
            sp.dma_start(cols[:, :], a[f"{name}_cols"]).then_inc(loaded, 16)
            sp.dma_start(wto[:, :], a[f"{name}_W_toT"]).then_inc(loaded, 16)
            sp.dma_start(wfrom[:, :], a[f"{name}_W_fromT"]).then_inc(loaded, 16)
            sp.dma_start(w1[:, :], a[f"{name}_W1T"]).then_inc(loaded, 16)
            sp.dma_start(b1[:, :], a[f"{name}_b1"]).then_inc(loaded, 16)
            sp.dma_start(w2[:, :, :], a[f"{name}_W2T"].rearrange("(c p) d -> p c d", p=P)).then_inc(loaded, 16)
            sp.dma_start(b2[:, :], a[f"{name}_b2"].broadcast_to([P, D])).then_inc(loaded, 16)

        @block.tensor
        def _(pe):
            ln_tensor(c, pe, V, A, PE, tp, n2)
            pe.wait_ge(*V.at("in_T2"))
            pe.wait_ge(*A.at("in_T3"))
            for i in range(4):
                if i >= 2:
                    pe.wait_ge(*(A if i % 2 else V).at(f"u{i - 2}"))
                nc.tensor.matmul(big[0:F2, i % 2, :], wto[:, :], hT[:, 512 * i:512 * i + 512], start=True, stop=True)\
                    .then_inc(PE.did(f"u{i}"), 1)
            pe.wait_ge(*V.at("u2"))
            pe.wait_ge(*A.at("u3"))
            with pe.Fori(0, S // 2) as k:
                for u in (0, 1):
                    t = 2 * k + u
                    pe.wait_ge(*V.before("clip", t))
                    nc.tensor.matmul(step[0:F2, u, 0:B], rot_u[:, :], u3[:, :, bass.ds(t, 1)], start=True, stop=False)
                    nc.tensor.matmul(step[0:F2, u, 0:B], rot_z[:, :], z[:, :, bass.ds(t, 1)], start=False, stop=True)\
                        .then_inc(PE.did("step"), 1)
            pe.wait_ge(*V.at("clip", S - 1))
            for i in range(4):
                if i >= 2:
                    pe.wait_ge(*V.at(f"x2_{i - 2}"))
                for j in range(4):
                    for b in (0, 1):
                        last = nc.tensor.matmul(big[S * b:S * b + S, i % 2, P * j:P * j + P], z[:, 8 * i + 2 * j + b, 1:S + 1],
                                                wfrom[:, :], start=True, stop=True)
                last.then_inc(PE.did(f"from{i}"), 1)
            ln_tensor(c, pe, V, A, PE, tp, n3)
            pe.wait_ge(*V.at("ff_T2"))
            pe.wait_ge(*A.at("ff_T3"))
            with pe.Fori(0, 4) as i:
                for k in range(4):
                    pe.wait_ge(*(A.at(f"g{k - 2}", i) if k >= 2 else A.before(f"g{k + 2}", i)))
                    nc.tensor.matmul(tp[k % 2], w1[:, P * k:P * k + P], hT[:, bass.ds(512 * i, 512)], start=True, stop=True)\
                        .then_inc(PE.did(f"h{k}"), 1)
                pe.wait_ge(*A.at("g3", i))
                pe.wait_ge(*V.before("x", i))
                for j in range(4):
                    for k in range(4):
                        last = nc.tensor.matmul(big[:, 0, P * j:P * j + P], g[:, k, P * j:P * j + P], w2[:, k, :],
                                                start=(k == 0), stop=(k == 3))
                last.then_inc(PE.did("out"), 1)

        @block.vector
        def _(dve):
            dve.wait_ge(loaded, 176)
            nc.vector.tensor_scalar(b2s[:, :], b2[:, :], 0.1, None, ALU.mult).then_inc(V.did("b2s"), 1)
            nc.vector.memset(z[:, :, 0:1], 0.0).then_inc(V.did("z0"), 1)
            nc.vector.memset(rot[:, :], 0.0).then_inc(V.did("rot"), 1)
            dve.wait_ge(*A.at("half"))
            nc.vector.tensor_tensor(half2[:, :], half[:, :], half[:, :], ALU.mult).then_inc(V.did("half2"), 1)
            dve.wait_ge(*V.at("half2"))
            nc.vector.tensor_scalar(cosine[:, :], half2[:, :], -2.0, 1.0, ALU.mult, ALU.add).then_inc(V.did("cosine"), 1)
            nc.vector.tensor_tensor(part[:, 0:1], sine[:, :], halves[:, 1:2], ALU.mult).then_inc(V.did("part0"), 1)
            nc.vector.tensor_tensor(part[:, 1:2], sine[:, :], halves[:, 0:1], ALU.mult).then_inc(V.did("part1"), 1)
            dve.wait_ge(*V.at("part1"))
            nc.vector.scalar_tensor_tensor(out=factor[:, 0:1], in0=cosine[:, :], scalar=halves[:, 0:1], in1=part[:, 0:1],
                                           op0=ALU.mult, op1=ALU.subtract).then_inc(V.did("factor0"), 1)
            nc.vector.scalar_tensor_tensor(out=factor[:, 1:2], in0=cosine[:, :], scalar=halves[:, 1:2], in1=part[:, 1:2],
                                           op0=ALU.mult, op1=ALU.add).then_inc(V.did("factor1"), 1)
            dve.wait_ge(*V.at("factor1"))
            for i in (0, 1):
                nc.vector.tensor_scalar(rot[:, 32 * i:32 * i + 32], freq[:, :], factor[:, i:i + 1], None, ALU.mult)\
                    .then_inc(V.did(f"rot{i}"), 1)
            dve.wait_ge(*V.at("rot1"))
            nc.vector.tensor_scalar(rot_u[:, :], rot[:, :], 0.1, None, ALU.mult).then_inc(V.did("rot_u"), 1)
            nc.vector.tensor_scalar(rot_z[:, :], rot[:, :], decay[:, 0:1], None, ALU.mult).then_inc(V.did("rot_z"), 1)
            ln_vector(c, dve, V, A, PE, tp, n1)
            dve.wait_ge(*V.at("ln_xn"))
            ln_vector(c, dve, V, A, PE, tp, n2)
            for i in (0, 2):
                dve.wait_ge(*PE.at(f"u{i}"))
                nc.vector.tensor_copy(uT[:, 512 * i:512 * i + 512], big[0:F2, 0, :]).then_inc(V.did(f"u{i}"), 1)
            with dve.Fori(0, S // 2) as k:
                for u in (0, 1):
                    t = 2 * k + u
                    dve.wait_ge(*PE.at("step", t))
                    nc.vector.tensor_scalar(z[:, :, bass.ds(t + 1, 1)], step[0:F2, u, 0:B].unsqueeze(2), 10.0, -10.0,
                                            ALU.min, ALU.max).then_inc(V.did("clip"), 1)
            for i in range(4):
                dve.wait_ge(*PE.at(f"from{i}"))
                nc.vector.scalar_tensor_tensor(out=x2[:, 4 * i:4 * i + 4, :].rearrange("p i d -> p (i d)"), in0=big[:, i % 2, :],
                                               scalar=0.1, in1=c.xn[:, 4 * i:4 * i + 4, :].rearrange("p i d -> p (i d)"),
                                               op0=ALU.mult, op1=ALU.add).then_inc(V.did(f"x2_{i}"), 1)
            dve.wait_ge(*V.at("x2_3"))
            ln_vector(c, dve, V, A, PE, tp, n3)
            nc.vector.tensor_tensor(x2b[:, :, :], x2[:, :, :], b2s[:, :].unsqueeze(1).broadcast_to([P, NT, D]), ALU.add)\
                .then_inc(V.did("x2b"), 1)
            dve.wait_ge(*V.at("x2b"))
            nc.vector.tensor_tensor(c.x[:, :, :], c.x[:, :, :], x2b[:, :, :], ALU.add).then_inc(V.did("xb"), 1)
            dve.wait_ge(*V.at("xb"))
            with dve.Fori(0, 4) as i:
                dve.wait_ge(*PE.at("out", i))
                xs = c.x[:, bass.ds(4 * i, 4), :].rearrange("p i d -> p (i d)")
                nc.vector.scalar_tensor_tensor(out=xs, in0=big[:, 0, :], scalar=0.1, in1=xs, op0=ALU.mult, op1=ALU.add)\
                    .then_inc(V.did("x"), 1)

        @block.scalar
        def _(act):
            act.wait_ge(loaded, 176)
            nc.scalar.activation(omega[:, :], raw[:, 1:2], ACT.Tanh).then_inc(A.did("omega"), 1)
            nc.scalar.activation(decay[:, :], raw[:, 0:1], ACT.Sigmoid).then_inc(A.did("decay"), 1)
            act.wait_ge(*A.at("omega"))
            nc.scalar.activation(sine[:, :], omega[:, :], ACT.Sin, scale=0.1).then_inc(A.did("sine"), 1)
            nc.scalar.activation(half[:, :], omega[:, :], ACT.Sin, scale=0.05).then_inc(A.did("half"), 1)
            ln_scalar(c, act, V, A, PE, tp, n1)
            ln_scalar(c, act, V, A, PE, tp, n2)
            for i in (1, 3):
                act.wait_ge(*PE.at(f"u{i}"))
                nc.scalar.copy(uT[:, 512 * i:512 * i + 512], big[0:F2, 1, :]).then_inc(A.did(f"u{i}"), 1)
            ln_scalar(c, act, V, A, PE, tp, n3)
            with act.Fori(0, 4) as i:
                act.wait_ge(*PE.before("out", i))
                for k in range(4):
                    act.wait_ge(*PE.at(f"h{k}", i))
                    nc.scalar.activation(g[:, k, :], tp[k % 2], ACT.Gelu, bias=b1[:, k:k + 1]).then_inc(A.did(f"g{k}"), 1)


def capacity_experts(c, name):
    E, CAP, F = 16, TOK // 16, 512
    FC = F // P
    with Stage(c, name) as s:
        nc, a = c.nc, c.a
        wg = s.sb("wg", [P, E])
        earlier, ones = s.sb("earlier", [P, P]), s.sb("ones", [P, P])
        iota = s.sb("iota", [P, NT, E])
        lg, ex = s.sb("logits", [P, NT, E]), s.sb("exps", [P, NT, E])
        mx, total, gate = s.sb("mx", [P, NT]), s.sb("total", [P, NT]), s.sb("gate", [P, NT])
        top = s.sb("top", [P, NT, 8])
        topi = s.sb("topi", [P, NT, 8], U32)
        best = s.sb("best", [P, NT])
        hot = s.sb("hot", [P, NT, E])
        sums = s.sb("sums", [P, 2, NT, E])
        place, mine = s.sb("place", [P, NT, E]), s.sb("mine", [P, NT, E])
        loc, valid = s.sb("loc", [P, NT]), s.sb("valid", [P, NT])
        base, near, far = s.sb("base", [P, NT]), s.sb("near", [P, NT]), s.sb("far", [P, NT])
        to, frm = s.sb("to", [P, NT], U32), s.sb("frm", [P, NT], U32)
        weight = s.sb("weight", [P, NT])
        zero = s.sb("zero", [P, E, D])
        slots = s.sb("slots", [P, E, D])
        slotsT = s.sb("slotsT", [P, E * P])
        w1, w2 = s.sb("w1", [P, 2, F]), s.sb("w2", [P, 2, FC, D])
        hT = s.sb("hT", [P, 2, FC, P])
        done = s.sb("done", [P, E, D])
        got = s.sb("got", [P, NT, D])
        turn = s.ps("turn", [P, 2, 512])
        small = s.ps("small", [P, 2, 512])
        ph = s.ps("h", [P, 2, 512])
        po = s.ps("o", [P, 2, 512])
        loaded, zeroed, sent, read = s.sem("loaded"), s.sem("zeroed"), s.sem("sent"), s.sem("read")
        w_in = [s.sem("w_in0"), s.sem("w_in1")]
        stored, fetched = s.sem("stored"), s.sem("fetched")
        scans = [1, 2, 4, 8]
        V = Steps(s.sem("vector_steps"),
                  (1, ["zero", "ones"] + LN_V + ["logits", "mx", "less", "total", "gate"] + [f"top{i}" for i in range(NT)] +
                   [f"topi{i}" for i in range(NT)] + ["best", "hot", "sums"] +
                   [f"{w}{k}" for k in scans for w in ("head", "tail")] + ["place0", "place", "mine", "loc", "valid", "base", "near",
                    "far1", "far", "to", "near1", "near2", "frm", "weight", "sT0", "sT2"]),
                  (E, ["out"], 2), (1, ["weighted", "x"]))
        A = Steps(s.sem("scalar_steps"), (1, LN_A + ["exp", "sT1", "sT3"]), (E, ["relu"], 2))
        PE = Steps(s.sem("tensor_steps"), (1, LN_P + ["logits", "counts"] + [f"sT{i}" for i in range(4)]),
                   (E, ["h", "out"], 2))
        tp = [turn[:, i, :] for i in (0, 1)]
        e16 = lambda m: m.rearrange("p (t e) -> p t e", e=E)
        wide = lambda m: m[:, :].unsqueeze(2).broadcast_to([P, NT, E])
        dispatched, results = a["scratch_in"], a["scratch_out"]
        block = s.block()

        @block.sync
        def _(sp):
            sp.dma_start(wg[:, :], a[f"{name}_Wg"]).then_inc(loaded, 16)
            sp.dma_start(earlier[:, :], a["c_earlier"]).then_inc(loaded, 16)
            sp.dma_start(iota[:, :, :], a["c_sixteen"]).then_inc(loaded, 16)
            sp.wait_ge(*V.at("zero"))
            sp.dma_start(dispatched.rearrange("(e p) d -> p e d", p=P), zero[:, :, :]).then_inc(zeroed, 16)
            sp.wait_ge(sent, 16 * NT)
            sp.dma_start(slots[:, :, :], dispatched.rearrange("(e p) d -> p e d", p=P)).then_inc(read, 16)

            def load(e, u):
                sp.dma_start(w1[:, u, :], a[f"{name}_w1"][bass.ds(e, 1), :, :].rearrange("a d f -> (a d) f"))\
                    .then_inc(w_in[u], 16)
                sp.dma_start(w2[:, u, :, :], a[f"{name}_w2"][bass.ds(e, 1), :, :].rearrange("a (c p) d -> p (a c) d", p=P))\
                    .then_inc(w_in[u], 16)

            load(0, 0)
            load(1, 1)
            with sp.Fori(1, E // 2) as e2:
                for u in (0, 1):
                    sp.wait_ge(*PE.at("out", 2 * e2 + u - 2))
                    load(2 * e2 + u, u)
            sp.wait_ge(*V.at("out", E - 1))
            sp.dma_start(results.rearrange("(e p) d -> p e d", p=P), done[:, :, :]).then_inc(stored, 16)

        @block.gpsimd
        def _(pool):
            pool.wait_ge(*V.at("to"))
            pool.wait_ge(zeroed, 16)
            for t in range(NT):
                nc.gpsimd.indirect_dma_start(dispatched, bass.IndirectOffsetOnAxis(ap=to[:, t:t + 1], axis=0), c.xn[:, t, :], None,
                                             bounds_check=TOK - 1, oob_is_err=False).then_inc(sent, 16)
            pool.wait_ge(*V.at("frm"))
            pool.wait_ge(stored, 16)
            for t in range(NT):
                nc.gpsimd.indirect_dma_start(got[:, t, :], None, results, bass.IndirectOffsetOnAxis(ap=frm[:, t:t + 1], axis=0),
                                             bounds_check=TOK - 1, oob_is_err=False).then_inc(fetched, 16)

        @block.tensor
        def _(pe):
            ln_tensor(c, pe, V, A, PE, tp)
            pe.wait_ge(*V.at("ln_T2"))
            pe.wait_ge(*A.at("ln_T3"))
            pe.wait_ge(loaded, 48)
            for t in range(NT):
                last = nc.tensor.matmul(small[:, 0, E * t:E * t + E], c.xnT[:, P * t:P * t + P], wg[:, :], start=True, stop=True)
            last.then_inc(PE.did("logits"), 1)
            pe.wait_ge(*V.at("hot"))
            hots = hot[:, :, :].rearrange("p t e -> p (t e)")
            nc.tensor.matmul(small[:, 1, 0:NT * E], earlier[:, :], hots, start=True, stop=True)
            nc.tensor.matmul(small[:, 1, NT * E:2 * NT * E], ones[:, :], hots, start=True, stop=True)\
                .then_inc(PE.did("counts"), 1)
            pe.wait_ge(read, 16)
            for i in range(4):
                if i >= 2:
                    pe.wait_ge(*(A if i % 2 else V).at(f"sT{i - 2}"))
                for j in range(4):
                    last = nc.tensor.transpose(tp[i % 2][:, P * j:P * j + P], slots[:, 4 * i + j, :], c.ident[:, :])
                last.then_inc(PE.did(f"sT{i}"), 1)
            pe.wait_ge(*V.at("sT2"))
            pe.wait_ge(*A.at("sT3"))
            with pe.Fori(0, E // 2) as e2:
                for u in (0, 1):
                    e = 2 * e2 + u
                    pe.wait_ge(w_in[u], 32 * e2 + 32)
                    for k in range(FC):
                        last = nc.tensor.matmul(ph[:, u, P * k:P * k + P], w1[:, u, P * k:P * k + P], slotsT[:, bass.ds(P * e, P)],
                                                start=True, stop=True)
                    last.then_inc(PE.did("h"), 1)
                    pe.wait_ge(*V.before("out", e, 2))
                    pe.wait_ge(*A.at("relu", e))
                    for k in range(FC):
                        last = nc.tensor.matmul(po[:, u, 0:P], hT[:, u, k, :], w2[:, u, k, :], start=(k == 0), stop=(k == FC - 1))
                    last.then_inc(PE.did("out"), 1)

        @block.vector
        def _(dve):
            nc.vector.memset(zero[:, :, :], 0.0).then_inc(V.did("zero"), 1)
            nc.vector.memset(ones[:, :], 1.0).then_inc(V.did("ones"), 1)
            ln_vector(c, dve, V, A, PE, tp)
            dve.wait_ge(*PE.at("logits"))
            nc.vector.tensor_copy(lg[:, :, :], e16(small[:, 0, 0:NT * E])).then_inc(V.did("logits"), 1)
            dve.wait_ge(*V.at("logits"))
            nc.vector.tensor_reduce(mx[:, :], lg[:, :, :], AX.X, ALU.max).then_inc(V.did("mx"), 1)
            dve.wait_ge(*V.at("mx"))
            nc.vector.tensor_tensor(ex[:, :, :], lg[:, :, :], wide(mx), ALU.subtract).then_inc(V.did("less"), 1)
            dve.wait_ge(*A.at("exp"))
            nc.vector.tensor_reduce(total[:, :], ex[:, :, :], AX.X, ALU.add).then_inc(V.did("total"), 1)
            dve.wait_ge(*V.at("total"))
            nc.vector.reciprocal(gate[:, :], total[:, :]).then_inc(V.did("gate"), 1)
            for t in range(NT):
                nc.vector.max(top[:, t, :], lg[:, t, :]).then_inc(V.did(f"top{t}"), 1)
            dve.wait_ge(*V.at(f"top{NT - 1}"))
            for t in range(NT):
                nc.vector.max_index(topi[:, t, :], top[:, t, :], lg[:, t, :]).then_inc(V.did(f"topi{t}"), 1)
            dve.wait_ge(*V.at(f"topi{NT - 1}"))
            nc.vector.tensor_copy(best[:, :].unsqueeze(2), topi[:, :, 0:1]).then_inc(V.did("best"), 1)
            dve.wait_ge(*V.at("best"))
            dve.wait_ge(loaded, 48)
            nc.vector.tensor_tensor(hot[:, :, :], iota[:, :, :], wide(best), ALU.is_equal).then_inc(V.did("hot"), 1)
            dve.wait_ge(*PE.at("counts"))
            nc.vector.tensor_copy(sums[:, 0, :, :], e16(small[:, 1, NT * E:2 * NT * E])).then_inc(V.did("sums"), 1)
            prev = "sums"
            for n, k in enumerate(scans):
                src, dst = sums[:, n % 2, :, :], sums[:, (n + 1) % 2, :, :]
                dve.wait_ge(*V.at(prev))
                nc.vector.tensor_copy(dst[:, 0:k, :], src[:, 0:k, :]).then_inc(V.did(f"head{k}"), 1)
                nc.vector.tensor_tensor(dst[:, k:NT, :], src[:, k:NT, :], src[:, 0:NT - k, :], ALU.add)\
                    .then_inc(V.did(f"tail{k}"), 1)
                prev = f"tail{k}"
            dve.wait_ge(*V.at(prev))
            nc.vector.tensor_copy(place[:, 0:1, :], e16(small[:, 1, 0:NT * E])[:, 0:1, :]).then_inc(V.did("place0"), 1)
            nc.vector.tensor_tensor(place[:, 1:NT, :], e16(small[:, 1, 0:NT * E])[:, 1:NT, :], sums[:, 0, 0:NT - 1, :], ALU.add)\
                .then_inc(V.did("place"), 1)
            dve.wait_ge(*V.at("place"))
            nc.vector.tensor_tensor(mine[:, :, :], place[:, :, :], hot[:, :, :], ALU.mult).then_inc(V.did("mine"), 1)
            dve.wait_ge(*V.at("mine"))
            nc.vector.tensor_reduce(loc[:, :], mine[:, :, :], AX.X, ALU.add).then_inc(V.did("loc"), 1)
            dve.wait_ge(*V.at("loc"))
            nc.vector.tensor_scalar(valid[:, :], loc[:, :], float(CAP), None, ALU.is_lt).then_inc(V.did("valid"), 1)
            nc.vector.tensor_scalar(base[:, :], best[:, :], float(CAP), None, ALU.mult).then_inc(V.did("base"), 1)
            dve.wait_ge(*V.at("base"))
            nc.vector.tensor_tensor(near[:, :], base[:, :], loc[:, :], ALU.add).then_inc(V.did("near"), 1)
            nc.vector.tensor_scalar(far[:, :], loc[:, :], float(CAP), float(4 * TOK), ALU.is_ge, ALU.mult).then_inc(V.did("far1"), 1)
            dve.wait_ge(*V.at("far1"))
            nc.vector.tensor_tensor(mx[:, :], far[:, :], near[:, :], ALU.add).then_inc(V.did("far"), 1)
            dve.wait_ge(*V.at("far"))
            nc.vector.tensor_copy(to[:, :], mx[:, :]).then_inc(V.did("to"), 1)
            nc.vector.tensor_scalar(loc[:, :], loc[:, :], float(CAP - 1), None, ALU.min).then_inc(V.did("near1"), 1)
            dve.wait_ge(*V.at("near1"))
            nc.vector.tensor_tensor(total[:, :], base[:, :], loc[:, :], ALU.add).then_inc(V.did("near2"), 1)
            dve.wait_ge(*V.at("near2"))
            nc.vector.tensor_copy(frm[:, :], total[:, :]).then_inc(V.did("frm"), 1)
            nc.vector.tensor_tensor(weight[:, :], gate[:, :], valid[:, :], ALU.mult).then_inc(V.did("weight"), 1)
            for i in (0, 2):
                dve.wait_ge(*PE.at(f"sT{i}"))
                nc.vector.tensor_copy(slotsT[:, 512 * i:512 * i + 512], tp[0]).then_inc(V.did(f"sT{i}"), 1)
            with dve.Fori(0, E // 2) as e2:
                for u in (0, 1):
                    e = 2 * e2 + u
                    dve.wait_ge(*PE.at("out", e))
                    nc.vector.tensor_copy(done[:, bass.ds(e, 1), :], po[:, u, 0:P].unsqueeze(1)).then_inc(V.did("out"), 1)
            dve.wait_ge(fetched, 16 * NT)
            nc.vector.tensor_tensor(got[:, :, :], got[:, :, :], weight[:, :].unsqueeze(2).broadcast_to([P, NT, D]), ALU.mult)\
                .then_inc(V.did("weighted"), 1)
            dve.wait_ge(*V.at("weighted"))
            nc.vector.tensor_tensor(c.x[:, :, :], c.x[:, :, :], got[:, :, :], ALU.add).then_inc(V.did("x"), 1)

        @block.scalar
        def _(act):
            ln_scalar(c, act, V, A, PE, tp)
            act.wait_ge(*V.at("less"))
            nc.scalar.activation(ex[:, :, :], ex[:, :, :], ACT.Exp).then_inc(A.did("exp"), 1)
            for i in (1, 3):
                act.wait_ge(*PE.at(f"sT{i}"))
                nc.scalar.copy(slotsT[:, 512 * i:512 * i + 512], tp[1]).then_inc(A.did(f"sT{i}"), 1)
            with act.Fori(0, E // 2) as e2:
                for u in (0, 1):
                    e = 2 * e2 + u
                    act.wait_ge(*PE.at("h", e))
                    nc.scalar.activation(hT[:, u, :, :].rearrange("p c k -> p (c k)"), ph[:, u, :], ACT.Relu)\
                        .then_inc(A.did("relu"), 1)


def routed_experts(c, name):
    E, F = 8, 512
    FC = F // P
    with Stage(c, name) as s:
        nc, a = c.nc, c.a
        emb, emb2 = s.sb("emb", [P, E]), s.sb("emb2", [P, E])
        bonus = s.sb("bonus", [P, E])
        ones = s.sb("ones", [P, P])
        iota = s.sb("iota", [P, NT, E])
        sim, score = s.sb("sim", [P, NT, E]), s.sb("score", [P, NT, E])
        tn, te = s.sb("tn", [P, NT]), s.sb("te", [P, E])
        rt, re = s.sb("rt", [P, NT]), s.sb("re", [P, E])
        top, topi = s.sb("top", [P, NT, 8]), s.sb("topi", [P, NT, 8], U32)
        last_i, hit = s.sb("last_i", [P, NT]), s.sb("hit", [P, NT, E])
        best, besti = s.sb("best", [P, NT, 8]), s.sb("besti", [P, NT, 8], U32)
        bi = s.sb("bi", [P, NT, 2])
        gap, ex, den = s.sb("gap", [P, NT]), s.sb("ex", [P, NT]), s.sb("den", [P, NT])
        wt = s.sb("wt", [P, NT, 2])
        hit1, hit2 = s.sb("hit1", [P, NT, E]), s.sb("hit2", [P, NT, E])
        part1, part2 = s.sb("part1", [P, NT, E]), s.sb("part2", [P, NT, E])
        weights = s.sb("weights", [P, NT, E])
        weightsT = s.sb("weightsT", [E, TOK])
        b1, b1e = s.sb("b1", [P, E, FC]), s.sb("b1e", [P, 2, FC])
        b2 = s.sb("b2", [E, D])
        w1, w2 = s.sb("w1", [P, 2, F]), s.sb("w2", [P, 2, FC, D])
        g = s.sb("gelu", [P, 2, FC, 512])
        turn = s.ps("turn", [P, 2, 512])
        ph = s.ps("h", [P, 4, 512])
        po = s.ps("o", [P, 2, 512])
        loaded, w_in = s.sem("loaded"), [s.sem("w_in0"), s.sem("w_in1")]
        ROUTE = ["sim", "tn", "tn_eps", "rt", "te", "te_eps", "re", "s1", "s2", "s3"] + [f"top{t}" for t in range(NT)] + \
            [f"topi{t}" for t in range(NT)] + ["last", "hit", "s4"] + [f"best{t}" for t in range(NT)] + \
            [f"besti{t}" for t in range(NT)] + ["bi", "gap", "den", "w1", "w2", "hit1", "hit2", "part1", "part2", "weights"]
        V = Steps(s.sem("vector_steps"), (1, ["ones", "bonus"] + LN_V + ["emb2"] + ROUTE + ["wT0", "wT2"] +
                                          [f"b2_{i}" for i in range(4)]), (E, [f"x{i}" for i in range(4)], 2))
        A = Steps(s.sem("scalar_steps"), (1, LN_A + ["sq", "tn", "te", "exp", "wT1", "wT3"]),
                  (E, ["b1e"] + [f"g{i}{k}" for i in range(4) for k in range(FC)], 2))
        PE = Steps(s.sem("tensor_steps"), (1, LN_P + ["sim", "te"] + [f"wT{i}" for i in range(4)] + [f"b2_{i}" for i in range(4)]),
                   (E, sum([[f"h{i}{k}" for k in range(FC)] + [f"out{i}"] for i in range(4)], []), 2))
        tp = [turn[:, i, :] for i in (0, 1)]
        wide = lambda m: m.unsqueeze(2).broadcast_to([P, NT, E])
        each = lambda m: m[:, :].unsqueeze(1).broadcast_to([P, NT, E])
        block = s.block()

        @block.sync
        def _(sp):
            sp.dma_start(emb[:, :], a[f"{name}_embT"]).then_inc(loaded, 16)
            sp.dma_start(te[:, :], a[f"{name}_bonus"].broadcast_to([P, E])).then_inc(loaded, 16)
            sp.dma_start(iota[:, :, :], a["c_eight"]).then_inc(loaded, 16)
            sp.dma_start(b1[:, :, :], a[f"{name}_b1"]).then_inc(loaded, 16)
            sp.dma_start(b2[:, :], a[f"{name}_b2"]).then_inc(loaded, 16)

            def load(e, u):
                sp.dma_start(w1[:, u, :], a[f"{name}_W1"][bass.ds(e, 1), :, :].rearrange("a d f -> (a d) f"))\
                    .then_inc(w_in[u], 16)
                sp.dma_start(w2[:, u, :, :], a[f"{name}_W2"][bass.ds(e, 1), :, :].rearrange("a (c p) d -> p (a c) d", p=P))\
                    .then_inc(w_in[u], 16)

            load(0, 0)
            load(1, 1)
            with sp.Fori(1, E // 2) as e2:
                for u in (0, 1):
                    sp.wait_ge(*PE.at("out3", 2 * e2 + u - 2))
                    load(2 * e2 + u, u)

        @block.tensor
        def _(pe):
            ln_tensor(c, pe, V, A, PE, tp)
            pe.wait_ge(*V.at("ln_T2"))
            pe.wait_ge(*A.at("ln_T3"))
            pe.wait_ge(loaded, 80)
            for t in range(NT):
                last = nc.tensor.matmul(tp[0][:, E * t:E * t + E], c.xnT[:, P * t:P * t + P], emb[:, :], start=True, stop=True)
            last.then_inc(PE.did("sim"), 1)
            pe.wait_ge(*V.at("emb2"))
            nc.tensor.matmul(tp[1][:, 0:E], ones[:, :], emb2[:, :], start=True, stop=True).then_inc(PE.did("te"), 1)
            pe.wait_ge(*V.at("weights"))
            for i in range(4):
                if i >= 2:
                    pe.wait_ge(*(A if i % 2 else V).at(f"wT{i - 2}"))
                for j in range(4):
                    last = nc.tensor.transpose(tp[i % 2][0:E, P * j:P * j + P], weights[:, 4 * i + j, :], c.ident[:, :])
                last.then_inc(PE.did(f"wT{i}"), 1)
            pe.wait_ge(*V.at("wT2"))
            pe.wait_ge(*A.at("wT3"))
            for i in range(4):
                if i >= 2:
                    pe.wait_ge(*V.at(f"b2_{i - 2}"))
                for j in range(4):
                    t = 4 * i + j
                    last = nc.tensor.matmul(po[:, i % 2, P * j:P * j + P], weightsT[:, P * t:P * t + P], b2[:, :],
                                            start=True, stop=True)
                last.then_inc(PE.did(f"b2_{i}"), 1)
            with pe.Fori(0, E // 2) as e2:
                for u in (0, 1):
                    e = 2 * e2 + u
                    pe.wait_ge(w_in[u], 32 * e2 + 32)
                    for i in range(4):
                        for k in range(FC):
                            if i or u:
                                pe.wait_ge(*A.at(f"g{i - 1}{k}" if i else f"g3{k}", e if i else e - 1))
                            else:
                                pe.wait_ge(*A.before(f"g3{k}", e))
                            nc.tensor.matmul(ph[:, k, :], w1[:, u, P * k:P * k + P], c.xnT[:, 512 * i:512 * i + 512],
                                             start=True, stop=True).then_inc(PE.did(f"h{i}{k}"), 1)
                        pe.wait_ge(*A.at(f"g{i}{FC - 1}", e))
                        pe.wait_ge(*(V.at(f"x{i - 2}", e) if i >= 2 else V.before(f"x{i + 2}", e)))
                        for j in range(4):
                            for k in range(FC):
                                last = nc.tensor.matmul(po[:, i % 2, P * j:P * j + P], g[:, i % 2, k, P * j:P * j + P],
                                                        w2[:, u, k, :], start=(k == 0), stop=(k == FC - 1))
                        last.then_inc(PE.did(f"out{i}"), 1)

        @block.vector
        def _(dve):
            nc.vector.memset(ones[:, :], 1.0).then_inc(V.did("ones"), 1)
            dve.wait_ge(loaded, 80)
            nc.vector.tensor_scalar(bonus[:, :], te[:, :], 0.1, None, ALU.mult).then_inc(V.did("bonus"), 1)
            ln_vector(c, dve, V, A, PE, tp)
            nc.vector.tensor_tensor(emb2[:, :], emb[:, :], emb[:, :], ALU.mult).then_inc(V.did("emb2"), 1)
            dve.wait_ge(*PE.at("sim"))
            nc.vector.tensor_copy(sim[:, :, :], tp[0][:, 0:NT * E].rearrange("p (t e) -> p t e", e=E)).then_inc(V.did("sim"), 1)
            dve.wait_ge(*A.at("sq"))
            nc.vector.tensor_reduce(tn[:, :], c.sq[:, :, :], AX.X, ALU.add).then_inc(V.did("tn"), 1)
            dve.wait_ge(*A.at("tn"))
            nc.vector.tensor_scalar(tn[:, :], tn[:, :], 1e-8, None, ALU.add).then_inc(V.did("tn_eps"), 1)
            dve.wait_ge(*V.at("tn_eps"))
            nc.vector.reciprocal(rt[:, :], tn[:, :]).then_inc(V.did("rt"), 1)
            dve.wait_ge(*PE.at("te"))
            nc.vector.tensor_copy(te[:, :], tp[1][:, 0:E]).then_inc(V.did("te"), 1)
            dve.wait_ge(*A.at("te"))
            nc.vector.tensor_scalar(te[:, :], te[:, :], 1e-8, None, ALU.add).then_inc(V.did("te_eps"), 1)
            dve.wait_ge(*V.at("te_eps"))
            nc.vector.reciprocal(re[:, :], te[:, :]).then_inc(V.did("re"), 1)
            dve.wait_ge(*V.at("re"))
            nc.vector.tensor_tensor(score[:, :, :], sim[:, :, :], wide(rt[:, :]), ALU.mult).then_inc(V.did("s1"), 1)
            dve.wait_ge(*V.at("s1"))
            nc.vector.tensor_tensor(score[:, :, :], score[:, :, :], each(re), ALU.mult).then_inc(V.did("s2"), 1)
            dve.wait_ge(*V.at("s2"))
            nc.vector.tensor_tensor(score[:, :, :], score[:, :, :], each(bonus), ALU.add).then_inc(V.did("s3"), 1)
            for t in range(NT):
                nc.vector.max(top[:, t, :], sim[:, t, :]).then_inc(V.did(f"top{t}"), 1)
            dve.wait_ge(*V.at(f"top{NT - 1}"))
            for t in range(NT):
                nc.vector.max_index(topi[:, t, :], top[:, t, :], sim[:, t, :]).then_inc(V.did(f"topi{t}"), 1)
            dve.wait_ge(*V.at(f"topi{NT - 1}"))
            nc.vector.tensor_copy(last_i[:, :].unsqueeze(2), topi[:, :, 7:8]).then_inc(V.did("last"), 1)
            dve.wait_ge(*V.at("last"))
            nc.vector.tensor_tensor(hit[:, :, :], iota[:, :, :], wide(last_i[:, :]), ALU.is_equal).then_inc(V.did("hit"), 1)
            dve.wait_ge(*V.at("hit"))
            nc.vector.scalar_tensor_tensor(out=score[:, :, :], in0=hit[:, :, :], scalar=OUT, in1=score[:, :, :],
                                           op0=ALU.mult, op1=ALU.add).then_inc(V.did("s4"), 1)
            dve.wait_ge(*V.at("s4"))
            for t in range(NT):
                nc.vector.max(best[:, t, :], score[:, t, :]).then_inc(V.did(f"best{t}"), 1)
            dve.wait_ge(*V.at(f"best{NT - 1}"))
            for t in range(NT):
                nc.vector.max_index(besti[:, t, :], best[:, t, :], score[:, t, :]).then_inc(V.did(f"besti{t}"), 1)
            dve.wait_ge(*V.at(f"besti{NT - 1}"))
            nc.vector.tensor_copy(bi[:, :, :], besti[:, :, 0:2]).then_inc(V.did("bi"), 1)
            nc.vector.tensor_tensor(gap[:, :].unsqueeze(2), best[:, :, 1:2], best[:, :, 0:1], ALU.subtract).then_inc(V.did("gap"), 1)
            dve.wait_ge(*A.at("exp"))
            nc.vector.tensor_scalar(den[:, :], ex[:, :], 1.0, None, ALU.add).then_inc(V.did("den"), 1)
            dve.wait_ge(*V.at("den"))
            nc.vector.reciprocal(wt[:, :, 0:1], den[:, :].unsqueeze(2)).then_inc(V.did("w1"), 1)
            dve.wait_ge(*V.at("w1"))
            nc.vector.tensor_tensor(wt[:, :, 1:2], wt[:, :, 0:1], ex[:, :].unsqueeze(2), ALU.mult).then_inc(V.did("w2"), 1)
            nc.vector.tensor_tensor(hit1[:, :, :], iota[:, :, :], bi[:, :, 0:1].broadcast_to([P, NT, E]), ALU.is_equal)\
                .then_inc(V.did("hit1"), 1)
            nc.vector.tensor_tensor(hit2[:, :, :], iota[:, :, :], bi[:, :, 1:2].broadcast_to([P, NT, E]), ALU.is_equal)\
                .then_inc(V.did("hit2"), 1)
            dve.wait_ge(*V.at("hit2"))
            nc.vector.tensor_tensor(part1[:, :, :], hit1[:, :, :], wt[:, :, 0:1].broadcast_to([P, NT, E]), ALU.mult)\
                .then_inc(V.did("part1"), 1)
            nc.vector.tensor_tensor(part2[:, :, :], hit2[:, :, :], wt[:, :, 1:2].broadcast_to([P, NT, E]), ALU.mult)\
                .then_inc(V.did("part2"), 1)
            dve.wait_ge(*V.at("part2"))
            nc.vector.tensor_tensor(weights[:, :, :], part1[:, :, :], part2[:, :, :], ALU.add).then_inc(V.did("weights"), 1)
            for i in (0, 2):
                dve.wait_ge(*PE.at(f"wT{i}"))
                nc.vector.tensor_copy(weightsT[:, 512 * i:512 * i + 512], tp[0][0:E, :]).then_inc(V.did(f"wT{i}"), 1)
            for i in range(4):
                dve.wait_ge(*PE.at(f"b2_{i}"))
                xs = c.x[:, 4 * i:4 * i + 4, :].rearrange("p i d -> p (i d)")
                nc.vector.tensor_tensor(xs, po[:, i % 2, :], xs, ALU.add).then_inc(V.did(f"b2_{i}"), 1)
            dve.wait_ge(*V.at("b2_3"))
            with dve.Fori(0, E // 2) as e2:
                for u in (0, 1):
                    e = 2 * e2 + u
                    for i in range(4):
                        dve.wait_ge(*V.before(f"x{i}", e))
                        dve.wait_ge(*PE.at(f"out{i}", e))
                        for j in range(4):
                            xs = c.x[:, 4 * i + j, :]
                            last = nc.vector.scalar_tensor_tensor(out=xs, in0=po[:, i % 2, P * j:P * j + P],
                                                                  scalar=weights[:, 4 * i + j, bass.ds(e, 1)], in1=xs,
                                                                  op0=ALU.mult, op1=ALU.add)
                        last.then_inc(V.did(f"x{i}"), 1)

        @block.scalar
        def _(act):
            ln_scalar(c, act, V, A, PE, tp)
            act.wait_ge(*V.at("ln_xn"))
            nc.scalar.activation(c.sq[:, :, :], c.xn[:, :, :], ACT.Square).then_inc(A.did("sq"), 1)
            act.wait_ge(*V.at("tn"))
            nc.scalar.activation(tn[:, :], tn[:, :], ACT.Sqrt).then_inc(A.did("tn"), 1)
            act.wait_ge(*V.at("te"))
            nc.scalar.activation(te[:, :], te[:, :], ACT.Sqrt).then_inc(A.did("te"), 1)
            act.wait_ge(*V.at("gap"))
            nc.scalar.activation(ex[:, :], gap[:, :], ACT.Exp).then_inc(A.did("exp"), 1)
            for i in (1, 3):
                act.wait_ge(*PE.at(f"wT{i}"))
                nc.scalar.copy(weightsT[:, 512 * i:512 * i + 512], tp[1][0:E, :]).then_inc(A.did(f"wT{i}"), 1)
            with act.Fori(0, E // 2) as e2:
                for u in (0, 1):
                    e = 2 * e2 + u
                    act.wait_ge(*A.before("g33", e))
                    nc.scalar.copy(b1e[:, u, :], b1[:, bass.ds(e, 1), :].rearrange("p a k -> p (a k)")).then_inc(A.did("b1e"), 1)
                    act.wait_ge(*A.at("b1e", e))
                    for i in range(4):
                        for k in range(FC):
                            if k == 0:
                                act.wait_ge(*(PE.at(f"out{i - 2}", e) if i >= 2 else PE.before(f"out{i + 2}", e)))
                            act.wait_ge(*PE.at(f"h{i}{k}", e))
                            nc.scalar.activation(g[:, i % 2, k, :], ph[:, k, :], ACT.Gelu, bias=b1e[:, u, k:k + 1]).then_inc(A.did(f"g{i}{k}"), 1)


def selective_scan_layer(c, name):
    N, R, HALF = 16, 64, 2
    DT_MIN, DT_MAX = 0.001, 0.1
    with Stage(c, name) as s:
        nc, a = c.nc, c.a
        cols = s.sb("cols", [P, 2])
        win = s.sb("win", [P, 4 * D])
        taps, cb = s.sb("taps", [P, HALF, 4]), s.sb("cb", [P, HALF])
        wx, wdt = s.sb("wx", [P, HALF, R + 2 * N]), s.sb("wdt", [R, HALF * P])
        bdt, dp = s.sb("bdt", [P, HALF]), s.sb("dp", [P, HALF])
        la, na = s.sb("la", [P, HALF, N]), s.sb("na", [P, HALF, N])
        wo = s.sb("wo", [P, HALF, D])
        zeros = s.sb("zeros", [P, P])
        hT = s.sb("hT", [P, TOK])
        xi = s.sb("xi", [P, HALF, TOK])
        zs = s.sb("zs", [P, HALF, TOK])
        cv = s.sb("u", [P, HALF, TOK])
        dt = s.sb("dt", [P, HALF, TOK])
        xbc = s.sb("xbc", [R + 2 * N, TOK])
        bb, cc = s.sb("bb", [P, 2, TOK]), s.sb("cc", [P, 2, TOK])
        da, db = s.sb("da", [P, HALF, TOK]), s.sb("db", [P, HALF, TOK])
        hs = [[db[:, 0, :], db[:, 1, :]], [c.sq[:, :, :].rearrange("p t d -> p (t d)"), hT[:, :]]]
        ps = s.ps("all", [P, 8, 512])
        loaded, stored = s.sem("loaded"), s.sem("stored")
        b_in, c_in = [s.sem("b_in0"), s.sem("b_in1")], [s.sem("c_in0"), s.sem("c_in1")]
        n1 = Norm(c, turned=False)
        n2 = Norm(c, "in", c.xn, xi[:, 0, :].rearrange("p (t d) -> p t d", d=D), hT, cols[:, 0:1], cols[:, 1:2])
        quads = [(hf, i) for hf in range(HALF) for i in range(4)]
        V = Steps(s.sem("vector_steps"),
                  (1, ["zeros", "na", "da0"] + n1.V + n2.V + [f"xi{n}" for n in range(8)] +
                   [f"cv{hf}{k}" for hf in range(HALF) for k in (3, 2, 1, 0)] + ["xbc0", "xbc2"] +
                   [f"pre{n}" for n in range(8)] + ["low", "dt", "dtu"]),
                  (N, ["db0", "scan0", "db1", "scan1"], 2), (1, ["skip0", "gate0", "skip1", "gate1", "res"] + [f"x{i}" for i in range(4)]))
        A = Steps(s.sem("scalar_steps"),
                  (1, ["la"] + n1.A + n2.A + [f"z{n}" for n in range(8)] + ["u0", "u1", "xbc1", "xbc3", "e", "ln"]),
                  (N, ["da0", "da1"], 2))
        G = Steps(s.sem("gpsimd_steps"), (N, ["hc0", "hc1"], 2))
        PE = Steps(s.sem("tensor_steps"),
                   (1, n2.P + [f"in{n}" for n in range(16)] + [f"xbc{i}" for i in range(4)] + [f"dt{n}" for n in range(8)]),
                   (N, ["y0", "y1"], 2), (1, ["ysum"] + [f"out{i}" for i in range(4)]))
        tp = [ps[:, 6 + i, :] for i in (0, 1)]
        seq = lambda m: m.rearrange("p (b q) -> p b q", q=S)
        block = s.block()

        @block.sync
        def _(sp):
            for dst, src in ((cols[:, :], a[f"{name}_cols"]), (win[:, :], a[f"{name}_W_inT"]),
                             (taps[:, :, :], a[f"{name}_conv_w"].rearrange("(h p) k -> p h k", p=P)),
                             (wx[:, :, :], a[f"{name}_W_xT"].rearrange("(h p) n -> p h n", p=P)),
                             (wdt[:, :], a[f"{name}_W_dtT"]), (la[:, :, :], a[f"{name}_log_A"].rearrange("(h p) n -> p h n", p=P)),
                             (wo[:, :, :], a[f"{name}_W_outT"].rearrange("(h p) n -> p h n", p=P)),
                             (cb[:, :], a[f"{name}_vecs"][0]), (bdt[:, :], a[f"{name}_vecs"][1]), (dp[:, :], a[f"{name}_vecs"][2])):
                sp.dma_start(dst, src).then_inc(loaded, 16)
            sp.wait_ge(*V.at("xbc2"))
            sp.wait_ge(*A.at("xbc3"))
            sp.dma_start(a["scratch_rows"], xbc[R:R + 2 * N, :]).then_inc(stored, 16)
            sp.wait_ge(stored, 16)

            def load(n, u):
                sp.dma_start(bb[:, u, :], a["scratch_rows"][bass.ds(n, 1), :].broadcast_to([P, TOK])).then_inc(b_in[u], 16)
                sp.dma_start(cc[:, u, :], a["scratch_rows"][bass.ds(n + N, 1), :].broadcast_to([P, TOK])).then_inc(c_in[u], 16)

            load(0, 0)
            load(1, 1)
            with sp.Fori(1, N // 2) as n2_:
                for u in (0, 1):
                    sp.wait_ge(*G.at("hc1", 2 * n2_ + u - 2))
                    load(2 * n2_ + u, u)

        @block.tensor
        def _(pe):
            ln_tensor(c, pe, V, A, PE, tp, n2)
            pe.wait_ge(*V.at("in_T2"))
            pe.wait_ge(*A.at("in_T3"))
            pe.wait_ge(loaded, 160)
            order = [(blk, i) for pair in (0, 1) for i in range(4) for blk in (pair, 2 + pair)]
            for n, (blk, i) in enumerate(order):
                if n >= 4:
                    pe.wait_ge(*(V.at(f"xi{(n - 4) // 2}") if blk < 2 else A.at(f"z{(n - 4) // 2}")))
                nc.tensor.matmul(ps[:, (0 if blk < 2 else 2) + i % 2, :], win[:, P * blk:P * blk + P], hT[:, 512 * i:512 * i + 512],
                                 start=True, stop=True).then_inc(PE.did(f"in{n}"), 1)
            pe.wait_ge(*A.at("u1"))
            for i in range(4):
                if i >= 2:
                    pe.wait_ge(*(A if i % 2 else V).at(f"xbc{i - 2}"))
                for hf in range(HALF):
                    last = nc.tensor.matmul(ps[0:R + 2 * N, 4 + i % 2, :], wx[:, hf, :], cv[:, hf, 512 * i:512 * i + 512],
                                            start=(hf == 0), stop=(hf == 1))
                last.then_inc(PE.did(f"xbc{i}"), 1)
            pe.wait_ge(*V.at("xbc2"))
            pe.wait_ge(*A.at("xbc3"))
            for n, (hf, i) in enumerate(quads):
                if n >= 4:
                    pe.wait_ge(*V.at(f"pre{n - 4}"))
                nc.tensor.matmul(ps[:, n % 4, :], wdt[:, P * hf:P * hf + P], xbc[0:R, 512 * i:512 * i + 512],
                                 start=True, stop=True).then_inc(PE.did(f"dt{n}"), 1)
            pe.wait_ge(*V.at("dt"))
            for b in range(8):
                nc.tensor.matmul(ps[:, b, :], zeros[:, :], cv[:, 0, 0:512], start=True, stop=False, skip_group_check=True)
            with pe.Fori(0, N // 2) as n2_:
                for u in (0, 1):
                    n = 2 * n2_ + u
                    for hf in range(HALF):
                        pe.wait_ge(*G.at(f"hc{hf}", n))
                        for i in range(4):
                            last = nc.tensor.matmul(ps[:, 4 * hf + i, :], c.ident[:, :], hs[u][hf][:, 512 * i:512 * i + 512],
                                                    start=False, stop=False, skip_group_check=True)
                        last.then_inc(PE.did(f"y{hf}"), 1)
            for b in range(8):
                last = nc.tensor.matmul(ps[:, b, :], zeros[:, :], cv[:, 0, 0:512], start=False, stop=True, skip_group_check=True)
            last.then_inc(PE.did("ysum"), 1)
            pe.wait_ge(*V.at("gate1"))
            for i in range(4):
                for j in range(4):
                    t = 4 * i + j
                    for hf in range(HALF):
                        last = nc.tensor.matmul(ps[:, i, P * j:P * j + P], xi[:, hf, P * t:P * t + P], wo[:, hf, :],
                                                start=(hf == 0), stop=(hf == 1))
                last.then_inc(PE.did(f"out{i}"), 1)

        @block.gpsimd
        def _(pool):
            with pool.Fori(0, N // 2) as n2_:
                for u in (0, 1):
                    n = 2 * n2_ + u
                    pool.wait_ge(c_in[u], 16 * n2_ + 16)
                    for hf in range(HALF):
                        pool.wait_ge(*V.at(f"scan{hf}", n))
                        nc.gpsimd.tensor_tensor(hs[u][hf], hs[u][hf], cc[:, u, :], ALU.mult).then_inc(G.did(f"hc{hf}"), 1)

        @block.vector
        def _(dve):
            nc.vector.memset(zeros[:, :], 0.0).then_inc(V.did("zeros"), 1)
            dve.wait_ge(*A.at("la"))
            nc.vector.tensor_scalar(na[:, :, :], la[:, :, :], -1.0, None, ALU.mult).then_inc(V.did("na"), 1)
            nc.vector.memset(da[:, :, :], 0.0).then_inc(V.did("da0"), 1)
            ln_vector(c, dve, V, A, PE, tp, n1)
            dve.wait_ge(*V.at("ln_xn"))
            ln_vector(c, dve, V, A, PE, tp, n2)
            order = [(hf, i) for hf in (0, 1) for i in range(4)]
            for n, (hf, i) in enumerate(order):
                dve.wait_ge(*PE.at(f"in{2 * n}"))
                nc.vector.tensor_copy(xi[:, hf, 512 * i:512 * i + 512], ps[:, i % 2, :]).then_inc(V.did(f"xi{n}"), 1)
            dve.wait_ge(*V.at("xi7"))
            for hf in range(HALF):
                x3, u3 = seq(xi[:, hf, :]), seq(cv[:, hf, :])
                nc.vector.tensor_scalar(cv[:, hf, :], xi[:, hf, :], taps[:, hf, 3:4], cb[:, hf:hf + 1], ALU.mult, ALU.add)\
                    .then_inc(V.did(f"cv{hf}3"), 1)
                for k in (2, 1, 0):
                    m = 3 - k
                    dve.wait_ge(*V.at(f"cv{hf}{k + 1}"))
                    nc.vector.scalar_tensor_tensor(out=u3[:, :, m:S], in0=x3[:, :, 0:S - m], scalar=taps[:, hf, k:k + 1],
                                                   in1=u3[:, :, m:S], op0=ALU.mult, op1=ALU.add).then_inc(V.did(f"cv{hf}{k}"), 1)
            for i in (0, 2):
                dve.wait_ge(*PE.at(f"xbc{i}"))
                nc.vector.tensor_copy(xbc[:, 512 * i:512 * i + 512], ps[0:R + 2 * N, 4, :]).then_inc(V.did(f"xbc{i}"), 1)
            for n, (hf, i) in enumerate(quads):
                dve.wait_ge(*PE.at(f"dt{n}"))
                nc.vector.tensor_scalar(dt[:, hf, 512 * i:512 * i + 512], ps[:, n % 4, :], bdt[:, hf:hf + 1], 0.0, ALU.add, ALU.min)\
                    .then_inc(V.did(f"pre{n}"), 1)
            dve.wait_ge(*A.at("ln"))
            nc.vector.tensor_scalar(dt[:, :, :], dt[:, :, :], DT_MIN, DT_MIN, ALU.add, ALU.max).then_inc(V.did("low"), 1)
            dve.wait_ge(*V.at("low"))
            nc.vector.tensor_scalar(dt[:, :, :], dt[:, :, :], DT_MAX, None, ALU.min).then_inc(V.did("dt"), 1)
            dve.wait_ge(*V.at("dt"))
            nc.vector.tensor_tensor(xi[:, :, :], dt[:, :, :], cv[:, :, :], ALU.mult).then_inc(V.did("dtu"), 1)
            with dve.Fori(0, N // 2) as n2_:
                for u in (0, 1):
                    n = 2 * n2_ + u
                    dve.wait_ge(b_in[u], 16 * n2_ + 16)
                    for hf in range(HALF):
                        dve.wait_ge(*PE.before(f"y{hf}", n, 2))
                        dve.wait_ge(*V.before("scan1", n))
                        nc.vector.tensor_tensor(hs[u][hf], xi[:, hf, :], bb[:, u, :], ALU.mult).then_inc(V.did(f"db{hf}"), 1)
                        dve.wait_ge(*V.at(f"db{hf}", n))
                        dve.wait_ge(*A.at(f"da{hf}", n))
                        nc.vector.tensor_tensor_scan(hs[u][hf], da[:, hf, :], hs[u][hf], 0.0, ALU.mult, ALU.add)\
                            .then_inc(V.did(f"scan{hf}"), 1)
            for hf in range(HALF):
                dve.wait_ge(*PE.at("ysum"))
                nc.vector.scalar_tensor_tensor(out=db[:, hf, :], in0=cv[:, hf, :], scalar=dp[:, hf:hf + 1],
                                               in1=ps[:, 4 * hf:4 * hf + 4, :].rearrange("p i n -> p (i n)"),
                                               op0=ALU.mult, op1=ALU.add).then_inc(V.did(f"skip{hf}"), 1)
                dve.wait_ge(*V.at(f"skip{hf}"))
                nc.vector.tensor_tensor(xi[:, hf, :], db[:, hf, :], zs[:, hf, :], ALU.mult).then_inc(V.did(f"gate{hf}"), 1)
            nc.vector.tensor_tensor(c.x[:, :, :], c.x[:, :, :], c.xn[:, :, :], ALU.add).then_inc(V.did("res"), 1)
            dve.wait_ge(*V.at("res"))
            for i in range(4):
                dve.wait_ge(*PE.at(f"out{i}"))
                xs = c.x[:, 4 * i:4 * i + 4, :].rearrange("p i d -> p (i d)")
                nc.vector.tensor_tensor(xs, ps[:, i, :], xs, ALU.add).then_inc(V.did(f"x{i}"), 1)

        @block.scalar
        def _(act):
            act.wait_ge(loaded, 160)
            nc.scalar.activation(la[:, :, :], la[:, :, :], ACT.Exp).then_inc(A.did("la"), 1)
            ln_scalar(c, act, V, A, PE, tp, n1)
            ln_scalar(c, act, V, A, PE, tp, n2)
            for n, (hf, i) in enumerate(quads):
                act.wait_ge(*PE.at(f"in{2 * n + 1}"))
                nc.scalar.activation(zs[:, hf, 512 * i:512 * i + 512], ps[:, 2 + i % 2, :], ACT.Silu).then_inc(A.did(f"z{n}"), 1)
            for hf in range(HALF):
                act.wait_ge(*V.at(f"cv{hf}0"))
                nc.scalar.activation(cv[:, hf, :], cv[:, hf, :], ACT.Silu).then_inc(A.did(f"u{hf}"), 1)
            for i in (1, 3):
                act.wait_ge(*PE.at(f"xbc{i}"))
                nc.scalar.copy(xbc[:, 512 * i:512 * i + 512], ps[0:R + 2 * N, 5, :]).then_inc(A.did(f"xbc{i}"), 1)
            act.wait_ge(*V.at("pre7"))
            nc.scalar.activation(dt[:, :, :], dt[:, :, :], ACT.Exp).then_inc(A.did("e"), 1)
            act.wait_ge(*A.at("e"))
            nc.scalar.activation(dt[:, :, :], dt[:, :, :], ACT.Ln, bias=1.0).then_inc(A.did("ln"), 1)
            act.wait_ge(*V.at("dt"))
            with act.Fori(0, N // 2) as n2_:
                for u in (0, 1):
                    n = 2 * n2_ + u
                    for hf in range(HALF):
                        act.wait_ge(*V.before(f"scan{hf}", n))
                        nc.scalar.activation(seq(da[:, hf, :])[:, :, 1:S], seq(dt[:, hf, :])[:, :, 1:S], ACT.Exp,
                                             scale=na[:, hf, bass.ds(n, 1)]).then_inc(A.did(f"da{hf}"), 1)


def chosen_adapters(c, name):
    E, HID, R = 8, 32, 64
    with Stage(c, name) as s:
        nc, a = c.nc, c.a
        wd1, bd1 = s.sb("wd1", [P, 2 * P]), s.sb("bd1", [P, 2])
        wd2, bd2 = s.sb("wd2", [P, 2, D]), s.sb("bd2", [P, E])
        wad, bad = s.sb("wad", [P, 4 * P]), s.sb("bad", [P, 4])
        wau, bau = s.sb("wau", [P, 4, D]), s.sb("bau", [E, D])
        wb, bb = s.sb("wb", [P, D]), s.sb("bb", [P, D])
        rank, diag = s.sb("rank", [P, E, B]), s.sb("diag", [E, E])
        ones = s.sb("ones", [P, P])
        hid = s.sb("hid", [P, 2, 512])
        diff, sq = s.sb("diff", [P, 2, 512]), s.sb("sq", [P, 2, 512])
        loss = s.sb("loss", [P, E, B])
        full = s.sb("full", [P, E, B])
        least, vote, most = s.sb("least", [P, B]), s.sb("vote", [P, E, B]), s.sb("most", [P, B])
        hot = s.sb("hot", [P, E, B])
        mask = s.sb("mask", [P, 4, B])
        own, hot8 = s.sb("own", [E, E, B]), s.sb("hot8", [E, B])
        xg, hg = s.sb("xg", [P, 512]), s.sb("hg", [E, 512])
        ad, adm = s.sb("ad", [P, 4, 512]), s.sb("adm", [P, 4, 512])
        turn = s.ps("turn", [P, 2, 512])
        ps = s.ps("ps", [P, 6, 512])
        loaded = s.sem("loaded")
        V = Steps(s.sem("vector_steps"), (1, LN_V + ["ones", "bb"]),
                  (4, sum([[f"diff{e}", f"loss{e}"] for e in range(E)], [])),
                  (1, ["full", "least", "vote", "votes", "most", "hot", "mask0", "mask1", "own", "hot8"]),
                  (4, ["hg"] + [f"adm{k}" for k in range(4)] + ["x"]))
        A = Steps(s.sem("scalar_steps"), (1, LN_A), (4, ["hid0", "hid1"] + [f"sq{e}" for e in range(E)]),
                  (4, ["xg"] + [f"ad{k}" for k in range(4)]))
        PE = Steps(s.sem("tensor_steps"), (1, LN_P), (4, ["hid0", "hid1"] + [f"rec{e}" for e in range(E)]),
                   (1, ["full"]), (4, [f"ad{k}" for k in range(4)] + ["out"]))
        tp = [turn[:, i, :] for i in (0, 1)]
        seq = lambda m: m.rearrange("p (b q) -> p b q", q=S)
        block = s.block()

        @block.sync
        def _(sp):
            for dst, src in ((wd1, "wd1"), (bd1, "bd1"), (bd2, "bd2"), (wad, "wad"), (bad, "bad"), (bau, "bau"), (wb, "wb")):
                sp.dma_start(dst[:, :], a[f"{name}_{src}"]).then_inc(loaded, 16)
            sp.dma_start(wd2[:, :, :], a[f"{name}_wd2"].rearrange("(c p) d -> p c d", p=P)).then_inc(loaded, 16)
            sp.dma_start(wau[:, :, :], a[f"{name}_wau"].rearrange("(c p) d -> p c d", p=P)).then_inc(loaded, 16)
            sp.dma_start(bb[:, :], a[f"{name}_bb"].broadcast_to([P, D])).then_inc(loaded, 16)
            sp.dma_start(rank[:, :, :], a["c_rank"]).then_inc(loaded, 16)
            sp.dma_start(diag[:, :], a["c_ident"][0:E, 0:E]).then_inc(loaded, 16)

        @block.tensor
        def _(pe):
            ln_tensor(c, pe, V, A, PE, tp)
            pe.wait_ge(*V.at("ln_T2"))
            pe.wait_ge(*A.at("ln_T3"))
            pe.wait_ge(loaded, 192)
            with pe.Fori(0, 4) as i:
                pe.wait_ge(*A.before("sq7", i))
                for k in (0, 1):
                    nc.tensor.matmul(ps[:, k, :], wd1[:, P * k:P * k + P], c.xnT[:, bass.ds(512 * i, 512)], start=True, stop=True)\
                        .then_inc(PE.did(f"hid{k}"), 1)
                for e in range(E):
                    if e % 4 == 0:
                        pe.wait_ge(*A.at(f"hid{e // 4}", i))
                    pe.wait_ge(*(V.at(f"diff{e - 4}", i) if e >= 4 else V.before(f"diff{e + 4}", i)))
                    lo = HID * (e % 4)
                    nc.tensor.matmul(ps[:, 2 + e % 4, :], wd2[lo:lo + HID, e // 4, :], hid[lo:lo + HID, e // 4, :],
                                     start=True, stop=True, tile_position=(lo, 0)).then_inc(PE.did(f"rec{e}"), 1)
            pe.wait_ge(*V.at("loss7", 3))
            nc.tensor.matmul(ps[:, 0, 0:E * B], ones[:, :], loss[:, :, :].rearrange("p e b -> p (e b)"), start=True, stop=True)\
                .then_inc(PE.did("full"), 1)
            pe.wait_ge(*V.at("hot8"))
            with pe.Fori(0, 4) as i:
                for k in range(4):
                    pe.wait_ge(*A.before(f"ad{k}", i))
                    nc.tensor.matmul(ps[:, k, :], wad[:, P * k:P * k + P], c.xnT[:, bass.ds(512 * i, 512)], start=True, stop=True)\
                        .then_inc(PE.did(f"ad{k}"), 1)
                pe.wait_ge(*A.at("xg", i))
                pe.wait_ge(*V.at("adm3", i))
                for j in range(4):
                    part = slice(P * j, P * j + P)
                    nc.tensor.matmul(ps[:, 4, part], xg[:, part], wb[:, :], start=True, stop=False)
                    for k in range(4):
                        nc.tensor.matmul(ps[:, 4, part], adm[:, k, part], wau[:, k, :], start=False, stop=False)
                    last = nc.tensor.matmul(ps[:, 4, part], hg[:, part], bau[:, :], start=False, stop=True)
                last.then_inc(PE.did("out"), 1)

        @block.vector
        def _(dve):
            ln_vector(c, dve, V, A, PE, tp)
            dve.wait_ge(loaded, 192)
            nc.vector.memset(ones[:, :], 1.0).then_inc(V.did("ones"), 1)
            nc.vector.tensor_tensor(c.x[:, :, :], c.x[:, :, :], bb[:, :].unsqueeze(1).broadcast_to([P, NT, D]), ALU.add)\
                .then_inc(V.did("bb"), 1)
            dve.wait_ge(*A.at("ln_T3"))
            dve.wait_ge(*V.at("ln_T2"))
            with dve.Fori(0, 4) as i:
                for e in range(E):
                    dve.wait_ge(*(A.at(f"sq{e - 2}", i) if e >= 2 else A.before(f"sq{e + 6}", i)))
                    dve.wait_ge(*PE.at(f"rec{e}", i))
                    nc.vector.scalar_tensor_tensor(out=diff[:, e % 2, :], in0=ps[:, 2 + e % 4, :], scalar=bd2[:, e:e + 1],
                                                   in1=c.xnT[:, bass.ds(512 * i, 512)], op0=ALU.add, op1=ALU.subtract)\
                        .then_inc(V.did(f"diff{e}"), 1)
                    dve.wait_ge(*A.at(f"sq{e}", i))
                    nc.vector.tensor_reduce(loss[:, e, bass.ds(8 * i, 8)], seq(sq[:, e % 2, :]), AX.X, ALU.add)\
                        .then_inc(V.did(f"loss{e}"), 1)
            dve.wait_ge(*PE.at("full"))
            nc.vector.tensor_copy(full[:, :, :], ps[:, 0, 0:E * B].rearrange("p (e b) -> p e b", e=E)).then_inc(V.did("full"), 1)
            dve.wait_ge(*V.at("full"))
            nc.vector.tensor_reduce(least[:, :], full[:, :, :].rearrange("p e b -> p b e"), AX.X, ALU.min).then_inc(V.did("least"), 1)
            dve.wait_ge(*V.at("least"))
            nc.vector.tensor_tensor(vote[:, :, :], full[:, :, :], least[:, :].unsqueeze(1).broadcast_to([P, E, B]), ALU.is_equal)\
                .then_inc(V.did("vote"), 1)
            dve.wait_ge(*V.at("vote"))
            nc.vector.tensor_tensor(vote[:, :, :], vote[:, :, :], rank[:, :, :], ALU.mult).then_inc(V.did("votes"), 1)
            dve.wait_ge(*V.at("votes"))
            nc.vector.tensor_reduce(most[:, :], vote[:, :, :].rearrange("p e b -> p b e"), AX.X, ALU.max).then_inc(V.did("most"), 1)
            dve.wait_ge(*V.at("most"))
            nc.vector.tensor_tensor(hot[:, :, :], vote[:, :, :], most[:, :].unsqueeze(1).broadcast_to([P, E, B]), ALU.is_equal)\
                .then_inc(V.did("hot"), 1)
            dve.wait_ge(*V.at("hot"))
            pairs = hot[:, :, :].rearrange("p (k e) b -> p k e b", e=2)
            for e in (0, 1):
                nc.vector.tensor_copy(mask[R * e:R * e + R, :, :], pairs[R * e:R * e + R, :, e, :]).then_inc(V.did(f"mask{e}"), 1)
            nc.vector.tensor_tensor(own[:, :, :], hot[0:E, :, :], diag[:, :].unsqueeze(2).broadcast_to([E, E, B]), ALU.mult)\
                .then_inc(V.did("own"), 1)
            dve.wait_ge(*V.at("own"))
            nc.vector.tensor_reduce(hot8[:, :], own[:, :, :].rearrange("p e b -> p b e"), AX.X, ALU.add).then_inc(V.did("hot8"), 1)
            dve.wait_ge(*V.at("hot8"))
            with dve.Fori(0, 4) as i:
                dve.wait_ge(*V.before("x", i))
                nc.vector.tensor_copy(seq(hg[:, :]), hot8[:, bass.ds(8 * i, 8)].unsqueeze(2).broadcast_to([E, 8, S]))\
                    .then_inc(V.did("hg"), 1)
                for k in range(4):
                    dve.wait_ge(*A.at(f"ad{k}", i))
                    nc.vector.tensor_tensor(seq(adm[:, k, :]), seq(ad[:, k, :]),
                                            mask[:, k, bass.ds(8 * i, 8)].unsqueeze(2).broadcast_to([P, 8, S]), ALU.mult)\
                        .then_inc(V.did(f"adm{k}"), 1)
                dve.wait_ge(*PE.at("out", i))
                xs = c.x[:, bass.ds(4 * i, 4), :].rearrange("p i d -> p (i d)")
                nc.vector.tensor_tensor(xs, ps[:, 4, :], xs, ALU.add).then_inc(V.did("x"), 1)

        @block.scalar
        def _(act):
            ln_scalar(c, act, V, A, PE, tp)
            act.wait_ge(loaded, 192)
            with act.Fori(0, 4) as i:
                act.wait_ge(*V.before("loss7", i))
                for k in (0, 1):
                    act.wait_ge(*PE.at(f"hid{k}", i))
                    nc.scalar.activation(hid[:, k, :], ps[:, k, :], ACT.Relu, bias=bd1[:, k:k + 1]).then_inc(A.did(f"hid{k}"), 1)
                for e in range(E):
                    if e >= 2:
                        act.wait_ge(*V.at(f"loss{e - 2}", i))
                    act.wait_ge(*V.at(f"diff{e}", i))
                    nc.scalar.activation(sq[:, e % 2, :], diff[:, e % 2, :], ACT.Square).then_inc(A.did(f"sq{e}"), 1)
            with act.Fori(0, 4) as i:
                act.wait_ge(*V.before("x", i))
                nc.scalar.copy(xg[:, :], c.xnT[:, bass.ds(512 * i, 512)]).then_inc(A.did("xg"), 1)
                for k in range(4):
                    act.wait_ge(*PE.at(f"ad{k}", i))
                    nc.scalar.activation(ad[:, k, :], ps[:, k, :], ACT.Relu, bias=bad[:, k:k + 1]).then_inc(A.did(f"ad{k}"), 1)


BLK = 16
Q_V = ["amax", "scale", "rscale", "y", "a7", "a6", "a5", "b4", "b3", "b2", "b1", "q", "signed", "out"]
Q_A = ["abs", "sign"]


class Quant:

    def __init__(self, s, tag, n):
        self.n = n
        self.scale, self.rscale = s.sb(f"{tag}_scale", [P, n]), s.sb(f"{tag}_rscale", [P, n])
        self.y, self.ay, self.sign = (s.sb(f"{tag}_{k}", [P, n * BLK]) for k in ("y", "ay", "sign"))
        self.a, self.b = s.sb(f"{tag}_a", [P, n * BLK]), s.sb(f"{tag}_b", [P, n * BLK])


def quant_vector(c, dve, q, V, A, tag, t, src, dst):
    nc = c.nc
    blocks = lambda m: m.rearrange("p (n k) -> p n k", k=BLK)
    wide = lambda m: m[:, :].unsqueeze(2).broadcast_to([P, q.n, BLK])
    step = lambda n: (V.did(f"{tag}_{n}"), 1)

    def then(n):
        dve.wait_ge(*V.at(f"{tag}_{n}", t))

    nc.vector.tensor_reduce(q.scale[:, :], blocks(src), AX.X, ALU.max, apply_absolute_value=True).then_inc(*step("amax"))
    then("amax")
    nc.vector.tensor_scalar(q.scale[:, :], q.scale[:, :], 1.0 / 6.0, 1e-12, ALU.mult, ALU.max).then_inc(*step("scale"))
    then("scale")
    nc.vector.reciprocal(q.rscale[:, :], q.scale[:, :]).then_inc(*step("rscale"))
    then("rscale")
    nc.vector.tensor_tensor(blocks(q.y[:, :]), blocks(src), wide(q.rscale), ALU.mult).then_inc(*step("y"))
    dve.wait_ge(*A.at(f"{tag}_abs", t))
    nc.vector.tensor_scalar(q.a[:, :], q.ay[:, :], 5.0, 2.0, ALU.is_gt, ALU.mult).then_inc(*step("a7"))
    then("a7")
    nc.vector.scalar_tensor_tensor(out=q.a[:, :], in0=q.ay[:, :], scalar=3.5, in1=q.a[:, :], op0=ALU.is_gt, op1=ALU.add)\
        .then_inc(*step("a6"))
    then("a6")
    nc.vector.scalar_tensor_tensor(out=q.a[:, :], in0=q.ay[:, :], scalar=2.5, in1=q.a[:, :], op0=ALU.is_gt, op1=ALU.add)\
        .then_inc(*step("a5"))
    nc.vector.tensor_scalar(q.b[:, :], q.ay[:, :], 1.75, None, ALU.is_gt).then_inc(*step("b4"))
    for n, middle in (("b3", 1.25), ("b2", 0.75), ("b1", 0.25)):
        then(f"b{int(n[1]) + 1}")
        nc.vector.scalar_tensor_tensor(out=q.b[:, :], in0=q.ay[:, :], scalar=middle, in1=q.b[:, :], op0=ALU.is_gt,
                                       op1=ALU.add).then_inc(*step(n))
    then("b1")
    nc.vector.scalar_tensor_tensor(out=q.a[:, :], in0=q.b[:, :], scalar=0.5, in1=q.a[:, :], op0=ALU.mult, op1=ALU.add)\
        .then_inc(*step("q"))
    then("q")
    dve.wait_ge(*A.at(f"{tag}_sign", t))
    nc.vector.tensor_tensor(q.a[:, :], q.a[:, :], q.sign[:, :], ALU.mult).then_inc(*step("signed"))
    then("signed")
    nc.vector.tensor_tensor(blocks(dst), blocks(q.a[:, :]), wide(q.scale), ALU.mult).then_inc(*step("out"))


def quant_scalar(c, act, q, V, A, tag, t):
    nc = c.nc
    act.wait_ge(*V.at(f"{tag}_y", t))
    nc.scalar.activation(q.ay[:, :], q.y[:, :], ACT.Abs).then_inc(A.did(f"{tag}_abs"), 1)
    nc.scalar.activation(q.sign[:, :], q.y[:, :], ACT.Sign).then_inc(A.did(f"{tag}_sign"), 1)


def quantised_ffn(c, name):
    I = 352
    IC = -(-I // P)
    IP = IC * P
    rest = I - (IC - 1) * P
    wide_ = [P, P, rest]
    with Stage(c, name) as s:
        nc, a = c.nc, c.a
        w = s.sb("w", [P, 2 * IP + I])
        wguT = s.sb("wguT", [P, 2, IP])
        wdT = s.sb("wdT", [P, IC, D])
        xq = s.sb("xq", [P, NT, D])
        xqT = s.sb("xqT", [P, TOK])
        qw, qx, qh = Quant(s, "qw", (2 * IP + I) // BLK), Quant(s, "qx", TOK // BLK), Quant(s, "qh", 4 * I // BLK)
        xg = s.sb("xg", [P, 512])
        gate = s.sb("gate", [P, 4, I])
        hh, hq = s.sb("hh", [P, 4, I]), s.sb("hq", [P, 4, I])
        hT = s.sb("hT", [P, IC, 512])
        ps = s.ps("all", [P, 8, 512])
        loaded = s.sem("loaded")
        V = RoundSteps(s.sem("vector_steps"), of("w", *Q_V) + ["wgT", "wdT"] + Norm(c, turned=False).V + of("x", *Q_V) + ["xT0", "xT2"],
                       of("h", *Q_V) + ["h0", "h1", "hT0", "hT2", "h2", "x", "h3"])
        A = RoundSteps(s.sem("scalar_steps"), of("w", *Q_A) + ["wuT"] + Norm(c, turned=False).A + of("x", *Q_A) + ["xT1", "xT3"],
                       of("h", *Q_A) + ["xg", "silu0", "silu1", "hT1", "silu2", "silu3"])
        PE = RoundSteps(s.sem("tensor_steps"), ["wgT", "wuT", "wdT"] + [f"xT{i}" for i in range(4)],
                        ["gu0", "gu1"] + [f"hT{k}" for k in range(IC)] + ["gu2", "out", "gu3"])
        n1 = Norm(c, turned=False)
        flat = lambda m: m[:, :, :].rearrange("p i k -> p (i k)")
        block = s.block()

        def rounds(engine, body):
            body(0, None, False, True)
            with engine.Fori(0, 3) as g:
                body(g + 1, g, True, True)
            body(4, 3, True, False)

        @block.sync
        def _(sp):
            sp.dma_start(w[:, :], a[f"{name}_w"]).then_inc(loaded, 16)

        @block.tensor
        def _(pe):
            pe.wait_ge(*V.at("w_out"))
            for m, n in ((0, "wgT"), (1, "wuT")):
                for k in range(IC):
                    last = nc.tensor.transpose(ps[:, m, P * k:P * k + P], w[:, IP * m + P * k:IP * m + P * k + P], c.ident[:, :])
                last.then_inc(PE.did(n), 1)
            for k in range(IC):
                last = nc.tensor.transpose(ps[0:wide_[k], 2, P * k:P * k + P], w[:, 2 * IP + P * k:2 * IP + P * k + wide_[k]],
                                           c.ident[:, :])
            last.then_inc(PE.did("wdT"), 1)
            pe.wait_ge(*V.at("x_out"))
            for i in range(4):
                if i >= 2:
                    pe.wait_ge(*(A if i % 2 else V).at(f"xT{i - 2}"))
                for j in range(4):
                    last = nc.tensor.transpose(ps[:, 6 + i % 2, P * j:P * j + P], xq[:, 4 * i + j, :], c.ident[:, :])
                last.then_inc(PE.did(f"xT{i}"), 1)

            def body(r, g, finishing, beginning):
                def products(j):
                    if not beginning:
                        return
                    if j == 0:
                        pe.wait_ge(*A.at("xg", r))
                    if j >= 2:
                        pe.wait_ge(*V.at(f"h{j - 2}", r))
                    elif finishing:
                        pe.wait_ge(*V.at(f"h{j + 2}", r - 1))
                    for m in (0, 1):
                        last = nc.tensor.matmul(ps[:, 2 * m + j % 2, 0:I], xg[:, P * j:P * j + P], wguT[:, m, 0:I],
                                                start=True, stop=True)
                    last.then_inc(*PE.inc(f"gu{j}"))

                products(0)
                products(1)
                if finishing:
                    pe.wait_ge(*V.at("h_out", r))
                    for k in range(IC):
                        for j in range(4):
                            last = nc.tensor.transpose(ps[0:wide_[k], 4 + k, P * j:P * j + P], hq[:, j, P * k:P * k + wide_[k]],
                                                       c.ident[:, :])
                        last.then_inc(*PE.inc(f"hT{k}"))
                products(2)
                if finishing:
                    pe.wait_ge(*A.at("hT1", r))
                    pe.wait_ge(*V.at("hT2", r))
                    for j in range(4):
                        for k in range(IC):
                            last = nc.tensor.matmul(ps[:, 7, P * j:P * j + P], hT[0:wide_[k], k, P * j:P * j + P],
                                                    wdT[0:wide_[k], k, :], start=(k == 0), stop=(k == IC - 1))
                    last.then_inc(*PE.inc("out"))
                products(3)

            rounds(pe, body)

        @block.vector
        def _(dve):
            dve.wait_ge(loaded, 16)
            quant_vector(c, dve, qw, V, A, "w", 0, w[:, :], w[:, :])
            dve.wait_ge(*PE.at("wgT"))
            nc.vector.tensor_copy(wguT[:, 0, :], ps[:, 0, 0:IP]).then_inc(V.did("wgT"), 1)
            dve.wait_ge(*PE.at("wdT"))
            nc.vector.tensor_copy(wdT[:, 0:2, :].rearrange("p k d -> p (k d)"), ps[:, 2, 0:2 * P])
            nc.vector.tensor_copy(wdT[0:rest, 2, :], ps[0:rest, 2, 2 * P:3 * P]).then_inc(V.did("wdT"), 1)
            ln_vector(c, dve, V, A, PE, None, n1)
            dve.wait_ge(*V.at("ln_xn"))
            quant_vector(c, dve, qx, V, A, "x", 0, flat(c.xn), flat(xq))
            for i in (0, 2):
                dve.wait_ge(*PE.at(f"xT{i}"))
                nc.vector.tensor_copy(xqT[:, 512 * i:512 * i + 512], ps[:, 6, :]).then_inc(V.did(f"xT{i}"), 1)

            def body(r, g, finishing, beginning):
                def product(j):
                    if beginning:
                        dve.wait_ge(*A.at(f"silu{j}", r))
                        nc.vector.tensor_tensor(hh[:, j, :], gate[:, j, :], ps[:, 2 + j % 2, 0:I], ALU.mult).then_inc(*V.inc(f"h{j}"))

                if finishing:
                    dve.wait_ge(*V.at("h3", r - 1))
                    quant_vector(c, dve, qh, V, A, "h", r, flat(hh), flat(hq))
                product(0)
                product(1)
                if finishing:
                    for k in (0, 2):
                        dve.wait_ge(*PE.at(f"hT{k}", r))
                        nc.vector.tensor_copy(hT[0:wide_[k], k, :], ps[0:wide_[k], 4 + k, :]).then_inc(*V.inc(f"hT{k}"))
                product(2)
                if finishing:
                    dve.wait_ge(*PE.at("out", r))
                    xs = c.x[:, bass.ds(4 * g, 4), :].rearrange("p i d -> p (i d)")
                    nc.vector.tensor_tensor(xs, ps[:, 7, :], xs, ALU.add).then_inc(*V.inc("x"))
                product(3)

            rounds(dve, body)

        @block.scalar
        def _(act):
            quant_scalar(c, act, qw, V, A, "w", 0)
            act.wait_ge(*PE.at("wuT"))
            nc.scalar.copy(wguT[:, 1, :], ps[:, 1, 0:IP]).then_inc(A.did("wuT"), 1)
            ln_scalar(c, act, V, A, PE, None, n1)
            quant_scalar(c, act, qx, V, A, "x", 0)
            for i in (1, 3):
                act.wait_ge(*PE.at(f"xT{i}"))
                nc.scalar.copy(xqT[:, 512 * i:512 * i + 512], ps[:, 7, :]).then_inc(A.did(f"xT{i}"), 1)
            act.wait_ge(*V.at("xT2"))
            act.wait_ge(*A.at("xT3"))

            def body(r, g, finishing, beginning):
                def silu(j):
                    if beginning:
                        act.wait_ge(*PE.at(f"gu{j}", r))
                        nc.scalar.activation(gate[:, j, :], ps[:, j % 2, 0:I], ACT.Silu).then_inc(*A.inc(f"silu{j}"))

                if finishing:
                    quant_scalar(c, act, qh, V, A, "h", r)
                if beginning:
                    if finishing:
                        act.wait_ge(*PE.at("gu3", r - 1))
                    nc.scalar.copy(xg[:, :], xqT[:, bass.ds(512 * r, 512)]).then_inc(*A.inc("xg"))
                silu(0)
                silu(1)
                if finishing:
                    act.wait_ge(*PE.at("hT1", r))
                    nc.scalar.copy(hT[:, 1, :], ps[:, 5, :]).then_inc(*A.inc("hT1"))
                silu(2)
                silu(3)

            rounds(act, body)


def many_head_cross_attention(c, name):
    TILES = H // 2
    NG = len(SPANS)
    wide_ = [w for _, w in SPANS]
    part = [min(4, KC - 4 * m) for m in range(NG)]
    chunk = [min(P, KEYS - P * j) for j in range(KC)]
    HALF = 1024
    halves = ((0, HALF), (HALF, KEYS))
    TERMS = ((0, 0), (0, 1), (1, 0), (1, 1), (0, 2), (2, 0))
    with Stage(c, name) as s:
        nc, a = c.nc, c.a
        wq, wk, wv, wo = (s.sb(n, [P, D]) for n in ("wq", "wk", "wv", "wo"))
        pair_half, own_dims, delta = s.sb("pair_half", [P, 2]), s.sb("own_dims", [P, D]), s.sb("delta", [P, S])
        mask, shift = s.sb("mask", [P, KEYS], U8), s.sb("shift", [P, KEYS])
        qr = s.sb("qr", [P, 2, TILES, S], BF16)
        qd = s.sb("qd", [P, 2, TILES, 2, S], BF16)
        ctx, ctxT = s.sb("ctx", [P, 2, KC, D]), s.sb("ctxT", [P, KEYS])
        k_parts = s.sb("k_parts", [P, 3, KEYS], BF16)
        ones = s.sb("ones", [P, 1])
        k_rest = s.sb("k_rest", [P, 2, 512])
        kr = s.sb("kr", [P, 2, TILES, KEYS], BF16)
        v = s.sb("v", [P, 2, KC, D])
        sc = s.sb("sc", [P, 4, KEYS])
        tops, top = s.sb("tops", [P, 2]), s.sb("top", [P, 1])
        ntop, rows = s.sb("ntop", [P, 2, TILES]), s.sb("rows", [P, 2, TILES])
        rinv, vinv, coef = s.sb("rinv", [P, TILES]), s.sb("vinv", [P, TILES]), s.sb("coef", [P, D])
        pT = s.sb("pT", [P, 2, KC, P])
        pvs, place, qT = c.xn[:, 0:TILES, :], c.xn[:, TILES:2 * TILES, :], c.sq[:, :, :].rearrange("p t d -> p (t d)")
        own, yT, pause = s.sb("own", [P, D]), s.sb("yT", [P, S]), s.sb("pause", [P, 2])
        ps = s.ps("scores", [P, 2048])
        turn = s.ps("turn", [P, 2, 512])
        prep = s.ps("prep", [P, 512])
        pv = s.ps("pv", [P, 512])
        tile_pv, sums = pv[:, 0:P], pv[:, P:2 * P]
        loaded, ctx_in = s.sem("loaded"), [s.sem("ctx_in0"), s.sem("ctx_in1")]
        qd_made = s.sem("qd_made")
        q_parts = kr[:, 1, :, :].rearrange("p t k -> p (t k)")[:, 0:3 * TOK].rearrange("p (a q) -> p a q", a=3)
        placed, q_stored = s.sem("placed"), s.sem("q_stored")
        k_stored = [s.sem("k_stored0"), s.sem("k_stored1")]
        qr_in, kr_in = [s.sem("qr_in0"), s.sem("qr_in1")], [s.sem("kr_in0"), s.sem("kr_in1")]
        slots = lambda f: sum([f(t) for t in range(TILES)], [])
        PREPS = {"v0": "b0", "v1": "a1", "v2": "b1", "v3": "a2", "ctxT0": "b2", "ctxT1": "a3", "ctxT2": "b3", "ctxT3": "a4",
                 "k0": "b4", "k1": "b5", "yT": "a6", "k2": "b6", "out": "a7", "k3": "b7"}
        IN = {at: step for step, at in PREPS.items()}
        of_slot = lambda at, who: [IN[at]] if IN.get(at) in who else []
        V_PREPS = [ "k0", "k1", "k2", "k3", "yT", "out"]
        A_PREPS = [f"{w}{m}" for w in ("v", "ctxT") for m in range(NG)] + [ "k0", "k1", "k2", "k3"]
        V = RoundSteps(s.sem("vector_steps"), ["shift", "zero"] + LN_V + [f"q{i}{x}" for i in range(4) for x in "abcde"], slots(
            lambda t: [f"T{t}0", f"T{t}1", f"mA{t}"] + (["rinv", "vinv", "coef"] if t == 0 else []) + [f"pv{t}"] +
            of_slot(f"a{t}", V_PREPS) + [f"mB{t}", f"top{t}", f"ntop{t}"] + ["own"] * (t == 0) + of_slot(f"b{t}", V_PREPS)))
        A = RoundSteps(s.sem("scalar_steps"), LN_A, slots(
            lambda t: [f"exp{t}"] + of_slot(f"a{t}", A_PREPS) + [f"T{t}2", f"T{t}3"] + of_slot(f"b{t}", A_PREPS)))
        PE = RoundSteps(s.sem("tensor_steps"), LN_P + [f"q{i}" for i in range(4)], slots(
            lambda t: [f"T{t}0", f"T{t}1"] + of_slot(f"a{t}", IN.values()) + [f"SA{t}", f"T{t}2", f"T{t}3", f"PV{t}", f"SB{t}"] +
            ["sums"] * (t == 0) + of_slot(f"b{t}", IN.values())))
        G = RoundSteps(s.sem("gpsimd_steps"), ["zero"], [f"k{m}{x}" for m in range(NG) for x in "abc"])
        tp = [turn[:, i, :] for i in (0, 1)]
        block = s.block()

        def rounds(engine, body):
            for r in (0, 1, 2):
                body(r, r % 2, r // 2, None)
            with engine.Fori(0, B // 2 - 2) as t:
                body(2 * t + 3, 1, t + 1, t)
                body(2 * t + 4, 0, t + 2, t)
            for r in range(B - 1, B + 3):
                body(r, r % 2, r // 2, (r - 3) // 2)

        def kind(r):
            fixed = isinstance(r, int)
            return not fixed or 3 <= r, not fixed or 2 <= r <= B + 1, not fixed or 1 <= r <= B, not fixed or r < B

        def active(step, r):
            finishing, _, coming, far = kind(r)
            return coming if step[0] == "v" else finishing if step in ("yT", "out") else far

        def reader(step):
            return V if step in V_PREPS else A

        def put(engine_copy, dst, src, m, sem_inc):
            k = min(P, KEYS - 512 * m)
            engine_copy(dst[0:k, 4 * m:4 * m + part[m], :].rearrange("p j d -> p (j d)"), src[0:k, 0:P * part[m]])\
                .then_inc(*sem_inc)

        def span(m):
            return slice(512 * m, 512 * m + wide_[m])

        @block.sync
        def _(sp):
            for dst, src in ((wq, "wq"), (wk, "wk"), (wv, "wv"), (wo, "wo")):
                sp.dma_start(dst[:, :], a[f"{name}_{src}"]).then_inc(loaded, 16)
            sp.dma_start(pair_half[:, :], a["c_pair_half"]).then_inc(loaded, 16)
            sp.dma_start(own_dims[:, :], a["c_own_dims"]).then_inc(loaded, 16)
            sp.dma_start(delta[:, :], a["c_delta"]).then_inc(loaded, 16)
            for h in (0, 1):
                sp.dma_start(mask[S * h:S * h + S, :], a["mask_all"]).then_inc(loaded, 16)

            def load(n, u):
                keys = a["ctx"][bass.ds(n, 1), :, :].rearrange("a k d -> (a k) d")
                sp.dma_start(ctx[:, u, 0:KC - 1, :], keys[0:(KC - 1) * P, :].rearrange("(j p) d -> p j d", p=P))\
                    .then_inc(ctx_in[u], 16)
                sp.dma_start(ctx[0:KREST, u, KC - 1, :], keys[(KC - 1) * P:KEYS, :]).then_inc(ctx_in[u], 16)

            load(0, 0)
            load(1, 1)
            sp.wait_ge(*PE.at("ln_PT3"))
            sp.dma_start(place, a["c_place"]).then_inc(placed, 16)
            sp.wait_ge(*V.at("q3e"))
            sp.dma_start(a["scratch_q"].rearrange("a p q -> p a q"), q_parts).then_inc(q_stored, 16)
            sp.wait_ge(*G.at("zero"))

            def body(r, par, pair, tile):
                if not kind(r)[3]:
                    return
                if kind(r)[2] and not (isinstance(r, int) and r + 1 >= B):
                    sp.wait_ge(*PE.at("ctxT3", r - 1))
                    load(r + 1, 1 - par)
                sp.wait_ge(*G.at("k3c", r))
                if kind(r)[1]:
                    sp.wait_ge(kr_in[par], 96 * pair)
                sp.dma_start(a["scratch_k"][par].rearrange("a p k -> p a k"), k_parts[:, :, :]).then_inc(k_stored[par], 16)
                if kind(r)[1]:
                    sp.wait_ge(qd_made, r - 1)
                for j, (of_q, _) in enumerate(TERMS):
                    sp.dma_start(qr[16 * j:16 * j + 16, par, :, :],
                                 a["scratch_q"][of_q, :, bass.ds(S * r, S)].rearrange("(k i) q -> i k q", i=16))\
                        .then_inc(qr_in[par], 16)
                sp.wait_ge(k_stored[par], 16 * pair + 16)
                for j, (_, of_k) in enumerate(TERMS):
                    sp.dma_start(kr[16 * j:16 * j + 16, par, :, :],
                                 a["scratch_k"][par, of_k].rearrange("(k i) n -> i k n", i=16)).then_inc(kr_in[par], 16)

            rounds(sp, body)

        @block.gpsimd
        def _(pool):
            nc.gpsimd.memset(ones[:, :], 1.0)
            nc.gpsimd.memset(qr[:, :, :, :], 0.0)
            nc.gpsimd.memset(kr[:, 0, :, :], 0.0)
            pool.wait_ge(loaded, 144)
            pool.wait_ge(q_stored, 16)
            nc.gpsimd.memset(kr[:, 1, :, :], 0.0).then_inc(*G.inc("zero"))
            pool.wait_ge(*G.at("zero"))

            def body(r, par, pair, tile):
                if not kind(r)[3]:
                    return
                for m in range(NG):
                    pool.wait_ge(*A.at(f"k{m}", r))
                    rest = k_rest[:, m % 2, 0:wide_[m]]
                    nc.gpsimd.tensor_tensor(rest, rest, k_parts[:, 0, span(m)], ALU.subtract).then_inc(*G.inc(f"k{m}a"))
                    pool.wait_ge(*G.at(f"k{m}a", r))
                    nc.gpsimd.tensor_tensor(k_parts[:, 1, span(m)], rest, ones[:, :].broadcast_to([P, wide_[m]]),
                                            ALU.mult).then_inc(*G.inc(f"k{m}b"))
                    pool.wait_ge(*G.at(f"k{m}b", r))
                    nc.gpsimd.tensor_tensor(k_parts[:, 2, span(m)], rest, k_parts[:, 1, span(m)], ALU.subtract)\
                        .then_inc(*G.inc(f"k{m}c"))
                if kind(r)[1]:
                    pool.wait_ge(*PE.at("SB5", r))
                pool.wait_ge(qr_in[par], 96 * pair + 96)
                nc.gpsimd.tensor_tensor(qd[:, par, :, :, :], qr[:, par, :, :].unsqueeze(2).broadcast_to([P, TILES, 2, S]),
                                        pair_half[:, :].unsqueeze(1).unsqueeze(3).broadcast_to([P, TILES, 2, S]), ALU.mult)\
                    .then_inc(qd_made, 1)

            rounds(pool, body)

        @block.tensor
        def _(pe):
            ln_tensor(c, pe, V, A, PE, tp)
            pe.wait_ge(*V.at("ln_T2"))
            pe.wait_ge(*A.at("ln_T3"))
            pe.wait_ge(loaded, 144)
            for i in range(4):
                nc.tensor.matmul(ps[:, 512 * i:512 * i + 512], wq[:, :], c.xnT[:, 512 * i:512 * i + 512], start=True, stop=True)\
                    .then_inc(*PE.inc(f"q{i}"))
            pe.wait_ge(placed, 16)

            def body(r, par, pair, tile):
                finishing, tiles, coming, far = kind(r)

                def turns(t, m):
                    if m < 2:
                        pe.wait_ge(*(A.at(f"exp{t - 1}", r) if t else A.at("exp7", r - 1)))
                        if t:
                            pe.wait_ge(*A.at(f"T{t - 1}{m + 2}", r))
                        elif finishing:
                            pe.wait_ge(*A.at(f"T7{m + 2}", r - 1))
                    else:
                        pe.wait_ge(*V.at(f"T{t}{m - 2}", r))
                    for i in range(4 * m, 4 * m + part[m]):
                        last = nc.tensor.transpose(tp[m % 2][0:chunk[i], P * (i - 4 * m):P * (i - 4 * m) + P],
                                                   sc[:, t % 4, P * i:P * i + chunk[i]], c.ident[:, :])
                    last.then_inc(*PE.inc(f"T{t}{m}"))

                def scores(t, half):
                    k, buf = (t + 2, par) if t < 6 else (t - 6, 1 - par)
                    if t == 6 and half == 0:
                        pe.wait_ge(qd_made, r)
                        pe.wait_ge(kr_in[1 - par], 96 * (pair + 1 if par else pair))
                    step = "AB"[half]
                    if t and (tiles or t == 7):
                        pe.wait_ge(*V.at(f"m{step}{t - 1}", r))
                    elif t == 0:
                        pe.wait_ge(*V.at(f"m{step}7", r - 1))
                    for m in (2 * half, 2 * half + 1):
                        last = nc.tensor.matmul(ps[:, span(m)], qd[:, buf, k, :, :].rearrange("p h q -> p (h q)"),
                                                kr[:, buf, k, span(m)], start=True, stop=True)
                    last.then_inc(*PE.inc(f"S{step}{t}"))

                def values(t):
                    k, buf = (t - 1, par) if t else (TILES - 1, 1 - par)
                    pe.wait_ge(*V.at(f"T{k}1", r if t else r - 1))
                    pe.wait_ge(*A.at(f"T{k}3", r if t else r - 1))
                    if t == 1 and finishing:
                        pe.wait_ge(*V.at("own", r))
                    elif t > 1:
                        pe.wait_ge(*V.at(f"pv{t - 1}", r))
                    elif t == 0:
                        pe.wait_ge(*V.at("pv7", r - 1))
                    for i in range(KC):
                        q = i % 4
                        last = nc.tensor.matmul(pv[32 * q:32 * q + 16, 0:P], v[0:chunk[i], buf, i, 16 * k:16 * k + 16],
                                                pT[0:chunk[i], k % 2, i, :], start=(i < 4), stop=(i >= KC - 4),
                                                tile_position=(0, 32 * q))
                    last.then_inc(*PE.inc(f"PV{t}"))

                def add_tiles():
                    pe.wait_ge(*V.at("pv0", r))
                    for k in range(TILES):
                        last = nc.tensor.matmul(sums, pvs[:, k, :], place[:, k, :], start=(k == 0), stop=(k == TILES - 1))
                    last.then_inc(*PE.inc("sums"))

                def prepare(at):
                    step = IN.get(at)
                    if step is None or not active(step, r):
                        return
                    order = list(PREPS)
                    before = [(x, r) for x in order[:order.index(step)] if active(x, r)]
                    if not before and not (isinstance(r, int) and r == 0):
                        before = [(x, r - 1) for x in order if not isinstance(r, int) or active(x, r - 1)]
                    if before:
                        pe.wait_ge(*reader(before[-1][0]).at(*before[-1]))
                    what, m = step[:-1], step[-1]
                    if step == "yT":
                        pe.wait_ge(*V.at("own", r))
                        last = nc.tensor.matmul(prep[:, 0:S], own[:, :], delta[:, :], start=True, stop=True)
                    elif step == "out":
                        pe.wait_ge(*V.at("yT", r))
                        last = nc.tensor.matmul(prep[S * (1 - par):S * (2 - par), 0:D], yT[:, :], wo[:, :], start=True, stop=True)
                    elif what == "k":
                        m = int(m)
                        last = nc.tensor.matmul(prep[:, 0:wide_[m]], wk[:, :], ctxT[:, span(m)], start=True, stop=True)
                    else:
                        m = int(m)
                        if step == "ctxT0":
                            pe.wait_ge(ctx_in[par], 32 * pair + 32)
                        for j in range(4 * m, 4 * m + part[m]):
                            to = P * (j - 4 * m)
                            if what == "ctxT":
                                last = nc.tensor.transpose(prep[:, to:to + chunk[j]], ctx[0:chunk[j], par, j, :],
                                                           c.ident[0:chunk[j], 0:chunk[j]])
                            else:
                                last = nc.tensor.matmul(prep[0:chunk[j], to:to + P], ctxT[:, P * j:P * j + chunk[j]], wv[:, :],
                                                        start=True, stop=True)
                    last.then_inc(*PE.inc(step))

                for t in range(TILES):
                    scored = (t < 6 and tiles) or (t >= 6 and coming)
                    if tiles:
                        turns(t, 0)
                        turns(t, 1)
                    prepare(f"a{t}")
                    if scored:
                        scores(t, 0)
                    if tiles:
                        turns(t, 2)
                        turns(t, 3)
                    if (t == 0 and finishing) or (t and tiles):
                        values(t)
                    if scored:
                        scores(t, 1)
                    if t == 0 and finishing:
                        add_tiles()
                    prepare(f"b{t}")

            rounds(pe, body)

        @block.vector
        def _(dve):
            dve.wait_ge(loaded, 144)
            nc.vector.tensor_scalar(shift[:, :], mask[:, :], OUT, None, ALU.mult).then_inc(*V.inc("shift"))
            nc.vector.memset(pv[:, :], 0.0).then_inc(*V.inc("zero"))
            ln_vector(c, dve, V, A, PE, tp)
            for i in range(4):
                q, parts = qT[:, 512 * i:512 * i + 512], q_parts[:, :, 512 * i:512 * i + 512]
                dve.wait_ge(*PE.at(f"q{i}"))
                nc.vector.tensor_scalar(q, ps[:, 512 * i:512 * i + 512], DH ** -0.5, None, ALU.mult).then_inc(*V.inc(f"q{i}a"))
                dve.wait_ge(*V.at(f"q{i}a"))
                nc.vector.tensor_copy(parts[:, 0, :], q).then_inc(*V.inc(f"q{i}b"))
                dve.wait_ge(*V.at(f"q{i}b"))
                nc.vector.tensor_tensor(q, q, parts[:, 0, :], ALU.subtract).then_inc(*V.inc(f"q{i}c"))
                dve.wait_ge(*V.at(f"q{i}c"))
                nc.vector.tensor_copy(parts[:, 1, :], q).then_inc(*V.inc(f"q{i}d"))
                dve.wait_ge(*V.at(f"q{i}d"))
                nc.vector.tensor_tensor(parts[:, 2, :], q, parts[:, 1, :], ALU.subtract).then_inc(*V.inc(f"q{i}e"))

            def body(r, par, pair, tile):
                finishing, tiles, coming, far = kind(r)

                def masked(t, half):
                    k = (t + 2) % TILES
                    step, keys = "AB"[half], slice(*halves[half])
                    dve.wait_ge(*PE.at(f"S{step}{t}", r))
                    nc.vector.memset(pause[:, half:half + 1], 0.0)
                    nc.vector.tensor_tensor_reduce(out=sc[:, k % 4, keys], in0=ps[:, keys], in1=shift[:, keys],
                                                   scale=1.0, scalar=3 * OUT, op0=ALU.add, op1=ALU.max,
                                                   accum_out=tops[:, half:half + 1]).then_inc(*V.inc(f"m{step}{t}"))

                def prepared(at):
                    step = IN.get(at)
                    if step not in V_PREPS or not active(step, r):
                        return
                    dve.wait_ge(*PE.at(step, r))
                    if step == "yT":
                        nc.vector.tensor_copy(yT[:, :], prep[:, 0:S]).then_inc(*V.inc("yT"))
                    elif step == "out":
                        half = slice(S * (1 - par), S * (2 - par))
                        xs = c.x[half, bass.ds(tile, 1), :].rearrange("p a d -> p (a d)")
                        nc.vector.tensor_tensor(xs, prep[half, 0:D], xs, ALU.add).then_inc(*V.inc("out"))
                    elif step[0] == "k":
                        m = int(step[1])
                        if m >= 2:
                            dve.wait_ge(*G.at(f"k{m - 2}c", r))
                        elif not isinstance(r, int) or r:
                            dve.wait_ge(*G.at(f"k{m + 2}c", r - 1))
                        nc.vector.tensor_copy(k_rest[:, m % 2, 0:wide_[m]], prep[:, 0:wide_[m]]).then_inc(*V.inc(step))
                    elif step[0] == "v":
                        put(nc.vector.tensor_copy, v[:, 1 - par, :, :], prep, int(step[1]), V.inc(step))
                    else:
                        m = int(step[4])
                        nc.vector.tensor_copy(ctxT[:, span(m)], prep[:, 0:wide_[m]]).then_inc(*V.inc(step))

                for t in range(TILES):
                    scored = (t < 6 and tiles) or (t >= 6 and coming)
                    if tiles:
                        for m in (0, 1):
                            dve.wait_ge(*PE.at(f"T{t}{m}", r))
                            put(nc.vector.tensor_copy, pT[:, t % 2, :, :], tp[m % 2], m, V.inc(f"T{t}{m}"))
                    if scored:
                        masked(t, 0)
                    if t == 0 and finishing:
                        dve.wait_ge(*A.at("exp6", r - 1))
                        nc.vector.reciprocal(rinv[:, :], rows[:, 1 - par, :]).then_inc(*V.inc("rinv"))
                        dve.wait_ge(*V.at("rinv", r))
                        nc.vector.scalar_tensor_tensor(out=vinv[:, :], in0=ntop[:, 1 - par, :], scalar=-0.5 * OUT, in1=rinv[:, :],
                                                       op0=ALU.is_lt, op1=ALU.mult).then_inc(*V.inc("vinv"))
                        dve.wait_ge(*V.at("vinv", r))
                        nc.vector.tensor_tensor(coef[:, :].rearrange("p (k d) -> p k d", k=TILES),
                                                vinv[:, :].unsqueeze(2).broadcast_to([P, TILES, 16]),
                                                own_dims[:, :].rearrange("p (k d) -> p k d", k=TILES), ALU.mult)\
                            .then_inc(*V.inc("coef"))
                    if (t == 0 and finishing) or (t and tiles):
                        dve.wait_ge(*PE.at(f"PV{t}", r))
                        nc.vector.tensor_copy(pvs[:, (t - 1) % TILES, :], tile_pv).then_inc(*V.inc(f"pv{t}"))
                    prepared(f"a{t}")
                    if scored:
                        buf = par if t < 6 else 1 - par
                        k = (t + 2) % TILES
                        masked(t, 1)
                        dve.wait_ge(*V.at(f"mB{t}", r))
                        nc.vector.tensor_reduce(top[:, :], tops[:, :], AX.X, ALU.max).then_inc(*V.inc(f"top{t}"))
                        dve.wait_ge(*V.at(f"top{t}", r))
                        nc.vector.tensor_scalar(ntop[:, buf, k:k + 1], top[:, :], -1.0, None, ALU.mult).then_inc(*V.inc(f"ntop{t}"))
                    if t == 0 and finishing:
                        dve.wait_ge(*V.at("coef", r))
                        dve.wait_ge(*PE.at("sums", r))
                        nc.vector.tensor_tensor(own[:, :], sums, coef[:, :], ALU.mult).then_inc(*V.inc("own"))
                    prepared(f"b{t}")

            rounds(dve, body)

        @block.scalar
        def _(act):
            ln_scalar(c, act, V, A, PE, tp)

            def body(r, par, pair, tile):
                finishing, tiles, coming, far = kind(r)

                def prepared(at):
                    step = IN.get(at)
                    if step not in A_PREPS or not active(step, r):
                        return
                    if step == "k0" and not (isinstance(r, int) and r == 0):
                        act.wait_ge(k_stored[1 - par], 16 * (pair + 1 if par else pair))
                    act.wait_ge(*(V if step[0] == "k" else PE).at(step, r))
                    if step[0] == "k":
                        m = int(step[1])
                        nc.scalar.copy(k_parts[:, 0, span(m)], k_rest[:, m % 2, 0:wide_[m]]).then_inc(*A.inc(step))
                    elif step[0] == "v":
                        put(nc.scalar.copy, v[:, 1 - par, :, :], prep, int(step[1]), A.inc(step))
                    else:
                        m = int(step[4])
                        nc.scalar.copy(ctxT[:, span(m)], prep[:, 0:wide_[m]]).then_inc(*A.inc(step))

                for t in range(TILES):
                    if (t < 7 and tiles) or (t == 7 and coming):
                        k, buf = (t + 1, par) if t < 7 else (0, 1 - par)
                        act.wait_ge(*(V.at(f"ntop{t - 1}", r) if t else V.at("ntop7", r - 1)))
                        nc.scalar.activation(sc[:, k % 4, :], sc[:, k % 4, :], ACT.Exp, bias=ntop[:, buf, k:k + 1], scale=1.0,
                                             accum_out=rows[:, buf, k:k + 1]).then_inc(*A.inc(f"exp{t}"))
                    prepared(f"a{t}")
                    if tiles:
                        for m in (2, 3):
                            act.wait_ge(*PE.at(f"T{t}{m}", r))
                            put(nc.scalar.copy, pT[:, t % 2, :, :], tp[m % 2], m, A.inc(f"T{t}{m}"))
                    prepared(f"b{t}")

            rounds(act, body)


def build(nc, a):
    with ExitStack() as ctx:
        c = Core(nc, ctx, a)
        start(c)
        cross_attention(c, "L0_xattn", "mask_keys", 1)
        spectral_layer(c, "L0_attn")
        capacity_experts(c, "L0_ffn")
        causal_cross_attention(c, "L1_xattn")
        two_step_attention(c, "L1_attn")
        routed_experts(c, "L1_ffn")
        many_head_cross_attention(c, "L2_xattn")
        selective_scan_layer(c, "L2_attn")
        chosen_adapters(c, "L2_ffn")
        cross_attention(c, "L3_xattn", "mask_pairs", S)
        self_attention(c, "L3_attn")
        quantised_ffn(c, "L3_ffn")
        finish(c)


def constants():
    p = np.arange(P)
    same = p[:, None] // S == p[None, :] // S
    f = np.float32
    half = DH // 2
    angle = np.arange(S, dtype=f)[None, :] * (f(1) / f(10000) ** ((p % half).astype(f) / f(half)))[:, None]
    return {
        "c_heads": (p[:, None] % 32 // DH == np.arange(4)).astype(f),
        "c_sixteen_heads": (p[:, None] // DH == np.arange(H)).astype(f),
        "c_own_dims": (p[:, None] // S == p[None, :] // DH % 2).astype(f),
        "c_place": ((p[:, None, None] % 32 < 16) & (p[None, None, :] == 16 * np.arange(8)[None, :, None] + p[:, None, None] % 32)).astype(f),
        "c_which": (p[None, None, :] // DH == 2 * np.arange(8)[None, :, None] + p[:, None, None] // S).astype(f),
        "c_pair_half": (p[:, None] // DH % 2 == np.arange(2)).astype(f),
        "c_delta": (p[:, None] % S == np.arange(S)).astype(f),
        "c_later": ((p[:, None] % S == np.arange(S)) & (np.arange(S) > 0)).astype(f),
        "c_causal": np.where(np.arange(S) <= p[:, None] % S, 0, OUT).astype(f),
        "c_strict": np.where(np.arange(S) < p[:, None] % S, 0, OUT).astype(f),
        "c_halves": np.stack([p < 32, (p >= 32) & (p < 64)], axis=1).astype(f),
        "c_freq": ((p[:, None] % 32 == np.arange(32)) & (p[:, None] < 64)).astype(f),
        "c_earlier": (p[:, None] < p[None, :]).astype(f),
        "c_sixteen": np.broadcast_to(np.arange(16, dtype=f), (P, NT, 16)),
        "c_rank": np.broadcast_to((8 - np.arange(8, dtype=f))[None, :, None], (P, 8, B)),
        "c_eight": np.broadcast_to(np.arange(8, dtype=f), (P, NT, 8)),
        "c_cos": np.cos(angle).astype(f),
        "c_sin": (np.sin(angle) * np.where(p % DH < half, -1, 1)[:, None]).astype(f),
        "c_ident": np.eye(P, dtype=f),
        "c_pair_causal": np.where(same & (p[None, :] <= p[:, None]), 0, OUT).astype(f),
    }


def kernel(**inputs):
    import concourse.bacc as bacc
    from concourse.bass_utils import run_bass_kernel_spmd

    i = {k: np.asarray(v) for k, v in inputs.items()}
    arrays = {
        "x": i["x"].reshape(TOK, D),
        "ctx": i["ctx_1024"],
        "mask_keys": i["mask_BxS2_ik0"].reshape(B, 1, KEYS),
        "mask_pairs": i["mask_BxSxS2_bk1"],
    }
    for n in ("L0_xattn", "L3_xattn"):
        arrays.update({f"{n}_Wq": i[f"{n}_Wq"], f"{n}_WkT": i[f"{n}_Wk"].T, f"{n}_Wv": i[f"{n}_Wv"],
                       f"{n}_bq": i[f"{n}_bq"].reshape(D, 1), f"{n}_bk": i[f"{n}_bk"].reshape(D, 1),
                       f"{n}_bv": i[f"{n}_bv"].reshape(1, D)})
    arrays.update({"L1_xattn_Wq": i["L1_xattn_Wq"], "L1_xattn_WqT": i["L1_xattn_Wq"].T})
    arrays.update({
        "L1_attn_w": np.stack([i["L1_attn_W_attn"][:, :D], i["L1_attn_W_attn"][:, D:], i["L1_attn_W_k2"]]),
        "L1_attn_bias": np.stack([i["L1_attn_b_attn"][:D], i["L1_attn_b_attn"][D:], i["L1_attn_b_k2"]], axis=1),
        "L1_attn_W_proj": i["L1_attn_W_proj"], "L1_attn_b_proj": i["L1_attn_b_proj"].reshape(1, D),
    })
    swapped = np.arange(D).reshape(H, 2, DH // 2)[:, ::-1].reshape(D)
    wq, wk, wv = i["L3_attn_w_qkv"].reshape(3, D, D)
    arrays.update({"L3_attn_w": np.stack([wq.T, wq[swapped].T, wk.T, wk[swapped].T, wv.T]),
                   "L3_attn_wo": i["L3_attn_w_out"].T})
    twice = lambda v: np.concatenate([v, v, np.zeros_like(v), np.zeros_like(v)]).reshape(-1, 1)
    filled = lambda w: np.concatenate([w, np.zeros((P - w.shape[0],) + w.shape[1:], w.dtype)])
    arrays.update({
        "L0_attn_cols": np.stack([i[f"L0_attn_{n}"] for n in ("ln1_g", "ln1_b", "ln3_g", "ln3_b")], axis=1),
        "L0_attn_W_toT": filled(i["L0_attn_W_to"]).T, "L0_attn_W_fromT": filled(i["L0_attn_W_from"].T),
        "L0_attn_decay": twice(i["L0_attn_log_decay"]), "L0_attn_freq": twice(i["L0_attn_frequencies"]),
        "L0_attn_W1T": i["L0_attn_W_ffn1"].T, "L0_attn_b1": i["L0_attn_b_ffn1"].reshape(4, P).T,
        "L0_attn_W2T": i["L0_attn_W_ffn2"].T, "L0_attn_b2": i["L0_attn_b_ffn2"].reshape(1, D),
        "L0_ffn_Wg": i["L0_ffn_Wg"], "L0_ffn_w1": i["L0_ffn_w1"], "L0_ffn_w2": i["L0_ffn_w2"],
    })
    arrays.update({
        "L1_ffn_embT": i["L1_ffn_uzman_embeddings"].T, "L1_ffn_bonus": i["L1_ffn_onbellek_durumu"].reshape(1, -1),
        "L1_ffn_b1": i["L1_ffn_b1"].reshape(8, 4, P).transpose(2, 0, 1), "L1_ffn_b2": i["L1_ffn_b2"], "L1_ffn_W1": i["L1_ffn_W1"], "L1_ffn_W2": i["L1_ffn_W2"],
        "L2_attn_cols": np.stack([i["L2_attn_ln_w"], i["L2_attn_ln_b"]], axis=1),
        "L2_attn_W_inT": i["L2_attn_W_in"].T, "L2_attn_conv_w": i["L2_attn_conv_w"].reshape(2 * D, 4),
        "L2_attn_W_xT": i["L2_attn_W_x"].T, "L2_attn_W_dtT": i["L2_attn_W_dt"].T, "L2_attn_log_A": i["L2_attn_log_A"],
        "L2_attn_W_outT": i["L2_attn_W_out"].T,
        "L2_attn_vecs": np.stack([i[f"L2_attn_{n}"].reshape(2, P).T for n in ("conv_b", "b_dt", "D_param")]),
    })
    side_by_side = lambda w: w.transpose(1, 0, 2).reshape(D, -1)
    adapter = {n: i[f"L2_ffn_{n}"] for n in ("W_base", "b_base", "Wd1", "bd1", "Wd2", "bd2", "Wa_down", "ba_down", "Wa_up", "ba_up")}
    arrays.update({
        "L2_ffn_wd1": side_by_side(adapter["Wd1"]), "L2_ffn_bd1": adapter["bd1"].reshape(2, P).T,
        "L2_ffn_wd2": adapter["Wd2"].reshape(2 * P, D), "L2_ffn_bd2": adapter["bd2"].T,
        "L2_ffn_wad": side_by_side(adapter["Wa_down"]), "L2_ffn_bad": adapter["ba_down"].reshape(4, P).T,
        "L2_ffn_wau": adapter["Wa_up"].reshape(4 * P, D), "L2_ffn_bau": adapter["ba_up"],
        "L2_ffn_wb": adapter["W_base"], "L2_ffn_bb": adapter["b_base"].reshape(1, D),
    })
    rows = lambda w: np.concatenate([w, np.zeros((384 - w.shape[0], D), w.dtype)]).reshape(3, P, D).transpose(1, 0, 2).reshape(P, -1)
    arrays["L3_ffn_w"] = np.concatenate([rows(i["L3_ffn_w_gate"]), rows(i["L3_ffn_w_up"]), i["L3_ffn_w_down"]], axis=1)
    arrays.update({f"L2_xattn_w{n}": i[f"L2_xattn_W_{n}"].T for n in "qkvo"})
    arrays["mask_all"] = i["mask_1x1xSxS2_bk1"].reshape(S, KEYS)
    arrays.update(constants())

    nc = bacc.Bacc("TRN2", target_bir_lowering=False, num_devices=1)
    arrays = {f"in_{k}": np.ascontiguousarray(v) for k, v in arrays.items()}
    a = {k[3:]: nc.dram_tensor(k, v.shape, mybir.dt.from_np(v.dtype), kind="ExternalInput").ap()
         for k, v in arrays.items()}
    a["out"] = nc.dram_tensor("out", (TOK, D), F32, kind="ExternalOutput").ap()
    a["scratch_in"] = nc.dram_tensor("scratch_in", (TOK, D), F32).ap()
    a["scratch_out"] = nc.dram_tensor("scratch_out", (TOK, D), F32).ap()
    a["scratch_rows"] = nc.dram_tensor("scratch_rows", (32, TOK), F32).ap()
    a["scratch_q"] = nc.dram_tensor("scratch_q", (3, P, TOK), BF16).ap()
    a["scratch_k"] = nc.dram_tensor("scratch_k", (2, 3, P, KEYS), BF16).ap()
    build(nc, a)
    r = run_bass_kernel_spmd(nc, [arrays], core_ids=[0])
    return r.results[0]["out"].reshape(B, S, D)
```
